# Optimizing a Trainium2 kernel written in Bass

```python
import numpy as np
import jax
import jax.numpy as jnp

def _softmax(x, axis=-1):
    return jax.nn.softmax(x, axis=axis)

def _gelu(x):
    return jax.nn.gelu(x, approximate=True)

def _silu(x):
    return jax.nn.silu(x)

def _sigmoid(x):
    return jax.nn.sigmoid(x)

def _layernorm(x, axis=-1, eps=1e-05):
    m = jnp.mean(x, axis=axis, keepdims=True)
    v = jnp.var(x, axis=axis, keepdims=True)
    return (x - m) / jnp.sqrt(v + eps)

def _scatter_add(tgt, idx, src, axis=0):
    return tgt.at[idx].add(src)

def _segment_sum(src, seg, n):
    return jax.ops.segment_sum(src, seg, n)
kernel_name = 'mk_decoder_postln_d2_seqx_r4_e5b0bc'

def setup_inputs(seed: int=0):
    np.random.seed(seed)
    _w = jnp.asarray

    def _rec_inputs():
        import jax
        import jax.numpy as jnp
        _rk = jax.random.key(seed)
        x = -0.0002928 + 1 * jax.random.normal(jax.random.fold_in(_rk, 1), (4, 1024, 256), jnp.float32)
        _lenS = 1024 - jax.random.randint(jax.random.fold_in(_rk, 7), (4,), 0, max(1, 1024 // 4) + 1, jnp.int32)
        _lenS2 = 64 - jax.random.randint(jax.random.fold_in(_rk, 8), (4,), 0, max(1, 64 // 4) + 1, jnp.int32)
        _ctx_768P = jax.random.normal(jax.random.fold_in(_rk, 11), (4, 16, 192), jnp.float32)
        _ctx_768c = jax.random.dirichlet(jax.random.fold_in(_rk, 511), 0.3 * jnp.ones((16,), jnp.float32), (4, 64))
        _ctx_768t = jnp.einsum('bsk,bkd->bsd', _ctx_768c, _ctx_768P)
        _ctx_768t = _ctx_768t * jax.lax.rsqrt(jnp.mean(jnp.square(_ctx_768t)) + 1e-12) * 0.953939
        ctx_768 = 2.09791e-05 + 1.00001 * (_ctx_768t + 0.3 * jax.random.normal(jax.random.fold_in(_rk, 611), (4, 64, 192), jnp.float32))
        _validS = jnp.arange(1024)[None, :] < _lenS[:, None]
        _validS2 = jnp.arange(64)[None, :] < _lenS2[:, None]
        _causal = jnp.tril(jnp.ones((1024, 1024), dtype=bool))
        mask_BxS2_bk0 = jnp.logical_not(jnp.broadcast_to(_validS2[:, :], (4, 64)))
        return (x, ctx_768, mask_BxS2_bk0)
    x, ctx_768, mask_BxS2_bk0 = _rec_inputs()

    def _L0_attn_setup():
        import jax, jax.numpy as jnp
        import numpy as np
        D_MODEL = 256
        N_HEADS = 16
        HEAD_DIM = D_MODEL // N_HEADS
        ROPE_BASE = 10000.0

        def _rope_cos_sin(seq_len, dtype):
            inv_freq = 1.0 / ROPE_BASE ** (jnp.arange(0, HEAD_DIM, 2, dtype=jnp.float32) / HEAD_DIM)
            t = jnp.arange(seq_len, dtype=jnp.float32)
            freqs = jnp.outer(t, inv_freq)
            emb = jnp.concatenate([freqs, freqs], axis=-1)
            return (jnp.cos(emb).astype(dtype), jnp.sin(emb).astype(dtype))

        def _rotate_half(v):
            v1, v2 = jnp.split(v, 2, axis=-1)
            return jnp.concatenate([-v2, v1], axis=-1)
        key = jax.random.key(seed)
        ks = jax.random.split(key, 5)
        B, S = (2, 512)
        x = jax.random.normal(ks[0], (B, S, D_MODEL), dtype=jnp.float32)
        scale = 1.0 / np.sqrt(D_MODEL)
        Wq = jax.random.normal(ks[1], (D_MODEL, D_MODEL), dtype=jnp.float32) * scale
        Wk = jax.random.normal(ks[2], (D_MODEL, D_MODEL), dtype=jnp.float32) * scale
        Wv = jax.random.normal(ks[3], (D_MODEL, D_MODEL), dtype=jnp.float32) * scale
        Wo = jax.random.normal(ks[4], (D_MODEL, D_MODEL), dtype=jnp.float32) * scale
        return {'x': x, 'Wq': Wq, 'Wk': Wk, 'Wv': Wv, 'Wo': Wo}
    _L0_attn_all = _L0_attn_setup()
    _L0_attn_in = {k: v for k, v in _L0_attn_all.items() if k in ('Wq', 'Wk', 'Wv', 'Wo')}
    del _L0_attn_all

    def _L0_xattn_setup():
        import jax, jax.numpy as jnp
        import numpy as np
        QUERY_DIM, KV_DIM, EMBED_DIM, NUM_HEADS = (256, 192, 256, 16)
        HEAD_DIM = EMBED_DIM // NUM_HEADS
        SCALE = HEAD_DIM ** (-0.5)
        LN_EPS = 1e-05

        def _l2norm(x, eps=1e-12):
            n = jnp.sqrt(jnp.sum(x * x, axis=-1, keepdims=True))
            return x / jnp.maximum(n, eps)
        key = jax.random.key(seed)
        ks = jax.random.split(key, 12)
        B, Nq, Nk = (2, 512, 512)
        s = lambda d: 1.0 / np.sqrt(d)
        return {'query': jax.random.normal(ks[0], (B, Nq, QUERY_DIM), jnp.float32), 'key': jax.random.normal(ks[1], (B, Nk, KV_DIM), jnp.float32), 'value': jax.random.normal(ks[2], (B, Nk, KV_DIM), jnp.float32), 'Wq': jax.random.normal(ks[3], (QUERY_DIM, EMBED_DIM), jnp.float32) * s(QUERY_DIM), 'bq': jnp.zeros((EMBED_DIM,), jnp.float32), 'Wk': jax.random.normal(ks[4], (KV_DIM, EMBED_DIM), jnp.float32) * s(KV_DIM), 'bk': jnp.zeros((EMBED_DIM,), jnp.float32), 'Wv': jax.random.normal(ks[5], (KV_DIM, EMBED_DIM), jnp.float32) * s(KV_DIM), 'bv': jnp.zeros((EMBED_DIM,), jnp.float32), 'Wo': jax.random.normal(ks[6], (EMBED_DIM, EMBED_DIM), jnp.float32) * s(EMBED_DIM), 'bo': jnp.zeros((EMBED_DIM,), jnp.float32), 'ln_gamma': jnp.ones((EMBED_DIM,), jnp.float32), 'ln_beta': jnp.zeros((EMBED_DIM,), jnp.float32)}
    _L0_xattn_all = _L0_xattn_setup()
    _L0_xattn_in = {k: v for k, v in _L0_xattn_all.items() if k in ('Wq', 'bq', 'Wk', 'bk', 'Wv', 'bv', 'Wo', 'bo', 'ln_gamma', 'ln_beta')}
    del _L0_xattn_all

    def _L0_ffn_setup():
        import jax, jax.numpy as jnp
        import numpy as np
        B, T, D, E, TOP_K = (4, 1024, 256, 8, 2)
        CAPACITY_FACTOR = 1.5
        key = jax.random.key(seed)
        k1, k2, k3 = jax.random.split(key, 3)
        x = jax.random.normal(k1, (B, T, D), dtype=jnp.float32)
        Wr = jax.random.normal(k2, (E, D), dtype=jnp.float32) * 0.02
        We = jax.random.normal(k3, (E, D, D), dtype=jnp.float32) * 0.02
        return {'x': x, 'Wr': Wr, 'We': We}
    _L0_ffn_all = _L0_ffn_setup()
    _L0_ffn_in = {k: v for k, v in _L0_ffn_all.items() if k in ('Wr', 'We')}
    del _L0_ffn_all

    def _L1_attn_setup():
        import jax, jax.numpy as jnp
        import numpy as np
        import math
        EMBED_DIM = 256
        NUM_HEADS = 16
        DEPTH = 12
        HEAD_DIM = EMBED_DIM // NUM_HEADS // 2
        LAMBDA_INIT = 0.8 - 0.6 * math.exp(-0.3 * DEPTH)
        SCALE = HEAD_DIM ** (-0.5)
        RMS_EPS = 1e-05
        BATCH, SEQ = (2, 512)

        def _freqs(seq_len):
            angle = 1.0 / 10000.0 ** jnp.linspace(0.0, 1.0, HEAD_DIM // 2)
            idx = jnp.arange(seq_len, dtype=jnp.float32)
            f = idx[:, None] * angle[None, :]
            return (jnp.cos(f), jnp.sin(f))

        def _rope_interleaved(x, cos, sin):
            x1, x2 = (x[..., 0::2], x[..., 1::2])
            c = cos[None, :, None, :]
            s = sin[None, :, None, :]
            o1 = x1 * c - x2 * s
            o2 = x1 * s + x2 * c
            return jnp.stack([o1, o2], axis=-1).reshape(x.shape)

        def _forward(x, Wq, Wk, Wv, Wo, lambda_q1, lambda_k1, lambda_q2, lambda_k2, rms_weight):
            b, t, _ = x.shape
            q = (x @ Wq.T).reshape(b, t, 2 * NUM_HEADS, HEAD_DIM)
            k = (x @ Wk.T).reshape(b, t, 2 * NUM_HEADS, HEAD_DIM)
            v = (x @ Wv.T).reshape(b, t, NUM_HEADS, 2, HEAD_DIM)
            cos, sin = _freqs(t)
            q = _rope_interleaved(q, cos, sin)
            k = _rope_interleaved(k, cos, sin)
            q = q.reshape(b, t, NUM_HEADS, 2, HEAD_DIM)
            k = k.reshape(b, t, NUM_HEADS, 2, HEAD_DIM)
            q1, q2 = (q[..., 0, :], q[..., 1, :])
            k1, k2 = (k[..., 0, :], k[..., 1, :])
            v12 = v.reshape(b, t, NUM_HEADS, 2 * HEAD_DIM)

            def attend(qh, kh):
                scores = jnp.einsum('bthd,bshd->bhts', qh, kh) * SCALE
                p = jax.nn.softmax(scores, axis=-1)
                return jnp.einsum('bhts,bshe->bthe', p, v12)
            attn1 = attend(q1, k1)
            attn2 = attend(q2, k2)
            lam = jnp.exp(jnp.sum(lambda_q1 * lambda_k1)) - jnp.exp(jnp.sum(lambda_q2 * lambda_k2)) + LAMBDA_INIT
            a = attn1 - lam * attn2
            a = a * jax.lax.rsqrt(jnp.mean(a * a, axis=-1, keepdims=True) + RMS_EPS) * rms_weight
            a = a * (1.0 - LAMBDA_INIT)
            a = a.reshape(b, t, NUM_HEADS * 2 * HEAD_DIM)
            return a @ Wo.T
        key = jax.random.key(seed)
        ks = jax.random.split(key, 9)
        std = EMBED_DIM ** (-0.5)
        return {'x': jax.random.normal(ks[0], (BATCH, SEQ, EMBED_DIM), jnp.float32), 'Wq': jax.random.normal(ks[1], (EMBED_DIM, EMBED_DIM), jnp.float32) * std, 'Wk': jax.random.normal(ks[2], (EMBED_DIM, EMBED_DIM), jnp.float32) * std, 'Wv': jax.random.normal(ks[3], (EMBED_DIM, EMBED_DIM), jnp.float32) * std, 'Wo': jax.random.normal(ks[4], (EMBED_DIM, EMBED_DIM), jnp.float32) * std, 'lambda_q1': jax.random.normal(ks[5], (HEAD_DIM,), jnp.float32) * 0.1, 'lambda_k1': jax.random.normal(ks[6], (HEAD_DIM,), jnp.float32) * 0.1, 'lambda_q2': jax.random.normal(ks[7], (HEAD_DIM,), jnp.float32) * 0.1, 'lambda_k2': jax.random.normal(ks[8], (HEAD_DIM,), jnp.float32) * 0.1, 'rms_weight': jnp.ones((2 * HEAD_DIM,), jnp.float32)}
    _L1_attn_all = _L1_attn_setup()
    _L1_attn_in = {k: v for k, v in _L1_attn_all.items() if k in ('Wq', 'Wk', 'Wv', 'Wo', 'lambda_q1', 'lambda_k1', 'lambda_q2', 'lambda_k2', 'rms_weight')}
    del _L1_attn_all

    def _L1_xattn_setup():
        import jax, jax.numpy as jnp
        import numpy as np
        DIM_IN, DIM_LAT, DIM_HEAD = (192, 256, 64)
        INNER = max(DIM_LAT, DIM_IN)
        HEADS = INNER // DIM_HEAD
        SCALE = DIM_HEAD ** (-0.5)
        RMS_EPS = 1e-08
        LN_EPS = 1e-05

        def layernorm(x, g, b):
            mu = jnp.mean(x, axis=-1, keepdims=True)
            var = jnp.mean((x - mu) ** 2, axis=-1, keepdims=True)
            return (x - mu) * jax.lax.rsqrt(var + LN_EPS) * g + b

        def rmsnorm(x, gamma):
            norm = jnp.sqrt(jnp.sum(x * x, axis=-1, keepdims=True)) * x.shape[-1] ** (-0.5)
            return x / jnp.maximum(norm, RMS_EPS) * gamma
        key = jax.random.key(seed)
        ks = jax.random.split(key, 12)
        b, n, m = (4, 1024, 128)
        x = jax.random.normal(ks[0], (b, n, DIM_IN), jnp.float32)
        latents = jax.random.normal(ks[1], (b, m, DIM_LAT), jnp.float32)
        mask = jax.random.randint(ks[2], (b, n), 0, 2).astype(bool)
        s = lambda k, sh, fan: jax.random.normal(k, sh, jnp.float32) * fan ** (-0.5)
        return {'x': x, 'latents': latents, 'mask': mask, 'ln_x_g': jnp.ones((DIM_IN,), jnp.float32), 'ln_x_b': jnp.zeros((DIM_IN,), jnp.float32), 'ln_l_g': jnp.ones((DIM_LAT,), jnp.float32), 'ln_l_b': jnp.zeros((DIM_LAT,), jnp.float32), 'qn_g': jnp.ones((DIM_HEAD,), jnp.float32), 'kn_g': jnp.ones((DIM_HEAD,), jnp.float32), 'Wq': s(ks[3], (INNER, DIM_LAT), DIM_LAT), 'Wkv': s(ks[4], (2 * INNER, DIM_IN), DIM_IN), 'Wlkv': s(ks[5], (2 * INNER, DIM_LAT), DIM_LAT), 'Wo': s(ks[6], (DIM_LAT, INNER), INNER), 'bo': jnp.zeros((DIM_LAT,), jnp.float32)}
    _L1_xattn_all = _L1_xattn_setup()
    _L1_xattn_in = {k: v for k, v in _L1_xattn_all.items() if k in ('ln_x_g', 'ln_x_b', 'ln_l_g', 'ln_l_b', 'qn_g', 'kn_g', 'Wq', 'Wkv', 'Wlkv', 'Wo', 'bo')}
    del _L1_xattn_all

    def _L1_ffn_setup():
        import jax, jax.numpy as jnp
        import numpy as np
        TOPK = 2
        CAPACITY_FACTOR = 1.0
        EPS = 1e-06
        B, S, D = (4, 1024, 256)
        E = 8
        SUB_H = 512 // E
        key = jax.random.key(seed)
        ks = jax.random.split(key, 7)
        x = jax.random.normal(ks[0], (B, S, D), dtype=jnp.float32)
        w_gate_w = jax.random.normal(ks[1], (D, E), dtype=jnp.float32) * 0.02
        w_gate_b = jnp.zeros((E,), jnp.float32)
        W1 = jax.random.normal(ks[2], (E, D, SUB_H), dtype=jnp.float32) * 0.02
        b1 = jnp.zeros((E, SUB_H), jnp.float32)
        W2 = jax.random.normal(ks[3], (E, SUB_H, D), dtype=jnp.float32) * 0.02
        b2 = jnp.zeros((E, D), jnp.float32)
        return {'x': x, 'w_gate_w': w_gate_w, 'w_gate_b': w_gate_b, 'W1': W1, 'b1': b1, 'W2': W2, 'b2': b2}
    _L1_ffn_all = _L1_ffn_setup()
    _L1_ffn_in = {k: v for k, v in _L1_ffn_all.items() if k in ('w_gate_w', 'w_gate_b', 'W1', 'b1', 'W2', 'b2')}
    del _L1_ffn_all
    return {'x': x, 'ctx_768': ctx_768, 'mask_BxS2_bk0': mask_BxS2_bk0, 'L0_attn_Wq': _L0_attn_in['Wq'], 'L0_attn_Wk': _L0_attn_in['Wk'], 'L0_attn_Wv': _L0_attn_in['Wv'], 'L0_attn_Wo': _L0_attn_in['Wo'], 'L0_xattn_Wq': _L0_xattn_in['Wq'], 'L0_xattn_bq': _L0_xattn_in['bq'], 'L0_xattn_Wk': _L0_xattn_in['Wk'], 'L0_xattn_bk': _L0_xattn_in['bk'], 'L0_xattn_Wv': _L0_xattn_in['Wv'], 'L0_xattn_bv': _L0_xattn_in['bv'], 'L0_xattn_Wo': _L0_xattn_in['Wo'], 'L0_xattn_bo': _L0_xattn_in['bo'], 'L0_xattn_ln_gamma': _L0_xattn_in['ln_gamma'], 'L0_xattn_ln_beta': _L0_xattn_in['ln_beta'], 'L0_ffn_Wr': _L0_ffn_in['Wr'], 'L0_ffn_We': _L0_ffn_in['We'], 'L1_attn_Wq': _L1_attn_in['Wq'], 'L1_attn_Wk': _L1_attn_in['Wk'], 'L1_attn_Wv': _L1_attn_in['Wv'], 'L1_attn_Wo': _L1_attn_in['Wo'], 'L1_attn_lambda_q1': _L1_attn_in['lambda_q1'], 'L1_attn_lambda_k1': _L1_attn_in['lambda_k1'], 'L1_attn_lambda_q2': _L1_attn_in['lambda_q2'], 'L1_attn_lambda_k2': _L1_attn_in['lambda_k2'], 'L1_attn_rms_weight': _L1_attn_in['rms_weight'], 'L1_xattn_ln_x_g': _L1_xattn_in['ln_x_g'], 'L1_xattn_ln_x_b': _L1_xattn_in['ln_x_b'], 'L1_xattn_ln_l_g': _L1_xattn_in['ln_l_g'], 'L1_xattn_ln_l_b': _L1_xattn_in['ln_l_b'], 'L1_xattn_qn_g': _L1_xattn_in['qn_g'], 'L1_xattn_kn_g': _L1_xattn_in['kn_g'], 'L1_xattn_Wq': _L1_xattn_in['Wq'], 'L1_xattn_Wkv': _L1_xattn_in['Wkv'], 'L1_xattn_Wlkv': _L1_xattn_in['Wlkv'], 'L1_xattn_Wo': _L1_xattn_in['Wo'], 'L1_xattn_bo': _L1_xattn_in['bo'], 'L1_ffn_w_gate_w': _L1_ffn_in['w_gate_w'], 'L1_ffn_w_gate_b': _L1_ffn_in['w_gate_b'], 'L1_ffn_W1': _L1_ffn_in['W1'], 'L1_ffn_b1': _L1_ffn_in['b1'], 'L1_ffn_W2': _L1_ffn_in['W2'], 'L1_ffn_b2': _L1_ffn_in['b2']}

def reference(x, ctx_768, mask_BxS2_bk0, L0_attn_Wq, L0_attn_Wk, L0_attn_Wv, L0_attn_Wo, L0_xattn_Wq, L0_xattn_bq, L0_xattn_Wk, L0_xattn_bk, L0_xattn_Wv, L0_xattn_bv, L0_xattn_Wo, L0_xattn_bo, L0_xattn_ln_gamma, L0_xattn_ln_beta, L0_ffn_Wr, L0_ffn_We, L1_attn_Wq, L1_attn_Wk, L1_attn_Wv, L1_attn_Wo, L1_attn_lambda_q1, L1_attn_lambda_k1, L1_attn_lambda_q2, L1_attn_lambda_k2, L1_attn_rms_weight, L1_xattn_ln_x_g, L1_xattn_ln_x_b, L1_xattn_ln_l_g, L1_xattn_ln_l_b, L1_xattn_qn_g, L1_xattn_kn_g, L1_xattn_Wq, L1_xattn_Wkv, L1_xattn_Wlkv, L1_xattn_Wo, L1_xattn_bo, L1_ffn_w_gate_w, L1_ffn_w_gate_b, L1_ffn_W1, L1_ffn_b1, L1_ffn_W2, L1_ffn_b2):
    import jax
    import jax.numpy as jnp

    def _L0_attn_ref(x, Wq, Wk, Wv, Wo):
        import jax, jax.numpy as jnp
        import numpy as np
        D_MODEL = 256
        N_HEADS = 16
        HEAD_DIM = D_MODEL // N_HEADS
        ROPE_BASE = 10000.0

        def _rope_cos_sin(seq_len, dtype):
            inv_freq = 1.0 / ROPE_BASE ** (jnp.arange(0, HEAD_DIM, 2, dtype=jnp.float32) / HEAD_DIM)
            t = jnp.arange(seq_len, dtype=jnp.float32)
            freqs = jnp.outer(t, inv_freq)
            emb = jnp.concatenate([freqs, freqs], axis=-1)
            return (jnp.cos(emb).astype(dtype), jnp.sin(emb).astype(dtype))

        def _rotate_half(v):
            v1, v2 = jnp.split(v, 2, axis=-1)
            return jnp.concatenate([-v2, v1], axis=-1)
        B, S, _ = x.shape

        def proj(W):
            y = jnp.einsum('bsd,ed->bse', x, W)
            return y.reshape(B, S, N_HEADS, HEAD_DIM).transpose(0, 2, 1, 3)
        q, k, v = (proj(Wq), proj(Wk), proj(Wv))
        cos, sin = _rope_cos_sin(S, x.dtype)
        cos = cos[None, None]
        sin = sin[None, None]
        q = q * cos + _rotate_half(q) * sin
        k = k * cos + _rotate_half(k) * sin
        scale = 1.0 / np.sqrt(HEAD_DIM)
        scores = jnp.einsum('bhqd,bhkd->bhqk', q, k) * scale
        causal = jnp.triu(jnp.ones((S, S), dtype=bool), k=1)
        scores = jnp.where(causal, jnp.finfo(scores.dtype).min, scores)
        attn = jax.nn.softmax(scores, axis=-1)
        out = jnp.einsum('bhqk,bhkd->bhqd', attn, v)
        out = out.transpose(0, 2, 1, 3).reshape(B, S, D_MODEL)
        return jnp.einsum('bsd,ed->bse', out, Wo)

    def _L0_xattn_ref(query, key, value, Wq, bq, Wk, bk, Wv, bv, Wo, bo, ln_gamma, ln_beta):
        import jax, jax.numpy as jnp
        import numpy as np
        QUERY_DIM, KV_DIM, EMBED_DIM, NUM_HEADS = (256, 192, 256, 16)
        HEAD_DIM = EMBED_DIM // NUM_HEADS
        SCALE = HEAD_DIM ** (-0.5)
        LN_EPS = 1e-05

        def _l2norm(x, eps=1e-12):
            n = jnp.sqrt(jnp.sum(x * x, axis=-1, keepdims=True))
            return x / jnp.maximum(n, eps)
        B, Nq, _ = query.shape
        Nk = key.shape[1]
        Qp = query @ Wq + bq
        K = _l2norm(key @ Wk + bk)
        V = value @ Wv + bv
        Q = _l2norm(Qp)
        Q = Q.reshape(B, Nq, NUM_HEADS, HEAD_DIM).transpose(0, 2, 1, 3)
        K = K.reshape(B, Nk, NUM_HEADS, HEAD_DIM).transpose(0, 2, 1, 3)
        V = V.reshape(B, Nk, NUM_HEADS, HEAD_DIM).transpose(0, 2, 1, 3)
        scores = jnp.einsum('bhqd,bhkd->bhqk', Q, K) * SCALE
        attn = jax.nn.softmax(scores, axis=-1)
        out = jnp.einsum('bhqk,bhkd->bhqd', attn, V)
        out = out.transpose(0, 2, 1, 3).reshape(B, Nq, EMBED_DIM)
        out = out @ Wo + bo
        x = out + Qp
        mu = jnp.mean(x, axis=-1, keepdims=True)
        var = jnp.mean((x - mu) ** 2, axis=-1, keepdims=True)
        return (x - mu) / jnp.sqrt(var + LN_EPS) * ln_gamma + ln_beta

    def _L0_ffn_ref(x, Wr, We):
        import jax, jax.numpy as jnp
        import numpy as np
        B, T, D, E, TOP_K = (4, 1024, 256, 8, 2)
        CAPACITY_FACTOR = 1.5
        Bb, Tt, Dd = x.shape
        Ee = Wr.shape[0]
        K = TOP_K
        C = int(Tt * K / Ee * CAPACITY_FACTOR) + 1
        logits = jnp.einsum('btd,ed->bte', x, Wr)
        top_vals, top_idx = jax.lax.top_k(logits, K)
        w = jax.nn.softmax(top_vals, axis=-1)
        flat_e = top_idx.reshape(Bb, Tt * K)
        oh = jax.nn.one_hot(flat_e, Ee, dtype=jnp.int32)
        pos_all = jnp.cumsum(oh, axis=1) - oh
        pos = jnp.take_along_axis(pos_all, flat_e[..., None], axis=-1)[..., 0]
        keep = pos < C
        b_idx = jnp.arange(Bb, dtype=jnp.int32)[:, None]
        dst = (b_idx * Ee + flat_e) * C + pos
        dst = jnp.where(keep, dst, Bb * Ee * C).reshape(-1)
        x_rep = jnp.repeat(x, K, axis=1).reshape(-1, Dd)
        buf = jnp.zeros((Bb * Ee * C, Dd), dtype=x.dtype).at[dst].add(x_rep, mode='drop')
        expert_in = buf.reshape(Bb, Ee, C, Dd)
        expert_out = jnp.einsum('becd,edf->becf', expert_in, We)
        gathered = jnp.take(expert_out.reshape(Bb * Ee * C, Dd), dst, axis=0, mode='fill', fill_value=0.0)
        gathered = gathered.reshape(Bb, Tt, K, Dd)
        out = jnp.einsum('btk,btkd->btd', w, gathered)
        return out

    def _L1_attn_ref(x, Wq, Wk, Wv, Wo, lambda_q1, lambda_k1, lambda_q2, lambda_k2, rms_weight):
        import jax, jax.numpy as jnp
        import numpy as np
        import math
        EMBED_DIM = 256
        NUM_HEADS = 16
        DEPTH = 12
        HEAD_DIM = EMBED_DIM // NUM_HEADS // 2
        LAMBDA_INIT = 0.8 - 0.6 * math.exp(-0.3 * DEPTH)
        SCALE = HEAD_DIM ** (-0.5)
        RMS_EPS = 1e-05
        BATCH, SEQ = (2, 512)

        def _freqs(seq_len):
            angle = 1.0 / 10000.0 ** jnp.linspace(0.0, 1.0, HEAD_DIM // 2)
            idx = jnp.arange(seq_len, dtype=jnp.float32)
            f = idx[:, None] * angle[None, :]
            return (jnp.cos(f), jnp.sin(f))

        def _rope_interleaved(x, cos, sin):
            x1, x2 = (x[..., 0::2], x[..., 1::2])
            c = cos[None, :, None, :]
            s = sin[None, :, None, :]
            o1 = x1 * c - x2 * s
            o2 = x1 * s + x2 * c
            return jnp.stack([o1, o2], axis=-1).reshape(x.shape)

        def _forward(x, Wq, Wk, Wv, Wo, lambda_q1, lambda_k1, lambda_q2, lambda_k2, rms_weight):
            b, t, _ = x.shape
            q = (x @ Wq.T).reshape(b, t, 2 * NUM_HEADS, HEAD_DIM)
            k = (x @ Wk.T).reshape(b, t, 2 * NUM_HEADS, HEAD_DIM)
            v = (x @ Wv.T).reshape(b, t, NUM_HEADS, 2, HEAD_DIM)
            cos, sin = _freqs(t)
            q = _rope_interleaved(q, cos, sin)
            k = _rope_interleaved(k, cos, sin)
            q = q.reshape(b, t, NUM_HEADS, 2, HEAD_DIM)
            k = k.reshape(b, t, NUM_HEADS, 2, HEAD_DIM)
            q1, q2 = (q[..., 0, :], q[..., 1, :])
            k1, k2 = (k[..., 0, :], k[..., 1, :])
            v12 = v.reshape(b, t, NUM_HEADS, 2 * HEAD_DIM)

            def attend(qh, kh):
                scores = jnp.einsum('bthd,bshd->bhts', qh, kh) * SCALE
                p = jax.nn.softmax(scores, axis=-1)
                return jnp.einsum('bhts,bshe->bthe', p, v12)
            attn1 = attend(q1, k1)
            attn2 = attend(q2, k2)
            lam = jnp.exp(jnp.sum(lambda_q1 * lambda_k1)) - jnp.exp(jnp.sum(lambda_q2 * lambda_k2)) + LAMBDA_INIT
            a = attn1 - lam * attn2
            a = a * jax.lax.rsqrt(jnp.mean(a * a, axis=-1, keepdims=True) + RMS_EPS) * rms_weight
            a = a * (1.0 - LAMBDA_INIT)
            a = a.reshape(b, t, NUM_HEADS * 2 * HEAD_DIM)
            return a @ Wo.T
        return _forward(x, Wq, Wk, Wv, Wo, lambda_q1, lambda_k1, lambda_q2, lambda_k2, rms_weight)

    def _L1_xattn_ref(x, latents, mask, ln_x_g, ln_x_b, ln_l_g, ln_l_b, qn_g, kn_g, Wq, Wkv, Wlkv, Wo, bo):
        import jax, jax.numpy as jnp
        import numpy as np
        DIM_IN, DIM_LAT, DIM_HEAD = (192, 256, 64)
        INNER = max(DIM_LAT, DIM_IN)
        HEADS = INNER // DIM_HEAD
        SCALE = DIM_HEAD ** (-0.5)
        RMS_EPS = 1e-08
        LN_EPS = 1e-05

        def layernorm(x, g, b):
            mu = jnp.mean(x, axis=-1, keepdims=True)
            var = jnp.mean((x - mu) ** 2, axis=-1, keepdims=True)
            return (x - mu) * jax.lax.rsqrt(var + LN_EPS) * g + b

        def rmsnorm(x, gamma):
            norm = jnp.sqrt(jnp.sum(x * x, axis=-1, keepdims=True)) * x.shape[-1] ** (-0.5)
            return x / jnp.maximum(norm, RMS_EPS) * gamma
        b, n, _ = x.shape
        m = latents.shape[1]
        xn = layernorm(x, ln_x_g, ln_x_b)
        ln = layernorm(latents, ln_l_g, ln_l_b)
        q = ln @ Wq.T
        kv = jnp.concatenate([xn @ Wkv.T, ln @ Wlkv.T], axis=1)
        k, v = (kv[..., :INNER], kv[..., INNER:])
        split_heads = lambda t: t.reshape(t.shape[0], t.shape[1], HEADS, DIM_HEAD).transpose(0, 2, 1, 3)
        q, k, v = (split_heads(q), split_heads(k), split_heads(v))
        qn = rmsnorm(q, qn_g) * SCALE
        kn = rmsnorm(k, kn_g)
        attn = jnp.einsum('bhid,bhjd->bhij', qn, kn)
        full_mask = jnp.pad(mask, ((0, 0), (0, m)), constant_values=True)
        attn = jnp.where(full_mask[:, None, None, :], attn, -jnp.finfo(attn.dtype).max)
        attn = jax.nn.softmax(attn, axis=-1)
        out = jnp.einsum('bhij,bhjd->bhid', attn, v)
        out = out.transpose(0, 2, 1, 3).reshape(b, m, INNER)
        return out @ Wo.T + bo

    def _L1_ffn_ref(x, w_gate_w, w_gate_b, W1, b1, W2, b2):
        import jax, jax.numpy as jnp
        import numpy as np
        TOPK = 2
        CAPACITY_FACTOR = 1.0
        EPS = 1e-06
        B, S, D = (4, 1024, 256)
        E = 8
        SUB_H = 512 // E
        Bx, Sx, Dx = x.shape
        Ex = w_gate_b.shape[0]
        K = Sx // 2
        capacity = int(CAPACITY_FACTOR * Bx)
        gate_scores = jax.nn.softmax(x @ w_gate_w + w_gate_b, axis=-1)
        _, top_idx = jax.lax.top_k(gate_scores, TOPK)
        mask = jax.nn.one_hot(top_idx, Ex, dtype=gate_scores.dtype).sum(axis=-2)
        masked = gate_scores * mask
        denom = masked.sum(axis=0, keepdims=True) + EPS
        route = masked / denom * capacity
        route_eb = jnp.transpose(route, (2, 0, 1))
        _, seq_ids = jax.lax.top_k(route_eb, K)
        seq_ids = jnp.sort(seq_ids, axis=-1)
        xg = jax.vmap(lambda idx: jnp.take_along_axis(x, idx[..., None], axis=1))(seq_ids)
        h = jnp.einsum('ebkd,edh->ebkh', xg, W1) + b1[:, None, None, :]
        h = jax.nn.gelu(h, approximate=False)
        o = jnp.einsum('ebkh,ehd->ebkd', h, W2) + b2[:, None, None, :]
        flat_ids = (jnp.arange(Bx)[None, :, None] * Sx + seq_ids).reshape(-1)
        outs = jnp.zeros((Bx * Sx, Dx), x.dtype).at[flat_ids].add(o.reshape(-1, Dx))
        return outs.reshape(Bx, Sx, Dx)
    x = _layernorm(x + _L0_attn_ref(x, L0_attn_Wq, L0_attn_Wk, L0_attn_Wv, L0_attn_Wo), axis=-1)
    x = _layernorm(x + _L0_xattn_ref(x, ctx_768, ctx_768, L0_xattn_Wq, L0_xattn_bq, L0_xattn_Wk, L0_xattn_bk, L0_xattn_Wv, L0_xattn_bv, L0_xattn_Wo, L0_xattn_bo, L0_xattn_ln_gamma, L0_xattn_ln_beta), axis=-1)
    x = _layernorm(x + _L0_ffn_ref(x, L0_ffn_Wr, L0_ffn_We), axis=-1)
    x = _layernorm(x + _L1_attn_ref(x, L1_attn_Wq, L1_attn_Wk, L1_attn_Wv, L1_attn_Wo, L1_attn_lambda_q1, L1_attn_lambda_k1, L1_attn_lambda_q2, L1_attn_lambda_k2, L1_attn_rms_weight), axis=-1)
    x = _layernorm(x + _L1_xattn_ref(ctx_768, x, mask_BxS2_bk0, L1_xattn_ln_x_g, L1_xattn_ln_x_b, L1_xattn_ln_l_g, L1_xattn_ln_l_b, L1_xattn_qn_g, L1_xattn_kn_g, L1_xattn_Wq, L1_xattn_Wkv, L1_xattn_Wlkv, L1_xattn_Wo, L1_xattn_bo), axis=-1)
    x = _layernorm(x + _L1_ffn_ref(x, L1_ffn_w_gate_w, L1_ffn_w_gate_b, L1_ffn_W1, L1_ffn_b1, L1_ffn_W2, L1_ffn_b2), axis=-1)
    return x

_drawn_inputs = setup_inputs


def setup_inputs(seed=0):
    import zlib

    import numpy as np

    out = dict(_drawn_inputs(seed))
    spreads = {'L0_xattn_bq': (0.0, 0.1),
     'L0_xattn_bk': (0.0, 0.8),
     'L0_xattn_bv': (0.0, 0.1),
     'L0_xattn_bo': (0.0, 0.1),
     'L0_xattn_ln_gamma': (1.0, 0.2),
     'L0_xattn_ln_beta': (0.0, 0.1),
     'L1_attn_rms_weight': (1.0, 0.2),
     'L1_xattn_ln_x_g': (1.0, 0.6),
     'L1_xattn_ln_x_b': (0.0, 0.8),
     'L1_xattn_ln_l_g': (1.0, 0.2),
     'L1_xattn_ln_l_b': (0.0, 0.1),
     'L1_xattn_qn_g': (1.0, 0.2),
     'L1_xattn_kn_g': (1.0, 0.2),
     'L1_xattn_bo': (0.0, 0.1),
     'L1_ffn_w_gate_b': (0.0, 0.1),
     'L1_ffn_b1': (0.0, 0.464),
     'L1_ffn_b2': (0.0, 0.1)}
    factors = {'L0_xattn_Wk': 7.269, 'L1_attn_lambda_q1': 2.907, 'L1_xattn_Wkv': 2.906}
    for name, (base, spread) in spreads.items():
        noise = np.random.default_rng([zlib.crc32(name.encode()), seed]).standard_normal(out[name].shape)
        drawn = base * np.exp(spread * noise) if base else spread * noise
        out[name] = jnp.asarray(drawn.astype(out[name].dtype))
    for name, factor in factors.items():
        out[name] = (out[name] * factor).astype(out[name].dtype)
    return out
```

```python
import math
from contextlib import ExitStack

import numpy as np
import concourse.bass as bass
from concourse import mybir

F32 = mybir.dt.float32
BF16 = mybir.dt.bfloat16
I32 = mybir.dt.int32
U32 = mybir.dt.uint32
ALU = mybir.AluOpType
ACT = mybir.ActivationFunctionType
AX = mybir.AxisListType.X

P = 128
B, S, D = 4, 1024, 256
NT = B * S // P
TB = S // P
DC = D // P
HALF = 512
H = 16
DV = D // H
LN_EPS = 1e-5
MASKED = -1.0e30
LOWEST = -3.0e38
SPLIT_Q = [0, 0, 1, 1, 0, 2]
SPLIT_K = [0, 1, 0, 1, 2, 0]
MAX_ROW = 96
STACK = MAX_ROW + 3


class Mem:

    def __init__(self, nc, ctx):
        self.nc, self.ctx, self.n = nc, ctx, 0

    def sb(self, name, shape, dt=F32):
        return self.ctx.enter_context(self.nc.sbuf_tensor(name, shape, dt))

    def ps(self, name, cols, dt=F32):
        return self.ctx.enter_context(self.nc.psum_tensor(name, [P, cols], dt))

    def sem(self, name):
        return self.nc.alloc_semaphore(name=name)


class At:

    def __init__(self, base, n=None, step=3):
        self.base, self.n, self.step = base, n, step

    def __add__(self, k):
        return At(self.base + k, self.n, self.step)

    def times(self, a, b=0):
        if self.n is None:
            return a * self.base + b
        return self.n * (self.step * a) + (a * self.base + b)

    def over(self, a, b=0):
        whole = a * (self.base // self.step) + b
        return whole if self.n is None else self.n * a + whole

    def span(self, width=1):
        if self.n is None:
            return slice(self.base * width, (self.base + 1) * width)
        return bass.ds(self.times(width), width)

    @property
    def slot(self):
        return self.base % self.step


def run_turns(eng, turn, count, lag, step, first=0):
    peeled = lag + first + (count - lag - first) % step
    for t in range(peeled):
        turn(At(t, None, step), [t >= j for j in range(lag + 1)])
    if count > peeled:
        with eng.Fori(0, (count - peeled) // step) as n:
            for k in range(step):
                turn(At(peeled + k, n, step), [True] * (lag + 1))
    for t in range(count, count + lag):
        turn(At(t, None, step), [t - j < count for j in range(lag + 1)])


def load_start(nc, a, keep, sems):
    X, ident, identb = keep["X"], keep["ident"], keep["identb"]
    loaded = sems.sem("start_loaded")
    with nc.Block() as block:
        @block.sync
        def _(sp):
            sp.dma_start(X[:], a["x"].rearrange("(t p) d -> p t d", p=P)).then_inc(loaded, 16)
            sp.dma_start(ident[:], a["ident"]).then_inc(loaded, 16)

        @block.vector
        def _(dve):
            dve.wait_ge(loaded, 32)
            dve.tensor_copy(identb[:], ident[:])


def project(nc, a, keep, sems, tag, ne, groups):
    ns = 64 // ne
    gb = groups // B
    w = D // gb
    X, ident, VA = keep["X"], keep["ident"], keep["VA"]
    PT = keep["PT"]
    with ExitStack() as ctx:
        m = Mem(nc, ctx)
        xs = [m.sb(f"{tag}_proj_xs{k}", [P, TB, D]) for k in range(2)]
        xt = [m.sb(f"{tag}_proj_xt{k}", [P, DC, S]) for k in range(2)]
        wqk = m.sb(f"{tag}_proj_wqk", [P, DC, 2 * D])
        wv = m.sb(f"{tag}_proj_wv", [P, DC, D])
        cos = m.sb(f"{tag}_proj_cos", [P, S])
        sin = m.sb(f"{tag}_proj_sin", [P, S])
        t1 = [m.sb(f"{tag}_proj_t1{k}", [P, HALF]) for k in range(2)]
        t2 = [m.sb(f"{tag}_proj_t2{k}", [P, HALF]) for k in range(2)]
        rot = [m.sb(f"{tag}_proj_rot{k}", [P, HALF]) for k in range(4)]
        rest = [m.sb(f"{tag}_proj_rest{k}", [P, HALF]) for k in range(4)]
        parts = [m.sb(f"{tag}_proj_parts{k}", [P, 3, S], BF16) for k in range(2)]
        psT = [m.ps(f"{tag}_proj_psT{k}", HALF) for k in range(2)]
        psQ = [m.ps(f"{tag}_proj_psQ{k}", HALF) for k in range(2)]
        psV = [m.ps(f"{tag}_proj_psV{k}", HALF) for k in range(2)]
        weights = sems.sem(f"{tag}_proj_weights")
        xs_in = [sems.sem(f"{tag}_proj_xs_in{k}") for k in range(2)]
        turned = sems.sem(f"{tag}_proj_turned")
        xt_in = sems.sem(f"{tag}_proj_xt_in")
        qk_done = sems.sem(f"{tag}_proj_qk_done")
        qk_read = sems.sem(f"{tag}_proj_qk_read")
        added = sems.sem(f"{tag}_proj_added")
        hi = sems.sem(f"{tag}_proj_hi")
        less = sems.sem(f"{tag}_proj_less")
        mid = sems.sem(f"{tag}_proj_mid")
        low = sems.sem(f"{tag}_proj_low")
        out = [sems.sem(f"{tag}_proj_out{k}") for k in range(2)]
        v_done = sems.sem(f"{tag}_proj_v_done")
        v_read = sems.sem(f"{tag}_proj_v_read")
        PERB = 8
        N = 2 * PERB
        OUT = 96
        with nc.Block() as block:
            @block.sync
            def _(sp):
                for k in range(2):
                    sp.dma_start(xs[k][:], X[:, k * TB:(k + 1) * TB, :]).then_inc(xs_in[k], 16)
                    if k == 0:
                        sp.dma_start(wqk[:], a[f"{tag}_wqk"]).then_inc(weights, 16)
                        sp.dma_start(wv[:], a[f"{tag}_wv"]).then_inc(weights, 16)
                        sp.dma_start(cos[:], a[f"{tag}_cos"]).then_inc(weights, 16)
                        sp.dma_start(sin[:], a[f"{tag}_sin"]).then_inc(weights, 16)
                with sp.Fori(0, B // 2) as i:
                    for u in range(8):
                        k, qk, c = u // 4, u % 4 // 2, u % 2
                        sp.wait_ge(low, i * N + 2 * u + 2)
                        dst = PT[qk].rearrange("k (b c s h e) t -> k b c h s e t", b=B, c=DC, h=2, e=ne)
                        for p in range(3):
                            for h in range(2):
                                sp.dma_start(dst[p, bass.ds(2 * i + k, 1), c, h].rearrange("o s e t -> (o s) e t"),
                                             parts[u % 2][64 * h:64 * h + 64, p, :]).then_inc(out[u % 2], 16)
                for k in range(2):
                    sp.wait_ge(out[k], OUT * 4 * (B // 2))
                    sp.wait_ge(xs_in[k], 16 * (B // 2 + 1))

            @block.gpsimd
            def _(pool):
                with pool.Fori(0, B // 2) as i:
                    for n in range(N):
                        pool.wait_ge(qk_read, i * (3 * N) + 6 + 3 * (n + 1))
                        pool.tensor_tensor(rot[n % 4][:], t1[n % 2][:], t2[n % 2][:], ALU.add).then_inc(added, 1)

            @block.scalar
            def _(act):
                act.sem_inc(xt_in, 2)
                act.sem_inc(v_read, 2)

                def second(i, n):
                    act.wait_ge(less, i * N + n + 1)
                    act.activation(parts[n // 2 % 2][:, 1, (n % 2) * HALF:(n % 2 + 1) * HALF],
                                   rest[n % 4][:], ACT.Copy).then_inc(mid, 1)

                with act.Fori(0, B // 2) as i:
                    for k in range(2):
                        for u in range(4):
                            c, h = u // 2, u % 2
                            act.wait_ge(turned, i * 8 + 4 * k + u + 1)
                            act.activation(xt[k][:, c, h * HALF:(h + 1) * HALF], psT[u % 2][:],
                                           ACT.Copy).then_inc(xt_in, 1)
                        act.dma_start(xs[k][:], X[:, bass.ds(2 * TB - 2 * TB * i + k * TB, TB), :]).then_inc(xs_in[k], 16)
                        for n in range(PERB * k, PERB * (k + 1)):
                            if n % 4 == 0 or n % 4 == 2:
                                act.wait_ge(out[n // 2 % 2], i * (4 * OUT) + OUT * (n // 4))
                            act.wait_ge(added, i * N + n + 1)
                            act.activation(parts[n // 2 % 2][:, 0, (n % 2) * HALF:(n % 2 + 1) * HALF],
                                           rot[n % 4][:], ACT.Copy).then_inc(hi, 1)
                            if n:
                                second(i, n - 1)
                        for j in range(4):
                            act.wait_ge(v_done, i * 8 + 4 * k + j + 1)
                            src = psV[j % 2][:].rearrange("p (t g w) -> p g t w", t=2, g=gb)
                            act.activation(VA[:, bass.ds((2 * i + k) * gb, gb), 2 * j:2 * j + 2, :], src,
                                           ACT.Copy).then_inc(v_read, 1)
                    second(i, N - 1)

            @block.vector
            def _(dve):
                dve.sem_inc(qk_read, 6)
                dve.wait_ge(weights, 64)

                def rotate(i, n):
                    h = n % 2
                    dve.wait_ge(qk_done, i * N + n + 1)
                    if n >= 2:
                        dve.wait_ge(added, i * N + n - 1)
                    ps, col = psQ[n % 2], slice(h * HALF, (h + 1) * HALF)
                    dve.tensor_tensor(t1[n % 2][:], ps[:], cos[:, col], ALU.mult).then_inc(qk_read, 1)
                    for q in range(2):
                        a0, b0 = 64 * q, 64 * (1 - q)
                        dve.tensor_tensor(t2[n % 2][a0:a0 + 64, :], ps[b0:b0 + 64, :], sin[b0:b0 + 64, col],
                                          ALU.mult).then_inc(qk_read, 1)

                def subtract(i, n):
                    dve.wait_ge(hi, i * N + n + 1)
                    dve.tensor_tensor(rest[n % 4][:], rot[n % 4][:],
                                      parts[n // 2 % 2][:, 0, (n % 2) * HALF:(n % 2 + 1) * HALF],
                                      ALU.subtract).then_inc(less, 1)

                def third(i, n):
                    dve.wait_ge(mid, i * N + n + 1)
                    col = slice((n % 2) * HALF, (n % 2 + 1) * HALF)
                    dve.tensor_tensor(parts[n // 2 % 2][:, 2, col], rest[n % 4][:], parts[n // 2 % 2][:, 1, col],
                                      ALU.subtract).then_inc(low, 1)

                with dve.Fori(0, B // 2) as i:
                    for n in range(N + 2):
                        if n < N:
                            rotate(i, n)
                        if 1 <= n <= N:
                            subtract(i, n - 1)
                        if n >= 2:
                            third(i, n - 2)

            @block.tensor
            def _(pe):
                pe.wait_ge(weights, 64)
                with pe.Fori(0, B // 2) as i:
                    for k in range(2):
                        pe.wait_ge(xs_in[k], i * 16 + 16)
                        for u in range(4):
                            c, h = u // 2, u % 2
                            pe.wait_ge(xt_in, i * 8 + 4 * k + u + 1)
                            for t in range(4):
                                last = pe.transpose(psT[u % 2][:, t * P:(t + 1) * P],
                                                    xs[k][:, 4 * h + t, c * P:(c + 1) * P], ident[:])
                            last.then_inc(turned, 1)
                        pe.wait_ge(xt_in, i * 8 + 4 * k + 6)
                        for n in range(PERB):
                            g, h = n // 2, n % 2
                            pe.wait_ge(qk_read, i * (3 * N) + 3 * (PERB * k + n) + 3)
                            for c in range(DC):
                                last = pe.matmul(psQ[n % 2][:], wqk[:, c, g * P:(g + 1) * P],
                                                 xt[k][:, c, h * HALF:(h + 1) * HALF], start=(c == 0), stop=(c == DC - 1))
                            last.then_inc(qk_done, 1)
                        for j in range(4):
                            pe.wait_ge(v_read, i * 8 + 4 * k + j + 1)
                            for t in range(2):
                                for c in range(DC):
                                    last = pe.matmul(psV[j % 2][:, t * D:(t + 1) * D],
                                                     xt[k][:, c, (2 * j + t) * P:(2 * j + t + 1) * P], wv[:, c, :],
                                                     start=(c == 0), stop=(c == DC - 1))
                            last.then_inc(v_done, 1)
def attend(nc, a, keep, sems, tag, dh, groups, causal):
    gb = groups // B
    scale = dh ** -0.5
    shared = 4 * DV // (D // gb)
    vh = 4 // shared
    VA, AO, PT, ident, identb = keep["VA"], keep["AO"], keep["PT"], keep["ident"], keep["identb"]
    steps = [(q, t, max(0, t - 4 * q) * P if causal else 0) for q in range(2) for t in range(TB)
             if not causal or t < 4 * (q + 1)]
    ends = [max(n for n, st in enumerate(steps) if st[0] == q) for q in range(2)]
    pieces = []
    for s in range(4):
        for t in range(TB):
            keys = (t + 1) * P if causal else S
            for h in range(2):
                n = min(HALF, keys - h * HALF)
                if n > 0:
                    pieces.append((s, t, h, n, causal and h * HALF + n == keys))
    NS, NPc = len(steps), len(pieces)
    per = -(-NPc // (NS - 3))
    assert NS % 2 == 0 and NPc % 2 == 0
    NL = len(SPLIT_Q) * 2
    LD = 16 * NL

    with ExitStack() as ctx:
        m = Mem(nc, ctx)
        Q = [m.sb(f"{tag}_attn_Q{k}", [P, 4, S], BF16) for k in range(3)]
        K = [m.sb(f"{tag}_attn_K{k}", [P, 4, S], BF16) for k in range(3)]
        V = [m.sb(f"{tag}_attn_V{k}", [P, TB, vh, 32]) for k in range(3)]
        E = [m.sb(f"{tag}_attn_E{k}", [P, 2, HALF]) for k in range(4)]
        mask = m.sb(f"{tag}_attn_mask", [P, 2, P])
        maskb = m.sb(f"{tag}_attn_maskb", [P, 2, P], BF16)
        tops = m.sb(f"{tag}_attn_tops", [P, 4 * TB, 2])
        negm = [m.sb(f"{tag}_attn_negm{k}", [P, 4 * TB]) for k in range(3)]
        mrest = [m.sb(f"{tag}_attn_mrest{k}", [4 * TB, 2, P]) for k in range(3)]
        mparts = [m.sb(f"{tag}_attn_mparts{k}", [4 * TB, 3, P], BF16) for k in range(3)]
        oT = [m.sb(f"{tag}_attn_oT{k}", [P, HALF]) for k in range(2)]
        rec = [m.sb(f"{tag}_attn_rec{k}", [P, 4, 4]) for k in range(2)]
        if shared == 2:
            lam4 = m.sb(f"{tag}_attn_lam4", [P, 4, dh])
            lamp = m.sb(f"{tag}_attn_lamp", [P, 2, dh])
            lams = m.sb(f"{tag}_attn_lams", [P, 2])
            lame = m.sb(f"{tag}_attn_lame", [P, 2])
            lamd = m.sb(f"{tag}_attn_lamd", [P, 1])
            neglam = m.sb(f"{tag}_attn_neglam", [P, 1])
            o1 = [m.sb(f"{tag}_attn_o1{k}", [P, 4, 2, DV]) for k in range(2)]
            o2 = [m.sb(f"{tag}_attn_o2{k}", [P, 4, 2, DV]) for k in range(2)]
        psS = [m.ps(f"{tag}_attn_psS{k}", 2 * HALF) for k in range(2)]
        psM = [m.ps(f"{tag}_attn_psM{k}", HALF) for k in range(2)]
        psO = [m.ps(f"{tag}_attn_psO{k}", HALF) for k in range(2)]
        ones = sems.sem(f"{tag}_attn_ones")
        v_blank = sems.sem(f"{tag}_attn_v_blank")
        blank = sems.sem(f"{tag}_attn_blank")
        maskin = sems.sem(f"{tag}_attn_maskin")
        masks = sems.sem(f"{tag}_attn_masks")
        ld = [sems.sem(f"{tag}_attn_ld{k}") for k in range(3)]
        mx = [sems.sem(f"{tag}_attn_mx{k}") for k in range(3)]
        v_in = sems.sem(f"{tag}_attn_v_in")
        s_done = sems.sem(f"{tag}_attn_s_done")
        e_done = sems.sem(f"{tag}_attn_e_done")
        o_done = sems.sem(f"{tag}_attn_o_done")
        o_out = sems.sem(f"{tag}_attn_o_out")
        o_back = sems.sem(f"{tag}_attn_o_back")
        o_read = sems.sem(f"{tag}_attn_o_read")
        o_rec = sems.sem(f"{tag}_attn_o_rec")
        m_done = sems.sem(f"{tag}_attn_m_done")
        m_read = sems.sem(f"{tag}_attn_m_read")
        m_neg = sems.sem(f"{tag}_attn_m_neg")
        m_cut = sems.sem(f"{tag}_attn_m_cut")
        lam = sems.sem(f"{tag}_attn_lam")
        lamin = sems.sem(f"{tag}_attn_lamin")
        NM = NPc + 1
        NR = 1 if shared == 1 else 3

        def run(eng, turn):
            run_turns(eng, lambda t, live: turn(t, *live), groups, 2, 3)

        with nc.Block() as block:
            @block.sync
            def _(sp):
                sp.dma_start(mask[:], a["causal"]).then_inc(maskin, 16)
                if shared == 2:
                    sp.dma_start(lam4[:], a[f"{tag}_lambda"].rearrange("(o k) d -> o k d", o=1).broadcast_to([P, 4, dh])).then_inc(lamin, 16)

                def load(g):
                    if g.base >= 3 or g.n is not None:
                        sp.wait_ge(s_done, (g + -2).times(2 * NS))
                    for (buf, split, src) in ((Q, SPLIT_Q, PT[0]), (K, SPLIT_K, PT[1])):
                        for j, p in enumerate(split):
                            view = src[p].rearrange("(g s e) t -> g e s t", s=4, e=dh)
                            one = view[g.span()]
                            sp.dma_start(buf[g.slot][dh * j:dh * (j + 1), :, :],
                                         one.rearrange("o e s t -> (o e) s t")).then_inc(ld[g.slot], 16)

                def turn(t, maxima, exps, end):
                    if maxima:
                        load(t)
                    if exps:
                        g = t + -1
                        sp.wait_ge(m_cut, g.times(5, 5))
                        for j in range(3):
                            sp.dma_start(Q[g.slot][MAX_ROW + j:MAX_ROW + j + 1, :, :],
                                         mparts[g.slot][:, j, :]).then_inc(mx[g.slot], 16)

                sp.wait_ge(blank, 1)
                run(sp, turn)
                for k in range(3):
                    n = len(range(k, groups, 3))
                    sp.wait_ge(mx[k], 48 * n)

            @block.gpsimd
            def _(pool):
                for k in range(3):
                    pool.memset(K[k][MAX_ROW:STACK, :, :], 1.0).then_inc(ones, 1)
                    pool.wait_ge(ones, k + 1)
                pool.wait_ge(blank, 1)

                def copy(g):
                    if g.base >= 3 or g.n is not None:
                        pool.wait_ge(o_done, (g + -2).times(NS, 2))
                    src = VA[:, g.span(), :, :]
                    pool.tensor_copy(V[g.slot][:, :, :, 0:DV],
                                     src.rearrange("p o t (h d) -> p (o t) h d", d=DV)).then_inc(v_in, 1)

                def turn(t, maxima, exps, end):
                    if maxima:
                        copy(t)

                run(pool, turn)

            @block.scalar
            def _(act):
                act.sem_inc(e_done, 2)
                if shared == 2:
                    act.wait_ge(lam, 2)
                    act.activation(lame[:], lams[:], ACT.Exp).then_inc(lam, 1)

                def turn(t, maxima, exps, end):
                    if not exps:
                        return
                    g = t + -1
                    for n, (q, kt, c0) in enumerate(steps):
                        act.wait_ge(o_done, g.times(NS, n + 1))
                        for u in range(2):
                            act.wait_ge(s_done, g.times(2 * NS, 2 * n + u + 1))
                            src = psS[u][:].rearrange("p (s q) -> p s q", s=2)
                            act.activation(E[(2 * n + u) % 4][:, :, c0:], src[:, :, c0:], ACT.Exp,
                                           scale=scale).then_inc(e_done, 1)

                run(act, turn)

            @block.vector
            def _(dve):
                dve.sem_inc(o_read, 2)
                for k in range(3):
                    dve.memset(V[k][:], 0.0).then_inc(v_blank, 1)
                dve.wait_ge(v_blank, 3)
                for k in range(3):
                    dve.memset(V[k][:, :, :, DV:DV + 1], 1.0).then_inc(v_blank, 1)
                dve.wait_ge(v_blank, 6)
                if len(SPLIT_Q) * dh < MAX_ROW:
                    for k in range(3):
                        for buf in (Q, K):
                            dve.memset(buf[k][0:MAX_ROW, :, :].bitcast(U32), 0).then_inc(v_blank, 1)
                    dve.wait_ge(v_blank, 12)
                dve.memset(tops[:], LOWEST).then_inc(m_neg, 1)
                dve.wait_ge(maskin, 16)
                dve.tensor_copy(maskb[:], mask[:]).then_inc(masks, 1)
                dve.wait_ge(masks, 1)
                dve.sem_inc(blank, 1)
                dve.wait_ge(m_neg, 1)
                if shared == 2:
                    dve.wait_ge(lamin, 16)
                    pairs = lam4[:].rearrange("p (c k) d -> p c k d", c=2)
                    dve.tensor_tensor(lamp[:], pairs[:, :, 0, :], pairs[:, :, 1, :], ALU.mult).then_inc(lam, 1)
                    dve.wait_ge(lam, 1)
                    dve.tensor_reduce(lams[:], lamp[:], AX, ALU.add).then_inc(lam, 1)
                    dve.wait_ge(lam, 3)
                    dve.tensor_tensor(lamd[:], lame[:, 1:2], lame[:, 0:1], ALU.subtract).then_inc(lam, 1)
                    dve.wait_ge(lam, 4)
                    dve.tensor_scalar(neglam[:], lamd[:], -LAMBDA_INIT, None, ALU.add).then_inc(lam, 1)
                    dve.wait_ge(lam, 5)

                def evacuate(g, q):
                    dve.wait_ge(o_done, g.times(NS, 2 + ends[q] + 1))
                    dve.tensor_copy(oT[q][:], psO[q][:]).then_inc(o_out, 1)

                def normalise(g, q):
                    dve.wait_ge(o_back, g.times(2, q + 1))
                    ps = psO[q][:].rearrange("p (t s c) -> p t s c", t=4, s=4)
                    dve.reciprocal(rec[q][:], ps[:, :, :, DV]).then_inc(o_rec, 1)
                    dve.wait_ge(o_rec, g.times(2 * NR, NR * q + 1))
                    dst = AO[:, g.span(), 4 * q:4 * q + 4, :].rearrange("p o t w -> p (o t) w")
                    if shared == 1:
                        dve.tensor_tensor(dst.rearrange("p t (s c) -> p t s c", s=4), ps[:, :, :, 0:DV],
                                          rec[q][:].unsqueeze(3).broadcast_to([P, 4, 4, DV]), ALU.mult).then_inc(o_read, 1)
                        return
                    for c, o in ((1, o2), (0, o1)):
                        src = ps.rearrange("p t (h c) d -> p t h c d", c=2)[:, :, :, c, 0:DV]
                        r = rec[q][:].rearrange("p t (h c) -> p t h c", c=2)[:, :, :, c]
                        ins = dve.tensor_tensor(o[q][:], src, r.unsqueeze(3).broadcast_to([P, 4, 2, DV]), ALU.mult)
                        ins.then_inc(o_rec if c else o_read, 1)
                    dve.wait_ge(o_rec, g.times(2 * NR, NR * q + 2))
                    dve.wait_ge(o_read, g.times(2, q + 3))
                    dve.scalar_tensor_tensor(out=dst, in0=o2[q][:].rearrange("p t h d -> p t (h d)"), scalar=neglam[:],
                                             in1=o1[q][:].rearrange("p t h d -> p t (h d)"), op0=ALU.mult,
                                             op1=ALU.add).then_inc(o_rec, 1)

                def reduce(t, p):
                    s, qt, h, n, _ = pieces[p]
                    dve.wait_ge(m_done, t.times(NM, p + 1))
                    dve.tensor_reduce(tops[:, s * TB + qt, h:h + 1], psM[p % 2][:, 0:n], AX, ALU.max).then_inc(m_read, 1)

                def combine(t):
                    dve.wait_ge(m_read, t.times(NM, NPc))
                    dve.tensor_reduce(negm[t.slot][:], tops[:], AX, ALU.max, negate=True).then_inc(m_neg, 1)

                def cut(t):
                    r, pt, ps = mrest[t.slot], mparts[t.slot], psM[0][0:4 * TB, 0:P]
                    dve.wait_ge(mx[t.slot], t.over(48))
                    dve.wait_ge(m_done, t.times(NM, NM))
                    dve.tensor_copy(pt[:, 0, :], ps).then_inc(m_cut, 1)
                    dve.wait_ge(m_cut, t.times(5, 1))
                    dve.tensor_tensor(r[:, 0, :], ps, pt[:, 0, :], ALU.subtract).then_inc(m_read, 1)
                    dve.wait_ge(m_read, t.times(NM, NM))
                    dve.tensor_copy(pt[:, 1, :], r[:, 0, :]).then_inc(m_cut, 1)
                    dve.wait_ge(m_cut, t.times(5, 2))
                    dve.tensor_tensor(r[:, 1, :], r[:, 0, :], pt[:, 1, :], ALU.subtract).then_inc(m_cut, 1)
                    dve.wait_ge(m_cut, t.times(5, 3))
                    dve.tensor_copy(pt[:, 2, :], r[:, 1, :]).then_inc(m_cut, 2)

                def turn(t, maxima, exps, end):
                    p = 0
                    for n in range(NS if maxima or exps else 5):
                        if end and n == 1:
                            evacuate(t + -2, 1)
                        if end and n == 3:
                            normalise(t + -2, 1)
                        if exps and n == ends[0] + 2:
                            evacuate(t + -1, 0)
                        if exps and n == ends[0] + 4:
                            normalise(t + -1, 0)
                        for _ in range(per):
                            if maxima and p < NPc:
                                reduce(t, p)
                                p += 1
                                if p == NPc:
                                    combine(t)
                                    done = n
                        if maxima and p == NPc and n == done + 1:
                            cut(t)
                            p += 1

                run(dve, turn)
                dve.wait_ge(o_rec, 2 * NR * groups)

            @block.tensor
            def _(pe):
                pe.sem_inc(o_done, 2)
                pe.wait_ge(ones, 3)
                pe.wait_ge(blank, 1)
                pe.wait_ge(masks, 1)

                def scores(g, n, u):
                    q, kt, c0 = steps[n]
                    Qg, Kg = Q[g.slot], K[g.slot]
                    pe.wait_ge(e_done, g.times(2 * NS, 2 * n + u + 1))
                    for s in range(2 * u, 2 * u + 2):
                        diagonal = causal and kt >= 4 * q
                        out = psS[u][:, (s % 2) * HALF + c0:(s % 2 + 1) * HALF]
                        if diagonal:
                            pe.matmul(psS[u][:, (s % 2) * HALF + c0:(s % 2) * HALF + c0 + P], identb[:], maskb[:, 1, :],
                                      start=True, stop=False, skip_group_check=True)
                        last = pe.matmul(out, Kg[0:STACK, s, kt * P:(kt + 1) * P], Qg[0:STACK, s, q * HALF + c0:(q + 1) * HALF],
                                         start=not diagonal, stop=True, skip_group_check=True)
                    last.then_inc(s_done, 1)

                def product(g, n):
                    q, kt, c0 = steps[n]
                    if n == 0 or steps[n - 1][0] != q:
                        pe.wait_ge(o_read, g.times(2, q + 1))
                    if n == 0:
                        pe.wait_ge(v_in, g.times(1, 1))
                    pe.wait_ge(e_done, g.times(2 * NS, 2 * n + 2 + 2))
                    for s in range(4):
                        last = pe.matmul(psO[q][32 * s:32 * s + 32, c0:HALF], V[g.slot][:, kt, s // shared, :],
                                         E[(2 * n + s // 2) % 4][:, s % 2, c0:], start=(kt == 0), stop=(n == ends[q]),
                                         skip_group_check=True)
                    last.then_inc(o_done, 1)

                def turn_back(g, q):
                    pe.wait_ge(o_out, g.times(2, q + 1))
                    for j in range(4):
                        last = pe.transpose(psO[q][:, j * P:(j + 1) * P], oT[q][:, j * P:(j + 1) * P], ident[:])
                    last.then_inc(o_back, 1)

                def piece(t, p):
                    s, qt, h, n, masked = pieces[p]
                    pe.wait_ge(m_read, t.times(NM, max(p - 1, 0)))
                    Qt, Kt = Q[t.slot], K[t.slot]
                    if masked:
                        pe.matmul(psM[p % 2][:, n - P:n], identb[:], maskb[:, 0, :], start=True, stop=False,
                                  skip_group_check=True)
                    last = pe.matmul(psM[p % 2][:, 0:n], Qt[0:MAX_ROW, s, qt * P:(qt + 1) * P], Kt[0:MAX_ROW, s, h * HALF:h * HALF + n],
                                     start=not masked, stop=True, skip_group_check=True)
                    last.then_inc(m_done, 1)

                def turn_maxima(t):
                    pe.wait_ge(m_neg, t.times(1, 2))
                    pe.wait_ge(m_read, t.times(NM, NPc))
                    pe.transpose(psM[0][0:4 * TB, 0:P], negm[t.slot][:], ident[:]).then_inc(m_done, 1)

                def turn(t, maxima, exps, end):
                    p = 0
                    if maxima:
                        pe.wait_ge(ld[t.slot], t.over(LD, LD))
                    if exps:
                        g = t + -1
                        pe.wait_ge(mx[g.slot], g.over(48, 48))
                    for n in range(NS if maxima or exps else 5):
                        if maxima and p == NPc:
                            turn_maxima(t)
                            p += 1
                        for u in range(2):
                            if exps:
                                scores(t + -1, n, u)
                            for _ in range(per // 2 + (per % 2) * u):
                                if maxima and p < NPc:
                                    piece(t, p)
                                    p += 1
                        if exps and n >= 1:
                            product(t + -1, n - 1)
                        if end and n == 0:
                            product(t + -2, NS - 1)
                        if end and n == 2:
                            turn_back(t + -2, 1)
                        if exps and n == ends[0] + 3:
                            turn_back(t + -1, 0)

                run(pe, turn)
LAMBDA_INIT = 0.8 - 0.6 * math.exp(-0.3 * 12)
BLK = 4


def merge(nc, a, keep, sems, tag, groups, rms, bias=None):
    gb = groups // B
    dense = groups == 1
    X, ident, AO = keep["X"], keep["ident"], keep["AO"]
    NB = NT // BLK
    with ExitStack() as ctx:
        m = Mem(nc, ctx)
        h = [m.sb(f"{tag}_merge_h{k}", [P, BLK, D]) for k in range(2)]
        hT = [m.sb(f"{tag}_merge_hT{k}", [P, BLK, DC, P]) for k in range(2)]
        wo = m.sb(f"{tag}_merge_wo", [P, DC, D])
        y = [m.sb(f"{tag}_merge_y{k}", [P, BLK, D]) for k in range(2)]
        st = m.sb(f"{tag}_merge_st", [P, BLK, 6])
        mv = [m.sb(f"{tag}_merge_mv{k}", [P, BLK, 2]) for k in range(2)]
        sd = [m.sb(f"{tag}_merge_sd{k}", [P, BLK]) for k in range(2)]
        rs = [m.sb(f"{tag}_merge_rs{k}", [P, BLK]) for k in range(2)]
        eps = m.sb(f"{tag}_merge_eps", [P, 1])
        psT = [m.ps(f"{tag}_merge_psT{k}", BLK * DC * P) for k in range(2)]
        psY = [m.ps(f"{tag}_merge_psY{k}", BLK * D) for k in range(2)]
        if bias:
            bo, ones = m.sb(f"{tag}_merge_bo", [1, D]), keep["ones1"]
        if rms:
            rw = m.sb(f"{tag}_merge_rw", [P, DV])
            sq = m.sb(f"{tag}_merge_sq", [P, BLK, D])
            hn = [m.sb(f"{tag}_merge_hn{k}", [P, BLK, D]) for k in range(2)]
            ss = m.sb(f"{tag}_merge_ss", [P, BLK * H])
            sr = m.sb(f"{tag}_merge_sr", [P, BLK * H])
            ri = m.sb(f"{tag}_merge_ri", [P, BLK * H])
        loaded = sems.sem(f"{tag}_merge_wo_in")
        h_in = [sems.sem(f"{tag}_merge_h_in{k}") for k in range(2)]
        const = sems.sem(f"{tag}_merge_const")
        hr = sems.sem(f"{tag}_merge_hr")
        hq = sems.sem(f"{tag}_merge_hq")
        turned = sems.sem(f"{tag}_merge_turned")
        hT_in = sems.sem(f"{tag}_merge_hT_in")
        y_done = sems.sem(f"{tag}_merge_y_done")
        y_read = sems.sem(f"{tag}_merge_y_read")
        stat = sems.sem(f"{tag}_merge_stat")
        root = sems.sem(f"{tag}_merge_root")
        passed = sems.sem(f"{tag}_merge_passed")
        NSTAT = 4
        NHR = 5
        HIN = 16 if dense else 16 * BLK
        with nc.Block() as block:
            @block.sync
            def _(sp):
                sp.dma_start(wo[:], a[f"{tag}_wo"]).then_inc(loaded, 16)
                if rms:
                    sp.dma_start(rw[:], a["L1_attn_rms_weight"].rearrange("(o d) -> o d", o=1).broadcast_to([P, DV])).then_inc(loaded, 16)
                if bias:
                    sp.dma_start(bo[:], a[bias].rearrange("(o d) -> o d", o=1)).then_inc(loaded, 16)
                with sp.Fori(0, B) as b:
                    for k in range(2):
                        if rms:
                            sp.wait_ge(hr, b * (2 * NHR) + (k + 2) * NHR)
                        else:
                            sp.wait_ge(turned, b * 2 + k)
                        if dense:
                            sp.dma_start(h[k][:], AO[:, bass.ds(b * TB + BLK * k, BLK), :]).then_inc(h_in[k], 16)
                        for t in range(0 if dense else BLK):
                            sp.dma_start(h[k][:, t, :].rearrange("p (g w) -> p g w", g=gb), AO[:, bass.ds(b * gb, gb), BLK * k + t, :]).then_inc(h_in[k], 16)

            @block.scalar
            def _(act):
                act.sem_inc(hT_in, 2)
                act.wait_ge(const, 1)
                with act.Fori(0, B) as b:
                    for k in range(2):
                        if rms:
                            act.wait_ge(hr, b * (2 * NHR) + (k + 2) * NHR + 2)
                            act.activation(sr[:], ss[:], ACT.Sqrt, bias=eps[:], scale=1.0 / DV).then_inc(hq, 1)
                        act.wait_ge(turned, b * 2 + k + 1)
                        act.activation(hT[k][:].rearrange("p t c n -> p (t c n)"), psT[k][:], ACT.Copy).then_inc(hT_in, 1)
                        act.wait_ge(stat, b * (2 * NSTAT) + NSTAT * k + 2)
                        act.activation(sd[k][:], mv[k][:, :, 1], ACT.Sqrt, bias=eps[:]).then_inc(root, 1)

            @block.tensor
            def _(pe):
                pe.wait_ge(loaded, 32 if rms or bias else 16)
                src = hn if rms else h
                with pe.Fori(0, B) as b:
                    for k in range(2):
                        if rms:
                            pe.wait_ge(hr, b * (2 * NHR) + (k + 3) * NHR)
                        else:
                            pe.wait_ge(h_in[k], b * HIN + HIN)
                        for t in range(BLK):
                            for c in range(DC):
                                last = pe.transpose(psT[k][:, (t * DC + c) * P:(t * DC + c + 1) * P],
                                                    src[k][:, t, c * P:(c + 1) * P], ident[:])
                        last.then_inc(turned, 1)
                        pe.wait_ge(hT_in, b * 2 + k + 3)
                        pe.wait_ge(y_read, b * 2 + k + 1)
                        for t in range(BLK):
                            if bias:
                                pe.matmul(psY[k][:, t * D:(t + 1) * D], ones[:], bo[:], start=True, stop=False)
                            for c in range(DC):
                                last = pe.matmul(psY[k][:, t * D:(t + 1) * D], hT[k][:, t, c, :], wo[:, c, :],
                                                 start=(c == 0 and not bias), stop=(c == DC - 1))
                        last.then_inc(y_done, 1)

            @block.vector
            def _(dve):
                dve.sem_inc(y_read, 2)
                dve.memset(eps[:], LN_EPS).then_inc(const, 1)
                if rms:
                    dve.sem_inc(hr, 2 * NHR)
                    dve.wait_ge(loaded, 32)
                    dve.tensor_scalar(rw[:], rw[:], 1.0 - LAMBDA_INIT, None, ALU.mult).then_inc(const, 1)
                    dve.wait_ge(const, 2)

                def root_mean_square(b, k):
                    n = b * (2 * NHR) + (k + 2) * NHR
                    dve.wait_ge(h_in[k], b * HIN + HIN)
                    flat = h[k][:].rearrange("p t f -> p (t f)")
                    dve.tensor_tensor(sq[:].rearrange("p t f -> p (t f)"), flat, flat, ALU.mult).then_inc(hr, 1)
                    dve.wait_ge(hr, n + 1)
                    heads = lambda x: x[:].rearrange("p t (h d) -> p (t h) d", d=DV)
                    dve.tensor_reduce(ss[:], heads(sq), AX, ALU.add).then_inc(hr, 1)
                    dve.wait_ge(hq, b * 2 + k + 1)
                    dve.reciprocal(ri[:], sr[:]).then_inc(hr, 1)
                    dve.wait_ge(hr, n + 3)
                    dve.tensor_tensor(heads(sq), heads(h[k]), ri[:].unsqueeze(2).broadcast_to([P, BLK * H, DV]),
                                      ALU.mult).then_inc(hr, 1)
                    dve.wait_ge(hr, n + 4)
                    dve.tensor_tensor(heads(hn[k]), heads(sq), rw[:].unsqueeze(1).broadcast_to([P, BLK * H, DV]),
                                      ALU.mult).then_inc(hr, 1)

                with dve.Fori(0, B) as b:
                    for k in range(2):
                        if rms:
                            root_mean_square(b, k)
                        n = b * (2 * NSTAT) + NSTAT * k
                        dve.wait_ge(y_done, b * 2 + k + 1)
                        xb = X[:, bass.ds(b * TB + BLK * k, BLK), :].rearrange("p t d -> p (t d)")
                        dve.tensor_tensor(y[k][:].rearrange("p t d -> p (t d)"), psY[k][:], xb, ALU.add).then_inc(y_read, 1)
                        dve.wait_ge(y_read, b * 2 + k + 3)
                        for t in range(BLK):
                            last = dve.bn_stats(st[:, t, :], y[k][:, t, :])
                        last.then_inc(stat, 1)
                        dve.wait_ge(stat, n + 1)
                        dve.sem_inc(passed, 1)
                        for t in range(BLK):
                            last = dve.bn_aggr(mv[k][:, t, :], st[:, t, :])
                        last.then_inc(stat, 1)
                        dve.wait_ge(root, b * 2 + k + 1)
                        dve.reciprocal(rs[k][:], sd[k][:]).then_inc(stat, 1)
                        dve.wait_ge(stat, n + 3)
                        for t in range(BLK):
                            last = dve.tensor_scalar(X[:, bass.ds(b * TB + BLK * k + t, 1), :].rearrange("p o d -> p (o d)"),
                                                     y[k][:, t, :], mv[k][:, t, 0:1], rs[k][:, t:t + 1],
                                                     ALU.subtract, ALU.mult)
                        last.then_inc(stat, 1)


class Chain:

    def __init__(self, eng, sem):
        self.eng, self.sem, self.n = eng, sem, 0

    def did(self, ins):
        self.n += 1
        ins.then_inc(self.sem, 1)

    def wait(self):
        self.eng.wait_ge(self.sem, self.n)


class Steps:

    def __init__(self, eng, sem, item, per, k=0):
        self.eng, self.sem, self.item, self.per, self.k = eng, sem, item, per, k

    def did(self, ins):
        self.k += 1
        assert self.k <= self.per
        ins.then_inc(self.sem, 1)

    def wait(self):
        self.eng.wait_ge(self.sem, self.item.times(self.per, self.k))


def cross_setup(nc, a, keep, sems):
    KT, VBD, bq, bo, lg, lb, heads8 = (keep[k] for k in ("KT", "VBD", "bq", "bo", "lg", "lb", "heads8"))
    ident = keep["ident"]
    CK = 96
    with ExitStack() as ctx:
        m = Mem(nc, ctx)
        ctxT = m.sb("x0s_ctxT", [CK, 2, B, P])
        wkv = m.sb("x0s_wkv", [CK, 2, 2 * D])
        bkv = m.sb("x0s_bkv", [P, 2 * D])
        kp = m.sb("x0s_kp", [P, B, D])
        sq = m.sb("x0s_sq", [P, B, D])
        ss = m.sb("x0s_ss", [P, B])
        nr = m.sb("x0s_nr", [P, B])
        kn = m.sb("x0s_kn", [P, B, D])
        ps = m.ps("x0s_ps", B * 2 * D)
        psT = m.ps("x0s_psT", 2 * B * 64)
        loaded = sems.sem("x0s_loaded")
        products = sems.sem("x0s_products")
        done = sems.sem("x0s_done")
        root = sems.sem("x0s_root")
        turned = sems.sem("x0s_turned")
        with nc.Block() as block:
            @block.sync
            def _(sp):
                for dst, src in ((ctxT[:], a["ctxT2"]), (wkv[:], a["L0x_wkv"]),
                                 (bkv[:, 0:D], a["L0_xattn_bk"].rearrange("(o d) -> o d", o=1).broadcast_to([P, D])),
                                 (bkv[:, D:], a["L0_xattn_bv"].rearrange("(o d) -> o d", o=1).broadcast_to([P, D])),
                                 (bq[:], a["L0_xattn_bq"].rearrange("(o d) -> o d", o=1).broadcast_to([P, D])),
                                 (bo[:], a["L0_xattn_bo"].rearrange("(o d) -> o d", o=1).broadcast_to([P, D])),
                                 (lg[:], a["L0_xattn_ln_gamma"].rearrange("(o d) -> o d", o=1).broadcast_to([P, D])),
                                 (lb[:], a["L0_xattn_ln_beta"].rearrange("(o d) -> o d", o=1).broadcast_to([P, D])),
                                 (heads8[:], a["heads8"])):
                    sp.dma_start(dst, src).then_inc(loaded, 16)

            @block.tensor
            def _(pe):
                pe.wait_ge(loaded, 144)
                for b in range(B):
                    for c in range(2):
                        last = pe.matmul(ps[:, b * 2 * D:(b + 1) * 2 * D], ctxT[:, c, b, :], wkv[:, c, :],
                                         start=(c == 0), stop=(c == 1))
                last.then_inc(products, 1)
                pe.wait_ge(done, 8)
                for c in range(DC):
                    for b in range(B):
                        last = pe.transpose(psT[:, (c * B + b) * 64:(c * B + b + 1) * 64], kn[0:64, b, c * P:(c + 1) * P],
                                            ident[0:64, 0:64])
                last.then_inc(turned, 1)

            @block.scalar
            def _(act):
                act.wait_ge(done, 5)
                act.activation(nr[:], ss[:], ACT.Sqrt).then_inc(root, 1)

            @block.vector
            def _(dve):
                chain = Chain(dve, done)
                chain.did(dve.memset(VBD[:], 0.0))
                dve.wait_ge(done, 1)
                chain.did(dve.memset(VBD[0:64, :, :, DV:DV + 1], 1.0))
                chain.did(dve.memset(VBD[64:P, :, :, 2 * DV + 1:2 * DV + 2], 1.0))
                dve.wait_ge(products, 1)
                pv = ps[:].rearrange("p (b n) -> p b n", b=B)
                for b in range(B):
                    last = dve.tensor_tensor(kp[:, b, :], pv[:, b, 0:D], bkv[:, 0:D], ALU.add)
                chain.did(last)
                dve.wait_ge(done, 4)
                dve.tensor_tensor(sq[:], kp[:], kp[:], ALU.mult).then_inc(root, 1)
                dve.wait_ge(root, 1)
                chain.did(dve.tensor_reduce(ss[:], sq[:], AX, ALU.add))
                dve.wait_ge(root, 2)
                chain.did(dve.tensor_scalar(nr[:], nr[:], 1e-12, None, ALU.max))
                dve.wait_ge(done, 6)
                chain.did(dve.reciprocal(ss[:], nr[:]))
                dve.wait_ge(done, 7)
                for b in range(B):
                    last = dve.tensor_scalar(kn[:, b, :], kp[:, b, :], ss[:, b:b + 1], None, ALU.mult)
                chain.did(last)
                for b in range(B):
                    for h in range(2):
                        r = slice(64 * h, 64 * h + 64)
                        view = lambda x: x.rearrange("p (a h d) -> p a h d", a=H // 2, h=2)[:, :, h, :]
                        last = dve.tensor_tensor(VBD[r, b, :, (DV + 1) * h:(DV + 1) * h + DV], view(pv[r, b, D:]),
                                                 view(bkv[r, D:]), ALU.add)
                chain.did(last)
                dve.wait_ge(turned, 1)
                chain.did(dve.tensor_copy(KT[:], psT[:].rearrange("p (c b k) -> p c b k", c=DC, b=B)))


def cross(nc, a, keep, sems):
    X, ident = keep["X"], keep["ident"]
    KT, VBD, bq, bo, lg, lb, heads8 = (keep[k] for k in ("KT", "VBD", "bq", "bo", "lg", "lb", "heads8"))
    NB = NT // BLK
    HP = H // 2
    W2 = 2 * (DV + 1)
    with ExitStack() as ctx:
        m = Mem(nc, ctx)
        two = lambda name, shape, dt=F32: [m.sb(f"x0_{name}{k}", shape, dt) for k in range(2)]
        QP = m.sb("x0_QP", [P, NT, D])
        wq = m.sb("x0_wq", [P, DC, D])
        wo = m.sb("x0_wo", [P, DC, D])
        xs = two("xs", [P, BLK, D])
        xT = m.sb("x0_xT", [P, DC, HALF])
        qp = m.sb("x0_qp", [P, BLK, D])
        sq = m.sb("x0_sq", [P, BLK, D])
        ss = m.sb("x0_ss", [P, BLK])
        nr = m.sb("x0_nr", [P, BLK])
        ns = m.sb("x0_ns", [P, BLK])
        rn = m.sb("x0_rn", [P, BLK])
        qn = m.sb("x0_qn", [P, BLK, D])
        qT = two("qT", [P, DC, HALF])
        KB = two("KB", [P, HP, P])
        E = m.sb("x0_E", [P, HP, HALF])
        rec = m.sb("x0_rec", [P, BLK, H])
        at = two("at", [P, BLK, D])
        aT = m.sb("x0_aT", [P, BLK, DC, P])
        y = m.sb("x0_y", [P, BLK, D])
        z = m.sb("x0_z", [P, BLK, D])
        zg = m.sb("x0_zg", [P, BLK, D])
        zb = m.sb("x0_zb", [P, BLK, D])
        w = m.sb("x0_w", [P, BLK, D])
        st = m.sb("x0_st", [P, BLK, 6])
        mv = m.sb("x0_mv", [P, BLK, 2])
        sd = m.sb("x0_sd", [P, BLK])
        rs = m.sb("x0_rs", [P, BLK])
        eps = m.sb("x0_eps", [P, 1])
        psA = m.ps("x0_psA", BLK * D)
        psS = [m.ps(f"x0_psS{k}", HALF) for k in range(2)]
        psO = [m.ps(f"x0_psO{k}", HALF) for k in range(2)]
        psC = m.ps("x0_psC", BLK * D)
        sem = lambda name: sems.sem(f"x0_{name}")
        weights = sem("weights")
        xs_in = [sem(f"xs_in{k}") for k in range(2)]
        a_pe = sem("a_pe")
        a_act = sem("a_act")
        a_dve = sem("a_dve")
        a_rec = sem("a_rec")
        kb_in = sem("kb_in")
        qp_in = sem("qp_in")
        s_done = sem("s_done")
        e_done = sem("e_done")
        o_done = sem("o_done")
        o_rec = sem("o_rec")
        o_read = sem("o_read")
        c_pe = sem("c_pe")
        c_act = sem("c_act")
        c_dve = sem("c_dve")
        c_pool = sem("c_pool")
        passed = sem("passed")
        held = sem("held")
        const = sem("const")
        NA, NCD = 5, 10
        with nc.Block() as block:
            @block.sync
            def _(sp):
                sp.dma_start(wq[:], a["L0x_wq"]).then_inc(weights, 16)
                sp.dma_start(wo[:], a["L0x_wo"]).then_inc(weights, 16)

                def turn(t, live):
                    if live[0]:
                        if t.base >= 2 or t.n is not None:
                            sp.wait_ge(a_pe, (t + -2).times(3, 1))
                        sp.dma_start(xs[t.slot][:], X[:, t.span(BLK), :]).then_inc(xs_in[t.slot], 16)

                run_turns(sp, turn, NB, 2, 2)

            @block.tensor
            def _(pe):
                pe.wait_ge(weights, 32)

                def scores(g, hp):
                    pe.wait_ge(e_done, g.times(HP, hp + 1))
                    pe.matmul(psS[hp % 2][:], KB[g.slot][:, hp, :], qT[g.slot][:, hp // 4, :], start=True,
                              stop=True).then_inc(s_done, 1)

                def turn(t, live):
                    u, v = t + -1, t + -2
                    if live[0]:
                        pe.wait_ge(xs_in[t.slot], t.over(16, 16))
                        pe.wait_ge(a_act, t.times(3))
                        for c in range(DC):
                            for k in range(BLK):
                                last = pe.transpose(psA[:, (c * BLK + k) * P:(c * BLK + k + 1) * P],
                                                    xs[t.slot][:, k, c * P:(c + 1) * P], ident[:])
                        last.then_inc(a_pe, 1)
                    if live[1]:
                        pe.wait_ge(kb_in, u.times(1, 1))
                        pe.wait_ge(a_act, u.times(3, 3))
                        for hp in range(4):
                            scores(u, hp)
                    if live[0]:
                        pe.wait_ge(a_act, t.times(3, 1))
                        for k in range(BLK):
                            for c in range(DC):
                                last = pe.matmul(psA[:, k * D:(k + 1) * D], xT[:, c, k * P:(k + 1) * P], wq[:, c, :],
                                                 start=(c == 0), stop=(c == DC - 1))
                        last.then_inc(a_pe, 1)
                    if live[1]:
                        for hp in range(4, HP):
                            scores(u, hp)
                    if live[2]:
                        pe.wait_ge(o_read, v.times(BLK, BLK + 2))
                        pe.wait_ge(c_dve, v.times(NCD))
                        for k in range(BLK):
                            for c in range(DC):
                                last = pe.transpose(psC[:, (k * DC + c) * P:(k * DC + c + 1) * P],
                                                    at[v.slot][:, k, c * P:(c + 1) * P], ident[:])
                        last.then_inc(c_pe, 1)
                    if live[0]:
                        pe.wait_ge(a_dve, t.times(NA, NA))
                        for c in range(DC):
                            for k in range(BLK):
                                last = pe.transpose(psA[:, (c * BLK + k) * P:(c * BLK + k + 1) * P],
                                                    qn[:, k, c * P:(c + 1) * P], ident[:])
                        last.then_inc(a_pe, 1)
                    if live[1]:
                        pe.wait_ge(e_done, u.times(HP, HP + 2))
                        for k in range(BLK):
                            pe.wait_ge(o_read, u.times(BLK, k + 1))
                            for hp in range(HP):
                                last = pe.matmul(psO[k % 2][:, hp * W2:(hp + 1) * W2], E[:, hp, k * P:(k + 1) * P],
                                                 VBD[:, bass.ds(u.over(1), 1) if u.n is not None else slice(u.over(1), u.over(1) + 1), hp, :]
                                                 .rearrange("p o n -> p (o n)"), start=True, stop=True)
                            last.then_inc(o_done, 1)
                    if live[2]:
                        pe.wait_ge(c_act, v.times(3, 1))
                        for k in range(BLK):
                            for c in range(DC):
                                last = pe.matmul(psC[:, k * D:(k + 1) * D], aT[:, k, c, :], wo[:, c, :],
                                                 start=(c == 0), stop=(c == DC - 1))
                        last.then_inc(c_pe, 1)

                run_turns(pe, turn, NB, 2, 2)

            @block.scalar
            def _(act):
                act.sem_inc(e_done, 2)
                act.wait_ge(const, 1)

                def turn(t, live):
                    u, v = t + -1, t + -2
                    if live[0]:
                        act.wait_ge(a_pe, t.times(3, 1))
                        act.activation(xT[:].rearrange("p c n -> p (c n)"), psA[:], ACT.Copy).then_inc(a_act, 1)
                    if live[1]:
                        act.wait_ge(o_done, u.times(BLK))
                        for hp in range(HP):
                            act.wait_ge(s_done, u.times(HP, hp + 1))
                            act.activation(E[:, hp, :], psS[hp % 2][:], ACT.Exp, scale=0.25).then_inc(e_done, 1)
                    if live[0]:
                        act.wait_ge(a_dve, t.times(NA, 3))
                        act.activation(nr[:], ss[:], ACT.Sqrt).then_inc(a_act, 1)
                    if live[2]:
                        act.wait_ge(c_pe, v.times(2, 1))
                        act.activation(aT[:].rearrange("p k c n -> p (k c n)"), psC[:], ACT.Copy).then_inc(c_act, 1)
                    if live[0]:
                        act.wait_ge(a_pe, t.times(3, 3))
                        act.activation(qT[t.slot][:].rearrange("p c n -> p (c n)"), psA[:], ACT.Copy).then_inc(a_act, 1)
                    if live[2]:
                        for n in range(2):
                            act.wait_ge(c_dve, v.times(NCD, 3 + 5 * n))
                            act.activation(sd[:], mv[:, :, 1], ACT.Sqrt, bias=eps[:]).then_inc(c_act, 1)

                run_turns(act, turn, NB, 2, 2)

            @block.gpsimd
            def _(pool):
                def turn(t, live):
                    v = t + -2
                    if live[0]:
                        if t.base >= 2 or t.n is not None:
                            pool.wait_ge(s_done, (t + -1).times(HP))
                            pool.sem_inc(held, 1)
                        for c in range(DC):
                            src = KT[:, c, bass.ds(t.over(1), 1) if t.n is not None else slice(t.over(1), t.over(1) + 1), :]
                            last = pool.tensor_tensor(KB[t.slot][:, c * 4:(c + 1) * 4, :].rearrange("p a (h k) -> p (a h) k", h=2),
                                                      src.broadcast_to([P, 8, 64]), heads8[:].unsqueeze(2).broadcast_to([P, 8, 64]),
                                                      ALU.mult)
                        last.then_inc(kb_in, 1)
                        pool.wait_ge(a_dve, t.times(NA, 1))
                        pool.sem_inc(held, 1)
                        pool.tensor_tensor(QP[:, t.span(BLK), :], qp[:], bo[:].unsqueeze(1).broadcast_to([P, BLK, D]),
                                           ALU.add).then_inc(qp_in, 1)
                    if live[2]:
                        pool.wait_ge(c_dve, v.times(NCD, 5))
                        pool.tensor_tensor(zg[:], z[:], lg[:].unsqueeze(1).broadcast_to([P, BLK, D]), ALU.mult).then_inc(c_pool, 1)
                        pool.wait_ge(c_pool, v.times(2, 1))
                        pool.tensor_tensor(zb[:], zg[:], lb[:].unsqueeze(1).broadcast_to([P, BLK, D]), ALU.add).then_inc(c_pool, 1)

                run_turns(pool, turn, NB, 2, 2)

            @block.vector
            def _(dve):
                dve.sem_inc(o_read, 2)
                dve.memset(eps[:], LN_EPS).then_inc(const, 1)

                def layernorm(v, n, src, out):
                    dve.wait_ge(c_dve, v.times(NCD, 1 + 5 * n))
                    for k in range(BLK):
                        last = dve.bn_stats(st[:, k, :], src[:, k, :])
                    last.then_inc(c_dve, 1)
                    dve.wait_ge(c_dve, v.times(NCD, 2 + 5 * n))
                    dve.sem_inc(passed, 1)
                    for k in range(BLK):
                        last = dve.bn_aggr(mv[:, k, :], st[:, k, :])
                    last.then_inc(c_dve, 1)
                    dve.wait_ge(c_act, v.times(3, 2 + n))
                    dve.reciprocal(rs[:], sd[:]).then_inc(c_dve, 1)
                    dve.wait_ge(c_dve, v.times(NCD, 4 + 5 * n))
                    for k in range(BLK):
                        last = dve.tensor_scalar(out(k), src[:, k, :], mv[:, k, 0:1], rs[:, k:k + 1], ALU.subtract, ALU.mult)
                    last.then_inc(c_dve, 1)

                def turn(t, live):
                    u, v = t + -1, t + -2
                    if live[0]:
                        dve.wait_ge(a_pe, t.times(3, 2))
                        dve.wait_ge(qp_in, t.times(1))
                        dve.tensor_tensor(qp[:], psA[:].rearrange("p (k d) -> p k d", k=BLK),
                                          bq[:].unsqueeze(1).broadcast_to([P, BLK, D]), ALU.add).then_inc(a_dve, 1)
                        dve.wait_ge(a_dve, t.times(NA, 1))
                        dve.tensor_tensor(sq[:], qp[:], qp[:], ALU.mult).then_inc(a_dve, 1)
                        dve.wait_ge(a_dve, t.times(NA, 2))
                        dve.tensor_reduce(ss[:], sq[:], AX, ALU.add).then_inc(a_dve, 1)
                        dve.wait_ge(a_act, t.times(3, 2))
                        dve.tensor_scalar(ns[:], nr[:], 1e-12, None, ALU.max).then_inc(a_dve, 1)
                        dve.wait_ge(a_dve, t.times(NA, 4))
                        dve.reciprocal(rn[:], ns[:]).then_inc(a_rec, 1)
                        dve.wait_ge(a_rec, t.times(1, 1))
                        for k in range(BLK):
                            last = dve.tensor_scalar(qn[:, k, :], qp[:, k, :], rn[:, k:k + 1], None, ALU.mult)
                        last.then_inc(a_dve, 1)
                    if live[1]:
                        for k in range(BLK):
                            dve.wait_ge(o_done, u.times(BLK, k + 1))
                            ps = psO[k % 2][:, 0:HP * W2].rearrange("p (h d) -> p h d", h=H)
                            dve.reciprocal(rec[:, k, :], ps[:, :, DV]).then_inc(o_rec, 1)
                            dve.wait_ge(o_rec, u.times(BLK, k + 1))
                            dve.tensor_tensor(at[u.slot][:, k, :].rearrange("p (h d) -> p h d", h=H), ps[:, :, 0:DV],
                                              rec[:, k, :].unsqueeze(2).broadcast_to([P, H, DV]), ALU.mult).then_inc(o_read, 1)
                    if live[2]:
                        dve.wait_ge(c_pe, v.times(2, 2))
                        dve.wait_ge(qp_in, v.times(1, 1))
                        dve.tensor_tensor(y[:], psC[:].rearrange("p (k d) -> p k d", k=BLK), QP[:, v.span(BLK), :],
                                          ALU.add).then_inc(c_dve, 1)
                        layernorm(v, 0, y, lambda k: z[:, k, :])
                        dve.wait_ge(c_pool, v.times(2, 2))
                        dve.tensor_tensor(w[:], zb[:], X[:, v.span(BLK), :], ALU.add).then_inc(c_dve, 1)
                        out = lambda k: X[:, bass.ds(v.times(BLK, k), 1) if v.n is not None
                                          else slice(v.times(BLK, k), v.times(BLK, k) + 1), :].rearrange("p o d -> p (o d)")
                        layernorm(v, 1, w, out)

                run_turns(dve, turn, NB, 2, 2)


EX = 8
CAPACITY = int(S * 2 / EX * 1.5) + 1


def experts(nc, a, keep, sems):
    X, ident, identb = keep["X"], keep["ident"], keep["identb"]
    NB = NT // BLK
    with nc.cleanup_on_exit(), ExitStack() as ctx:
        m = Mem(nc, ctx)
        sb = lambda name, shape, dt=F32: m.sb(f"m0_{name}", shape, dt)
        two = lambda name, shape, dt=F32: [m.sb(f"m0_{name}{k}", shape, dt) for k in range(2)]
        we, wr = sb("we", [P, DC, EX * D]), sb("wr", [P, DC, EX])
        tri, trib, onesb, iota = sb("tri", [P, P]), sb("trib", [P, P], BF16), sb("onesb", [P, P], BF16), sb("iota", [P, EX])
        xs, xT = two("xs", [P, BLK, D]), two("xT", [P, DC, HALF])
        logit, top, ix = sb("logit", [P, BLK, EX]), sb("top", [P, BLK, 8]), sb("ix", [P, BLK, 8], U32)
        ixf, d, ed, den, w1, w2 = (sb(n, [P, BLK, 2] if n == "ixf" else [P, BLK]) for n in ("ixf", "d", "ed", "den", "w1", "w2"))
        oh1, oh2, g1, g2, g12 = (sb(n, [P, BLK, EX]) for n in ("oh1", "oh2", "g1", "g2", "g12"))
        chosen, before = two("chosen", [P, BLK, EX], BF16), two("before", [P, BLK, EX], BF16)
        W = two("W", [P, BLK, EX])
        z = sb("z", [P, BLK, D])
        st, mv, sd, rs, eps = sb("st", [P, BLK, 6]), sb("mv", [P, BLK, 2]), sb("sd", [P, BLK]), sb("rs", [P, BLK]), sb("eps", [P, 1])
        psA = m.ps("m0_psA", BLK * D)
        psG = m.ps("m0_psG", HALF)
        psE = [m.ps(f"m0_psE{k}", HALF) for k in range(4)]
        sem = lambda name: sems.sem(f"m0_{name}")
        weights, const = sem("weights"), sem("const")
        xs_in = [sem(f"xs_in{k}") for k in range(2)]
        g_pe = sem("g_pe")
        g_act = sem("g_act")
        g_dve = sem("g_dve")
        y_pe = sem("y_pe")
        y_dve = sem("y_dve")
        n_dve = sem("n_dve")
        n_act = sem("n_act")
        passed = sem("passed")
        NG, G_D, G_CHOSEN = 19, 4, 14
        with nc.Block() as block:
            @block.sync
            def _(sp):
                for dst, src in ((we[:], a["L0f_we"]), (wr[:], a["L0f_wr"]), (tri[:], a["tri"]),
                                 (iota[:], a["iota8"].broadcast_to([P, EX]))):
                    sp.dma_start(dst, src).then_inc(weights, 16)

                def turn(t, live):
                    if live[0]:
                        if t.base >= 2 or t.n is not None:
                            sp.wait_ge(y_dve, (t + -1).times(BLK * EX))
                        sp.dma_start(xs[t.slot][:], X[:, t.span(BLK), :]).then_inc(xs_in[t.slot], 16)

                run_turns(sp, turn, NB, 1, 2)

            @block.tensor
            def _(pe):
                pe.wait_ge(weights, 64)
                pe.wait_ge(const, 3)

                def expert_products(u, k):
                    for e in range(EX // 2):
                        n = k * (EX // 2) + e
                        if n >= 4 or u.base >= 1 or u.n is not None:
                            pe.wait_ge(y_dve, u.times(BLK * EX, 2 * (n - 3)))
                        for c in range(DC):
                            last = pe.matmul(psE[e][:], xT[u.slot][:, c, k * P:(k + 1) * P],
                                             we[:, c, e * HALF:(e + 1) * HALF], start=(c == 0), stop=(c == DC - 1))
                        last.then_inc(y_pe, 1)

                def turn(t, live):
                    u = t + -1
                    if live[0]:
                        pe.wait_ge(xs_in[t.slot], t.over(16, 16))
                        pe.wait_ge(g_act, t.times(2))
                        for c in range(DC):
                            for k in range(BLK):
                                last = pe.transpose(psA[:, (c * BLK + k) * P:(c * BLK + k + 1) * P],
                                                    xs[t.slot][:, k, c * P:(c + 1) * P], ident[:])
                        last.then_inc(g_pe, 1)
                    if live[1]:
                        expert_products(u, 0)
                    if live[0]:
                        pe.wait_ge(g_act, t.times(2, 1))
                        pe.wait_ge(g_dve, t.times(NG))
                        for k in range(BLK):
                            for c in range(DC):
                                last = pe.matmul(psG[:, k * EX:(k + 1) * EX], xT[t.slot][:, c, k * P:(k + 1) * P], wr[:, c, :],
                                                 start=(c == 0), stop=(c == DC - 1))
                        last.then_inc(g_pe, 1)
                    if live[1]:
                        expert_products(u, 1)
                        expert_products(u, 2)
                    if live[0]:
                        pe.wait_ge(g_dve, t.times(NG, G_CHOSEN + 4))
                        pe.matmul(psG[:, 0:BLK * EX], trib[:], chosen[t.slot][:].rearrange("p k e -> p (k e)"), start=True, stop=False)
                        pe.matmul(psG[:, 0:BLK * EX], onesb[:], before[t.slot][:].rearrange("p k e -> p (k e)"), start=False,
                                  stop=True).then_inc(g_pe, 1)
                    if live[1]:
                        expert_products(u, 3)

                run_turns(pe, turn, NB, 1, 2)

            @block.scalar
            def _(act):
                act.wait_ge(const, 3)

                def turn(t, live):
                    u = t + -1
                    if live[0]:
                        act.wait_ge(g_pe, t.times(3, 1))
                        if t.base >= 2 or t.n is not None:
                            act.wait_ge(y_pe, (t + -1).times(BLK * EX // 2))
                        act.activation(xT[t.slot][:].rearrange("p c n -> p (c n)"), psA[:], ACT.Copy).then_inc(g_act, 1)
                        act.wait_ge(g_dve, t.times(NG, G_D))
                        act.activation(ed[:], d[:], ACT.Exp).then_inc(g_act, 1)
                    if live[1]:
                        act.wait_ge(n_dve, u.times(4, 2))
                        act.activation(sd[:], mv[:, :, 1], ACT.Sqrt, bias=eps[:]).then_inc(n_act, 1)

                run_turns(act, turn, NB, 1, 2)

            @block.vector
            def _(dve):
                dve.memset(eps[:], LN_EPS).then_inc(const, 1)
                dve.memset(onesb[:], 1.0).then_inc(const, 1)
                dve.wait_ge(weights, 64)
                dve.tensor_copy(trib[:], tri[:]).then_inc(const, 1)

                def add_experts(u, k):
                    dve.wait_ge(g_dve, u.times(NG, NG))
                    if k == 0:
                        dve.wait_ge(n_dve, u.times(4))
                    for e in range(EX):
                        n = k * EX + e
                        dve.wait_ge(y_pe, u.times(BLK * EX // 2, k * (EX // 2) + e // 2 + 1))
                        dve.wait_ge(y_dve, u.times(BLK * EX, n))
                        dve.scalar_tensor_tensor(out=z[:, k, :], in0=psE[e // 2][:, (e % 2) * D:(e % 2 + 1) * D],
                                                 scalar=W[u.slot][:, k, e:e + 1], in1=xs[u.slot][:, k, :] if e == 0 else z[:, k, :],
                                                 op0=ALU.mult, op1=ALU.add).then_inc(y_dve, 1)

                def first(t):
                    s = Steps(dve, g_dve, t, NG)
                    ch, bf = chosen[t.slot], before[t.slot]
                    dve.wait_ge(g_pe, t.times(3, 2))
                    s.did(dve.tensor_copy(logit[:], psG[:, 0:BLK * EX].rearrange("p (k e) -> p k e", k=BLK)))
                    s.wait()
                    dve.sem_inc(passed, 1)
                    for k in range(BLK):
                        last = dve.max(top[:, k, :], logit[:, k, :])
                    s.did(last)
                    s.wait()
                    dve.sem_inc(passed, 1)
                    for k in range(BLK):
                        last = dve.max_index(ix[:, k, :], top[:, k, :], logit[:, k, :])
                    s.did(last)
                    s.did(dve.tensor_tensor(d[:], top[:, :, 1], top[:, :, 0], ALU.subtract))
                    assert s.k == G_D
                    s.wait()
                    s.did(dve.tensor_copy(ixf[:], ix[:, :, 0:2]))
                    s.wait()
                    for n, oh in ((0, oh1), (1, oh2)):
                        s.did(dve.tensor_tensor(oh[:], iota[:].unsqueeze(1).broadcast_to([P, BLK, EX]),
                                                ixf[:, :, n:n + 1].broadcast_to([P, BLK, EX]), ALU.is_equal))
                    s.wait()
                    s.did(dve.tensor_tensor(ch[:], oh1[:], oh2[:], ALU.add))
                    dve.wait_ge(g_act, t.times(2, 2))
                    s.did(dve.tensor_scalar(den[:], ed[:], 1.0, None, ALU.add))
                    s.wait()
                    s.did(dve.reciprocal(w1[:], den[:]))
                    s.wait()
                    s.did(dve.tensor_tensor(w2[:], ed[:], w1[:], ALU.mult))
                    s.wait()
                    s.did(dve.tensor_tensor(g1[:], oh1[:], w1[:].unsqueeze(2).broadcast_to([P, BLK, EX]), ALU.mult))
                    s.did(dve.tensor_tensor(g2[:], oh2[:], w2[:].unsqueeze(2).broadcast_to([P, BLK, EX]), ALU.mult))
                    s.wait()
                    s.did(dve.tensor_tensor(g12[:], g1[:], g2[:], ALU.add))
                    assert s.k == G_CHOSEN
                    if t.slot == 0:
                        s.did(dve.memset(bf[:, 0, :], 0.0))
                    else:
                        s.did(dve.tensor_tensor(bf[:, 0, :], before[0][:, BLK - 1, :], chosen[0][:, BLK - 1, :], ALU.add))
                    for k in range(1, BLK):
                        s.wait()
                        s.did(dve.tensor_tensor(bf[:, k, :], bf[:, k - 1, :], ch[:, k - 1, :], ALU.add))

                def second(t):
                    s = Steps(dve, g_dve, t, NG, G_CHOSEN + 4)
                    dve.wait_ge(g_pe, t.times(3, 3))
                    ps = psG[:, 0:BLK * EX]
                    s.did(dve.scalar_tensor_tensor(out=W[t.slot][:].rearrange("p k e -> p (k e)"), in0=ps, scalar=float(CAPACITY),
                                                   in1=g12[:].rearrange("p k e -> p (k e)"), op0=ALU.is_lt, op1=ALU.mult))

                def norm(u):
                    dve.wait_ge(y_dve, u.times(BLK * EX, BLK * EX))
                    for k in range(BLK):
                        last = dve.bn_stats(st[:, k, :], z[:, k, :])
                    last.then_inc(n_dve, 1)
                    dve.wait_ge(n_dve, u.times(4, 1))
                    dve.sem_inc(passed, 1)
                    for k in range(BLK):
                        last = dve.bn_aggr(mv[:, k, :], st[:, k, :])
                    last.then_inc(n_dve, 1)
                    dve.wait_ge(n_act, u.times(1, 1))
                    dve.reciprocal(rs[:], sd[:]).then_inc(n_dve, 1)
                    dve.wait_ge(n_dve, u.times(4, 3))
                    for k in range(BLK):
                        out = X[:, bass.ds(u.times(BLK, k), 1) if u.n is not None else slice(u.times(BLK, k), u.times(BLK, k) + 1), :]
                        last = dve.tensor_scalar(out.rearrange("p o d -> p (o d)"), z[:, k, :], mv[:, k, 0:1], rs[:, k:k + 1],
                                                 ALU.subtract, ALU.mult)
                    last.then_inc(n_dve, 1)

                def turn(t, live):
                    u = t + -1
                    if live[1]:
                        add_experts(u, 0)
                    if live[0]:
                        first(t)
                    if live[1]:
                        add_experts(u, 1)
                        add_experts(u, 2)
                    if live[0]:
                        second(t)
                    if live[1]:
                        add_experts(u, 3)
                        norm(u)

                run_turns(dve, turn, NB, 1, 2)


LH, LD = 4, 64
CK = 96
CTX = 64
VW = LD + 1


def context_keys(nc, a, keep, sems):
    ident, kTc, Vc, gam, ones, maskrow = (keep[k] for k in ("ident", "kTc", "Vc", "gam", "ones1", "maskrow"))
    KD = 192
    with ExitStack() as ctx:
        m = Mem(nc, ctx)
        sb = lambda name, shape, dt=F32: m.sb(f"x1s_{name}", shape, dt)
        cx, xc, xn = sb("cx", [CTX, B, KD]), sb("xc", [CTX, B, KD]), sb("xn", [CTX, B, KD])
        lg, lb = sb("lg", [CTX, KD]), sb("lb", [CTX, KD])
        xT = sb("xT", [CK, 2, B, CTX])
        wkv = sb("wkv", [CK, 2, 2 * D])
        mask8, maskf = sb("mask8", [1, B * CTX], mybir.dt.uint8), sb("maskf", [1, B * CTX])
        st, mv, sd, rs, eps = sb("st", [CTX, B, 6]), sb("mv", [CTX, B, 2]), sb("sd", [CTX, B]), sb("rs", [CTX, B]), sb("eps", [P, 1])
        sq, kn = sb("sq", [CTX, B, D]), sb("kn", [CTX, B, D])
        ss, nr, rn = sb("ss", [CTX, B * LH]), sb("nr", [CTX, B * LH]), sb("rn", [CTX, B * LH])
        ps = m.ps("x1s_ps", B * 2 * D)
        psT = m.ps("x1s_psT", 2 * B * CTX)
        sem = lambda name: sems.sem(f"x1s_{name}")
        loaded, products, turned, done, roots = sem("loaded"), sem("products"), sem("turned"), sem("done"), sem("roots")
        kv = ps[0:CTX, :].rearrange("p (b n) -> p b n", b=B)
        row = lambda name, n: a[name].rearrange("(o d) -> o d", o=1).broadcast_to([n, a[name].shape[0]])
        with nc.Block() as block:
            @block.sync
            def _(sp):
                for dst, src in ((cx[:], a["ctx_tok"]), (wkv[:], a["L1x_wkv"]), (mask8[:], a["mask8"]),
                                 (lg[:], row("L1_xattn_ln_x_g", CTX)), (lb[:], row("L1_xattn_ln_x_b", CTX)),
                                 (gam[:, 0:LD], row("L1_xattn_qn_g", P)), (gam[:, LD:], row("L1_xattn_kn_g", P))):
                    sp.dma_start(dst, src).then_inc(loaded, 16)

            @block.tensor
            def _(pe):
                pe.wait_ge(done, 9)
                for c in range(2):
                    for b in range(B):
                        last = pe.transpose(psT[0:CK, (c * B + b) * CTX:(c * B + b + 1) * CTX], xn[:, b, c * CK:(c + 1) * CK],
                                            ident[0:CTX, 0:CTX])
                last.then_inc(turned, 1)
                pe.wait_ge(done, 10)
                for b in range(B):
                    for c in range(2):
                        last = pe.matmul(ps[0:CTX, b * 2 * D:(b + 1) * 2 * D], xT[:, c, b, :], wkv[:, c, :],
                                         start=(c == 0), stop=(c == 1))
                last.then_inc(products, 1)
                pe.wait_ge(done, 17)
                for c in range(DC):
                    for b in range(B):
                        last = pe.transpose(psT[:, (c * B + b) * CTX:(c * B + b + 1) * CTX], kn[:, b, c * P:(c + 1) * P],
                                            ident[0:CTX, 0:CTX])
                last.then_inc(turned, 1)

            @block.scalar
            def _(act):
                act.wait_ge(done, 5)
                act.activation(sd[:], mv[:, :, 1], ACT.Sqrt, bias=eps[0:CTX]).then_inc(roots, 1)
                act.wait_ge(done, 12)
                act.activation(nr[:], ss[:], ACT.Sqrt, scale=1.0 / LD).then_inc(roots, 1)

            @block.vector
            def _(dve):
                s = Chain(dve, done)
                s.did(dve.memset(eps[:], LN_EPS))
                s.did(dve.memset(ones[:], 1.0))
                s.did(dve.memset(Vc[:, :, :, LD:VW], 1.0))
                dve.wait_ge(loaded, 112)
                for b in range(B):
                    last = dve.bn_stats(st[:, b, :], cx[:, b, :])
                s.did(last)
                s.wait()
                for b in range(B):
                    last = dve.bn_aggr(mv[:, b, :], st[:, b, :])
                s.did(last)
                dve.wait_ge(roots, 1)
                s.did(dve.reciprocal(rs[:], sd[:]))
                s.wait()
                for b in range(B):
                    last = dve.tensor_scalar(xc[:, b, :], cx[:, b, :], mv[:, b, 0:1], rs[:, b:b + 1], ALU.subtract, ALU.mult)
                s.did(last)
                s.wait()
                s.did(dve.tensor_tensor(xc[:], xc[:], lg[:].unsqueeze(1).broadcast_to([CTX, B, KD]), ALU.mult))
                s.wait()
                s.did(dve.tensor_tensor(xn[:], xc[:], lb[:].unsqueeze(1).broadcast_to([CTX, B, KD]), ALU.add))
                assert s.n == 9
                dve.wait_ge(turned, 1)
                s.did(dve.tensor_copy(xT[:], psT[0:CK, :].rearrange("p (c b k) -> p c b k", c=2, b=B)))
                dve.wait_ge(products, 1)
                s.did(dve.tensor_copy(kn[:], kv[:, :, 0:D]))
                s.wait()
                dve.tensor_tensor(sq[:], kn[:], kn[:], ALU.mult).then_inc(products, 1)
                dve.wait_ge(products, 2)
                s.did(dve.tensor_reduce(ss[:], sq[:].rearrange("p b (h d) -> p (b h) d", h=LH), AX, ALU.add))
                dve.wait_ge(roots, 2)
                s.did(dve.tensor_scalar(nr[:], nr[:], 1e-8, None, ALU.max))
                s.wait()
                s.did(dve.reciprocal(rn[:], nr[:]))
                s.wait()
                s.did(dve.tensor_tensor(sq[:].rearrange("p b (h d) -> p (b h) d", h=LH), kn[:].rearrange("p b (h d) -> p (b h) d", h=LH),
                                        rn[:].unsqueeze(2).broadcast_to([CTX, B * LH, LD]), ALU.mult))
                s.did(dve.tensor_scalar(gam[:, 0:LD], gam[:, 0:LD], float(LD) ** -0.5, None, ALU.mult))
                s.wait()
                s.did(dve.tensor_tensor(kn[:].rearrange("p b (h d) -> p (b h) d", h=LH), sq[:].rearrange("p b (h d) -> p (b h) d", h=LH),
                                        gam[0:CTX, LD:].unsqueeze(1).broadcast_to([CTX, B * LH, LD]), ALU.mult))
                assert s.n == 17
                for b in range(B):
                    last = dve.tensor_copy(Vc[:, b, :, 0:LD], kv[:, b, D:].rearrange("p (h d) -> p h d", h=LH))
                s.did(last)
                s.did(dve.tensor_copy(maskf[:], mask8[:]))
                s.wait()
                s.did(dve.tensor_scalar(maskrow[:], maskf[:], 1.0, -MASKED, ALU.subtract, ALU.mult))
                dve.wait_ge(turned, 2)
                for half in range(2):
                    last = dve.tensor_copy(kTc[:].rearrange("p (c e) b k -> p c e (b k)", e=2)[:, :, half, :],
                                           psT[LD * half:LD * half + LD, :].rearrange("p (c n) -> p c n", c=DC))
                s.did(last)


def latent_project(nc, a, keep, sems):
    X, ident, QT, kT, VL, gam = (keep[k] for k in ("X", "ident", "QT", "kT", "VL", "gam"))
    NB = NT // BLK
    QK = 2 * D
    with ExitStack() as ctx:
        m = Mem(nc, ctx)
        sb = lambda name, shape, dt=F32: m.sb(f"x1p_{name}", shape, dt)
        w = sb("w", [P, DC, 3 * D])
        lg, lb = sb("lg", [P, D]), sb("lb", [P, D])
        st, mv, sd, rs, eps = sb("st", [P, BLK, 6]), sb("mv", [P, BLK, 2]), sb("sd", [P, BLK]), sb("rs", [P, BLK]), sb("eps", [P, 1])
        xc, ln = sb("xc", [P, BLK, D]), sb("ln", [P, BLK, D])
        lT = sb("lT", [P, DC, HALF])
        sq = sb("sq", [P, BLK, QK])
        nrm = sb("nrm", [P, BLK, QK])
        R = BLK * 2 * LH
        qo = [sb(f"qo{k}", [P, DC, HALF]) for k in range(2)]
        ss, nr, rn = sb("ss", [P, R]), sb("nr", [P, R]), sb("rn", [P, R])
        psT = m.ps("x1p_psT", BLK * D)
        psQ = m.ps("x1p_psQ", BLK * QK)
        psV = m.ps("x1p_psV", BLK * D)
        sem = lambda name: sems.sem(f"x1p_{name}")
        loaded, const = sem("loaded"), sem("const")
        l_dve = sem("l_dve")
        l_act = sem("l_act")
        l_pool = sem("l_pool")
        l_pe = sem("l_pe")
        lt_in = sem("lt_in")
        qkv = sem("qkv")
        v_in = sem("v_in")
        sq_in = sem("sq_in")
        n_dve = sem("n_dve")
        n_act = sem("n_act")
        n_pool = sem("n_pool")
        q_pe = sem("q_pe")
        q_in = sem("q_in")
        k_in = sem("k_in")
        q_out = [sem(f"q_out{k}") for k in range(2)]
        passed = sem("passed")
        row = lambda name, n: a[name].rearrange("(o d) -> o d", o=1).broadcast_to([n, a[name].shape[0]])
        with nc.Block() as block:
            @block.sync
            def _(sp):
                for dst, src in ((w[:], a["L1x_w"]), (lg[:], row("L1_xattn_ln_l_g", P)), (lb[:], row("L1_xattn_ln_l_b", P))):
                    sp.dma_start(dst, src).then_inc(loaded, 16)

                def turn(t, live):
                    sp.wait_ge(q_in, t.times(DC, DC))
                    sp.dma_start(QT.rearrange("(c p) n -> p c n", p=P)[:, :, t.span(HALF)], qo[t.slot][:]).then_inc(q_out[t.slot], 16)

                run_turns(sp, turn, NB, 0, 2)
                for k in range(2):
                    sp.wait_ge(q_out[k], 16 * (NB // 2))

            @block.tensor
            def _(pe):
                pe.wait_ge(loaded, 48)

                def turn(t, live):
                    u = t + -1
                    if live[1]:
                        pe.wait_ge(lt_in, u.times(1, 1))
                        pe.wait_ge(v_in, u.times(1))
                        pe.wait_ge(q_in, u.times(DC))
                        pe.wait_ge(k_in, u.times(DC))
                        for k in range(BLK):
                            for c in range(DC):
                                last = pe.matmul(psQ[:, k * QK:(k + 1) * QK], lT[:, c, k * P:(k + 1) * P], w[:, c, 0:QK],
                                                 start=(c == 0), stop=(c == DC - 1))
                        last.then_inc(qkv, 1)
                        for k in range(BLK):
                            for c in range(DC):
                                last = pe.matmul(psV[:, k * D:(k + 1) * D], lT[:, c, k * P:(k + 1) * P], w[:, c, QK:],
                                                 start=(c == 0), stop=(c == DC - 1))
                        last.then_inc(qkv, 1)
                    if live[0]:
                        pe.wait_ge(l_pool, t.times(2, 2))
                        pe.wait_ge(lt_in, t.times(1))
                        for c in range(DC):
                            for k in range(BLK):
                                last = pe.transpose(psT[:, (c * BLK + k) * P:(c * BLK + k + 1) * P], ln[:, k, c * P:(c + 1) * P], ident[:])
                        last.then_inc(l_pe, 1)
                    if live[1]:
                        pe.wait_ge(n_pool, u.times(1, 1))
                        for c in range(2 * DC):
                            for k in range(BLK):
                                last = pe.transpose(psQ[:, (c * BLK + k) * P:(c * BLK + k + 1) * P], nrm[:, k, c * P:(c + 1) * P], ident[:])
                            last.then_inc(q_pe, 1)

                run_turns(pe, turn, NB, 1, 2)

            @block.scalar
            def _(act):
                act.wait_ge(const, 1)

                def turn(t, live):
                    u = t + -1
                    if live[1]:
                        act.wait_ge(qkv, u.times(2, 1))
                        act.wait_ge(n_dve, u.times(4))
                        act.activation(sq[:].rearrange("p k n -> p (k n)"), psQ[:], ACT.Square).then_inc(sq_in, 1)
                    if live[0]:
                        act.wait_ge(l_dve, t.times(4, 2))
                        act.activation(sd[:], mv[:, :, 1], ACT.Sqrt, bias=eps[:]).then_inc(l_act, 1)
                    if live[1]:
                        act.wait_ge(n_dve, u.times(4, 1))
                        act.activation(nr[:], ss[:], ACT.Sqrt, scale=1.0 / LD).then_inc(n_act, 1)
                        act.wait_ge(qkv, u.times(2, 2))
                        act.activation(VL[:, u.span(BLK), :, 0:LD], psV[:].rearrange("p (k h d) -> p k h d", k=BLK, h=LH),
                                       ACT.Copy).then_inc(v_in, 1)
                    if live[0]:
                        act.wait_ge(l_pe, t.times(1, 1))
                        act.activation(lT[:].rearrange("p c n -> p (c n)"), psT[:], ACT.Copy).then_inc(lt_in, 1)
                    if live[1]:
                        if u.base >= 2 or u.n is not None:
                            act.wait_ge(q_out[u.slot], u.over(16))
                        for c in range(DC):
                            act.wait_ge(q_pe, u.times(4, c + 1))
                            act.activation(qo[u.slot][:, c, :], psQ[:, c * HALF:(c + 1) * HALF], ACT.Copy).then_inc(q_in, 1)

                run_turns(act, turn, NB, 1, 2)

            @block.gpsimd
            def _(pool):
                pool.wait_ge(loaded, 48)

                def turn(t, live):
                    u = t + -1
                    if live[0]:
                        pool.wait_ge(l_dve, t.times(4, 4))
                        pool.wait_ge(l_pe, t.times(1))
                        pool.tensor_tensor(ln[:], xc[:], lg[:].unsqueeze(1).broadcast_to([P, BLK, D]), ALU.mult).then_inc(l_pool, 1)
                        pool.wait_ge(l_pool, t.times(2, 1))
                        pool.tensor_tensor(ln[:], ln[:], lb[:].unsqueeze(1).broadcast_to([P, BLK, D]), ALU.add).then_inc(l_pool, 1)
                    if live[1]:
                        pool.wait_ge(n_dve, u.times(4, 4))
                        view = nrm[:].rearrange("p k (q h d) -> p (k q) h d", q=2, h=LH)
                        for q in range(2):
                            for k in range(BLK):
                                v = nrm[:, k, q * D:(q + 1) * D].rearrange("p (h d) -> p h d", h=LH)
                                last = pool.tensor_tensor(v, v, gam[:, q * LD:(q + 1) * LD].unsqueeze(1).broadcast_to([P, LH, LD]), ALU.mult)
                        last.then_inc(n_pool, 1)

                run_turns(pool, turn, NB, 1, 2)

            @block.vector
            def _(dve):
                dve.memset(eps[:], LN_EPS).then_inc(const, 1)
                dve.memset(VL[:, :, :, LD:VW], 1.0).then_inc(const, 1)

                def turn(t, live):
                    u = t + -1
                    if live[0]:
                        xk = lambda k: X[:, bass.ds(t.times(BLK, k), 1) if t.n is not None else slice(t.times(BLK, k), t.times(BLK, k) + 1), :]\
                            .rearrange("p o d -> p (o d)")
                        for k in range(BLK):
                            last = dve.bn_stats(st[:, k, :], xk(k))
                        last.then_inc(l_dve, 1)
                        dve.wait_ge(l_dve, t.times(4, 1))
                        dve.sem_inc(passed, 1)
                        for k in range(BLK):
                            last = dve.bn_aggr(mv[:, k, :], st[:, k, :])
                        last.then_inc(l_dve, 1)
                    if live[1]:
                        dve.wait_ge(sq_in, u.times(1, 1))
                        dve.tensor_reduce(ss[:], sq[:].rearrange("p k (h d) -> p (k h) d", h=2 * LH), AX, ALU.add).then_inc(n_dve, 1)
                    if live[0]:
                        dve.wait_ge(l_act, t.times(1, 1))
                        dve.reciprocal(rs[:], sd[:]).then_inc(l_dve, 1)
                        dve.wait_ge(l_dve, t.times(4, 3))
                        dve.wait_ge(l_pool, t.times(2))
                        for k in range(BLK):
                            last = dve.tensor_scalar(xc[:, k, :], xk(k), mv[:, k, 0:1], rs[:, k:k + 1], ALU.subtract, ALU.mult)
                        last.then_inc(l_dve, 1)
                    if live[1]:
                        dve.wait_ge(n_act, u.times(1, 1))
                        dve.tensor_scalar(nr[:], nr[:], 1e-8, None, ALU.max).then_inc(n_dve, 1)
                        dve.wait_ge(n_dve, u.times(4, 2))
                        dve.reciprocal(rn[:], nr[:]).then_inc(n_dve, 1)
                        dve.wait_ge(n_dve, u.times(4, 3))
                        dve.wait_ge(q_pe, u.times(4))
                        dve.tensor_tensor(nrm[:].rearrange("p k (h d) -> p (k h) d", h=2 * LH),
                                          psQ[:].rearrange("p (k h d) -> p (k h) d", k=BLK, h=2 * LH),
                                          rn[:].unsqueeze(2).broadcast_to([P, R, LD]), ALU.mult).then_inc(n_dve, 1)
                        for c in range(DC):
                            dve.wait_ge(q_pe, u.times(4, DC + c + 1))
                            for half in range(2):
                                last = dve.tensor_copy(kT[:, 2 * c + half, u.span(HALF)],
                                                       psQ[LD * half:LD * half + LD, (DC + c) * HALF:(DC + c + 1) * HALF])
                            last.then_inc(k_in, 1)

                run_turns(dve, turn, NB, 1, 2)


def latent_attend(nc, a, keep, sems):
    ident, QT, kT, VL, kTc, Vc, ones, maskrow, AO = (keep[k] for k in ("ident", "QT", "kT", "VL", "kTc", "Vc", "ones1", "maskrow", "AO"))
    UNITS = NT * LH
    STEP = 2 * LH
    PER_BATCH = TB * LH // STEP
    NP = TB + 1
    with ExitStack() as ctx:
        m = Mem(nc, ctx)
        two = lambda name, shape, dt=F32: [m.sb(f"x1_{name}{k}", shape, dt) for k in range(2)]
        qs = two("qs", [LD, LH, P])
        E, Ec = two("E", [P, S]), two("Ec", [P, CTX])
        ET = two("ET", [P, NP, P])
        mx = two("mx", [P, 2])
        nm = two("nm", [P, 1])
        rc = two("rc", [P, 1])
        psS = [m.ps(f"x1_psS{k}", S) for k in range(2)]
        psC = m.ps("x1_psC", HALF)
        psE = m.ps("x1_psE", S)
        psO = m.ps("x1_psO", HALF)
        sem = lambda name: sems.sem(f"x1_{name}")
        qs_in = [sem(f"qs_in{k}") for k in range(2)]
        s_pe = sem("s_pe")
        m_dve = sem("m_dve")
        e_act = sem("e_act")
        t_pe = sem("t_pe")
        t_dve = sem("t_dve")
        t_act = sem("t_act")
        c_pe = sem("c_pe")
        c_act = sem("c_act")
        o_pe = sem("o_pe")
        o_dve = sem("o_dve")
        passed = sem("passed")

        def batch(u):
            whole = u.base // STEP
            return whole // PER_BATCH if u.n is None else (u.n + whole) // PER_BATCH

        def at(x, width):
            return slice(x, x + width) if isinstance(x, int) else bass.ds(x, width)

        with nc.Block() as block:
            @block.sync
            def _(sp):
                def turn(t, live):
                    if t.base >= 2 or t.n is not None:
                        sp.wait_ge(s_pe, (t + -1).times(LH))
                    sp.dma_start(qs[t.slot][:], QT.rearrange("(h d) n -> d h n", d=LD)[:, :, t.span(P)]).then_inc(qs_in[t.slot], 16)

                run_turns(sp, turn, NT, 0, 2, 2)

            @block.tensor
            def _(pe):
                def scores(u):
                    h = u.slot % LH
                    tile, k = u.slot // LH, u.slot % 2
                    if h == 0:
                        pe.wait_ge(qs_in[tile], u.over(16, 16))
                    if u.base >= 2 or u.n is not None:
                        pe.wait_ge(e_act, (u + -1).times(2))
                    b = batch(u)
                    q = qs[tile][:, h, :]
                    cc = psC[:, k * CTX:(k + 1) * CTX]
                    pe.sem_inc(passed, 1)
                    for j in range(2):
                        pe.matmul(psS[k][:, j * HALF:(j + 1) * HALF], q, kT[:, h, at(b * S + j * HALF, HALF)],
                                  start=True, stop=True)
                    if u.base >= 1 or u.n is not None:
                        pe.wait_ge(e_act, (u + -1).times(2, 1))
                    if u.base >= 2 or u.n is not None:
                        pe.wait_ge(c_act, (u + -1).times(1))
                    pe.sem_inc(passed, 1)
                    pe.matmul(cc, ones[:], maskrow[:, at(b * CTX, CTX)], start=True, stop=False)
                    pe.matmul(cc, q, kTc[:, h, at(b, 1), :].rearrange("p o k -> p (o k)"), start=False,
                              stop=True).then_inc(s_pe, 1)

                def transposes(u):
                    k = u.slot % 2
                    pe.wait_ge(e_act, u.times(2, 2))
                    pe.wait_ge(t_dve, u.times(1))
                    for j in range(4):
                        last = pe.transpose(psE[:, j * P:(j + 1) * P], E[k][:, j * P:(j + 1) * P], ident[:])
                    last.then_inc(t_pe, 1)
                    pe.wait_ge(t_act, u.times(1))
                    for j in range(4, 8):
                        last = pe.transpose(psE[:, j * P:(j + 1) * P], E[k][:, j * P:(j + 1) * P], ident[:])
                    last.then_inc(t_pe, 1)

                def context_transposes(u, after):
                    pe.wait_ge(e_act, (u + after).times(2, 1 if after else 2))
                    pe.sem_inc(passed, 1)
                    pe.transpose(psC[0:CTX, P:2 * P], Ec[u.slot % 2][:], ident[:]).then_inc(c_pe, 1)

                def outputs(u):
                    k, h = u.slot % 2, u.slot % LH
                    b = batch(u)
                    pe.wait_ge(t_dve, u.times(1, 1))
                    pe.wait_ge(t_act, u.times(1, 1))
                    pe.wait_ge(c_act, u.times(1, 1))
                    pe.wait_ge(o_dve, u.times(2))
                    out = psO[:, h * VW:(h + 1) * VW]
                    for j in range(TB):
                        pe.matmul(out, ET[k][:, j, :], VL[:, at(b * TB + j, 1), h, :].rearrange("p o d -> p (o d)"),
                                  start=(j == 0), stop=False)
                    pe.matmul(out, ET[k][0:CTX, TB, :], Vc[:, at(b, 1), h, :].rearrange("p o d -> p (o d)"),
                              start=False, stop=True).then_inc(o_pe, 1)

                def turn(t, live):
                    if live[0]:
                        scores(t)
                    if live[1]:
                        transposes(t + -1)
                    if live[2]:
                        outputs(t + -2)
                    if live[1]:
                        context_transposes(t + -1, 1 if live[0] else 0)

                run_turns(pe, turn, UNITS, 2, STEP)

            @block.scalar
            def _(act):
                def turn(t, live):
                    if live[1]:
                        u = t + -1
                        k = u.slot % 2
                        act.wait_ge(t_pe, u.times(2, 2))
                        if u.base >= 2 or u.n is not None:
                            act.wait_ge(o_pe, (u + -1).times(1))
                        act.activation(ET[k][:, 4:8, :].rearrange("p j n -> p (j n)"), psE[:, HALF:], ACT.Copy).then_inc(t_act, 1)
                    if live[0]:
                        if t.base >= 2 or t.n is not None:
                            act.wait_ge(t_pe, (t + -1).times(2))
                            act.wait_ge(c_pe, (t + -1).times(1))
                        k = t.slot % 2
                        act.wait_ge(m_dve, t.times(2, 2))
                        act.activation(Ec[k][:], psC[:, k * CTX:(k + 1) * CTX], ACT.Exp, bias=nm[k][:]).then_inc(e_act, 1)
                        act.activation(E[k][:], psS[k][:], ACT.Exp, bias=nm[k][:]).then_inc(e_act, 1)
                    if live[1]:
                        u = t + -1
                        act.wait_ge(c_pe, u.times(1, 1))
                        act.activation(ET[u.slot % 2][0:CTX, TB, :], psC[0:CTX, P:2 * P], ACT.Copy).then_inc(c_act, 1)

                run_turns(act, turn, UNITS, 1, STEP)

            @block.vector
            def _(dve):
                def turn(t, live):
                    if live[1]:
                        u = t + -1
                        dve.wait_ge(t_pe, u.times(2, 1))
                        if u.base >= 2 or u.n is not None:
                            dve.wait_ge(o_pe, (u + -1).times(1))
                        dve.tensor_copy(ET[u.slot % 2][:, 0:4, :].rearrange("p j n -> p (j n)"), psE[:, 0:HALF]).then_inc(t_dve, 1)
                    if live[0]:
                        k = t.slot % 2
                        dve.wait_ge(s_pe, t.times(1, 1))
                        dve.tensor_reduce(mx[k][:, 0:1], psS[k][:], AX, ALU.max)
                        dve.tensor_reduce(mx[k][:, 1:2], psC[:, k * CTX:(k + 1) * CTX], AX, ALU.max).then_inc(m_dve, 1)
                        dve.wait_ge(m_dve, t.times(2, 1))
                        if t.base >= 2 or t.n is not None:
                            dve.wait_ge(e_act, (t + -1).times(2))
                        dve.tensor_scalar(nm[k][:], mx[k][:, 0:1], mx[k][:, 1:2], -1.0, ALU.max, ALU.mult).then_inc(m_dve, 1)
                    if live[2]:
                        u = t + -2
                        h, k = u.slot % LH, u.slot % 2
                        dve.wait_ge(o_pe, u.times(1, 1))
                        dve.reciprocal(rc[k][:], psO[:, h * VW + LD:(h + 1) * VW]).then_inc(o_dve, 1)
                        dve.wait_ge(o_dve, u.times(2, 1))
                        dve.tensor_scalar(AO[:, at(tile_of(u), 1), h * LD:(h + 1) * LD].rearrange("p o d -> p (o d)"),
                                          psO[:, h * VW:h * VW + LD], rc[k][:], None, ALU.mult).then_inc(o_dve, 1)

                def tile_of(u):
                    return u.base // LH if u.n is None else u.n * (STEP // LH) + u.base // LH

                run_turns(dve, turn, UNITS, 2, STEP)


HC = 4
TAKEN = S // 2


def choose(nc, a, keep, sems):
    X, ident, HT, SEL, SELB = (keep[k] for k in ("X", "ident", "HT", "SEL", "SELB"))
    NB = NT // BLK
    RE = B * EX
    BITS = 31
    with ExitStack() as ctx:
        m = Mem(nc, ctx)
        sb = lambda name, shape, dt=F32: m.sb(f"f1_{name}", shape, dt)
        xs = [sb(f"xs{k}", [P, BLK, D]) for k in range(2)]
        xt = [sb(f"xt{k}", [P, DC, HALF]) for k in range(2)]
        XT = sb("XT", [P, DC, B * S])
        w1, b1, wg, bg = sb("w1", [P, DC, HC * P]), sb("b1", [P, HC]), sb("wg", [P, DC, EX]), sb("bg", [P, EX])
        iota = sb("iota", [P, EX])
        G = [P, NT, EX]
        logit, less, ex, gate, hot1, hot2, hot, masked = (sb(n, G) for n in ("logit", "less", "ex", "gate", "hot1", "hot2", "hot", "masked"))
        top, ix = sb("top", [P, NT, 8]), sb("ix", [P, NT, 8], U32)
        ixf, mx, sm, rc = sb("ixf", [P, NT, 2]), sb("mx", [P, NT]), sb("sm", [P, NT]), sb("rc", [P, NT])
        den = [sb(f"den{k}", [P, TB, EX]) for k in range(4)]
        rden = sb("rden", [P, TB, EX])
        route, routes = sb("route", [P, TB, B, EX]), sb("routes", [P, TB, B, EX])
        v, gt, eq, rank, tie = (sb(n, [RE, S]) for n in ("v", "gt", "eq", "rank", "tie"))
        sel, selb = sb("sel", [RE, S]), sb("selb", [RE, S], BF16)
        bits_i, bits_f = sb("bits_i", [RE, BITS], I32), sb("bits_f", [RE, BITS])
        T, cand, gain = sb("T", [RE, 1], I32), sb("cand", [RE, 1], I32), sb("gain", [RE, 1], I32)
        cnt, above, room = sb("cnt", [RE, 1]), sb("above", [RE, 1]), sb("room", [RE, 1])
        psT = m.ps("f1_psT", BLK * D)
        psG = m.ps("f1_psG", HALF)
        psR = m.ps("f1_psR", S)
        psH = [m.ps(f"f1_psH{k}", HALF) for k in range(3)]
        sem = lambda name: sems.sem(f"f1_{name}")
        loaded = sem("loaded")
        xs_in = [sem(f"xs_in{k}") for k in range(2)]
        x_pe = sem("x_pe")
        x_act = sem("x_act")
        kept = [sem(f"kept{k}") for k in range(2)]
        g_pe = sem("g_pe")
        done = sem("done")
        exps = sem("exps")
        r_pe = sem("r_pe")
        h_pe = sem("h_pe")
        h_act = sem("h_act")
        found = sem("found")
        stored = sem("chosen")
        passed = sem("passed")
        NLESS, NROUTE = 3, 21
        with nc.Block() as block:
            @block.sync
            def _(sp):
                for dst, src in ((w1[:], a["L1f_w1"]), (b1[:], a["L1f_b1"]), (wg[:], a["L1f_wg"]),
                                 (bg[:], a["L1_ffn_w_gate_b"].rearrange("(o d) -> o d", o=1).broadcast_to([P, EX])),
                                 (iota[:], a["iota8"].broadcast_to([P, EX])),
                                 (bits_i[:], a["bits_i"].broadcast_to([RE, BITS])), (bits_f[:], a["bits_f"].broadcast_to([RE, BITS]))):
                    sp.dma_start(dst, src).then_inc(loaded, 16)

                def turn(t, live):
                    u = t + -1
                    if live[0]:
                        if t.base >= 2 or t.n is not None:
                            sp.wait_ge(x_pe, (t + -1).times(1))
                        sp.dma_start(xs[t.slot][:], X[:, t.span(BLK), :]).then_inc(xs_in[t.slot], 16)
                    if live[1]:
                        sp.wait_ge(x_act, u.times(1, 1))
                        sp.dma_start(XT[:, :, u.span(HALF)], xt[u.slot][:]).then_inc(kept[u.slot], 16)

                run_turns(sp, turn, NB, 1, 2)
                sp.wait_ge(done, NROUTE + 7)
                sp.dma_start(SEL, sel[:]).then_inc(stored, 16)
                sp.dma_start(SELB, selb[:]).then_inc(stored, 16)
                sp.wait_ge(stored, 32)

            @block.tensor
            def _(pe):
                pe.wait_ge(loaded, 112)

                def turn(t, live):
                    u = t + -1
                    if live[0]:
                        pe.wait_ge(xs_in[t.slot], t.over(16, 16))
                        pe.wait_ge(x_act, t.times(1))
                        for c in range(DC):
                            for k in range(BLK):
                                last = pe.transpose(psT[:, (c * BLK + k) * P:(c * BLK + k + 1) * P], xs[t.slot][:, k, c * P:(c + 1) * P], ident[:])
                        last.then_inc(x_pe, 1)
                    if live[1]:
                        pe.wait_ge(x_act, u.times(1, 1))
                        for k in range(BLK):
                            for c in range(DC):
                                col = slice((u.base * BLK + k) * EX, (u.base * BLK + k + 1) * EX) if u.n is None \
                                    else bass.ds(u.times(BLK * EX, k * EX), EX)
                                last = pe.matmul(psG[:, col], xt[u.slot][:, c, k * P:(k + 1) * P], wg[:, c, :],
                                                 start=(c == 0), stop=(c == DC - 1))
                        last.then_inc(g_pe, 1)

                run_turns(pe, turn, NB, 1, 2)
                for k in range(2):
                    pe.wait_ge(kept[k], 16 * (NB // 2))

                def hidden_block(i):
                    for h in range(HC):
                        n = i * HC + h
                        pe.wait_ge(h_act, n + 1)
                        for c in range(DC):
                            last = pe.matmul(psH[n % 3][:], w1[:, c, h * P:(h + 1) * P], XT[:, c, i * HALF:(i + 1) * HALF],
                                             start=(c == 0), stop=(c == DC - 1))
                        last.then_inc(h_pe, 1)

                hidden_block(0)
                hidden_block(1)
                pe.wait_ge(done, NROUTE)
                for t in range(TB):
                    last = pe.transpose(psR[0:RE, t * P:(t + 1) * P], routes[:, t, :, :].rearrange("p b e -> p (b e)"), ident[:])
                last.then_inc(r_pe, 1)
                for i in range(2, NB):
                    hidden_block(i)

            @block.scalar
            def _(act):
                act.sem_inc(h_act, 3)
                act.wait_ge(loaded, 112)

                def turn(t, live):
                    act.wait_ge(x_pe, t.times(1, 1))
                    if t.base >= 2 or t.n is not None:
                        act.wait_ge(kept[t.slot], t.over(16))
                        act.wait_ge(g_pe, (t + -1).times(1))
                    act.activation(xt[t.slot][:].rearrange("p c n -> p (c n)"), psT[:], ACT.Copy).then_inc(x_act, 1)

                run_turns(act, turn, NB, 0, 2, 2)
                act.wait_ge(done, NLESS)
                act.activation(ex[:], less[:], ACT.Exp).then_inc(exps, 1)
                for n in range(NB * HC):
                    act.wait_ge(h_pe, n + 1)
                    act.activation(HT[:, n % HC, n // HC * HALF:(n // HC + 1) * HALF], psH[n % 3][:], ACT.Gelu,
                                   bias=b1[:, n % HC:n % HC + 1]).then_inc(h_act, 1)

            @block.vector
            def _(dve):
                s = Chain(dve, done)
                dve.wait_ge(loaded, 112)
                dve.wait_ge(g_pe, NB)
                s.did(dve.tensor_tensor(logit[:], psG[:, 0:NT * EX].rearrange("p (t e) -> p t e", e=EX),
                                        bg[:].unsqueeze(1).broadcast_to(G), ALU.add))
                s.wait()
                s.did(dve.tensor_reduce(mx[:], logit[:], AX, ALU.max))
                s.wait()
                s.did(dve.tensor_tensor(less[:], logit[:], mx[:].unsqueeze(2).broadcast_to(G), ALU.subtract))
                assert s.n == NLESS
                dve.wait_ge(exps, 1)
                s.did(dve.tensor_reduce(sm[:], ex[:], AX, ALU.add))
                s.wait()
                s.did(dve.reciprocal(rc[:], sm[:]))
                s.wait()
                s.did(dve.tensor_tensor(gate[:], ex[:], rc[:].unsqueeze(2).broadcast_to(G), ALU.mult))
                s.wait()
                for t in range(NT):
                    last = dve.max(top[:, t, :], gate[:, t, :])
                s.did(last)
                s.wait()
                for t in range(NT):
                    last = dve.max_index(ix[:, t, :], top[:, t, :], gate[:, t, :])
                s.did(last)
                s.wait()
                s.did(dve.tensor_copy(ixf[:], ix[:, :, 0:2]))
                s.wait()
                for n, hot_n in ((0, hot1), (1, hot2)):
                    s.did(dve.tensor_tensor(hot_n[:], iota[:].unsqueeze(1).broadcast_to(G), ixf[:, :, n:n + 1].broadcast_to(G), ALU.is_equal))
                s.wait()
                s.did(dve.tensor_tensor(hot[:], hot1[:], hot2[:], ALU.add))
                s.wait()
                s.did(dve.tensor_tensor(masked[:], gate[:], hot[:], ALU.mult))
                s.wait()
                mb = masked[:].rearrange("p (b t) e -> p b t e", b=B)
                s.did(dve.tensor_tensor(den[0][:], mb[:, 0], mb[:, 1], ALU.add))
                for n in (2, 3):
                    s.wait()
                    s.did(dve.tensor_tensor(den[n - 1][:], den[n - 2][:], mb[:, n], ALU.add))
                s.wait()
                s.did(dve.tensor_scalar(den[3][:], den[2][:], 1e-6, None, ALU.add))
                s.wait()
                s.did(dve.reciprocal(rden[:], den[3][:]))
                s.wait()
                for b in range(B):
                    last = dve.tensor_tensor(route[:, :, b, :], mb[:, b], rden[:], ALU.mult)
                s.did(last)
                s.wait()
                s.did(dve.tensor_scalar(routes[:], route[:], float(B), None, ALU.mult))
                s.did(dve.memset(T[:], 0))
                assert s.n == NROUTE, s.n
                dve.wait_ge(r_pe, 1)
                s.did(dve.tensor_copy(v[:], psR[0:RE, :]))
                s.wait()
                with dve.Fori(0, BITS) as i:
                    dve.wait_ge(found, i * 4)
                    dve.tensor_tensor(cand[:], T[:], bits_i[:, bass.ds(i, 1)], ALU.bitwise_or).then_inc(found, 1)
                    dve.wait_ge(found, i * 4 + 1)
                    dve.tensor_scalar(gt[:], v[:], cand[:].bitcast(F32), None, ALU.is_ge, ALU.add, accum_out=cnt[:]).then_inc(found, 1)
                    dve.wait_ge(found, i * 4 + 2)
                    dve.scalar_tensor_tensor(out=gain[:], in0=cnt[:], scalar=float(TAKEN), in1=bits_f[:, bass.ds(i, 1)],
                                             op0=ALU.is_ge, op1=ALU.mult).then_inc(found, 1)
                    dve.wait_ge(found, i * 4 + 3)
                    dve.tensor_tensor(T[:], T[:], gain[:], ALU.bitwise_or).then_inc(found, 1)
                dve.wait_ge(found, BITS * 4)
                T_f = T[:].bitcast(F32)
                s.did(dve.tensor_scalar(gt[:], v[:], T_f, None, ALU.is_gt, ALU.add, accum_out=above[:]))
                s.did(dve.tensor_scalar(eq[:], v[:], T_f, None, ALU.is_equal))
                s.wait()
                s.did(dve.tensor_scalar(room[:], above[:], -1.0, float(TAKEN), ALU.mult, ALU.add))
                s.did(dve.tensor_tensor_scan(rank[:], eq[:], eq[:], 0.0, ALU.add, ALU.bypass))
                s.wait()
                s.did(dve.scalar_tensor_tensor(out=tie[:], in0=rank[:], scalar=room[:], in1=eq[:], op0=ALU.is_le, op1=ALU.mult))
                s.wait()
                dve.tensor_tensor(selb[:], tie[:], gt[:], ALU.add)
                s.did(dve.tensor_tensor(sel[:], tie[:], gt[:], ALU.add))
                assert s.n == NROUTE + 7, s.n


def take(nc, a, keep, sems):
    X, HT, SEL, SELB = (keep[k] for k in ("X", "HT", "SEL", "SELB"))
    NB = NT // BLK
    with ExitStack() as ctx:
        m = Mem(nc, ctx)
        sb = lambda name, shape, dt=F32: m.sb(f"f1t_{name}", shape, dt)
        w2, b2 = sb("w2", [P, HC, D]), sb("b2", [EX, D])
        sw = [sb(f"sw{k}", [P, HC, HALF], BF16) for k in range(2)]
        sk = [sb(f"sk{k}", [EX, HALF]) for k in range(2)]
        hm = [sb(f"hm{k}", [P, HC, HALF]) for k in range(2)]
        y = sb("y", [P, BLK, D])
        st, mv, sd, rs, eps = sb("st", [P, BLK, 6]), sb("mv", [P, BLK, 2]), sb("sd", [P, BLK]), sb("rs", [P, BLK]), sb("eps", [P, 1])
        psY = [m.ps(f"f1t_psY{k}", BLK * D) for k in range(2)]
        sem = lambda name: sems.sem(f"f1t_{name}")
        loaded, const = sem("loaded"), sem("const")
        s_in = [sem(f"s_in{k}") for k in range(2)]
        h_dve = sem("h_dve")
        y_pe = sem("y_pe")
        n_dve = sem("n_dve")
        n_act = sem("n_act")
        passed = sem("passed")
        with nc.Block() as block:
            @block.sync
            def _(sp):
                for dst, src in ((w2[:], a["L1f_w2"]), (b2[:], a["L1_ffn_b2"])):
                    sp.dma_start(dst, src).then_inc(loaded, 16)

                def turn(t, live):
                    if t.base >= 2 or t.n is not None:
                        sp.wait_ge(h_dve, (t + -1).times(1))
                        sp.wait_ge(y_pe, (t + -1).times(1))
                    n = slice(t.slot * HALF, (t.slot + 1) * HALF)
                    b = t.over(1) if t.n is None else bass.ds(t.over(1), 1)
                    b = slice(b, b + 1) if t.n is None else b
                    for e in range(2):
                        src = SELB.rearrange("(b c e) n -> e b c n", b=B, e=2)[e][b, :, n]
                        sp.dma_start(sw[t.slot][64 * e:64 * e + 64, :, :], src.broadcast_to([64, HC, HALF])).then_inc(s_in[t.slot], 16)
                    sp.dma_start(sk[t.slot][:], SEL.rearrange("(b e) n -> b e n", b=B)[b, :, n].rearrange("o e n -> (o e) n"))\
                        .then_inc(s_in[t.slot], 16)

                run_turns(sp, turn, NB, 0, 2, 2)

            @block.tensor
            def _(pe):
                pe.wait_ge(loaded, 32)

                def turn(t, live):
                    pe.wait_ge(h_dve, t.times(1, 1))
                    pe.wait_ge(s_in[t.slot], t.over(48, 48))
                    if t.base >= 2 or t.n is not None:
                        pe.wait_ge(n_dve, (t + -2).times(5, 1))
                    for k in range(BLK):
                        out = psY[t.slot][:, k * D:(k + 1) * D]
                        pe.matmul(out, sk[t.slot][:, k * P:(k + 1) * P], b2[:], start=True, stop=False)
                        for c in range(HC):
                            last = pe.matmul(out, hm[t.slot][:, c, k * P:(k + 1) * P], w2[:, c, :], start=False, stop=(c == HC - 1))
                    last.then_inc(y_pe, 1)

                run_turns(pe, turn, NB, 0, 2, 2)

            @block.scalar
            def _(act):
                act.wait_ge(const, 1)
                with act.Fori(0, NB) as i:
                    act.wait_ge(n_dve, i * 5 + 3)
                    act.activation(sd[:], mv[:, :, 1], ACT.Sqrt, bias=eps[:]).then_inc(n_act, 1)

            @block.vector
            def _(dve):
                dve.memset(eps[:], LN_EPS).then_inc(const, 1)

                def turn(t, live):
                    u = t + -1
                    if live[0]:
                        dve.wait_ge(s_in[t.slot], t.over(48, 48))
                        if t.base >= 2 or t.n is not None:
                            dve.wait_ge(y_pe, (t + -1).times(1))
                        dve.tensor_tensor(hm[t.slot][:], HT[:, :, t.span(HALF)], sw[t.slot][:], ALU.mult).then_inc(h_dve, 1)
                    if live[1]:
                        dve.wait_ge(y_pe, u.times(1, 1))
                        dve.wait_ge(n_dve, u.times(5))
                        dve.tensor_tensor(y[:], psY[u.slot][:].rearrange("p (k d) -> p k d", k=BLK), X[:, u.span(BLK), :],
                                          ALU.add).then_inc(n_dve, 1)
                        dve.wait_ge(n_dve, u.times(5, 1))
                        for k in range(BLK):
                            last = dve.bn_stats(st[:, k, :], y[:, k, :])
                        last.then_inc(n_dve, 1)
                        dve.wait_ge(n_dve, u.times(5, 2))
                        dve.sem_inc(passed, 1)
                        for k in range(BLK):
                            last = dve.bn_aggr(mv[:, k, :], st[:, k, :])
                        last.then_inc(n_dve, 1)
                        dve.wait_ge(n_act, u.times(1, 1))
                        dve.reciprocal(rs[:], sd[:]).then_inc(n_dve, 1)
                        dve.wait_ge(n_dve, u.times(5, 4))
                        for k in range(BLK):
                            out = X[:, bass.ds(u.times(BLK, k), 1) if u.n is not None else slice(u.times(BLK, k), u.times(BLK, k) + 1), :]
                            last = dve.tensor_scalar(out.rearrange("p o d -> p (o d)"), y[:, k, :], mv[:, k, 0:1], rs[:, k:k + 1],
                                                     ALU.subtract, ALU.mult)
                        last.then_inc(n_dve, 1)

                run_turns(dve, turn, NB, 1, 2, 2)


def store(nc, a, keep, sems):
    out = sems.sem("stored")
    with nc.Block() as block:
        @block.sync
        def _(sp):
            sp.dma_start(a["y"].rearrange("(t p) d -> p t d", p=P), keep["X"][:]).then_inc(out, 16)
            sp.wait_ge(out, 16)


def attention(nc, a, keep, sems, layer, dh, groups):
    with nc.cleanup_on_exit(), ExitStack() as own:
        w = 4 * DV * 16 // groups
        keep["AO"] = Mem(nc, own).sb(f"L{layer}_AO", [P, groups, TB, w])
        with ExitStack() as values:
            keep["VA"] = Mem(nc, values).sb(f"L{layer}_VA", [P, groups, TB, w])
            project(nc, a, keep, sems, f"L{layer}", dh // 2, groups)
            attend(nc, a, keep, sems, f"L{layer}", dh, groups, layer == 0)
        merge(nc, a, keep, sems, f"L{layer}", groups, layer == 1)


def cross_attention(nc, a, keep, sems):
    with nc.cleanup_on_exit(), ExitStack() as own:
        mem = Mem(nc, own)
        keep["KT"] = mem.sb("L0x_KT", [P, DC, B, 64])
        keep["VBD"] = mem.sb("L0x_VBD", [P, B, H // 2, 2 * (DV + 1)])
        for name in ("bq", "bo", "lg", "lb"):
            keep[name] = mem.sb(f"L0x_{name}", [P, D])
        keep["heads8"] = mem.sb("L0x_heads8", [P, 8])
        cross_setup(nc, a, keep, sems)
        cross(nc, a, keep, sems)


def latent_attention(nc, a, keep, sems):
    with nc.cleanup_on_exit(), ExitStack() as own:
        mem = Mem(nc, own)
        keep["QT"] = nc.dram_tensor("queries", (D, B * S), F32).ap()
        keep["ones1"], keep["maskrow"] = mem.sb("L1x_ones", [1, P]), mem.sb("L1x_maskrow", [1, B * CTX])
        keep["kTc"], keep["Vc"] = mem.sb("L1x_kTc", [LD, LH, B, CTX]), mem.sb("L1x_Vc", [CTX, B, LH, VW])
        keep["gam"] = mem.sb("L1x_gam", [P, 2 * LD])
        keep["kT"] = mem.sb("L1x_kT", [LD, LH, B * S])
        keep["VL"] = mem.sb("L1x_VL", [P, NT, LH, VW])
        context_keys(nc, a, keep, sems)
        latent_project(nc, a, keep, sems)
        keep["AO"] = mem.sb("L1x_AO", [P, NT, D])
        latent_attend(nc, a, keep, sems)
        merge(nc, a, keep, sems, "L1x", 1, False, bias="L1_xattn_bo")


def expert_choice(nc, a, keep, sems):
    with nc.cleanup_on_exit(), ExitStack() as own:
        keep["SEL"] = nc.dram_tensor("choice", (B * EX, S), F32).ap()
        keep["SELB"] = nc.dram_tensor("choice_bf16", (B * EX, S), BF16).ap()
        keep["HT"] = Mem(nc, own).sb("L1f_HT", [P, HC, B * S])
        choose(nc, a, keep, sems)
        take(nc, a, keep, sems)


def decoder(nc, a, stages=None):
    with ExitStack() as ctx:
        sems = Mem(nc, ctx)
        keep = {"X": sems.sb("X", [P, NT, D]), "ident": sems.sb("ident", [P, P]), "identb": sems.sb("identb", [P, P], BF16)}
        keep["PT"] = [nc.dram_tensor(f"parts_{n}", (3, B * D, S), BF16).ap() for n in "qk"]
        load_start(nc, a, keep, sems)
        for name, sublayer, args in (("A0", attention, (0, 16, 16)), ("X0", cross_attention, ()), ("M0", experts, ()),
                                     ("A1", attention, (1, 8, 32)), ("X1", latent_attention, ()), ("F1", expert_choice, ())):
            if stages is None or name in stages:
                sublayer(nc, a, keep, sems, *args)
        store(nc, a, keep, sems)


def layouts(x):
    o = {k: np.ascontiguousarray(v) for k, v in x.items()}
    f = {}

    def chunked(wt):
        return np.ascontiguousarray(wt.reshape(-1, P, wt.shape[1]).transpose(1, 0, 2))

    f["x"] = o["x"].reshape(B * S, D)
    f["ident"] = np.eye(P, dtype=np.float32)
    q, k = np.arange(P)[:, None], np.arange(P)[None, :]
    upper = np.where(k > q, np.float32(MASKED), np.float32(0))
    f["causal"] = np.ascontiguousarray(np.stack([upper, upper.T], 1)).astype(np.float32)
    t = np.arange(S, dtype=np.float32)
    for layer, ne in ((0, 8), (1, 4)):
        ns = 64 // ne
        c, h, s, e = np.meshgrid(np.arange(DC), np.arange(2), np.arange(ns), np.arange(ne), indexing="ij")
        inner = h * ne + e if layer == 0 else 2 * e + h
        order = ((c * ns + s) * 2 * ne + inner).reshape(-1)
        wq, wk = (o[f"L{layer}_attn_W{n}"][order] for n in "qk")
        f[f"L{layer}_wqk"] = chunked(np.concatenate([wq, wk], 0).T)
        f[f"L{layer}_wv"] = chunked(o[f"L{layer}_attn_Wv"].T)
        f[f"L{layer}_wo"] = chunked(o[f"L{layer}_attn_Wo"].T)
        if layer == 0:
            speed = np.float32(1) / np.power(np.float32(10000), np.arange(0, 16, 2, dtype=np.float32) / np.float32(16))
        else:
            speed = np.float32(1) / np.power(np.float32(10000), np.linspace(0, 1, 4, dtype=np.float32))
        angle = (speed.astype(np.float32)[:, None] * t[None, :]).astype(np.float32)
        f[f"L{layer}_cos"] = np.ascontiguousarray(np.tile(np.cos(angle), (P // ne, 1))).astype(np.float32)
        sin = np.tile(np.sin(angle), (64 // ne, 1)).astype(np.float32)
        f[f"L{layer}_sin"] = np.ascontiguousarray(np.concatenate([sin, -sin], 0))
    cT = o["ctx_768"].transpose(2, 0, 1).reshape(2, 96, B, 64)
    f["ctxT2"] = np.ascontiguousarray(np.concatenate([cT, cT], 3).transpose(1, 0, 2, 3))
    wkv = np.concatenate([o["L0_xattn_Wk"], o["L0_xattn_Wv"]], 1)
    f["L0x_wkv"] = np.ascontiguousarray(wkv.reshape(2, 96, 2 * D).transpose(1, 0, 2))
    f["L0x_wq"], f["L0x_wo"] = chunked(o["L0_xattn_Wq"]), chunked(o["L0_xattn_Wo"])
    for n in ("bq", "bk", "bv", "bo", "ln_gamma", "ln_beta"):
        f[f"L0_xattn_{n}"] = o[f"L0_xattn_{n}"]
    f["heads8"] = (np.arange(P)[:, None] // DV == np.arange(8)[None, :]).astype(np.float32)
    f["ctx_tok"] = np.ascontiguousarray(o["ctx_768"].transpose(1, 0, 2))
    f["mask8"] = o["mask_BxS2_bk0"].reshape(1, B * CTX)
    f["L1x_wkv"] = np.ascontiguousarray(o["L1_xattn_Wkv"].T.reshape(2, CK, 2 * D).transpose(1, 0, 2))
    f["L1x_w"] = chunked(np.concatenate([o["L1_xattn_Wq"], o["L1_xattn_Wlkv"]], 0).T)
    f["L1x_wo"] = chunked(o["L1_xattn_Wo"].T)
    for n in ("ln_x_g", "ln_x_b", "ln_l_g", "ln_l_b", "qn_g", "kn_g", "bo"):
        f[f"L1_xattn_{n}"] = o[f"L1_xattn_{n}"]
    f["L1f_w1"] = chunked(o["L1_ffn_W1"].transpose(1, 0, 2).reshape(D, HC * P))
    f["L1f_b1"] = np.ascontiguousarray(o["L1_ffn_b1"].reshape(HC, P).T)
    f["L1f_w2"] = chunked(o["L1_ffn_W2"].reshape(HC * P, D))
    f["L1f_wg"] = chunked(o["L1_ffn_w_gate_w"])
    f["bits_i"] = (1 << np.arange(30, -1, -1)).astype(np.int32)[None, :]
    f["bits_f"] = f["bits_i"].astype(np.float32)
    for n in ("w_gate_b", "b2"):
        f[f"L1_ffn_{n}"] = o[f"L1_ffn_{n}"]
    f["L0f_we"] = chunked(o["L0_ffn_We"].transpose(1, 0, 2).reshape(D, EX * D))
    f["L0f_wr"] = chunked(o["L0_ffn_Wr"].T)
    f["tri"] = np.triu(np.ones((P, P), np.float32), 1)
    f["iota8"] = np.arange(EX, dtype=np.float32)[None, :]
    f["L1_lambda"] = np.stack([o[f"L1_attn_lambda_{n}"] for n in ("q1", "k1", "q2", "k2")])
    f["L1_attn_rms_weight"] = o["L1_attn_rms_weight"]
    return f


def kernel(**inputs):
    import concourse.bacc as bacc
    from concourse.bass_utils import run_bass_kernel_spmd

    nc = bacc.Bacc("TRN2", target_bir_lowering=False, num_devices=1)
    arrays, a = {}, {}
    for name, value in layouts({k: np.asarray(v) for k, v in inputs.items()}).items():
        arrays[f"in_{name}"] = value
        a[name] = nc.dram_tensor(f"in_{name}", value.shape, mybir.dt.from_np(value.dtype), kind="ExternalInput").ap()
    a["y"] = nc.dram_tensor("out_y", (B * S, D), F32, kind="ExternalOutput").ap()
    decoder(nc, a)
    result = run_bass_kernel_spmd(nc, [arrays], core_ids=[0])
    return result.results[0]["out_y"].reshape(B, S, D)
```

```python
import math
from contextlib import ExitStack

import numpy as np
import concourse.bass as bass
from concourse import mybir

F32 = mybir.dt.float32
BF16 = mybir.dt.bfloat16
I32 = mybir.dt.int32
U32 = mybir.dt.uint32
ALU = mybir.AluOpType
ACT = mybir.ActivationFunctionType
AX = mybir.AxisListType.X

P = 128
B, S, D = 4, 1024, 256
NT = B * S // P
TB = S // P
DC = D // P
HALF = 512
H = 16
DV = D // H
LN_EPS = 1e-5
MASKED = -1.0e30
LOWEST = -3.0e38
SPLIT_Q = [0, 0, 1, 1, 0, 2]
SPLIT_K = [0, 1, 0, 1, 2, 0]
MAX_ROW = 96
STACK = MAX_ROW + 3


class Mem:

    def __init__(self, nc, ctx):
        self.nc, self.ctx, self.n = nc, ctx, 0

    def sb(self, name, shape, dt=F32):
        return self.ctx.enter_context(self.nc.sbuf_tensor(name, shape, dt))

    def ps(self, name, cols, dt=F32):
        return self.ctx.enter_context(self.nc.psum_tensor(name, [P, cols], dt))

    def sem(self, name):
        return self.nc.alloc_semaphore(name=name)


class At:

    def __init__(self, base, n=None, step=3):
        self.base, self.n, self.step = base, n, step

    def __add__(self, k):
        return At(self.base + k, self.n, self.step)

    def times(self, a, b=0):
        if self.n is None:
            return a * self.base + b
        return self.n * (self.step * a) + (a * self.base + b)

    def over(self, a, b=0):
        whole = a * (self.base // self.step) + b
        return whole if self.n is None else self.n * a + whole

    def span(self, width=1):
        if self.n is None:
            return slice(self.base * width, (self.base + 1) * width)
        return bass.ds(self.times(width), width)

    @property
    def slot(self):
        return self.base % self.step


def run_turns(eng, turn, count, lag, step, first=0):
    peeled = lag + first + (count - lag - first) % step
    for t in range(peeled):
        turn(At(t, None, step), [t >= j for j in range(lag + 1)])
    if count > peeled:
        with eng.Fori(0, (count - peeled) // step) as n:
            for k in range(step):
                turn(At(peeled + k, n, step), [True] * (lag + 1))
    for t in range(count, count + lag):
        turn(At(t, None, step), [t - j < count for j in range(lag + 1)])


def load_start(nc, a, keep, sems):
    X, ident, identb = keep["X"], keep["ident"], keep["identb"]
    loaded = sems.sem("start_loaded")
    with nc.Block() as block:
        @block.sync
        def _(sp):
            sp.dma_start(X[:], a["x"].rearrange("(t p) d -> p t d", p=P)).then_inc(loaded, 16)
            sp.dma_start(ident[:], a["ident"]).then_inc(loaded, 16)

        @block.vector
        def _(dve):
            dve.wait_ge(loaded, 32)
            dve.tensor_copy(identb[:], ident[:])


def project(nc, a, keep, sems, tag, ne, groups):
    ns = 64 // ne
    gb = groups // B
    w = D // gb
    X, ident, VA = keep["X"], keep["ident"], keep["VA"]
    PT = keep["PT"]
    with ExitStack() as ctx:
        m = Mem(nc, ctx)
        xs = [m.sb(f"{tag}_proj_xs{k}", [P, TB, D]) for k in range(2)]
        xt = [m.sb(f"{tag}_proj_xt{k}", [P, DC, S]) for k in range(2)]
        wqk = m.sb(f"{tag}_proj_wqk", [P, DC, 2 * D])
        wv = m.sb(f"{tag}_proj_wv", [P, DC, D])
        cos = m.sb(f"{tag}_proj_cos", [P, S])
        sin = m.sb(f"{tag}_proj_sin", [P, S])
        t1 = [m.sb(f"{tag}_proj_t1{k}", [P, HALF]) for k in range(2)]
        t2 = [m.sb(f"{tag}_proj_t2{k}", [P, HALF]) for k in range(2)]
        rot = [m.sb(f"{tag}_proj_rot{k}", [P, HALF]) for k in range(4)]
        rest = [m.sb(f"{tag}_proj_rest{k}", [P, HALF]) for k in range(4)]
        parts = [m.sb(f"{tag}_proj_parts{k}", [P, 3, S], BF16) for k in range(4)]
        psT = [m.ps(f"{tag}_proj_psT{k}", HALF) for k in range(2)]
        psQ = [m.ps(f"{tag}_proj_psQ{k}", HALF) for k in range(2)]
        psV = [m.ps(f"{tag}_proj_psV{k}", HALF) for k in range(2)]
        weights = sems.sem(f"{tag}_proj_weights")
        xs_in = [sems.sem(f"{tag}_proj_xs_in{k}") for k in range(2)]
        turned = sems.sem(f"{tag}_proj_turned")
        xt_in = sems.sem(f"{tag}_proj_xt_in")
        qk_done = sems.sem(f"{tag}_proj_qk_done")
        qk_read = sems.sem(f"{tag}_proj_qk_read")
        added = sems.sem(f"{tag}_proj_added")
        hi = sems.sem(f"{tag}_proj_hi")
        less = sems.sem(f"{tag}_proj_less")
        mid = sems.sem(f"{tag}_proj_mid")
        low = sems.sem(f"{tag}_proj_low")
        out = [sems.sem(f"{tag}_proj_out{k}") for k in range(4)]
        v_done = sems.sem(f"{tag}_proj_v_done")
        v_read = sems.sem(f"{tag}_proj_v_read")
        PERB = 8
        N = 2 * PERB
        OUT = 96
        with nc.Block() as block:
            @block.sync
            def _(sp):
                for k in range(2):
                    sp.dma_start(xs[k][:], X[:, k * TB:(k + 1) * TB, :]).then_inc(xs_in[k], 16)
                    if k == 0:
                        sp.dma_start(wqk[:], a[f"{tag}_wqk"]).then_inc(weights, 16)
                        sp.dma_start(wv[:], a[f"{tag}_wv"]).then_inc(weights, 16)
                        sp.dma_start(cos[:], a[f"{tag}_cos"]).then_inc(weights, 16)
                        sp.dma_start(sin[:], a[f"{tag}_sin"]).then_inc(weights, 16)
                with sp.Fori(0, B // 2) as i:
                    for u in range(N // 2):
                        k, qk, c = u // 4, u % 4 // 2, u % 2
                        sp.wait_ge(low, i * N + 2 * u + 2)
                        dst = PT[qk].rearrange("k (b c s h e) t -> k b c h s e t", b=B, c=DC, h=2, e=ne)
                        for p in range(3):
                            for h in range(2):
                                sp.dma_start(dst[p, bass.ds(2 * i + k, 1), c, h].rearrange("o s e t -> (o s) e t"),
                                             parts[u % 4][64 * h:64 * h + 64, p, :]).then_inc(out[u % 4], 16)
                for k in range(4):
                    sp.wait_ge(out[k], OUT * (N // 8) * (B // 2))
                sp.wait_ge(xs_in[0], 32)
                sp.wait_ge(xs_in[1], 48)

            @block.gpsimd
            def _(pool):
                with pool.Fori(0, B // 2) as i:
                    for n in range(N + 3):
                        if n < N:
                            pool.wait_ge(qk_read, i * (3 * N) + 6 + 3 * (n + 1))
                            pool.tensor_tensor(rot[n % 4][:], t1[n % 2][:], t2[n % 2][:], ALU.add).then_inc(added, 1)
                        if n >= 3:
                            u = n - 3
                            pool.wait_ge(mid, i * N + u + 1)
                            to = parts[u // 2 % 4]
                            col = slice((u % 2) * HALF, (u % 2 + 1) * HALF)
                            pool.tensor_tensor(to[:, 2, col], rest[u % 4][:], to[:, 1, col], ALU.subtract).then_inc(low, 1)

            @block.scalar
            def _(act):
                act.sem_inc(xt_in, 2)
                act.sem_inc(v_read, 2)

                def xt_copy(i, k, u, turns):
                    c, h = u // 2, u % 2
                    act.wait_ge(turned, i * 8 + turns + u + 1)
                    act.activation(xt[k][:, c, h * HALF:(h + 1) * HALF], psT[u % 2][:], ACT.Copy).then_inc(xt_in, 1)

                def first(i, n):
                    if n % 2 == 0:
                        act.wait_ge(out[n // 2 % 4], i * (N // 8 * OUT) + OUT * (n // 8))
                    act.wait_ge(added, i * N + n + 1)
                    act.activation(parts[n // 2 % 4][:, 0, (n % 2) * HALF:(n % 2 + 1) * HALF],
                                   rot[n % 4][:], ACT.Copy).then_inc(hi, 1)

                def second(i, n):
                    act.wait_ge(less, i * N + n + 1)
                    act.activation(parts[n // 2 % 4][:, 1, (n % 2) * HALF:(n % 2 + 1) * HALF],
                                   rest[n % 4][:], ACT.Copy).then_inc(mid, 1)

                for u in range(4):
                    xt_copy(0, 0, u, 0)
                act.dma_start(xs[0][:], X[:, 2 * TB:3 * TB, :]).then_inc(xs_in[0], 16)
                with act.Fori(0, B // 2) as i:
                    for n in range(N + 2):
                        if n < N:
                            k, j = n // PERB, n % PERB // 2
                            if n % 2 == 0:
                                xt_copy(i, 1 - k, j, 4 + 4 * k)
                                if n == 6:
                                    act.dma_start(xs[1][:], X[:, 3 * TB:4 * TB, :]).then_inc(xs_in[1], 16)
                            else:
                                act.wait_ge(v_done, i * 8 + 4 * k + j + 1)
                                src = psV[j % 2][:].rearrange("p (t g w) -> p g t w", t=2, g=gb)
                                act.activation(VA[:, bass.ds((2 * i + k) * gb, gb), 2 * j:2 * j + 2, :], src,
                                               ACT.Copy).then_inc(v_read, 1)
                            first(i, n)
                        if n >= 2:
                            second(i, n - 2)

            @block.vector
            def _(dve):
                dve.sem_inc(qk_read, 6)
                dve.wait_ge(weights, 64)

                def rotate(i, n):
                    h = n % 2
                    dve.wait_ge(qk_done, i * N + n + 1)
                    if n >= 2:
                        dve.wait_ge(added, i * N + n - 1)
                    ps, col = psQ[n % 2], slice(h * HALF, (h + 1) * HALF)
                    dve.tensor_tensor(t1[n % 2][:], ps[:], cos[:, col], ALU.mult).then_inc(qk_read, 1)
                    for q in range(2):
                        a0, b0 = 64 * q, 64 * (1 - q)
                        dve.tensor_tensor(t2[n % 2][a0:a0 + 64, :], ps[b0:b0 + 64, :], sin[b0:b0 + 64, col],
                                          ALU.mult).then_inc(qk_read, 1)

                def subtract(i, n):
                    dve.wait_ge(hi, i * N + n + 1)
                    dve.tensor_tensor(rest[n % 4][:], rot[n % 4][:],
                                      parts[n // 2 % 4][:, 0, (n % 2) * HALF:(n % 2 + 1) * HALF],
                                      ALU.subtract).then_inc(less, 1)

                with dve.Fori(0, B // 2) as i:
                    for n in range(N + 2):
                        if n < N:
                            rotate(i, n)
                        if n >= 2:
                            subtract(i, n - 2)

            @block.tensor
            def _(pe):
                pe.wait_ge(weights, 64)

                def transposes(i, k, u, turns):
                    c, h = u // 2, u % 2
                    pe.wait_ge(xt_in, i * 8 + turns + u + 1)
                    for t in range(4):
                        last = pe.transpose(psT[u % 2][:, t * P:(t + 1) * P], xs[k][:, 4 * h + t, c * P:(c + 1) * P], ident[:])
                    last.then_inc(turned, 1)

                pe.wait_ge(xs_in[0], 16)
                for u in range(4):
                    transposes(0, 0, u, 0)
                with pe.Fori(0, B // 2) as i:
                    for n in range(N):
                        k, unit = n // PERB, n % PERB
                        g, h, j = unit // 2, unit % 2, unit // 2
                        if unit == 0:
                            pe.wait_ge(xt_in, i * 8 + 4 * k + 6)
                            if k == 0:
                                pe.wait_ge(xs_in[1], i * 16 + 16)
                            else:
                                pe.wait_ge(xs_in[0], 32)
                        pe.wait_ge(qk_read, i * (3 * N) + 3 * n + 3)
                        for c in range(DC):
                            last = pe.matmul(psQ[n % 2][:], wqk[:, c, g * P:(g + 1) * P],
                                             xt[k][:, c, h * HALF:(h + 1) * HALF], start=(c == 0), stop=(c == DC - 1))
                        last.then_inc(qk_done, 1)
                        if h == 0:
                            transposes(i, 1 - k, j, 4 + 4 * k)
                        else:
                            pe.wait_ge(v_read, i * 8 + 4 * k + j + 1)
                            for t in range(2):
                                for c in range(DC):
                                    last = pe.matmul(psV[j % 2][:, t * D:(t + 1) * D],
                                                     xt[k][:, c, (2 * j + t) * P:(2 * j + t + 1) * P], wv[:, c, :],
                                                     start=(c == 0), stop=(c == DC - 1))
                            last.then_inc(v_done, 1)
def attend(nc, a, keep, sems, tag, dh, groups, causal):
    gb = groups // B
    scale = dh ** -0.5
    shared = 4 * DV // (D // gb)
    vh = 4 // shared
    VA, AO, PT, ident, identb = keep["VA"], keep["AO"], keep["PT"], keep["ident"], keep["identb"]
    steps = [(q, t, max(0, t - 4 * q) * P if causal else 0) for q in range(2) for t in range(TB)
             if not causal or t < 4 * (q + 1)]
    ends = [max(n for n, st in enumerate(steps) if st[0] == q) for q in range(2)]
    pieces = []
    for s in range(4):
        for t in range(TB):
            keys = (t + 1) * P if causal else S
            for h in range(2):
                n = min(HALF, keys - h * HALF)
                if n > 0:
                    pieces.append((s, t, h, n, causal and h * HALF + n == keys))
    NS, NPc = len(steps), len(pieces)
    per = NPc // NS
    LATE = 3
    assert NPc == per * NS
    NL = len(SPLIT_Q) * 2
    LD = 16 * NL

    with ExitStack() as ctx:
        m = Mem(nc, ctx)
        Q = [m.sb(f"{tag}_attn_Q{k}", [P, 4, S], BF16) for k in range(3)]
        K = [m.sb(f"{tag}_attn_K{k}", [P, 4, S], BF16) for k in range(3)]
        V = [m.sb(f"{tag}_attn_V{k}", [P, TB, vh, 32]) for k in range(3)]
        E = [m.sb(f"{tag}_attn_E{k}", [P, HALF]) for k in range(8)]
        mask = m.sb(f"{tag}_attn_mask", [P, 2, P])
        maskb = m.sb(f"{tag}_attn_maskb", [P, 2, P], BF16)
        tops = m.sb(f"{tag}_attn_tops", [P, 4 * TB, 2])
        negm = [m.sb(f"{tag}_attn_negm{k}", [P, 4 * TB]) for k in range(3)]
        mrest = [m.sb(f"{tag}_attn_mrest{k}", [4 * TB, 2, P]) for k in range(3)]
        mparts = [m.sb(f"{tag}_attn_mparts{k}", [4 * TB, 3, P], BF16) for k in range(3)]
        oT = [m.sb(f"{tag}_attn_oT{k}", [P, HALF]) for k in range(2)]
        rec = [m.sb(f"{tag}_attn_rec{k}", [P, 4, 4]) for k in range(2)]
        if shared == 2:
            lam4 = m.sb(f"{tag}_attn_lam4", [P, 4, dh])
            lamp = m.sb(f"{tag}_attn_lamp", [P, 2, dh])
            lams = m.sb(f"{tag}_attn_lams", [P, 2])
            lame = m.sb(f"{tag}_attn_lame", [P, 2])
            lamd = m.sb(f"{tag}_attn_lamd", [P, 1])
            neglam = m.sb(f"{tag}_attn_neglam", [P, 1])
            o1 = [m.sb(f"{tag}_attn_o1{k}", [P, 4, 2, DV]) for k in range(2)]
            o2 = [m.sb(f"{tag}_attn_o2{k}", [P, 4, 2, DV]) for k in range(2)]
        psS = [m.ps(f"{tag}_attn_psS{k}", HALF) for k in range(3)]
        psM = [m.ps(f"{tag}_attn_psM{k}", HALF) for k in range(3)]
        psO = [m.ps(f"{tag}_attn_psO{k}", HALF) for k in range(2)]
        ones = sems.sem(f"{tag}_attn_ones")
        v_blank = sems.sem(f"{tag}_attn_v_blank")
        blank = sems.sem(f"{tag}_attn_blank")
        maskin = sems.sem(f"{tag}_attn_maskin")
        masks = sems.sem(f"{tag}_attn_masks")
        ld = [sems.sem(f"{tag}_attn_ld{k}") for k in range(3)]
        mx = [sems.sem(f"{tag}_attn_mx{k}") for k in range(3)]
        v_in = sems.sem(f"{tag}_attn_v_in")
        s_done = sems.sem(f"{tag}_attn_s_done")
        e_done = sems.sem(f"{tag}_attn_e_done")
        o_done = sems.sem(f"{tag}_attn_o_done")
        o_out = sems.sem(f"{tag}_attn_o_out")
        o_back = sems.sem(f"{tag}_attn_o_back")
        o_read = sems.sem(f"{tag}_attn_o_read")
        o_rec = sems.sem(f"{tag}_attn_o_rec")
        m_done = sems.sem(f"{tag}_attn_m_done")
        m_read = sems.sem(f"{tag}_attn_m_read")
        m_neg = sems.sem(f"{tag}_attn_m_neg")
        m_cut = sems.sem(f"{tag}_attn_m_cut")
        lam = sems.sem(f"{tag}_attn_lam")
        lamin = sems.sem(f"{tag}_attn_lamin")
        NM = NPc + 1
        NR = 1 if shared == 1 else 3

        def bank(g, uses, k):
            return (g.base * uses + k) % 3

        def run(eng, turn):
            run_turns(eng, lambda t, live: turn(t, *live), groups, 2, 3)

        def in_turn(new, last):
            return range(NS if new or last else LATE + 5)

        with nc.Block() as block:
            @block.sync
            def _(sp):
                sp.dma_start(mask[:], a["causal"]).then_inc(maskin, 16)
                if shared == 2:
                    sp.dma_start(lam4[:], a[f"{tag}_lambda"].rearrange("(o k) d -> o k d", o=1).broadcast_to([P, 4, dh])).then_inc(lamin, 16)

                def load(g):
                    if g.base >= 3 or g.n is not None:
                        sp.wait_ge(s_done, (g + -2).times(4 * NS))
                    for (buf, split, src) in ((Q, SPLIT_Q, PT[0]), (K, SPLIT_K, PT[1])):
                        for j, p in enumerate(split):
                            view = src[p].rearrange("(g s e) t -> g e s t", s=4, e=dh)
                            one = view[g.span()]
                            sp.dma_start(buf[g.slot][dh * j:dh * (j + 1), :, :],
                                         one.rearrange("o e s t -> (o e) s t")).then_inc(ld[g.slot], 16)

                def turn(t, new, last, old):
                    if new:
                        load(t)
                    if last:
                        g = t + -1
                        sp.wait_ge(m_cut, g.times(5, 5))
                        for j in range(3):
                            sp.dma_start(Q[g.slot][MAX_ROW + j:MAX_ROW + j + 1, :, :],
                                         mparts[g.slot][:, j, :]).then_inc(mx[g.slot], 16)

                sp.wait_ge(blank, 1)
                run(sp, turn)
                for k in range(3):
                    n = len(range(k, groups, 3))
                    sp.wait_ge(mx[k], 48 * n)

            @block.gpsimd
            def _(pool):
                for k in range(3):
                    pool.memset(K[k][MAX_ROW:STACK, :, :], 1.0).then_inc(ones, 1)
                    pool.wait_ge(ones, k + 1)
                pool.wait_ge(blank, 1)

                def copy(g):
                    if g.base >= 3 or g.n is not None:
                        pool.wait_ge(o_done, (g + -2).times(NS, 2))
                    src = VA[:, g.span(), :, :]
                    pool.tensor_copy(V[g.slot][:, :, :, 0:DV],
                                     src.rearrange("p o t (h d) -> p (o t) h d", d=DV)).then_inc(v_in, 1)

                def turn(t, new, last, old):
                    if new:
                        copy(t)

                run(pool, turn)

            @block.scalar
            def _(act):
                act.sem_inc(e_done, 3)
                if shared == 2:
                    act.wait_ge(lam, 2)
                    act.activation(lame[:], lams[:], ACT.Exp).then_inc(lam, 1)

                def turn(t, new, last, old):
                    if not last:
                        return
                    g = t + -1
                    for n, (q, kt, c0) in enumerate(steps):
                        act.wait_ge(o_done, g.times(NS, n + 1))
                        for s in range(4):
                            act.wait_ge(s_done, g.times(4 * NS, 4 * n + s + 1))
                            act.activation(E[(4 * n + s) % 8][:, c0:], psS[bank(g, 4 * NS, 4 * n + s)][:, c0:], ACT.Exp,
                                           scale=scale).then_inc(e_done, 1)

                run(act, turn)

            @block.vector
            def _(dve):
                dve.sem_inc(o_read, 2)
                for k in range(3):
                    dve.memset(V[k][:], 0.0).then_inc(v_blank, 1)
                dve.wait_ge(v_blank, 3)
                for k in range(3):
                    dve.memset(V[k][:, :, :, DV:DV + 1], 1.0).then_inc(v_blank, 1)
                dve.wait_ge(v_blank, 6)
                if len(SPLIT_Q) * dh < MAX_ROW:
                    for k in range(3):
                        for buf in (Q, K):
                            dve.memset(buf[k][0:MAX_ROW, :, :].bitcast(U32), 0).then_inc(v_blank, 1)
                    dve.wait_ge(v_blank, 12)
                dve.memset(tops[:], LOWEST).then_inc(m_neg, 1)
                dve.wait_ge(maskin, 16)
                dve.tensor_copy(maskb[:], mask[:]).then_inc(masks, 1)
                dve.wait_ge(masks, 1)
                dve.sem_inc(blank, 1)
                dve.wait_ge(m_neg, 1)
                if shared == 2:
                    dve.wait_ge(lamin, 16)
                    pairs = lam4[:].rearrange("p (c k) d -> p c k d", c=2)
                    dve.tensor_tensor(lamp[:], pairs[:, :, 0, :], pairs[:, :, 1, :], ALU.mult).then_inc(lam, 1)
                    dve.wait_ge(lam, 1)
                    dve.tensor_reduce(lams[:], lamp[:], AX, ALU.add).then_inc(lam, 1)
                    dve.wait_ge(lam, 3)
                    dve.tensor_tensor(lamd[:], lame[:, 1:2], lame[:, 0:1], ALU.subtract).then_inc(lam, 1)
                    dve.wait_ge(lam, 4)
                    dve.tensor_scalar(neglam[:], lamd[:], -LAMBDA_INIT, None, ALU.add).then_inc(lam, 1)
                    dve.wait_ge(lam, 5)

                def evacuate(g, q):
                    dve.wait_ge(o_done, g.times(NS, 2 + ends[q] + 1))
                    dve.tensor_copy(oT[q][:], psO[q][:]).then_inc(o_out, 1)

                def normalise(g, q):
                    dve.wait_ge(o_back, g.times(2, q + 1))
                    ps = psO[q][:].rearrange("p (t s c) -> p t s c", t=4, s=4)
                    dve.reciprocal(rec[q][:], ps[:, :, :, DV]).then_inc(o_rec, 1)
                    dve.wait_ge(o_rec, g.times(2 * NR, NR * q + 1))
                    dst = AO[:, g.span(), 4 * q:4 * q + 4, :].rearrange("p o t w -> p (o t) w")
                    if shared == 1:
                        dve.tensor_tensor(dst.rearrange("p t (s c) -> p t s c", s=4), ps[:, :, :, 0:DV],
                                          rec[q][:].unsqueeze(3).broadcast_to([P, 4, 4, DV]), ALU.mult).then_inc(o_read, 1)
                        return
                    for c, o in ((1, o2), (0, o1)):
                        src = ps.rearrange("p t (h c) d -> p t h c d", c=2)[:, :, :, c, 0:DV]
                        r = rec[q][:].rearrange("p t (h c) -> p t h c", c=2)[:, :, :, c]
                        ins = dve.tensor_tensor(o[q][:], src, r.unsqueeze(3).broadcast_to([P, 4, 2, DV]), ALU.mult)
                        ins.then_inc(o_rec if c else o_read, 1)
                    dve.wait_ge(o_rec, g.times(2 * NR, NR * q + 2))
                    dve.wait_ge(o_read, g.times(2, q + 3))
                    dve.scalar_tensor_tensor(out=dst, in0=o2[q][:].rearrange("p t h d -> p t (h d)"), scalar=neglam[:],
                                             in1=o1[q][:].rearrange("p t h d -> p t (h d)"), op0=ALU.mult,
                                             op1=ALU.add).then_inc(o_rec, 1)

                def reduce(t, p):
                    s, qt, h, n, _ = pieces[p]
                    dve.wait_ge(m_done, t.times(NM, p + 1))
                    dve.tensor_reduce(tops[:, s * TB + qt, h:h + 1], psM[bank(t, NM, p)][:, 0:n], AX, ALU.max).then_inc(m_read, 1)

                def combine(t):
                    dve.wait_ge(m_read, t.times(NM, NPc))
                    dve.tensor_reduce(negm[t.slot][:], tops[:], AX, ALU.max, negate=True).then_inc(m_neg, 1)

                def cut(t):
                    r, pt, ps = mrest[t.slot], mparts[t.slot], psM[bank(t, NM, NPc)][0:4 * TB, 0:P]
                    dve.wait_ge(mx[t.slot], t.over(48))
                    dve.wait_ge(m_done, t.times(NM, NM))
                    dve.tensor_copy(pt[:, 0, :], ps).then_inc(m_cut, 1)
                    dve.wait_ge(m_cut, t.times(5, 1))
                    dve.tensor_tensor(r[:, 0, :], ps, pt[:, 0, :], ALU.subtract).then_inc(m_read, 1)
                    dve.wait_ge(m_read, t.times(NM, NM))
                    dve.tensor_copy(pt[:, 1, :], r[:, 0, :]).then_inc(m_cut, 1)
                    dve.wait_ge(m_cut, t.times(5, 2))
                    dve.tensor_tensor(r[:, 1, :], r[:, 0, :], pt[:, 1, :], ALU.subtract).then_inc(m_cut, 1)
                    dve.wait_ge(m_cut, t.times(5, 3))
                    dve.tensor_copy(pt[:, 2, :], r[:, 1, :]).then_inc(m_cut, 2)

                def turn(t, new, last, old):
                    if last:
                        cut(t + -1)
                    for n in in_turn(new, last):
                        k = n - LATE
                        if old and k == 1:
                            evacuate(t + -2, 1)
                        if old and k == 3:
                            normalise(t + -2, 1)
                        if last and k == ends[0] + 2:
                            evacuate(t + -1, 0)
                        if last and k == ends[0] + 4:
                            normalise(t + -1, 0)
                        if new:
                            for p in range(n * per, (n + 1) * per):
                                reduce(t, p)
                    if new:
                        combine(t)

                run(dve, turn)
                dve.wait_ge(o_rec, 2 * NR * groups)

            @block.tensor
            def _(pe):
                pe.sem_inc(o_done, 2)
                pe.wait_ge(ones, 3)
                pe.wait_ge(blank, 1)
                pe.wait_ge(masks, 1)

                def scores(g, n, s):
                    q, kt, c0 = steps[n]
                    Qg, Kg, ps = Q[g.slot], K[g.slot], psS[bank(g, 4 * NS, 4 * n + s)]
                    pe.wait_ge(e_done, g.times(4 * NS, 4 * n + s + 1))
                    diagonal = causal and kt >= 4 * q
                    if diagonal:
                        pe.matmul(ps[:, c0:c0 + P], identb[:], maskb[:, 1, :], start=True, stop=False, skip_group_check=True)
                    pe.matmul(ps[:, c0:], Kg[0:STACK, s, kt * P:(kt + 1) * P], Qg[0:STACK, s, q * HALF + c0:(q + 1) * HALF],
                              start=not diagonal, stop=True, skip_group_check=True).then_inc(s_done, 1)

                def product(g, n):
                    q, kt, c0 = steps[n]
                    if n == 0 or steps[n - 1][0] != q:
                        pe.wait_ge(o_read, g.times(2, q + 1))
                    if n == 0:
                        pe.wait_ge(v_in, g.times(1, 1))
                    pe.wait_ge(e_done, g.times(4 * NS, 4 * n + 4 + 3))
                    for s in range(4):
                        last = pe.matmul(psO[q][32 * s:32 * s + 32, c0:HALF], V[g.slot][:, kt, s // shared, :],
                                         E[(4 * n + s) % 8][:, c0:], start=(kt == 0), stop=(n == ends[q]),
                                         skip_group_check=True)
                    last.then_inc(o_done, 1)

                def turn_back(g, q):
                    pe.wait_ge(o_out, g.times(2, q + 1))
                    for j in range(4):
                        last = pe.transpose(psO[q][:, j * P:(j + 1) * P], oT[q][:, j * P:(j + 1) * P], ident[:])
                    last.then_inc(o_back, 1)

                def piece(t, p):
                    s, qt, h, n, masked = pieces[p]
                    if p >= 2 or t.base >= 1 or t.n is not None:
                        pe.wait_ge(m_read, t.times(NM, p - 2))
                    Qt, Kt, ps = Q[t.slot], K[t.slot], psM[bank(t, NM, p)]
                    if masked:
                        pe.matmul(ps[:, n - P:n], identb[:], maskb[:, 0, :], start=True, stop=False,
                                  skip_group_check=True)
                    last = pe.matmul(ps[:, 0:n], Qt[0:MAX_ROW, s, qt * P:(qt + 1) * P], Kt[0:MAX_ROW, s, h * HALF:h * HALF + n],
                                     start=not masked, stop=True, skip_group_check=True)
                    last.then_inc(m_done, 1)

                def turn_maxima(t):
                    pe.wait_ge(m_neg, t.times(1, 2))
                    pe.wait_ge(m_read, t.times(NM, NPc))
                    pe.transpose(psM[bank(t, NM, NPc)][0:4 * TB, 0:P], negm[t.slot][:], ident[:]).then_inc(m_done, 1)

                def turn(t, new, last, old):
                    if new:
                        pe.wait_ge(ld[t.slot], t.over(LD, LD))
                    for n in in_turn(new, last):
                        k = n - LATE
                        g, step = (t + -1, k) if k >= 0 else (t + -2, NS + k)
                        live = last if k >= 0 else old
                        if last and k == 0:
                            pe.wait_ge(mx[g.slot], g.over(48, 48))
                        todo = list(range(n * per, (n + 1) * per)) if new else []
                        for s in range(4):
                            if live:
                                scores(g, step, s)
                            if n == 0 and s == 1 and last:
                                turn_maxima(t + -1)
                            if todo and (n > 0 or s > 1):
                                piece(t, todo.pop(0))
                        if live and step >= 1:
                            product(g, step - 1)
                        if old and k == 0:
                            product(t + -2, NS - 1)
                        for p in todo:
                            piece(t, p)
                        if old and k == 2:
                            turn_back(t + -2, 1)
                        if last and k == ends[0] + 3:
                            turn_back(t + -1, 0)

                run(pe, turn)
LAMBDA_INIT = 0.8 - 0.6 * math.exp(-0.3 * 12)
BLK = 4


def merge(nc, a, keep, sems, tag, groups, rms, bias=None):
    gb = groups // B
    dense = groups == 1
    X, ident, AO = keep["X"], keep["ident"], keep["AO"]
    NB = NT // BLK
    with ExitStack() as ctx:
        m = Mem(nc, ctx)
        h = [m.sb(f"{tag}_merge_h{k}", [P, DC, HALF] if dense else [P, BLK, D]) for k in range(2)]
        hT = [m.sb(f"{tag}_merge_hT{k}", [P, BLK, DC, P]) for k in range(2)]
        wo = m.sb(f"{tag}_merge_wo", [P, DC, D])
        y = [m.sb(f"{tag}_merge_y{k}", [P, BLK, D]) for k in range(2)]
        st = m.sb(f"{tag}_merge_st", [P, BLK, 6])
        mv = [m.sb(f"{tag}_merge_mv{k}", [P, BLK, 2]) for k in range(2)]
        sd = [m.sb(f"{tag}_merge_sd{k}", [P, BLK]) for k in range(2)]
        rs = [m.sb(f"{tag}_merge_rs{k}", [P, BLK]) for k in range(2)]
        eps = m.sb(f"{tag}_merge_eps", [P, 1])
        psT = [m.ps(f"{tag}_merge_psT{k}", BLK * DC * P) for k in range(2)]
        psY = [m.ps(f"{tag}_merge_psY{k}", BLK * D) for k in range(2)]
        if bias:
            bo, ones = m.sb(f"{tag}_merge_bo", [1, D]), keep["ones1"]
        if rms:
            rw = m.sb(f"{tag}_merge_rw", [P, DV])
            sq = m.sb(f"{tag}_merge_sq", [P, BLK, D])
            hn = [m.sb(f"{tag}_merge_hn{k}", [P, BLK, D]) for k in range(2)]
            ss = m.sb(f"{tag}_merge_ss", [P, BLK * H])
            sr = m.sb(f"{tag}_merge_sr", [P, BLK * H])
            ri = m.sb(f"{tag}_merge_ri", [P, BLK * H])
        loaded = sems.sem(f"{tag}_merge_wo_in")
        h_in = [sems.sem(f"{tag}_merge_h_in{k}") for k in range(2)]
        const = sems.sem(f"{tag}_merge_const")
        hr = sems.sem(f"{tag}_merge_hr")
        hq = sems.sem(f"{tag}_merge_hq")
        turned = sems.sem(f"{tag}_merge_turned")
        hT_in = sems.sem(f"{tag}_merge_hT_in")
        y_done = sems.sem(f"{tag}_merge_y_done")
        y_read = sems.sem(f"{tag}_merge_y_read")
        stat = sems.sem(f"{tag}_merge_stat")
        root = sems.sem(f"{tag}_merge_root")
        passed = sems.sem(f"{tag}_merge_passed")
        NSTAT = 4
        NHR = 5
        HIN = 16 if dense else 16 * BLK
        with nc.Block() as block:
            @block.sync
            def _(sp):
                sp.dma_start(wo[:], a[f"{tag}_wo"]).then_inc(loaded, 16)
                if rms:
                    sp.dma_start(rw[:], a["L1_attn_rms_weight"].rearrange("(o d) -> o d", o=1).broadcast_to([P, DV])).then_inc(loaded, 16)
                if bias:
                    sp.dma_start(bo[:], a[bias].rearrange("(o d) -> o d", o=1)).then_inc(loaded, 16)
                with sp.Fori(0, B) as b:
                    for k in range(2):
                        if rms:
                            sp.wait_ge(hr, b * (2 * NHR) + (k + 2) * NHR)
                        elif not dense:
                            sp.wait_ge(turned, b * 2 + k)
                        if dense:
                            sp.wait_ge(y_done, b * 2 + k)
                            sp.dma_start(h[k][:], AO[:, :, bass.ds(b * S + HALF * k, HALF)]).then_inc(h_in[k], 16)
                        for t in range(0 if dense else BLK):
                            sp.dma_start(h[k][:, t, :].rearrange("p (g w) -> p g w", g=gb), AO[:, bass.ds(b * gb, gb), BLK * k + t, :]).then_inc(h_in[k], 16)

            @block.scalar
            def _(act):
                act.sem_inc(hT_in, 2)
                act.wait_ge(const, 1)
                with act.Fori(0, B) as b:
                    for k in range(2):
                        if rms:
                            act.wait_ge(hr, b * (2 * NHR) + (k + 2) * NHR + 2)
                            act.activation(sr[:], ss[:], ACT.Sqrt, bias=eps[:], scale=1.0 / DV).then_inc(hq, 1)
                        if not dense:
                            act.wait_ge(turned, b * 2 + k + 1)
                            act.activation(hT[k][:].rearrange("p t c n -> p (t c n)"), psT[k][:], ACT.Copy).then_inc(hT_in, 1)
                        act.wait_ge(stat, b * (2 * NSTAT) + NSTAT * k + 2)
                        act.activation(sd[k][:], mv[k][:, :, 1], ACT.Sqrt, bias=eps[:]).then_inc(root, 1)

            @block.tensor
            def _(pe):
                pe.wait_ge(loaded, 32 if rms or bias else 16)
                src = hn if rms else h
                with pe.Fori(0, B) as b:
                    for k in range(2):
                        if rms:
                            pe.wait_ge(hr, b * (2 * NHR) + (k + 3) * NHR)
                        else:
                            pe.wait_ge(h_in[k], b * HIN + HIN)
                        for t in range(0 if dense else BLK):
                            for c in range(DC):
                                last = pe.transpose(psT[k][:, (t * DC + c) * P:(t * DC + c + 1) * P],
                                                    src[k][:, t, c * P:(c + 1) * P], ident[:])
                        if not dense:
                            last.then_inc(turned, 1)
                            pe.wait_ge(hT_in, b * 2 + k + 3)
                        pe.wait_ge(y_read, b * 2 + k + 1)
                        for t in range(BLK):
                            if bias:
                                pe.matmul(psY[k][:, t * D:(t + 1) * D], ones[:], bo[:], start=True, stop=False)
                            for c in range(DC):
                                last = pe.matmul(psY[k][:, t * D:(t + 1) * D], h[k][:, c, t * P:(t + 1) * P] if dense else hT[k][:, t, c, :], wo[:, c, :],
                                                 start=(c == 0 and not bias), stop=(c == DC - 1))
                        last.then_inc(y_done, 1)

            @block.vector
            def _(dve):
                dve.sem_inc(y_read, 2)
                dve.memset(eps[:], LN_EPS).then_inc(const, 1)
                if rms:
                    dve.sem_inc(hr, 2 * NHR)
                    dve.wait_ge(loaded, 32)
                    dve.tensor_scalar(rw[:], rw[:], 1.0 - LAMBDA_INIT, None, ALU.mult).then_inc(const, 1)
                    dve.wait_ge(const, 2)

                def root_mean_square(b, k):
                    n = b * (2 * NHR) + (k + 2) * NHR
                    dve.wait_ge(h_in[k], b * HIN + HIN)
                    flat = h[k][:].rearrange("p t f -> p (t f)")
                    dve.tensor_tensor(sq[:].rearrange("p t f -> p (t f)"), flat, flat, ALU.mult).then_inc(hr, 1)
                    dve.wait_ge(hr, n + 1)
                    heads = lambda x: x[:].rearrange("p t (h d) -> p (t h) d", d=DV)
                    dve.tensor_reduce(ss[:], heads(sq), AX, ALU.add).then_inc(hr, 1)
                    dve.wait_ge(hq, b * 2 + k + 1)
                    dve.reciprocal(ri[:], sr[:]).then_inc(hr, 1)
                    dve.wait_ge(hr, n + 3)
                    dve.tensor_tensor(heads(sq), heads(h[k]), ri[:].unsqueeze(2).broadcast_to([P, BLK * H, DV]),
                                      ALU.mult).then_inc(hr, 1)
                    dve.wait_ge(hr, n + 4)
                    dve.tensor_tensor(heads(hn[k]), heads(sq), rw[:].unsqueeze(1).broadcast_to([P, BLK * H, DV]),
                                      ALU.mult).then_inc(hr, 1)

                with dve.Fori(0, B) as b:
                    for k in range(2):
                        if rms:
                            root_mean_square(b, k)
                        n = b * (2 * NSTAT) + NSTAT * k
                        dve.wait_ge(y_done, b * 2 + k + 1)
                        xb = X[:, bass.ds(b * TB + BLK * k, BLK), :].rearrange("p t d -> p (t d)")
                        dve.tensor_tensor(y[k][:].rearrange("p t d -> p (t d)"), psY[k][:], xb, ALU.add).then_inc(y_read, 1)
                        dve.wait_ge(y_read, b * 2 + k + 3)
                        for t in range(BLK):
                            last = dve.bn_stats(st[:, t, :], y[k][:, t, :])
                        last.then_inc(stat, 1)
                        dve.wait_ge(stat, n + 1)
                        dve.sem_inc(passed, 1)
                        for t in range(BLK):
                            last = dve.bn_aggr(mv[k][:, t, :], st[:, t, :])
                        last.then_inc(stat, 1)
                        dve.wait_ge(root, b * 2 + k + 1)
                        dve.reciprocal(rs[k][:], sd[k][:]).then_inc(stat, 1)
                        dve.wait_ge(stat, n + 3)
                        for t in range(BLK):
                            last = dve.tensor_scalar(X[:, bass.ds(b * TB + BLK * k + t, 1), :].rearrange("p o d -> p (o d)"),
                                                     y[k][:, t, :], mv[k][:, t, 0:1], rs[k][:, t:t + 1],
                                                     ALU.subtract, ALU.mult)
                        last.then_inc(stat, 1)


class Chain:

    def __init__(self, eng, sem):
        self.eng, self.sem, self.n = eng, sem, 0

    def did(self, ins):
        self.n += 1
        ins.then_inc(self.sem, 1)

    def wait(self):
        self.eng.wait_ge(self.sem, self.n)


class Steps:

    def __init__(self, eng, sem, item, per, k=0):
        self.eng, self.sem, self.item, self.per, self.k = eng, sem, item, per, k

    def did(self, ins):
        self.k += 1
        assert self.k <= self.per
        ins.then_inc(self.sem, 1)

    def wait(self):
        self.eng.wait_ge(self.sem, self.item.times(self.per, self.k))


def cross_setup(nc, a, keep, sems):
    KT, VBD, bq, bo, lg, lb, heads8 = (keep[k] for k in ("KT", "VBD", "bq", "bo", "lg", "lb", "heads8"))
    ident = keep["ident"]
    CK = 96
    with ExitStack() as ctx:
        m = Mem(nc, ctx)
        ctxT = m.sb("x0s_ctxT", [CK, 2, B, P])
        wkv = m.sb("x0s_wkv", [CK, 2, 2 * D])
        bkv = m.sb("x0s_bkv", [P, 2 * D])
        kp = m.sb("x0s_kp", [P, B, D])
        sq = m.sb("x0s_sq", [P, B, D])
        ss = m.sb("x0s_ss", [P, B])
        nr = m.sb("x0s_nr", [P, B])
        kn = m.sb("x0s_kn", [P, B, D])
        ps = m.ps("x0s_ps", B * 2 * D)
        psT = m.ps("x0s_psT", 2 * B * 64)
        loaded = sems.sem("x0s_loaded")
        products = sems.sem("x0s_products")
        done = sems.sem("x0s_done")
        root = sems.sem("x0s_root")
        turned = sems.sem("x0s_turned")
        with nc.Block() as block:
            @block.sync
            def _(sp):
                for dst, src in ((ctxT[:], a["ctxT2"]), (wkv[:], a["L0x_wkv"]),
                                 (bkv[:, 0:D], a["L0_xattn_bk"].rearrange("(o d) -> o d", o=1).broadcast_to([P, D])),
                                 (bkv[:, D:], a["L0_xattn_bv"].rearrange("(o d) -> o d", o=1).broadcast_to([P, D])),
                                 (bq[:], a["L0_xattn_bq"].rearrange("(o d) -> o d", o=1).broadcast_to([P, D])),
                                 (bo[:], a["L0_xattn_bo"].rearrange("(o d) -> o d", o=1).broadcast_to([P, D])),
                                 (lg[:], a["L0_xattn_ln_gamma"].rearrange("(o d) -> o d", o=1).broadcast_to([P, D])),
                                 (lb[:], a["L0_xattn_ln_beta"].rearrange("(o d) -> o d", o=1).broadcast_to([P, D])),
                                 (heads8[:], a["heads8"])):
                    sp.dma_start(dst, src).then_inc(loaded, 16)

            @block.tensor
            def _(pe):
                pe.wait_ge(loaded, 144)
                for b in range(B):
                    for c in range(2):
                        last = pe.matmul(ps[:, b * 2 * D:(b + 1) * 2 * D], ctxT[:, c, b, :], wkv[:, c, :],
                                         start=(c == 0), stop=(c == 1))
                last.then_inc(products, 1)
                pe.wait_ge(done, 8)
                for c in range(DC):
                    for b in range(B):
                        last = pe.transpose(psT[:, (c * B + b) * 64:(c * B + b + 1) * 64], kn[0:64, b, c * P:(c + 1) * P],
                                            ident[0:64, 0:64])
                last.then_inc(turned, 1)

            @block.scalar
            def _(act):
                act.wait_ge(done, 5)
                act.activation(nr[:], ss[:], ACT.Sqrt).then_inc(root, 1)

            @block.vector
            def _(dve):
                chain = Chain(dve, done)
                chain.did(dve.memset(VBD[:], 0.0))
                dve.wait_ge(done, 1)
                chain.did(dve.memset(VBD[0:64, :, :, DV:DV + 1], 1.0))
                chain.did(dve.memset(VBD[64:P, :, :, 2 * DV + 1:2 * DV + 2], 1.0))
                dve.wait_ge(products, 1)
                pv = ps[:].rearrange("p (b n) -> p b n", b=B)
                for b in range(B):
                    last = dve.tensor_tensor(kp[:, b, :], pv[:, b, 0:D], bkv[:, 0:D], ALU.add)
                chain.did(last)
                dve.wait_ge(done, 4)
                dve.tensor_tensor(sq[:], kp[:], kp[:], ALU.mult).then_inc(root, 1)
                dve.wait_ge(root, 1)
                chain.did(dve.tensor_reduce(ss[:], sq[:], AX, ALU.add))
                dve.wait_ge(root, 2)
                chain.did(dve.tensor_scalar(nr[:], nr[:], 1e-12, None, ALU.max))
                dve.wait_ge(done, 6)
                chain.did(dve.reciprocal(ss[:], nr[:]))
                dve.wait_ge(done, 7)
                for b in range(B):
                    last = dve.tensor_scalar(kn[:, b, :], kp[:, b, :], ss[:, b:b + 1], None, ALU.mult)
                chain.did(last)
                for b in range(B):
                    for h in range(2):
                        r = slice(64 * h, 64 * h + 64)
                        view = lambda x: x.rearrange("p (a h d) -> p a h d", a=H // 2, h=2)[:, :, h, :]
                        last = dve.tensor_tensor(VBD[r, b, :, (DV + 1) * h:(DV + 1) * h + DV], view(pv[r, b, D:]),
                                                 view(bkv[r, D:]), ALU.add)
                chain.did(last)
                dve.wait_ge(turned, 1)
                chain.did(dve.tensor_copy(KT[:], psT[:].rearrange("p (c b k) -> p c b k", c=DC, b=B)))


def cross(nc, a, keep, sems):
    X, ident = keep["X"], keep["ident"]
    KT, VBD, bq, bo, lg, lb, heads8 = (keep[k] for k in ("KT", "VBD", "bq", "bo", "lg", "lb", "heads8"))
    NB = NT // BLK
    HP = H // 2
    W2 = 2 * (DV + 1)
    with ExitStack() as ctx:
        m = Mem(nc, ctx)
        two = lambda name, shape, dt=F32: [m.sb(f"x0_{name}{k}", shape, dt) for k in range(2)]
        QP = m.sb("x0_QP", [P, NT, D])
        wq = m.sb("x0_wq", [P, DC, D])
        wo = m.sb("x0_wo", [P, DC, D])
        xs = two("xs", [P, BLK, D])
        xT = m.sb("x0_xT", [P, DC, HALF])
        qp = m.sb("x0_qp", [P, BLK, D])
        sq = m.sb("x0_sq", [P, BLK, D])
        ss = m.sb("x0_ss", [P, BLK])
        nr = m.sb("x0_nr", [P, BLK])
        ns = m.sb("x0_ns", [P, BLK])
        rn = m.sb("x0_rn", [P, BLK])
        qn = m.sb("x0_qn", [P, BLK, D])
        qT = two("qT", [P, DC, HALF])
        KB = two("KB", [P, HP, P])
        E = m.sb("x0_E", [P, HP, HALF])
        rec = m.sb("x0_rec", [P, BLK, H])
        at = two("at", [P, BLK, D])
        aT = m.sb("x0_aT", [P, BLK, DC, P])
        y = m.sb("x0_y", [P, BLK, D])
        z = m.sb("x0_z", [P, BLK, D])
        zg = m.sb("x0_zg", [P, BLK, D])
        zb = m.sb("x0_zb", [P, BLK, D])
        w = m.sb("x0_w", [P, BLK, D])
        st = m.sb("x0_st", [P, BLK, 6])
        mv = m.sb("x0_mv", [P, BLK, 2])
        sd = m.sb("x0_sd", [P, BLK])
        rs = m.sb("x0_rs", [P, BLK])
        eps = m.sb("x0_eps", [P, 1])
        psA = m.ps("x0_psA", BLK * D)
        psS = [m.ps(f"x0_psS{k}", HALF) for k in range(2)]
        psO = [m.ps(f"x0_psO{k}", HALF) for k in range(2)]
        psC = m.ps("x0_psC", BLK * D)
        sem = lambda name: sems.sem(f"x0_{name}")
        weights = sem("weights")
        xs_in = [sem(f"xs_in{k}") for k in range(2)]
        a_pe = sem("a_pe")
        a_act = sem("a_act")
        a_dve = sem("a_dve")
        a_rec = sem("a_rec")
        kb_in = sem("kb_in")
        qp_in = sem("qp_in")
        s_done = sem("s_done")
        e_done = sem("e_done")
        o_done = sem("o_done")
        o_rec = sem("o_rec")
        o_read = sem("o_read")
        c_pe = sem("c_pe")
        c_act = sem("c_act")
        c_dve = sem("c_dve")
        c_pool = sem("c_pool")
        passed = sem("passed")
        held = sem("held")
        const = sem("const")
        NA, NCD = 5, 10
        with nc.Block() as block:
            @block.sync
            def _(sp):
                sp.dma_start(wq[:], a["L0x_wq"]).then_inc(weights, 16)
                sp.dma_start(wo[:], a["L0x_wo"]).then_inc(weights, 16)

                def turn(t, live):
                    if live[0]:
                        if t.base >= 2 or t.n is not None:
                            sp.wait_ge(a_pe, (t + -2).times(3, 1))
                        sp.dma_start(xs[t.slot][:], X[:, t.span(BLK), :]).then_inc(xs_in[t.slot], 16)

                run_turns(sp, turn, NB, 2, 2)

            @block.tensor
            def _(pe):
                pe.wait_ge(weights, 32)

                def scores(g, hp):
                    pe.wait_ge(e_done, g.times(HP, hp + 1))
                    pe.matmul(psS[hp % 2][:], KB[g.slot][:, hp, :], qT[g.slot][:, hp // 4, :], start=True,
                              stop=True).then_inc(s_done, 1)

                def turn(t, live):
                    u, v = t + -1, t + -2
                    if live[0]:
                        pe.wait_ge(xs_in[t.slot], t.over(16, 16))
                        pe.wait_ge(a_act, t.times(3))
                        for c in range(DC):
                            for k in range(BLK):
                                last = pe.transpose(psA[:, (c * BLK + k) * P:(c * BLK + k + 1) * P],
                                                    xs[t.slot][:, k, c * P:(c + 1) * P], ident[:])
                        last.then_inc(a_pe, 1)
                    if live[1]:
                        pe.wait_ge(kb_in, u.times(1, 1))
                        pe.wait_ge(a_act, u.times(3, 3))
                        for hp in range(4):
                            scores(u, hp)
                    if live[0]:
                        pe.wait_ge(a_act, t.times(3, 1))
                        for k in range(BLK):
                            for c in range(DC):
                                last = pe.matmul(psA[:, k * D:(k + 1) * D], xT[:, c, k * P:(k + 1) * P], wq[:, c, :],
                                                 start=(c == 0), stop=(c == DC - 1))
                        last.then_inc(a_pe, 1)
                    if live[1]:
                        for hp in range(4, HP):
                            scores(u, hp)
                    if live[2]:
                        pe.wait_ge(o_read, v.times(BLK, BLK + 2))
                        pe.wait_ge(c_dve, v.times(NCD))
                        for k in range(BLK):
                            for c in range(DC):
                                last = pe.transpose(psC[:, (k * DC + c) * P:(k * DC + c + 1) * P],
                                                    at[v.slot][:, k, c * P:(c + 1) * P], ident[:])
                        last.then_inc(c_pe, 1)
                    if live[0]:
                        pe.wait_ge(a_dve, t.times(NA, NA))
                        for c in range(DC):
                            for k in range(BLK):
                                last = pe.transpose(psA[:, (c * BLK + k) * P:(c * BLK + k + 1) * P],
                                                    qn[:, k, c * P:(c + 1) * P], ident[:])
                        last.then_inc(a_pe, 1)
                    if live[1]:
                        pe.wait_ge(e_done, u.times(HP, HP + 2))
                        for k in range(BLK):
                            pe.wait_ge(o_read, u.times(BLK, k + 1))
                            for hp in range(HP):
                                last = pe.matmul(psO[k % 2][:, hp * W2:(hp + 1) * W2], E[:, hp, k * P:(k + 1) * P],
                                                 VBD[:, bass.ds(u.over(1), 1) if u.n is not None else slice(u.over(1), u.over(1) + 1), hp, :]
                                                 .rearrange("p o n -> p (o n)"), start=True, stop=True)
                            last.then_inc(o_done, 1)
                    if live[2]:
                        pe.wait_ge(c_act, v.times(3, 1))
                        for k in range(BLK):
                            for c in range(DC):
                                last = pe.matmul(psC[:, k * D:(k + 1) * D], aT[:, k, c, :], wo[:, c, :],
                                                 start=(c == 0), stop=(c == DC - 1))
                        last.then_inc(c_pe, 1)

                run_turns(pe, turn, NB, 2, 2)

            @block.scalar
            def _(act):
                act.sem_inc(e_done, 2)
                act.wait_ge(const, 1)

                def turn(t, live):
                    u, v = t + -1, t + -2
                    if live[0]:
                        act.wait_ge(a_pe, t.times(3, 1))
                        act.activation(xT[:].rearrange("p c n -> p (c n)"), psA[:], ACT.Copy).then_inc(a_act, 1)
                    if live[1]:
                        act.wait_ge(o_done, u.times(BLK))
                        for hp in range(HP):
                            act.wait_ge(s_done, u.times(HP, hp + 1))
                            act.activation(E[:, hp, :], psS[hp % 2][:], ACT.Exp, scale=0.25).then_inc(e_done, 1)
                    if live[0]:
                        act.wait_ge(a_dve, t.times(NA, 3))
                        act.activation(nr[:], ss[:], ACT.Sqrt).then_inc(a_act, 1)
                    if live[2]:
                        act.wait_ge(c_pe, v.times(2, 1))
                        act.activation(aT[:].rearrange("p k c n -> p (k c n)"), psC[:], ACT.Copy).then_inc(c_act, 1)
                    if live[0]:
                        act.wait_ge(a_pe, t.times(3, 3))
                        act.activation(qT[t.slot][:].rearrange("p c n -> p (c n)"), psA[:], ACT.Copy).then_inc(a_act, 1)
                    if live[2]:
                        for n in range(2):
                            act.wait_ge(c_dve, v.times(NCD, 3 + 5 * n))
                            act.activation(sd[:], mv[:, :, 1], ACT.Sqrt, bias=eps[:]).then_inc(c_act, 1)

                run_turns(act, turn, NB, 2, 2)

            @block.gpsimd
            def _(pool):
                def turn(t, live):
                    v = t + -2
                    if live[0]:
                        if t.base >= 2 or t.n is not None:
                            pool.wait_ge(s_done, (t + -1).times(HP))
                            pool.sem_inc(held, 1)
                        for c in range(DC):
                            src = KT[:, c, bass.ds(t.over(1), 1) if t.n is not None else slice(t.over(1), t.over(1) + 1), :]
                            last = pool.tensor_tensor(KB[t.slot][:, c * 4:(c + 1) * 4, :].rearrange("p a (h k) -> p (a h) k", h=2),
                                                      src.broadcast_to([P, 8, 64]), heads8[:].unsqueeze(2).broadcast_to([P, 8, 64]),
                                                      ALU.mult)
                        last.then_inc(kb_in, 1)
                        pool.wait_ge(a_dve, t.times(NA, 1))
                        pool.sem_inc(held, 1)
                        pool.tensor_tensor(QP[:, t.span(BLK), :], qp[:], bo[:].unsqueeze(1).broadcast_to([P, BLK, D]),
                                           ALU.add).then_inc(qp_in, 1)
                    if live[2]:
                        pool.wait_ge(c_dve, v.times(NCD, 5))
                        pool.tensor_tensor(zg[:], z[:], lg[:].unsqueeze(1).broadcast_to([P, BLK, D]), ALU.mult).then_inc(c_pool, 1)
                        pool.wait_ge(c_pool, v.times(2, 1))
                        pool.tensor_tensor(zb[:], zg[:], lb[:].unsqueeze(1).broadcast_to([P, BLK, D]), ALU.add).then_inc(c_pool, 1)

                run_turns(pool, turn, NB, 2, 2)

            @block.vector
            def _(dve):
                dve.sem_inc(o_read, 2)
                dve.memset(eps[:], LN_EPS).then_inc(const, 1)

                def layernorm(v, n, src, out):
                    dve.wait_ge(c_dve, v.times(NCD, 1 + 5 * n))
                    for k in range(BLK):
                        last = dve.bn_stats(st[:, k, :], src[:, k, :])
                    last.then_inc(c_dve, 1)
                    dve.wait_ge(c_dve, v.times(NCD, 2 + 5 * n))
                    dve.sem_inc(passed, 1)
                    for k in range(BLK):
                        last = dve.bn_aggr(mv[:, k, :], st[:, k, :])
                    last.then_inc(c_dve, 1)
                    dve.wait_ge(c_act, v.times(3, 2 + n))
                    dve.reciprocal(rs[:], sd[:]).then_inc(c_dve, 1)
                    dve.wait_ge(c_dve, v.times(NCD, 4 + 5 * n))
                    for k in range(BLK):
                        last = dve.tensor_scalar(out(k), src[:, k, :], mv[:, k, 0:1], rs[:, k:k + 1], ALU.subtract, ALU.mult)
                    last.then_inc(c_dve, 1)

                def turn(t, live):
                    u, v = t + -1, t + -2
                    if live[0]:
                        dve.wait_ge(a_pe, t.times(3, 2))
                        dve.wait_ge(qp_in, t.times(1))
                        dve.tensor_tensor(qp[:], psA[:].rearrange("p (k d) -> p k d", k=BLK),
                                          bq[:].unsqueeze(1).broadcast_to([P, BLK, D]), ALU.add).then_inc(a_dve, 1)
                        dve.wait_ge(a_dve, t.times(NA, 1))
                        dve.tensor_tensor(sq[:], qp[:], qp[:], ALU.mult).then_inc(a_dve, 1)
                        dve.wait_ge(a_dve, t.times(NA, 2))
                        dve.tensor_reduce(ss[:], sq[:], AX, ALU.add).then_inc(a_dve, 1)
                        dve.wait_ge(a_act, t.times(3, 2))
                        dve.tensor_scalar(ns[:], nr[:], 1e-12, None, ALU.max).then_inc(a_dve, 1)
                        dve.wait_ge(a_dve, t.times(NA, 4))
                        dve.reciprocal(rn[:], ns[:]).then_inc(a_rec, 1)
                        dve.wait_ge(a_rec, t.times(1, 1))
                        for k in range(BLK):
                            last = dve.tensor_scalar(qn[:, k, :], qp[:, k, :], rn[:, k:k + 1], None, ALU.mult)
                        last.then_inc(a_dve, 1)
                    if live[1]:
                        for k in range(BLK):
                            dve.wait_ge(o_done, u.times(BLK, k + 1))
                            ps = psO[k % 2][:, 0:HP * W2].rearrange("p (h d) -> p h d", h=H)
                            dve.reciprocal(rec[:, k, :], ps[:, :, DV]).then_inc(o_rec, 1)
                            dve.wait_ge(o_rec, u.times(BLK, k + 1))
                            dve.tensor_tensor(at[u.slot][:, k, :].rearrange("p (h d) -> p h d", h=H), ps[:, :, 0:DV],
                                              rec[:, k, :].unsqueeze(2).broadcast_to([P, H, DV]), ALU.mult).then_inc(o_read, 1)
                    if live[2]:
                        dve.wait_ge(c_pe, v.times(2, 2))
                        dve.wait_ge(qp_in, v.times(1, 1))
                        dve.tensor_tensor(y[:], psC[:].rearrange("p (k d) -> p k d", k=BLK), QP[:, v.span(BLK), :],
                                          ALU.add).then_inc(c_dve, 1)
                        layernorm(v, 0, y, lambda k: z[:, k, :])
                        dve.wait_ge(c_pool, v.times(2, 2))
                        dve.tensor_tensor(w[:], zb[:], X[:, v.span(BLK), :], ALU.add).then_inc(c_dve, 1)
                        out = lambda k: X[:, bass.ds(v.times(BLK, k), 1) if v.n is not None
                                          else slice(v.times(BLK, k), v.times(BLK, k) + 1), :].rearrange("p o d -> p (o d)")
                        layernorm(v, 1, w, out)

                run_turns(dve, turn, NB, 2, 2)


EX = 8
CAPACITY = int(S * 2 / EX * 1.5) + 1


def experts(nc, a, keep, sems):
    X, ident, identb = keep["X"], keep["ident"], keep["identb"]
    NB = NT // BLK
    with nc.cleanup_on_exit(), ExitStack() as ctx:
        m = Mem(nc, ctx)
        sb = lambda name, shape, dt=F32: m.sb(f"m0_{name}", shape, dt)
        two = lambda name, shape, dt=F32: [m.sb(f"m0_{name}{k}", shape, dt) for k in range(2)]
        we, wr = sb("we", [P, DC, EX * D]), sb("wr", [P, DC, EX])
        tri, trib, onesb, iota = sb("tri", [P, P]), sb("trib", [P, P], BF16), sb("onesb", [P, P], BF16), sb("iota", [P, EX])
        xs, xT = two("xs", [P, BLK, D]), two("xT", [P, DC, HALF])
        logit, top, ix = sb("logit", [P, BLK, EX]), sb("top", [P, BLK, 8]), sb("ix", [P, BLK, 8], U32)
        ixf, d, ed, den, w1, w2 = (sb(n, [P, BLK, 2] if n == "ixf" else [P, BLK]) for n in ("ixf", "d", "ed", "den", "w1", "w2"))
        oh1, oh2, g1, g2, g12 = (sb(n, [P, BLK, EX]) for n in ("oh1", "oh2", "g1", "g2", "g12"))
        chosen, before = two("chosen", [P, BLK, EX], BF16), two("before", [P, BLK, EX], BF16)
        W = two("W", [P, BLK, EX])
        z = sb("z", [P, BLK, D])
        st, mv, sd, rs, eps = sb("st", [P, BLK, 6]), sb("mv", [P, BLK, 2]), sb("sd", [P, BLK]), sb("rs", [P, BLK]), sb("eps", [P, 1])
        psA = m.ps("m0_psA", BLK * D)
        psG = m.ps("m0_psG", HALF)
        psE = [m.ps(f"m0_psE{k}", HALF) for k in range(4)]
        sem = lambda name: sems.sem(f"m0_{name}")
        weights, const = sem("weights"), sem("const")
        xs_in = [sem(f"xs_in{k}") for k in range(2)]
        g_pe = sem("g_pe")
        g_act = sem("g_act")
        g_dve = sem("g_dve")
        y_pe = sem("y_pe")
        y_dve = sem("y_dve")
        n_dve = sem("n_dve")
        n_act = sem("n_act")
        passed = sem("passed")
        NG, G_D, G_CHOSEN = 19, 4, 14
        with nc.Block() as block:
            @block.sync
            def _(sp):
                for dst, src in ((we[:], a["L0f_we"]), (wr[:], a["L0f_wr"]), (tri[:], a["tri"]),
                                 (iota[:], a["iota8"].broadcast_to([P, EX]))):
                    sp.dma_start(dst, src).then_inc(weights, 16)

                def turn(t, live):
                    if live[0]:
                        if t.base >= 2 or t.n is not None:
                            sp.wait_ge(y_dve, (t + -1).times(BLK * EX))
                        sp.dma_start(xs[t.slot][:], X[:, t.span(BLK), :]).then_inc(xs_in[t.slot], 16)

                run_turns(sp, turn, NB, 1, 2)

            @block.tensor
            def _(pe):
                pe.wait_ge(weights, 64)
                pe.wait_ge(const, 3)

                def expert_products(u, k):
                    for e in range(EX // 2):
                        n = k * (EX // 2) + e
                        if n >= 4 or u.base >= 1 or u.n is not None:
                            pe.wait_ge(y_dve, u.times(BLK * EX, 2 * (n - 3)))
                        for c in range(DC):
                            last = pe.matmul(psE[e][:], xT[u.slot][:, c, k * P:(k + 1) * P],
                                             we[:, c, e * HALF:(e + 1) * HALF], start=(c == 0), stop=(c == DC - 1))
                        last.then_inc(y_pe, 1)

                def turn(t, live):
                    u = t + -1
                    if live[0]:
                        pe.wait_ge(xs_in[t.slot], t.over(16, 16))
                        pe.wait_ge(g_act, t.times(2))
                        for c in range(DC):
                            for k in range(BLK):
                                last = pe.transpose(psA[:, (c * BLK + k) * P:(c * BLK + k + 1) * P],
                                                    xs[t.slot][:, k, c * P:(c + 1) * P], ident[:])
                        last.then_inc(g_pe, 1)
                    if live[1]:
                        expert_products(u, 0)
                    if live[0]:
                        pe.wait_ge(g_act, t.times(2, 1))
                        pe.wait_ge(g_dve, t.times(NG))
                        for k in range(BLK):
                            for c in range(DC):
                                last = pe.matmul(psG[:, k * EX:(k + 1) * EX], xT[t.slot][:, c, k * P:(k + 1) * P], wr[:, c, :],
                                                 start=(c == 0), stop=(c == DC - 1))
                        last.then_inc(g_pe, 1)
                    if live[1]:
                        expert_products(u, 1)
                        expert_products(u, 2)
                    if live[0]:
                        pe.wait_ge(g_dve, t.times(NG, G_CHOSEN + 4))
                        pe.matmul(psG[:, 0:BLK * EX], trib[:], chosen[t.slot][:].rearrange("p k e -> p (k e)"), start=True, stop=False)
                        pe.matmul(psG[:, 0:BLK * EX], onesb[:], before[t.slot][:].rearrange("p k e -> p (k e)"), start=False,
                                  stop=True).then_inc(g_pe, 1)
                    if live[1]:
                        expert_products(u, 3)

                run_turns(pe, turn, NB, 1, 2)

            @block.scalar
            def _(act):
                act.wait_ge(const, 3)

                def turn(t, live):
                    u = t + -1
                    if live[0]:
                        act.wait_ge(g_pe, t.times(3, 1))
                        if t.base >= 2 or t.n is not None:
                            act.wait_ge(y_pe, (t + -1).times(BLK * EX // 2))
                        act.activation(xT[t.slot][:].rearrange("p c n -> p (c n)"), psA[:], ACT.Copy).then_inc(g_act, 1)
                        act.wait_ge(g_dve, t.times(NG, G_D))
                        act.activation(ed[:], d[:], ACT.Exp).then_inc(g_act, 1)
                    if live[1]:
                        act.wait_ge(n_dve, u.times(4, 2))
                        act.activation(sd[:], mv[:, :, 1], ACT.Sqrt, bias=eps[:]).then_inc(n_act, 1)

                run_turns(act, turn, NB, 1, 2)

            @block.vector
            def _(dve):
                dve.memset(eps[:], LN_EPS).then_inc(const, 1)
                dve.memset(onesb[:], 1.0).then_inc(const, 1)
                dve.wait_ge(weights, 64)
                dve.tensor_copy(trib[:], tri[:]).then_inc(const, 1)

                def add_experts(u, k):
                    dve.wait_ge(g_dve, u.times(NG, NG))
                    if k == 0:
                        dve.wait_ge(n_dve, u.times(4))
                    for e in range(EX):
                        n = k * EX + e
                        dve.wait_ge(y_pe, u.times(BLK * EX // 2, k * (EX // 2) + e // 2 + 1))
                        dve.wait_ge(y_dve, u.times(BLK * EX, n))
                        dve.scalar_tensor_tensor(out=z[:, k, :], in0=psE[e // 2][:, (e % 2) * D:(e % 2 + 1) * D],
                                                 scalar=W[u.slot][:, k, e:e + 1], in1=xs[u.slot][:, k, :] if e == 0 else z[:, k, :],
                                                 op0=ALU.mult, op1=ALU.add).then_inc(y_dve, 1)

                def first(t):
                    s = Steps(dve, g_dve, t, NG)
                    ch, bf = chosen[t.slot], before[t.slot]
                    dve.wait_ge(g_pe, t.times(3, 2))
                    s.did(dve.tensor_copy(logit[:], psG[:, 0:BLK * EX].rearrange("p (k e) -> p k e", k=BLK)))
                    s.wait()
                    dve.sem_inc(passed, 1)
                    for k in range(BLK):
                        last = dve.max(top[:, k, :], logit[:, k, :])
                    s.did(last)
                    s.wait()
                    dve.sem_inc(passed, 1)
                    for k in range(BLK):
                        last = dve.max_index(ix[:, k, :], top[:, k, :], logit[:, k, :])
                    s.did(last)
                    s.did(dve.tensor_tensor(d[:], top[:, :, 1], top[:, :, 0], ALU.subtract))
                    assert s.k == G_D
                    s.wait()
                    s.did(dve.tensor_copy(ixf[:], ix[:, :, 0:2]))
                    s.wait()
                    for n, oh in ((0, oh1), (1, oh2)):
                        s.did(dve.tensor_tensor(oh[:], iota[:].unsqueeze(1).broadcast_to([P, BLK, EX]),
                                                ixf[:, :, n:n + 1].broadcast_to([P, BLK, EX]), ALU.is_equal))
                    s.wait()
                    s.did(dve.tensor_tensor(ch[:], oh1[:], oh2[:], ALU.add))
                    dve.wait_ge(g_act, t.times(2, 2))
                    s.did(dve.tensor_scalar(den[:], ed[:], 1.0, None, ALU.add))
                    s.wait()
                    s.did(dve.reciprocal(w1[:], den[:]))
                    s.wait()
                    s.did(dve.tensor_tensor(w2[:], ed[:], w1[:], ALU.mult))
                    s.wait()
                    s.did(dve.tensor_tensor(g1[:], oh1[:], w1[:].unsqueeze(2).broadcast_to([P, BLK, EX]), ALU.mult))
                    s.did(dve.tensor_tensor(g2[:], oh2[:], w2[:].unsqueeze(2).broadcast_to([P, BLK, EX]), ALU.mult))
                    s.wait()
                    s.did(dve.tensor_tensor(g12[:], g1[:], g2[:], ALU.add))
                    assert s.k == G_CHOSEN
                    if t.slot == 0:
                        s.did(dve.memset(bf[:, 0, :], 0.0))
                    else:
                        s.did(dve.tensor_tensor(bf[:, 0, :], before[0][:, BLK - 1, :], chosen[0][:, BLK - 1, :], ALU.add))
                    for k in range(1, BLK):
                        s.wait()
                        s.did(dve.tensor_tensor(bf[:, k, :], bf[:, k - 1, :], ch[:, k - 1, :], ALU.add))

                def second(t):
                    s = Steps(dve, g_dve, t, NG, G_CHOSEN + 4)
                    dve.wait_ge(g_pe, t.times(3, 3))
                    ps = psG[:, 0:BLK * EX]
                    s.did(dve.scalar_tensor_tensor(out=W[t.slot][:].rearrange("p k e -> p (k e)"), in0=ps, scalar=float(CAPACITY),
                                                   in1=g12[:].rearrange("p k e -> p (k e)"), op0=ALU.is_lt, op1=ALU.mult))

                def norm(u):
                    dve.wait_ge(y_dve, u.times(BLK * EX, BLK * EX))
                    for k in range(BLK):
                        last = dve.bn_stats(st[:, k, :], z[:, k, :])
                    last.then_inc(n_dve, 1)
                    dve.wait_ge(n_dve, u.times(4, 1))
                    dve.sem_inc(passed, 1)
                    for k in range(BLK):
                        last = dve.bn_aggr(mv[:, k, :], st[:, k, :])
                    last.then_inc(n_dve, 1)
                    dve.wait_ge(n_act, u.times(1, 1))
                    dve.reciprocal(rs[:], sd[:]).then_inc(n_dve, 1)
                    dve.wait_ge(n_dve, u.times(4, 3))
                    for k in range(BLK):
                        out = X[:, bass.ds(u.times(BLK, k), 1) if u.n is not None else slice(u.times(BLK, k), u.times(BLK, k) + 1), :]
                        last = dve.tensor_scalar(out.rearrange("p o d -> p (o d)"), z[:, k, :], mv[:, k, 0:1], rs[:, k:k + 1],
                                                 ALU.subtract, ALU.mult)
                    last.then_inc(n_dve, 1)

                def turn(t, live):
                    u = t + -1
                    if live[1]:
                        add_experts(u, 0)
                    if live[0]:
                        first(t)
                    if live[1]:
                        add_experts(u, 1)
                        add_experts(u, 2)
                    if live[0]:
                        second(t)
                    if live[1]:
                        add_experts(u, 3)
                        norm(u)

                run_turns(dve, turn, NB, 1, 2)


LH, LD = 4, 64
CK = 96
CTX = 64


def context_keys(nc, a, keep, sems):
    ident, kTc, Vc, gam, ones, maskrow = (keep[k] for k in ("ident", "kTc", "Vc", "gam", "ones1", "maskrow"))
    KD = 192
    with ExitStack() as ctx:
        m = Mem(nc, ctx)
        sb = lambda name, shape, dt=F32: m.sb(f"x1s_{name}", shape, dt)
        cx, xc, xn = sb("cx", [CTX, B, KD]), sb("xc", [CTX, B, KD]), sb("xn", [CTX, B, KD])
        lg, lb = sb("lg", [CTX, KD]), sb("lb", [CTX, KD])
        xT = sb("xT", [CK, 2, B, CTX])
        wkv = sb("wkv", [CK, 2, 2 * D])
        mask8, maskf = sb("mask8", [1, B * CTX], mybir.dt.uint8), sb("maskf", [1, B * CTX])
        st, mv, sd, rs, eps = sb("st", [CTX, B, 6]), sb("mv", [CTX, B, 2]), sb("sd", [CTX, B]), sb("rs", [CTX, B]), sb("eps", [P, 1])
        sq, kn = sb("sq", [CTX, B, D]), sb("kn", [CTX, B, D])
        ss, nr, rn = sb("ss", [CTX, B * LH]), sb("nr", [CTX, B * LH]), sb("rn", [CTX, B * LH])
        ps = m.ps("x1s_ps", B * 2 * D)
        psT = m.ps("x1s_psT", 2 * B * CTX)
        sem = lambda name: sems.sem(f"x1s_{name}")
        loaded, products, turned, done, roots = sem("loaded"), sem("products"), sem("turned"), sem("done"), sem("roots")
        kv = ps[0:CTX, :].rearrange("p (b n) -> p b n", b=B)
        row = lambda name, n: a[name].rearrange("(o d) -> o d", o=1).broadcast_to([n, a[name].shape[0]])
        with nc.Block() as block:
            @block.sync
            def _(sp):
                for dst, src in ((cx[:], a["ctx_tok"]), (wkv[:], a["L1x_wkv"]), (mask8[:], a["mask8"]),
                                 (lg[:], row("L1_xattn_ln_x_g", CTX)), (lb[:], row("L1_xattn_ln_x_b", CTX)),
                                 (gam[:, 0:LD], row("L1_xattn_qn_g", P)), (gam[:, LD:], row("L1_xattn_kn_g", P))):
                    sp.dma_start(dst, src).then_inc(loaded, 16)

            @block.tensor
            def _(pe):
                pe.wait_ge(done, 8)
                for c in range(2):
                    for b in range(B):
                        last = pe.transpose(psT[0:CK, (c * B + b) * CTX:(c * B + b + 1) * CTX], xn[:, b, c * CK:(c + 1) * CK],
                                            ident[0:CTX, 0:CTX])
                last.then_inc(turned, 1)
                pe.wait_ge(done, 9)
                for b in range(B):
                    for c in range(2):
                        last = pe.matmul(ps[0:CTX, b * 2 * D:(b + 1) * 2 * D], xT[:, c, b, :], wkv[:, c, :],
                                         start=(c == 0), stop=(c == 1))
                last.then_inc(products, 1)
                pe.wait_ge(done, 16)
                for c in range(DC):
                    for b in range(B):
                        last = pe.transpose(psT[:, (c * B + b) * CTX:(c * B + b + 1) * CTX], kn[:, b, c * P:(c + 1) * P],
                                            ident[0:CTX, 0:CTX])
                last.then_inc(turned, 1)

            @block.scalar
            def _(act):
                act.wait_ge(done, 4)
                act.activation(sd[:], mv[:, :, 1], ACT.Sqrt, bias=eps[0:CTX]).then_inc(roots, 1)
                act.wait_ge(done, 11)
                act.activation(nr[:], ss[:], ACT.Sqrt, scale=1.0 / LD).then_inc(roots, 1)

            @block.vector
            def _(dve):
                s = Chain(dve, done)
                s.did(dve.memset(eps[:], LN_EPS))
                s.did(dve.memset(ones[:], 1.0))
                dve.wait_ge(loaded, 112)
                for b in range(B):
                    last = dve.bn_stats(st[:, b, :], cx[:, b, :])
                s.did(last)
                s.wait()
                for b in range(B):
                    last = dve.bn_aggr(mv[:, b, :], st[:, b, :])
                s.did(last)
                dve.wait_ge(roots, 1)
                s.did(dve.reciprocal(rs[:], sd[:]))
                s.wait()
                for b in range(B):
                    last = dve.tensor_scalar(xc[:, b, :], cx[:, b, :], mv[:, b, 0:1], rs[:, b:b + 1], ALU.subtract, ALU.mult)
                s.did(last)
                s.wait()
                s.did(dve.tensor_tensor(xc[:], xc[:], lg[:].unsqueeze(1).broadcast_to([CTX, B, KD]), ALU.mult))
                s.wait()
                s.did(dve.tensor_tensor(xn[:], xc[:], lb[:].unsqueeze(1).broadcast_to([CTX, B, KD]), ALU.add))
                assert s.n == 8
                dve.wait_ge(turned, 1)
                s.did(dve.tensor_copy(xT[:], psT[0:CK, :].rearrange("p (c b k) -> p c b k", c=2, b=B)))
                dve.wait_ge(products, 1)
                s.did(dve.tensor_copy(kn[:], kv[:, :, 0:D]))
                s.wait()
                dve.tensor_tensor(sq[:], kn[:], kn[:], ALU.mult).then_inc(products, 1)
                dve.wait_ge(products, 2)
                s.did(dve.tensor_reduce(ss[:], sq[:].rearrange("p b (h d) -> p (b h) d", h=LH), AX, ALU.add))
                dve.wait_ge(roots, 2)
                s.did(dve.tensor_scalar(nr[:], nr[:], 1e-8, None, ALU.max))
                s.wait()
                s.did(dve.reciprocal(rn[:], nr[:]))
                s.wait()
                s.did(dve.tensor_tensor(sq[:].rearrange("p b (h d) -> p (b h) d", h=LH), kn[:].rearrange("p b (h d) -> p (b h) d", h=LH),
                                        rn[:].unsqueeze(2).broadcast_to([CTX, B * LH, LD]), ALU.mult))
                s.did(dve.tensor_scalar(gam[:, 0:LD], gam[:, 0:LD], float(LD) ** -0.5, None, ALU.mult))
                s.wait()
                s.did(dve.tensor_tensor(kn[:].rearrange("p b (h d) -> p (b h) d", h=LH), sq[:].rearrange("p b (h d) -> p (b h) d", h=LH),
                                        gam[0:CTX, LD:].unsqueeze(1).broadcast_to([CTX, B * LH, LD]), ALU.mult))
                assert s.n == 16
                for b in range(B):
                    last = dve.tensor_copy(Vc[:, b, :, :], kv[:, b, D:].rearrange("p (h d) -> p h d", h=LH))
                s.did(last)
                s.did(dve.tensor_copy(maskf[:], mask8[:]))
                s.wait()
                s.did(dve.tensor_scalar(maskrow[:], maskf[:], 1.0, -MASKED, ALU.subtract, ALU.mult))
                dve.wait_ge(turned, 2)
                s.did(dve.tensor_copy(kTc[:], psT[:].rearrange("p (c b k) -> p c b k", c=DC, b=B)))


def latent_project(nc, a, keep, sems):
    X, ident, QT, KD, VL, gam = (keep[k] for k in ("X", "ident", "QT", "KD", "VL", "gam"))
    NB = NT // BLK
    QK = 2 * D
    with ExitStack() as ctx:
        m = Mem(nc, ctx)
        sb = lambda name, shape, dt=F32: m.sb(f"x1p_{name}", shape, dt)
        w = sb("w", [P, DC, 3 * D])
        lg, lb = sb("lg", [P, D]), sb("lb", [P, D])
        st, mv, sd, rs, eps = sb("st", [P, BLK, 6]), sb("mv", [P, BLK, 2]), sb("sd", [P, BLK]), sb("rs", [P, BLK]), sb("eps", [P, 1])
        xc, ln = sb("xc", [P, BLK, D]), sb("ln", [P, BLK, D])
        lT = sb("lT", [P, DC, HALF])
        sq = sb("sq", [P, BLK, QK])
        nrm = sb("nrm", [P, BLK, QK])
        R = BLK * 2 * LH
        qo = [sb(f"qo{k}", [P, DC, HALF]) for k in range(2)]
        ko = [sb(f"ko{k}", [P, DC, HALF]) for k in range(2)]
        ss, nr, rn = sb("ss", [P, R]), sb("nr", [P, R]), sb("rn", [P, R])
        psT = m.ps("x1p_psT", BLK * D)
        psQ = m.ps("x1p_psQ", BLK * QK)
        psV = m.ps("x1p_psV", BLK * D)
        sem = lambda name: sems.sem(f"x1p_{name}")
        loaded, const = sem("loaded"), sem("const")
        l_dve = sem("l_dve")
        l_act = sem("l_act")
        l_pool = sem("l_pool")
        l_pe = sem("l_pe")
        lt_in = sem("lt_in")
        qkv = sem("qkv")
        v_in = sem("v_in")
        sq_in = sem("sq_in")
        n_dve = sem("n_dve")
        n_act = sem("n_act")
        n_pool = sem("n_pool")
        q_pe = sem("q_pe")
        q_in = sem("q_in")
        k_in = sem("k_in")
        out = [sem(f"out{k}") for k in range(2)]
        passed = sem("passed")
        row = lambda name, n: a[name].rearrange("(o d) -> o d", o=1).broadcast_to([n, a[name].shape[0]])
        with nc.Block() as block:
            @block.sync
            def _(sp):
                for dst, src in ((w[:], a["L1x_w"]), (lg[:], row("L1_xattn_ln_l_g", P)), (lb[:], row("L1_xattn_ln_l_b", P))):
                    sp.dma_start(dst, src).then_inc(loaded, 16)

                def turn(t, live):
                    for ready, dram, staged in ((q_in, QT, qo), (k_in, KD, ko)):
                        sp.wait_ge(ready, t.times(DC, DC))
                        sp.dma_start(dram.rearrange("(c p) n -> p c n", p=P)[:, :, t.span(HALF)], staged[t.slot][:])\
                            .then_inc(out[t.slot], 16)

                run_turns(sp, turn, NB, 0, 2)
                for k in range(2):
                    sp.wait_ge(out[k], 32 * (NB // 2))

            @block.tensor
            def _(pe):
                pe.wait_ge(loaded, 48)

                def turn(t, live):
                    u = t + -1
                    if live[1]:
                        pe.wait_ge(lt_in, u.times(1, 1))
                        pe.wait_ge(v_in, u.times(1))
                        pe.wait_ge(q_in, u.times(DC))
                        pe.wait_ge(k_in, u.times(DC))
                        for k in range(BLK):
                            for c in range(DC):
                                last = pe.matmul(psQ[:, k * QK:(k + 1) * QK], lT[:, c, k * P:(k + 1) * P], w[:, c, 0:QK],
                                                 start=(c == 0), stop=(c == DC - 1))
                        last.then_inc(qkv, 1)
                        for k in range(BLK):
                            for c in range(DC):
                                last = pe.matmul(psV[:, k * D:(k + 1) * D], lT[:, c, k * P:(k + 1) * P], w[:, c, QK:],
                                                 start=(c == 0), stop=(c == DC - 1))
                        last.then_inc(qkv, 1)
                    if live[0]:
                        pe.wait_ge(l_pool, t.times(2, 2))
                        pe.wait_ge(lt_in, t.times(1))
                        for c in range(DC):
                            for k in range(BLK):
                                last = pe.transpose(psT[:, (c * BLK + k) * P:(c * BLK + k + 1) * P], ln[:, k, c * P:(c + 1) * P], ident[:])
                        last.then_inc(l_pe, 1)
                    if live[1]:
                        pe.wait_ge(n_pool, u.times(1, 1))
                        for c in range(2 * DC):
                            for k in range(BLK):
                                last = pe.transpose(psQ[:, (c * BLK + k) * P:(c * BLK + k + 1) * P], nrm[:, k, c * P:(c + 1) * P], ident[:])
                            last.then_inc(q_pe, 1)

                run_turns(pe, turn, NB, 1, 2)

            @block.scalar
            def _(act):
                act.wait_ge(const, 1)

                def turn(t, live):
                    u = t + -1
                    if live[1]:
                        act.wait_ge(qkv, u.times(2, 1))
                        act.wait_ge(n_dve, u.times(4))
                        act.activation(sq[:].rearrange("p k n -> p (k n)"), psQ[:], ACT.Square).then_inc(sq_in, 1)
                    if live[0]:
                        act.wait_ge(l_dve, t.times(4, 2))
                        act.activation(sd[:], mv[:, :, 1], ACT.Sqrt, bias=eps[:]).then_inc(l_act, 1)
                    if live[1]:
                        act.wait_ge(n_dve, u.times(4, 1))
                        act.activation(nr[:], ss[:], ACT.Sqrt, scale=1.0 / LD).then_inc(n_act, 1)
                        act.wait_ge(qkv, u.times(2, 2))
                        act.activation(VL[:, u.span(BLK), :, :], psV[:].rearrange("p (k h d) -> p k h d", k=BLK, h=LH),
                                       ACT.Copy).then_inc(v_in, 1)
                    if live[0]:
                        act.wait_ge(l_pe, t.times(1, 1))
                        act.activation(lT[:].rearrange("p c n -> p (c n)"), psT[:], ACT.Copy).then_inc(lt_in, 1)
                    if live[1]:
                        if u.base >= 2 or u.n is not None:
                            act.wait_ge(out[u.slot], u.over(32))
                        for c in range(DC):
                            act.wait_ge(q_pe, u.times(4, c + 1))
                            act.activation(qo[u.slot][:, c, :], psQ[:, c * HALF:(c + 1) * HALF], ACT.Copy).then_inc(q_in, 1)

                run_turns(act, turn, NB, 1, 2)

            @block.gpsimd
            def _(pool):
                pool.wait_ge(loaded, 48)

                def turn(t, live):
                    u = t + -1
                    if live[0]:
                        pool.wait_ge(l_dve, t.times(4, 4))
                        pool.wait_ge(l_pe, t.times(1))
                        pool.tensor_tensor(ln[:], xc[:], lg[:].unsqueeze(1).broadcast_to([P, BLK, D]), ALU.mult).then_inc(l_pool, 1)
                        pool.wait_ge(l_pool, t.times(2, 1))
                        pool.tensor_tensor(ln[:], ln[:], lb[:].unsqueeze(1).broadcast_to([P, BLK, D]), ALU.add).then_inc(l_pool, 1)
                    if live[1]:
                        pool.wait_ge(n_dve, u.times(4, 4))
                        view = nrm[:].rearrange("p k (q h d) -> p (k q) h d", q=2, h=LH)
                        for q in range(2):
                            for k in range(BLK):
                                v = nrm[:, k, q * D:(q + 1) * D].rearrange("p (h d) -> p h d", h=LH)
                                last = pool.tensor_tensor(v, v, gam[:, q * LD:(q + 1) * LD].unsqueeze(1).broadcast_to([P, LH, LD]), ALU.mult)
                        last.then_inc(n_pool, 1)

                run_turns(pool, turn, NB, 1, 2)

            @block.vector
            def _(dve):
                dve.memset(eps[:], LN_EPS).then_inc(const, 1)

                def turn(t, live):
                    u = t + -1
                    if live[0]:
                        xk = lambda k: X[:, bass.ds(t.times(BLK, k), 1) if t.n is not None else slice(t.times(BLK, k), t.times(BLK, k) + 1), :]\
                            .rearrange("p o d -> p (o d)")
                        for k in range(BLK):
                            last = dve.bn_stats(st[:, k, :], xk(k))
                        last.then_inc(l_dve, 1)
                        dve.wait_ge(l_dve, t.times(4, 1))
                        dve.sem_inc(passed, 1)
                        for k in range(BLK):
                            last = dve.bn_aggr(mv[:, k, :], st[:, k, :])
                        last.then_inc(l_dve, 1)
                    if live[1]:
                        dve.wait_ge(sq_in, u.times(1, 1))
                        dve.tensor_reduce(ss[:], sq[:].rearrange("p k (h d) -> p (k h) d", h=2 * LH), AX, ALU.add).then_inc(n_dve, 1)
                    if live[0]:
                        dve.wait_ge(l_act, t.times(1, 1))
                        dve.reciprocal(rs[:], sd[:]).then_inc(l_dve, 1)
                        dve.wait_ge(l_dve, t.times(4, 3))
                        dve.wait_ge(l_pool, t.times(2))
                        for k in range(BLK):
                            last = dve.tensor_scalar(xc[:, k, :], xk(k), mv[:, k, 0:1], rs[:, k:k + 1], ALU.subtract, ALU.mult)
                        last.then_inc(l_dve, 1)
                    if live[1]:
                        dve.wait_ge(n_act, u.times(1, 1))
                        dve.tensor_scalar(nr[:], nr[:], 1e-8, None, ALU.max).then_inc(n_dve, 1)
                        dve.wait_ge(n_dve, u.times(4, 2))
                        dve.reciprocal(rn[:], nr[:]).then_inc(n_dve, 1)
                        dve.wait_ge(n_dve, u.times(4, 3))
                        dve.wait_ge(q_pe, u.times(4))
                        dve.tensor_tensor(nrm[:].rearrange("p k (h d) -> p (k h) d", h=2 * LH),
                                          psQ[:].rearrange("p (k h d) -> p (k h) d", k=BLK, h=2 * LH),
                                          rn[:].unsqueeze(2).broadcast_to([P, R, LD]), ALU.mult).then_inc(n_dve, 1)
                        if u.base >= 2 or u.n is not None:
                            dve.wait_ge(out[u.slot], u.over(32))
                        for c in range(DC):
                            dve.wait_ge(q_pe, u.times(4, DC + c + 1))
                            dve.tensor_copy(ko[u.slot][:, c, :], psQ[:, (DC + c) * HALF:(DC + c + 1) * HALF]).then_inc(k_in, 1)

                run_turns(dve, turn, NB, 1, 2)


def latent_attend(nc, a, keep, sems):
    ident, QT, KD, VL, kTc, Vc, ones, maskrow, AO = (keep[k] for k in ("ident", "QT", "KD", "VL", "kTc", "Vc", "ones1", "maskrow", "AO"))
    UNITS = TB * LH
    STEP = 2 * LH
    NP = TB + 1
    with ExitStack() as ctx:
        m = Mem(nc, ctx)
        two = lambda name, shape, dt=F32: [m.sb(f"x1_{name}{k}", shape, dt) for k in range(2)]
        qs = two("qs", [P, DC, P])
        Kb, Vb, mb = two("Kb", [P, DC, S + CTX]), two("Vb", [P, NP, LH, P]), two("mb", [1, CTX])
        E, Ec = two("E", [P, S]), two("Ec", [P, CTX])
        ET = two("ET", [P, NP, P])
        mx = two("mx", [P, 2])
        nm = two("nm", [P, 1])
        rc = two("rc", [P, P])
        psS = [m.ps(f"x1_psS{k}", S) for k in range(2)]
        psC = m.ps("x1_psC", HALF)
        psE = m.ps("x1_psE", S)
        psO = m.ps("x1_psO", HALF)
        sem = lambda name: sems.sem(f"x1_{name}")
        qs_in = [sem(f"qs_in{k}") for k in range(2)]
        kv_in = [sem(f"kv_in{k}") for k in range(2)]
        s_pe = sem("s_pe")
        m_dve = sem("m_dve")
        e_act = sem("e_act")
        t_pe = sem("t_pe")
        t_dve = sem("t_dve")
        t_act = sem("t_act")
        c_pe = sem("c_pe")
        c_act = sem("c_act")
        o_pe = sem("o_pe")
        o_dve = sem("o_dve")
        blank = sem("blank")
        passed = sem("passed")

        def batches(eng, body):
            with eng.Fori(0, B // 2) as o:
                for k in range(2):
                    def units(turn, count, lag, step, first=0):
                        run_turns(eng, lambda t, live: turn(In(t, o, k, count), live), count, lag, step, first)
                    body(units, k, o)

        class In(At):

            def __init__(self, t, o, k, count):
                super().__init__(t.base, t.n, t.step)
                self.o, self.k, self.count = o, k, count

            def __add__(self, d):
                return In(At(self.base + d, self.n, self.step), self.o, self.k, self.count)

            def times(self, a, b=0):
                return self.o * (2 * self.count * a) + (self.k * self.count * a + b) + At.times(self, a)

        with nc.Block() as block:
            @block.gpsimd
            def _(pool):
                for k in range(2):
                    pool.memset(Vb[k][:], 1.0).then_inc(blank, 1)
                    pool.wait_ge(blank, k + 1)
                for b in range(B):
                    k = b % 2
                    if b >= 2:
                        pool.wait_ge(o_pe, (b - 1) * UNITS + 1)
                    pairs = lambda x: x.rearrange("p t (c h) d -> p t c h d", h=2)
                    values = [(pairs(Vb[k][:, 0:TB])[:, :, :, h, LD * h:LD * h + LD], pairs(VL[:, b * TB:(b + 1) * TB])[:, :, :, h, :])
                              for h in range(2)]
                    values += [(pairs(Vb[k][0:CTX, TB:NP])[:, 0, :, h, LD * h:LD * h + LD], pairs(Vc[:, b:b + 1])[:, 0, :, h, :])
                               for h in range(2)]
                    for dst, src in (*values, (Kb[k][:, :, 0:S], KD.rearrange("(c p) n -> p c n", p=P)[:, :, b * S:(b + 1) * S]),
                                     (Kb[k][:, :, S:], kTc[:, :, b, :]), (mb[k][:], maskrow[:, b * CTX:(b + 1) * CTX])):
                        pool.dma_start(dst, src).then_inc(kv_in[k], 16)

            @block.sync
            def _(sp):
                def body(units, k, o):
                    def turn(t, live):
                        sp.wait_ge(s_pe, t.times(LH))
                        n = bass.ds(t.times(P), P)
                        sp.dma_start(qs[t.slot][:], QT.rearrange("(c p) n -> p c n", p=P)[:, :, n]).then_inc(qs_in[t.slot], 16)

                    units(turn, TB, 0, 2)

                batches(sp, body)

            @block.tensor
            def _(pe):
                pe.sem_inc(s_pe, LH)
                pe.sem_inc(t_pe, 2)
                pe.sem_inc(c_pe, 1)
                pe.sem_inc(o_pe, 1)

                def body(units, j, o):
                    def scores(u):
                        h, k = u.slot % LH, u.slot % 2
                        if h == 0:
                            tiles = u.o * TB + (j * TB // 2 + 1) + (u.base // STEP if u.n is None else u.n + u.base // STEP)
                            pe.wait_ge(qs_in[u.slot // LH], tiles * 16)
                        pe.wait_ge(e_act, u.times(2))
                        pe.sem_inc(passed, 1)
                        rows = slice(LD * (h % 2), LD * (h % 2) + LD)
                        q, key = qs[u.slot // LH][rows, h // 2, :], Kb[j][rows, h // 2, :]
                        for i in range(2):
                            pe.matmul(psS[k][:, i * HALF:(i + 1) * HALF], q, key[:, i * HALF:(i + 1) * HALF], start=True, stop=True)
                        pe.wait_ge(e_act, u.times(2, 1))
                        pe.wait_ge(c_act, u.times(1))
                        pe.sem_inc(passed, 1)
                        out = psC[:, k * CTX:(k + 1) * CTX]
                        pe.matmul(out, ones[:], mb[j][:], start=True, stop=False)
                        pe.matmul(out, q, key[:, S:], start=False, stop=True).then_inc(s_pe, 1)

                    def transposes(u):
                        k = u.slot % 2
                        pe.wait_ge(e_act, u.times(2, 4))
                        pe.wait_ge(t_dve, u.times(1))
                        for i in range(4):
                            last = pe.transpose(psE[:, i * P:(i + 1) * P], E[k][:, i * P:(i + 1) * P], ident[:])
                        last.then_inc(t_pe, 1)
                        pe.wait_ge(t_act, u.times(1))
                        for i in range(4, 8):
                            last = pe.transpose(psE[:, i * P:(i + 1) * P], E[k][:, i * P:(i + 1) * P], ident[:])
                        last.then_inc(t_pe, 1)

                    def context_transposes(u, after):
                        pe.wait_ge(e_act, (u + after).times(2, 3 if after else 4))
                        pe.sem_inc(passed, 1)
                        pe.transpose(psC[0:CTX, P:2 * P], Ec[u.slot % 2][:], ident[:]).then_inc(c_pe, 1)

                    def outputs(u):
                        k, h = u.slot % 2, u.slot % LH
                        pe.wait_ge(t_dve, u.times(1, 1))
                        pe.wait_ge(t_act, u.times(1, 1))
                        pe.wait_ge(c_act, u.times(1, 2))
                        pe.wait_ge(o_dve, u.times(2))
                        out = psO[:, h * P:(h + 1) * P]
                        for i in range(TB):
                            pe.matmul(out, Vb[j][:, i, h, :], ET[k][:, i, :], start=(i == 0), stop=False)
                        pe.matmul(out, Vb[j][0:CTX, TB, h, :], ET[k][0:CTX, TB, :], start=False, stop=True).then_inc(o_pe, 1)

                    def turn(t, live):
                        if live[0]:
                            scores(t)
                        if live[1]:
                            transposes(t + -1)
                        if live[2]:
                            outputs(t + -2)
                        if live[1]:
                            context_transposes(t + -1, 1 if live[0] else 0)

                    pe.wait_ge(kv_in[j], o * 112 + 112)
                    units(turn, UNITS, 2, STEP)

                batches(pe, body)

            @block.scalar
            def _(act):
                act.sem_inc(e_act, 2)
                act.sem_inc(c_act, 1)

                def turn(t, live):
                    if live[1]:
                        u = t + -1
                        k = u.slot % 2
                        act.wait_ge(t_pe, u.times(2, 4))
                        act.wait_ge(o_pe, u.times(1))
                        act.activation(ET[k][:, 4:8, :].rearrange("p j n -> p (j n)"), psE[:, HALF:], ACT.Copy).then_inc(t_act, 1)
                    if live[0]:
                        act.wait_ge(t_pe, t.times(2))
                        act.wait_ge(c_pe, t.times(1))
                        k = t.slot % 2
                        act.wait_ge(m_dve, t.times(2, 2))
                        act.activation(Ec[k][:], psC[:, k * CTX:(k + 1) * CTX], ACT.Exp, bias=nm[k][:]).then_inc(e_act, 1)
                        act.activation(E[k][:], psS[k][:], ACT.Exp, bias=nm[k][:]).then_inc(e_act, 1)
                    if live[1]:
                        u = t + -1
                        act.wait_ge(c_pe, u.times(1, 2))
                        act.activation(ET[u.slot % 2][0:CTX, TB, :], psC[0:CTX, P:2 * P], ACT.Copy).then_inc(c_act, 1)

                batches(act, lambda units, k, o: units(turn, UNITS, 1, STEP))

            @block.vector
            def _(dve):
                def turn(t, live):
                    if live[0]:
                        k = t.slot % 2
                        dve.wait_ge(s_pe, t.times(1, 1 + LH))
                        dve.tensor_reduce(mx[k][:, 0:1], psS[k][:], AX, ALU.max)
                        dve.tensor_reduce(mx[k][:, 1:2], psC[:, k * CTX:(k + 1) * CTX], AX, ALU.max).then_inc(m_dve, 1)
                        dve.wait_ge(m_dve, t.times(2, 1))
                        dve.wait_ge(e_act, t.times(2))
                        dve.tensor_scalar(nm[k][:], mx[k][:, 0:1], mx[k][:, 1:2], -1.0, ALU.max, ALU.mult).then_inc(m_dve, 1)
                    if live[1]:
                        u = t + -1
                        dve.wait_ge(t_pe, u.times(2, 3))
                        dve.wait_ge(o_pe, u.times(1))
                        dve.tensor_copy(ET[u.slot % 2][:, 0:4, :].rearrange("p j n -> p (j n)"), psE[:, 0:HALF]).then_inc(t_dve, 1)
                    if live[2]:
                        u = t + -2
                        h, k = u.slot % LH, u.slot % 2
                        dve.wait_ge(o_pe, u.times(1, 2))
                        mine, other = (slice(LD * r, LD * r + LD) for r in (h % 2, 1 - h % 2))
                        out = psO[:, h * P:(h + 1) * P]
                        dve.reciprocal(rc[k][mine, :], out[other, :]).then_inc(o_dve, 1)
                        dve.wait_ge(o_dve, u.times(2, 1))
                        tile = In(At(u.base // LH, u.n, STEP // LH), u.o, u.k, TB).times(P)
                        dve.tensor_tensor(AO[mine, h // 2, bass.ds(tile, P)], out[mine, :], rc[k][mine, :], ALU.mult).then_inc(o_dve, 1)

                batches(dve, lambda units, k, o: units(turn, UNITS, 2, STEP))


HC = 4
TAKEN = S // 2


def choose(nc, a, keep, sems):
    X, ident, HT, SEL, SELB = (keep[k] for k in ("X", "ident", "HT", "SEL", "SELB"))
    NB = NT // BLK
    RE = B * EX
    BITS = 31
    with ExitStack() as ctx:
        m = Mem(nc, ctx)
        sb = lambda name, shape, dt=F32: m.sb(f"f1_{name}", shape, dt)
        xs = [sb(f"xs{k}", [P, BLK, D]) for k in range(2)]
        xt = [sb(f"xt{k}", [P, DC, HALF]) for k in range(2)]
        XT = sb("XT", [P, DC, B * S])
        w1, b1, wg, bg = sb("w1", [P, DC, HC * P]), sb("b1", [P, HC]), sb("wg", [P, DC, EX]), sb("bg", [P, EX])
        iota = sb("iota", [P, EX])
        G = [P, NT, EX]
        logit, less, ex, gate, hot1, hot2, hot, masked = (sb(n, G) for n in ("logit", "less", "ex", "gate", "hot1", "hot2", "hot", "masked"))
        top, ix = sb("top", [P, NT, 8]), sb("ix", [P, NT, 8], U32)
        ixf, mx, sm, rc = sb("ixf", [P, NT, 2]), sb("mx", [P, NT]), sb("sm", [P, NT]), sb("rc", [P, NT])
        den = [sb(f"den{k}", [P, TB, EX]) for k in range(4)]
        rden = sb("rden", [P, TB, EX])
        route, routes = sb("route", [P, TB, B, EX]), sb("routes", [P, TB, B, EX])
        v, gt, eq, rank, tie = (sb(n, [RE, S]) for n in ("v", "gt", "eq", "rank", "tie"))
        sel, selb = sb("sel", [RE, S]), sb("selb", [RE, S], BF16)
        bits_i, bits_f = sb("bits_i", [RE, BITS], I32), sb("bits_f", [RE, BITS])
        T, cand, gain = sb("T", [RE, 1], I32), sb("cand", [RE, 1], I32), sb("gain", [RE, 1], I32)
        cnt, above, room = sb("cnt", [RE, 1]), sb("above", [RE, 1]), sb("room", [RE, 1])
        psT = m.ps("f1_psT", BLK * D)
        psG = m.ps("f1_psG", HALF)
        psR = m.ps("f1_psR", S)
        psH = [m.ps(f"f1_psH{k}", HALF) for k in range(3)]
        sem = lambda name: sems.sem(f"f1_{name}")
        loaded = sem("loaded")
        xs_in = [sem(f"xs_in{k}") for k in range(2)]
        x_pe = sem("x_pe")
        x_act = sem("x_act")
        kept = [sem(f"kept{k}") for k in range(2)]
        g_pe = sem("g_pe")
        done = sem("done")
        exps = sem("exps")
        r_pe = sem("r_pe")
        h_pe = sem("h_pe")
        h_act = sem("h_act")
        found = sem("found")
        stored = sem("chosen")
        passed = sem("passed")
        NLESS, NROUTE = 3, 21
        with nc.Block() as block:
            @block.sync
            def _(sp):
                for dst, src in ((w1[:], a["L1f_w1"]), (b1[:], a["L1f_b1"]), (wg[:], a["L1f_wg"]),
                                 (bg[:], a["L1_ffn_w_gate_b"].rearrange("(o d) -> o d", o=1).broadcast_to([P, EX])),
                                 (iota[:], a["iota8"].broadcast_to([P, EX])),
                                 (bits_i[:], a["bits_i"].broadcast_to([RE, BITS])), (bits_f[:], a["bits_f"].broadcast_to([RE, BITS]))):
                    sp.dma_start(dst, src).then_inc(loaded, 16)

                def turn(t, live):
                    u = t + -1
                    if live[0]:
                        if t.base >= 2 or t.n is not None:
                            sp.wait_ge(x_pe, (t + -1).times(1))
                        sp.dma_start(xs[t.slot][:], X[:, t.span(BLK), :]).then_inc(xs_in[t.slot], 16)
                    if live[1]:
                        sp.wait_ge(x_act, u.times(1, 1))
                        sp.dma_start(XT[:, :, u.span(HALF)], xt[u.slot][:]).then_inc(kept[u.slot], 16)

                run_turns(sp, turn, NB, 1, 2)
                sp.wait_ge(done, NROUTE + 7)
                sp.dma_start(SEL, sel[:]).then_inc(stored, 16)
                sp.dma_start(SELB, selb[:]).then_inc(stored, 16)
                sp.wait_ge(stored, 32)

            @block.tensor
            def _(pe):
                pe.wait_ge(loaded, 112)

                def turn(t, live):
                    u = t + -1
                    if live[0]:
                        pe.wait_ge(xs_in[t.slot], t.over(16, 16))
                        pe.wait_ge(x_act, t.times(1))
                        for c in range(DC):
                            for k in range(BLK):
                                last = pe.transpose(psT[:, (c * BLK + k) * P:(c * BLK + k + 1) * P], xs[t.slot][:, k, c * P:(c + 1) * P], ident[:])
                        last.then_inc(x_pe, 1)
                    if live[1]:
                        pe.wait_ge(x_act, u.times(1, 1))
                        for k in range(BLK):
                            for c in range(DC):
                                col = slice((u.base * BLK + k) * EX, (u.base * BLK + k + 1) * EX) if u.n is None \
                                    else bass.ds(u.times(BLK * EX, k * EX), EX)
                                last = pe.matmul(psG[:, col], xt[u.slot][:, c, k * P:(k + 1) * P], wg[:, c, :],
                                                 start=(c == 0), stop=(c == DC - 1))
                        last.then_inc(g_pe, 1)

                run_turns(pe, turn, NB, 1, 2)
                for k in range(2):
                    pe.wait_ge(kept[k], 16 * (NB // 2))

                def hidden_block(i):
                    for h in range(HC):
                        n = i * HC + h
                        pe.wait_ge(h_act, n + 1)
                        for c in range(DC):
                            last = pe.matmul(psH[n % 3][:], w1[:, c, h * P:(h + 1) * P], XT[:, c, i * HALF:(i + 1) * HALF],
                                             start=(c == 0), stop=(c == DC - 1))
                        last.then_inc(h_pe, 1)

                hidden_block(0)
                hidden_block(1)
                pe.wait_ge(done, NROUTE)
                for t in range(TB):
                    last = pe.transpose(psR[0:RE, t * P:(t + 1) * P], routes[:, t, :, :].rearrange("p b e -> p (b e)"), ident[:])
                last.then_inc(r_pe, 1)
                for i in range(2, NB):
                    hidden_block(i)

            @block.scalar
            def _(act):
                act.sem_inc(h_act, 3)
                act.wait_ge(loaded, 112)

                def turn(t, live):
                    act.wait_ge(x_pe, t.times(1, 1))
                    if t.base >= 2 or t.n is not None:
                        act.wait_ge(kept[t.slot], t.over(16))
                        act.wait_ge(g_pe, (t + -1).times(1))
                    act.activation(xt[t.slot][:].rearrange("p c n -> p (c n)"), psT[:], ACT.Copy).then_inc(x_act, 1)

                run_turns(act, turn, NB, 0, 2, 2)
                act.wait_ge(done, NLESS)
                act.activation(ex[:], less[:], ACT.Exp).then_inc(exps, 1)
                for n in range(NB * HC):
                    act.wait_ge(h_pe, n + 1)
                    act.activation(HT[:, n % HC, n // HC * HALF:(n // HC + 1) * HALF], psH[n % 3][:], ACT.Gelu,
                                   bias=b1[:, n % HC:n % HC + 1]).then_inc(h_act, 1)

            @block.vector
            def _(dve):
                s = Chain(dve, done)
                dve.wait_ge(loaded, 112)
                dve.wait_ge(g_pe, NB)
                s.did(dve.tensor_tensor(logit[:], psG[:, 0:NT * EX].rearrange("p (t e) -> p t e", e=EX),
                                        bg[:].unsqueeze(1).broadcast_to(G), ALU.add))
                s.wait()
                s.did(dve.tensor_reduce(mx[:], logit[:], AX, ALU.max))
                s.wait()
                s.did(dve.tensor_tensor(less[:], logit[:], mx[:].unsqueeze(2).broadcast_to(G), ALU.subtract))
                assert s.n == NLESS
                dve.wait_ge(exps, 1)
                s.did(dve.tensor_reduce(sm[:], ex[:], AX, ALU.add))
                s.wait()
                s.did(dve.reciprocal(rc[:], sm[:]))
                s.wait()
                s.did(dve.tensor_tensor(gate[:], ex[:], rc[:].unsqueeze(2).broadcast_to(G), ALU.mult))
                s.wait()
                for t in range(NT):
                    last = dve.max(top[:, t, :], gate[:, t, :])
                s.did(last)
                s.wait()
                for t in range(NT):
                    last = dve.max_index(ix[:, t, :], top[:, t, :], gate[:, t, :])
                s.did(last)
                s.wait()
                s.did(dve.tensor_copy(ixf[:], ix[:, :, 0:2]))
                s.wait()
                for n, hot_n in ((0, hot1), (1, hot2)):
                    s.did(dve.tensor_tensor(hot_n[:], iota[:].unsqueeze(1).broadcast_to(G), ixf[:, :, n:n + 1].broadcast_to(G), ALU.is_equal))
                s.wait()
                s.did(dve.tensor_tensor(hot[:], hot1[:], hot2[:], ALU.add))
                s.wait()
                s.did(dve.tensor_tensor(masked[:], gate[:], hot[:], ALU.mult))
                s.wait()
                mb = masked[:].rearrange("p (b t) e -> p b t e", b=B)
                s.did(dve.tensor_tensor(den[0][:], mb[:, 0], mb[:, 1], ALU.add))
                for n in (2, 3):
                    s.wait()
                    s.did(dve.tensor_tensor(den[n - 1][:], den[n - 2][:], mb[:, n], ALU.add))
                s.wait()
                s.did(dve.tensor_scalar(den[3][:], den[2][:], 1e-6, None, ALU.add))
                s.wait()
                s.did(dve.reciprocal(rden[:], den[3][:]))
                s.wait()
                for b in range(B):
                    last = dve.tensor_tensor(route[:, :, b, :], mb[:, b], rden[:], ALU.mult)
                s.did(last)
                s.wait()
                s.did(dve.tensor_scalar(routes[:], route[:], float(B), None, ALU.mult))
                s.did(dve.memset(T[:], 0))
                assert s.n == NROUTE, s.n
                dve.wait_ge(r_pe, 1)
                s.did(dve.tensor_copy(v[:], psR[0:RE, :]))
                s.wait()
                with dve.Fori(0, BITS) as i:
                    dve.wait_ge(found, i * 4)
                    dve.tensor_tensor(cand[:], T[:], bits_i[:, bass.ds(i, 1)], ALU.bitwise_or).then_inc(found, 1)
                    dve.wait_ge(found, i * 4 + 1)
                    dve.tensor_scalar(gt[:], v[:], cand[:].bitcast(F32), None, ALU.is_ge, ALU.add, accum_out=cnt[:]).then_inc(found, 1)
                    dve.wait_ge(found, i * 4 + 2)
                    dve.scalar_tensor_tensor(out=gain[:], in0=cnt[:], scalar=float(TAKEN), in1=bits_f[:, bass.ds(i, 1)],
                                             op0=ALU.is_ge, op1=ALU.mult).then_inc(found, 1)
                    dve.wait_ge(found, i * 4 + 3)
                    dve.tensor_tensor(T[:], T[:], gain[:], ALU.bitwise_or).then_inc(found, 1)
                dve.wait_ge(found, BITS * 4)
                T_f = T[:].bitcast(F32)
                s.did(dve.tensor_scalar(gt[:], v[:], T_f, None, ALU.is_gt, ALU.add, accum_out=above[:]))
                s.did(dve.tensor_scalar(eq[:], v[:], T_f, None, ALU.is_equal))
                s.wait()
                s.did(dve.tensor_scalar(room[:], above[:], -1.0, float(TAKEN), ALU.mult, ALU.add))
                s.did(dve.tensor_tensor_scan(rank[:], eq[:], eq[:], 0.0, ALU.add, ALU.bypass))
                s.wait()
                s.did(dve.scalar_tensor_tensor(out=tie[:], in0=rank[:], scalar=room[:], in1=eq[:], op0=ALU.is_le, op1=ALU.mult))
                s.wait()
                dve.tensor_tensor(selb[:], tie[:], gt[:], ALU.add)
                s.did(dve.tensor_tensor(sel[:], tie[:], gt[:], ALU.add))
                assert s.n == NROUTE + 7, s.n


def take(nc, a, keep, sems):
    X, HT, SEL, SELB = (keep[k] for k in ("X", "HT", "SEL", "SELB"))
    NB = NT // BLK
    with ExitStack() as ctx:
        m = Mem(nc, ctx)
        sb = lambda name, shape, dt=F32: m.sb(f"f1t_{name}", shape, dt)
        w2, b2 = sb("w2", [P, HC, D]), sb("b2", [EX, D])
        sw = [sb(f"sw{k}", [P, HC, HALF], BF16) for k in range(2)]
        sk = [sb(f"sk{k}", [EX, HALF]) for k in range(2)]
        hm = [sb(f"hm{k}", [P, HC, HALF]) for k in range(2)]
        y = sb("y", [P, BLK, D])
        st, mv, sd, rs, eps = sb("st", [P, BLK, 6]), sb("mv", [P, BLK, 2]), sb("sd", [P, BLK]), sb("rs", [P, BLK]), sb("eps", [P, 1])
        psY = [m.ps(f"f1t_psY{k}", BLK * D) for k in range(2)]
        sem = lambda name: sems.sem(f"f1t_{name}")
        loaded, const = sem("loaded"), sem("const")
        s_in = [sem(f"s_in{k}") for k in range(2)]
        h_dve = sem("h_dve")
        y_pe = sem("y_pe")
        n_dve = sem("n_dve")
        n_act = sem("n_act")
        passed = sem("passed")
        with nc.Block() as block:
            @block.sync
            def _(sp):
                for dst, src in ((w2[:], a["L1f_w2"]), (b2[:], a["L1_ffn_b2"])):
                    sp.dma_start(dst, src).then_inc(loaded, 16)

                def turn(t, live):
                    if t.base >= 2 or t.n is not None:
                        sp.wait_ge(h_dve, (t + -1).times(1))
                        sp.wait_ge(y_pe, (t + -1).times(1))
                    n = slice(t.slot * HALF, (t.slot + 1) * HALF)
                    b = t.over(1) if t.n is None else bass.ds(t.over(1), 1)
                    b = slice(b, b + 1) if t.n is None else b
                    for e in range(2):
                        src = SELB.rearrange("(b c e) n -> e b c n", b=B, e=2)[e][b, :, n]
                        sp.dma_start(sw[t.slot][64 * e:64 * e + 64, :, :], src.broadcast_to([64, HC, HALF])).then_inc(s_in[t.slot], 16)
                    sp.dma_start(sk[t.slot][:], SEL.rearrange("(b e) n -> b e n", b=B)[b, :, n].rearrange("o e n -> (o e) n"))\
                        .then_inc(s_in[t.slot], 16)

                run_turns(sp, turn, NB, 0, 2, 2)

            @block.tensor
            def _(pe):
                pe.wait_ge(loaded, 32)

                def turn(t, live):
                    pe.wait_ge(h_dve, t.times(1, 1))
                    pe.wait_ge(s_in[t.slot], t.over(48, 48))
                    if t.base >= 2 or t.n is not None:
                        pe.wait_ge(n_dve, (t + -2).times(5, 1))
                    for k in range(BLK):
                        out = psY[t.slot][:, k * D:(k + 1) * D]
                        pe.matmul(out, sk[t.slot][:, k * P:(k + 1) * P], b2[:], start=True, stop=False)
                        for c in range(HC):
                            last = pe.matmul(out, hm[t.slot][:, c, k * P:(k + 1) * P], w2[:, c, :], start=False, stop=(c == HC - 1))
                    last.then_inc(y_pe, 1)

                run_turns(pe, turn, NB, 0, 2, 2)

            @block.scalar
            def _(act):
                act.wait_ge(const, 1)
                with act.Fori(0, NB) as i:
                    act.wait_ge(n_dve, i * 5 + 3)
                    act.activation(sd[:], mv[:, :, 1], ACT.Sqrt, bias=eps[:]).then_inc(n_act, 1)

            @block.vector
            def _(dve):
                dve.memset(eps[:], LN_EPS).then_inc(const, 1)

                def turn(t, live):
                    u = t + -1
                    if live[0]:
                        dve.wait_ge(s_in[t.slot], t.over(48, 48))
                        if t.base >= 2 or t.n is not None:
                            dve.wait_ge(y_pe, (t + -1).times(1))
                        dve.tensor_tensor(hm[t.slot][:], HT[:, :, t.span(HALF)], sw[t.slot][:], ALU.mult).then_inc(h_dve, 1)
                    if live[1]:
                        dve.wait_ge(y_pe, u.times(1, 1))
                        dve.wait_ge(n_dve, u.times(5))
                        dve.tensor_tensor(y[:], psY[u.slot][:].rearrange("p (k d) -> p k d", k=BLK), X[:, u.span(BLK), :],
                                          ALU.add).then_inc(n_dve, 1)
                        dve.wait_ge(n_dve, u.times(5, 1))
                        for k in range(BLK):
                            last = dve.bn_stats(st[:, k, :], y[:, k, :])
                        last.then_inc(n_dve, 1)
                        dve.wait_ge(n_dve, u.times(5, 2))
                        dve.sem_inc(passed, 1)
                        for k in range(BLK):
                            last = dve.bn_aggr(mv[:, k, :], st[:, k, :])
                        last.then_inc(n_dve, 1)
                        dve.wait_ge(n_act, u.times(1, 1))
                        dve.reciprocal(rs[:], sd[:]).then_inc(n_dve, 1)
                        dve.wait_ge(n_dve, u.times(5, 4))
                        for k in range(BLK):
                            out = X[:, bass.ds(u.times(BLK, k), 1) if u.n is not None else slice(u.times(BLK, k), u.times(BLK, k) + 1), :]
                            last = dve.tensor_scalar(out.rearrange("p o d -> p (o d)"), y[:, k, :], mv[:, k, 0:1], rs[:, k:k + 1],
                                                     ALU.subtract, ALU.mult)
                        last.then_inc(n_dve, 1)

                run_turns(dve, turn, NB, 1, 2, 2)


def store(nc, a, keep, sems):
    out = sems.sem("stored")
    with nc.Block() as block:
        @block.sync
        def _(sp):
            sp.dma_start(a["y"].rearrange("(t p) d -> p t d", p=P), keep["X"][:]).then_inc(out, 16)
            sp.wait_ge(out, 16)


def attention(nc, a, keep, sems, layer, dh, groups):
    with nc.cleanup_on_exit(), ExitStack() as own:
        w = 4 * DV * 16 // groups
        mem = Mem(nc, own)
        keep["VA"] = mem.sb(f"L{layer}_VA", [P, groups, TB, w])
        project(nc, a, keep, sems, f"L{layer}", dh // 2, groups)
        keep["AO"] = mem.sb(f"L{layer}_AO", [P, groups, TB, w])
        attend(nc, a, keep, sems, f"L{layer}", dh, groups, layer == 0)
        merge(nc, a, keep, sems, f"L{layer}", groups, layer == 1)


def cross_attention(nc, a, keep, sems):
    with nc.cleanup_on_exit(), ExitStack() as own:
        mem = Mem(nc, own)
        keep["KT"] = mem.sb("L0x_KT", [P, DC, B, 64])
        keep["VBD"] = mem.sb("L0x_VBD", [P, B, H // 2, 2 * (DV + 1)])
        for name in ("bq", "bo", "lg", "lb"):
            keep[name] = mem.sb(f"L0x_{name}", [P, D])
        keep["heads8"] = mem.sb("L0x_heads8", [P, 8])
        cross_setup(nc, a, keep, sems)
        cross(nc, a, keep, sems)


def latent_attention(nc, a, keep, sems):
    with nc.cleanup_on_exit(), ExitStack() as own:
        mem = Mem(nc, own)
        keep["QT"], keep["KD"] = (nc.dram_tensor(n, (D, B * S), F32).ap() for n in ("queries", "keys"))
        keep["ones1"], keep["maskrow"] = mem.sb("L1x_ones", [1, P]), mem.sb("L1x_maskrow", [1, B * CTX])
        keep["kTc"], keep["Vc"] = mem.sb("L1x_kTc", [P, DC, B, CTX]), mem.sb("L1x_Vc", [CTX, B, LH, LD])
        keep["gam"] = mem.sb("L1x_gam", [P, 2 * LD])
        keep["VL"] = mem.sb("L1x_VL", [P, NT, LH, LD])
        context_keys(nc, a, keep, sems)
        latent_project(nc, a, keep, sems)
        keep["AO"] = mem.sb("L1x_AO", [P, DC, B * S])
        latent_attend(nc, a, keep, sems)
        merge(nc, a, keep, sems, "L1x", 1, False, bias="L1_xattn_bo")


def expert_choice(nc, a, keep, sems):
    with nc.cleanup_on_exit(), ExitStack() as own:
        keep["SEL"] = nc.dram_tensor("choice", (B * EX, S), F32).ap()
        keep["SELB"] = nc.dram_tensor("choice_bf16", (B * EX, S), BF16).ap()
        keep["HT"] = Mem(nc, own).sb("L1f_HT", [P, HC, B * S])
        choose(nc, a, keep, sems)
        take(nc, a, keep, sems)


def decoder(nc, a, stages=None):
    with ExitStack() as ctx:
        sems = Mem(nc, ctx)
        keep = {"X": sems.sb("X", [P, NT, D]), "ident": sems.sb("ident", [P, P]), "identb": sems.sb("identb", [P, P], BF16)}
        keep["PT"] = [nc.dram_tensor(f"parts_{n}", (3, B * D, S), BF16).ap() for n in "qk"]
        load_start(nc, a, keep, sems)
        for name, sublayer, args in (("A0", attention, (0, 16, 16)), ("X0", cross_attention, ()), ("M0", experts, ()),
                                     ("A1", attention, (1, 8, 32)), ("X1", latent_attention, ()), ("F1", expert_choice, ())):
            if stages is None or name in stages:
                sublayer(nc, a, keep, sems, *args)
        store(nc, a, keep, sems)


def layouts(x):
    o = {k: np.ascontiguousarray(v) for k, v in x.items()}
    f = {}

    def chunked(wt):
        return np.ascontiguousarray(wt.reshape(-1, P, wt.shape[1]).transpose(1, 0, 2))

    f["x"] = o["x"].reshape(B * S, D)
    f["ident"] = np.eye(P, dtype=np.float32)
    q, k = np.arange(P)[:, None], np.arange(P)[None, :]
    upper = np.where(k > q, np.float32(MASKED), np.float32(0))
    f["causal"] = np.ascontiguousarray(np.stack([upper, upper.T], 1)).astype(np.float32)
    t = np.arange(S, dtype=np.float32)
    for layer, ne in ((0, 8), (1, 4)):
        ns = 64 // ne
        c, h, s, e = np.meshgrid(np.arange(DC), np.arange(2), np.arange(ns), np.arange(ne), indexing="ij")
        inner = h * ne + e if layer == 0 else 2 * e + h
        order = ((c * ns + s) * 2 * ne + inner).reshape(-1)
        wq, wk = (o[f"L{layer}_attn_W{n}"][order] for n in "qk")
        f[f"L{layer}_wqk"] = chunked(np.concatenate([wq, wk], 0).T)
        f[f"L{layer}_wv"] = chunked(o[f"L{layer}_attn_Wv"].T)
        f[f"L{layer}_wo"] = chunked(o[f"L{layer}_attn_Wo"].T)
        if layer == 0:
            speed = np.float32(1) / np.power(np.float32(10000), np.arange(0, 16, 2, dtype=np.float32) / np.float32(16))
        else:
            speed = np.float32(1) / np.power(np.float32(10000), np.linspace(0, 1, 4, dtype=np.float32))
        angle = (speed.astype(np.float32)[:, None] * t[None, :]).astype(np.float32)
        f[f"L{layer}_cos"] = np.ascontiguousarray(np.tile(np.cos(angle), (P // ne, 1))).astype(np.float32)
        sin = np.tile(np.sin(angle), (64 // ne, 1)).astype(np.float32)
        f[f"L{layer}_sin"] = np.ascontiguousarray(np.concatenate([sin, -sin], 0))
    cT = o["ctx_768"].transpose(2, 0, 1).reshape(2, 96, B, 64)
    f["ctxT2"] = np.ascontiguousarray(np.concatenate([cT, cT], 3).transpose(1, 0, 2, 3))
    wkv = np.concatenate([o["L0_xattn_Wk"], o["L0_xattn_Wv"]], 1)
    f["L0x_wkv"] = np.ascontiguousarray(wkv.reshape(2, 96, 2 * D).transpose(1, 0, 2))
    f["L0x_wq"], f["L0x_wo"] = chunked(o["L0_xattn_Wq"]), chunked(o["L0_xattn_Wo"])
    for n in ("bq", "bk", "bv", "bo", "ln_gamma", "ln_beta"):
        f[f"L0_xattn_{n}"] = o[f"L0_xattn_{n}"]
    f["heads8"] = (np.arange(P)[:, None] // DV == np.arange(8)[None, :]).astype(np.float32)
    f["ctx_tok"] = np.ascontiguousarray(o["ctx_768"].transpose(1, 0, 2))
    f["mask8"] = o["mask_BxS2_bk0"].reshape(1, B * CTX)
    f["L1x_wkv"] = np.ascontiguousarray(o["L1_xattn_Wkv"].T.reshape(2, CK, 2 * D).transpose(1, 0, 2))
    f["L1x_w"] = chunked(np.concatenate([o["L1_xattn_Wq"], o["L1_xattn_Wlkv"]], 0).T)
    f["L1x_wo"] = chunked(o["L1_xattn_Wo"].T)
    for n in ("ln_x_g", "ln_x_b", "ln_l_g", "ln_l_b", "qn_g", "kn_g", "bo"):
        f[f"L1_xattn_{n}"] = o[f"L1_xattn_{n}"]
    f["L1f_w1"] = chunked(o["L1_ffn_W1"].transpose(1, 0, 2).reshape(D, HC * P))
    f["L1f_b1"] = np.ascontiguousarray(o["L1_ffn_b1"].reshape(HC, P).T)
    f["L1f_w2"] = chunked(o["L1_ffn_W2"].reshape(HC * P, D))
    f["L1f_wg"] = chunked(o["L1_ffn_w_gate_w"])
    f["bits_i"] = (1 << np.arange(30, -1, -1)).astype(np.int32)[None, :]
    f["bits_f"] = f["bits_i"].astype(np.float32)
    for n in ("w_gate_b", "b2"):
        f[f"L1_ffn_{n}"] = o[f"L1_ffn_{n}"]
    f["L0f_we"] = chunked(o["L0_ffn_We"].transpose(1, 0, 2).reshape(D, EX * D))
    f["L0f_wr"] = chunked(o["L0_ffn_Wr"].T)
    f["tri"] = np.triu(np.ones((P, P), np.float32), 1)
    f["iota8"] = np.arange(EX, dtype=np.float32)[None, :]
    f["L1_lambda"] = np.stack([o[f"L1_attn_lambda_{n}"] for n in ("q1", "k1", "q2", "k2")])
    f["L1_attn_rms_weight"] = o["L1_attn_rms_weight"]
    return f


def kernel(**inputs):
    import concourse.bacc as bacc
    from concourse.bass_utils import run_bass_kernel_spmd

    nc = bacc.Bacc("TRN2", target_bir_lowering=False, num_devices=1)
    arrays, a = {}, {}
    for name, value in layouts({k: np.asarray(v) for k, v in inputs.items()}).items():
        arrays[f"in_{name}"] = value
        a[name] = nc.dram_tensor(f"in_{name}", value.shape, mybir.dt.from_np(value.dtype), kind="ExternalInput").ap()
    a["y"] = nc.dram_tensor("out_y", (B * S, D), F32, kind="ExternalOutput").ap()
    decoder(nc, a)
    result = run_bass_kernel_spmd(nc, [arrays], core_ids=[0])
    return result.results[0]["out_y"].reshape(B, S, D)
```

```python
import math
from contextlib import ExitStack

import numpy as np
import concourse.bass as bass
from concourse import mybir

F32 = mybir.dt.float32
BF16 = mybir.dt.bfloat16
I32 = mybir.dt.int32
U32 = mybir.dt.uint32
ALU = mybir.AluOpType
ACT = mybir.ActivationFunctionType
AX = mybir.AxisListType.X

P = 128
B, S, D = 4, 1024, 256
NT = B * S // P
TB = S // P
DC = D // P
HALF = 512
H = 16
DV = D // H
LN_EPS = 1e-5
MASKED = -1.0e30
LOWEST = -3.0e38
SPLIT_Q = [0, 0, 1, 1, 0, 2]
SPLIT_K = [0, 1, 0, 1, 2, 0]
MAX_ROW = 96
STACK = MAX_ROW + 3


class Mem:

    def __init__(self, nc, ctx):
        self.nc, self.ctx, self.n = nc, ctx, 0

    def sb(self, name, shape, dt=F32):
        return self.ctx.enter_context(self.nc.sbuf_tensor(name, shape, dt))

    def ps(self, name, cols, dt=F32):
        return self.ctx.enter_context(self.nc.psum_tensor(name, [P, cols], dt))

    def sem(self, name):
        return self.nc.alloc_semaphore(name=name)


class At:

    def __init__(self, base, n=None, step=3):
        self.base, self.n, self.step = base, n, step

    def __add__(self, k):
        return At(self.base + k, self.n, self.step)

    def times(self, a, b=0):
        if self.n is None:
            return a * self.base + b
        return self.n * (self.step * a) + (a * self.base + b)

    def over(self, a, b=0):
        whole = a * (self.base // self.step) + b
        return whole if self.n is None else self.n * a + whole

    def span(self, width=1):
        if self.n is None:
            return slice(self.base * width, (self.base + 1) * width)
        return bass.ds(self.times(width), width)

    @property
    def slot(self):
        return self.base % self.step


def run_turns(eng, turn, count, lag, step, first=0):
    peeled = lag + first + (count - lag - first) % step
    for t in range(peeled):
        turn(At(t, None, step), [t >= j for j in range(lag + 1)])
    if count > peeled:
        with eng.Fori(0, (count - peeled) // step) as n:
            for k in range(step):
                turn(At(peeled + k, n, step), [True] * (lag + 1))
    for t in range(count, count + lag):
        turn(At(t, None, step), [t - j < count for j in range(lag + 1)])


class Chain:

    def __init__(self, eng, sem):
        self.eng, self.sem, self.n = eng, sem, 0

    def did(self, ins):
        self.n += 1
        ins.then_inc(self.sem, 1)

    def wait(self):
        self.eng.wait_ge(self.sem, self.n)


class Steps:

    def __init__(self, eng, sem, item, per, k=0):
        self.eng, self.sem, self.item, self.per, self.k = eng, sem, item, per, k

    def did(self, ins):
        self.k += 1
        assert self.k <= self.per
        ins.then_inc(self.sem, 1)

    def wait(self):
        self.eng.wait_ge(self.sem, self.item.times(self.per, self.k))


def load_start(nc, a, keep, sems):
    X, ident, identb = keep["X"], keep["ident"], keep["identb"]
    loaded = sems.sem("start_loaded")
    with nc.Block() as block:
        @block.sync
        def _(sp):
            sp.dma_start(X[:], a["x"].rearrange("(t p) d -> p t d", p=P)).then_inc(loaded, 16)
            sp.dma_start(ident[:], a["ident"]).then_inc(loaded, 16)

        @block.vector
        def _(dve):
            dve.wait_ge(loaded, 32)
            dve.tensor_copy(identb[:], ident[:])


def project(nc, a, keep, sems, tag, ne, groups):
    ns = 64 // ne
    gb = groups // B
    w = D // gb
    X, ident, VA = keep["X"], keep["ident"], keep["VA"]
    PT = keep["PT"]
    with ExitStack() as ctx:
        m = Mem(nc, ctx)
        xs = [m.sb(f"{tag}_proj_xs{k}", [P, TB, D]) for k in range(2)]
        xt = [m.sb(f"{tag}_proj_xt{k}", [P, DC, S]) for k in range(2)]
        wqk = m.sb(f"{tag}_proj_wqk", [P, DC, 2 * D])
        wv = m.sb(f"{tag}_proj_wv", [P, DC, D])
        cos = m.sb(f"{tag}_proj_cos", [P, S])
        sin = m.sb(f"{tag}_proj_sin", [P, S])
        t1 = [m.sb(f"{tag}_proj_t1{k}", [P, HALF]) for k in range(2)]
        t2 = [m.sb(f"{tag}_proj_t2{k}", [P, HALF]) for k in range(2)]
        rot = [m.sb(f"{tag}_proj_rot{k}", [P, HALF]) for k in range(4)]
        rest = [m.sb(f"{tag}_proj_rest{k}", [P, HALF]) for k in range(4)]
        parts = [m.sb(f"{tag}_proj_parts{k}", [P, 3, S], BF16) for k in range(4)]
        psT = [m.ps(f"{tag}_proj_psT{k}", HALF) for k in range(2)]
        psQ = [m.ps(f"{tag}_proj_psQ{k}", HALF) for k in range(2)]
        psV = [m.ps(f"{tag}_proj_psV{k}", HALF) for k in range(2)]
        weights = sems.sem(f"{tag}_proj_weights")
        xs_in = [sems.sem(f"{tag}_proj_xs_in{k}") for k in range(2)]
        turned = sems.sem(f"{tag}_proj_turned")
        xt_in = sems.sem(f"{tag}_proj_xt_in")
        qk_done = sems.sem(f"{tag}_proj_qk_done")
        qk_read = sems.sem(f"{tag}_proj_qk_read")
        added = sems.sem(f"{tag}_proj_added")
        hi = sems.sem(f"{tag}_proj_hi")
        less = sems.sem(f"{tag}_proj_less")
        mid = sems.sem(f"{tag}_proj_mid")
        low = sems.sem(f"{tag}_proj_low")
        out = [sems.sem(f"{tag}_proj_out{k}") for k in range(4)]
        v_done = sems.sem(f"{tag}_proj_v_done")
        v_read = sems.sem(f"{tag}_proj_v_read")
        PERB = 8
        N = 2 * PERB
        OUT = 96
        with nc.Block() as block:
            @block.sync
            def _(sp):
                for k in range(2):
                    sp.dma_start(xs[k][:], X[:, k * TB:(k + 1) * TB, :]).then_inc(xs_in[k], 16)
                    if k == 0:
                        sp.dma_start(wqk[:], a[f"{tag}_wqk"]).then_inc(weights, 16)
                        sp.dma_start(wv[:], a[f"{tag}_wv"]).then_inc(weights, 16)
                        sp.dma_start(cos[:], a[f"{tag}_cos"]).then_inc(weights, 16)
                        sp.dma_start(sin[:], a[f"{tag}_sin"]).then_inc(weights, 16)
                with sp.Fori(0, B // 2) as i:
                    for u in range(N // 2):
                        k, qk, c = u // 4, u % 4 // 2, u % 2
                        sp.wait_ge(low, i * N + 2 * u + 2)
                        dst = PT[qk].rearrange("k (b c s h e) t -> k b c h s e t", b=B, c=DC, h=2, e=ne)
                        for p in range(3):
                            for h in range(2):
                                sp.dma_start(dst[p, bass.ds(2 * i + k, 1), c, h].rearrange("o s e t -> (o s) e t"),
                                             parts[u % 4][64 * h:64 * h + 64, p, :]).then_inc(out[u % 4], 16)
                for k in range(4):
                    sp.wait_ge(out[k], OUT * (N // 8) * (B // 2))
                sp.wait_ge(xs_in[0], 32)
                sp.wait_ge(xs_in[1], 48)

            @block.gpsimd
            def _(pool):
                with pool.Fori(0, B // 2) as i:
                    for n in range(N + 3):
                        if n < N:
                            pool.wait_ge(qk_read, i * (3 * N) + 6 + 3 * (n + 1))
                            pool.tensor_tensor(rot[n % 4][:], t1[n % 2][:], t2[n % 2][:], ALU.add).then_inc(added, 1)
                        if n >= 3:
                            u = n - 3
                            pool.wait_ge(mid, i * N + u + 1)
                            to = parts[u // 2 % 4]
                            col = slice((u % 2) * HALF, (u % 2 + 1) * HALF)
                            pool.tensor_tensor(to[:, 2, col], rest[u % 4][:], to[:, 1, col], ALU.subtract).then_inc(low, 1)

            @block.scalar
            def _(act):
                act.sem_inc(xt_in, 2)
                act.sem_inc(v_read, 2)

                def xt_copy(i, k, u, turns):
                    c, h = u // 2, u % 2
                    act.wait_ge(turned, i * 8 + turns + u + 1)
                    act.activation(xt[k][:, c, h * HALF:(h + 1) * HALF], psT[u % 2][:], ACT.Copy).then_inc(xt_in, 1)

                def first(i, n):
                    if n % 2 == 0:
                        act.wait_ge(out[n // 2 % 4], i * (N // 8 * OUT) + OUT * (n // 8))
                    act.wait_ge(added, i * N + n + 1)
                    act.activation(parts[n // 2 % 4][:, 0, (n % 2) * HALF:(n % 2 + 1) * HALF],
                                   rot[n % 4][:], ACT.Copy).then_inc(hi, 1)

                def second(i, n):
                    act.wait_ge(less, i * N + n + 1)
                    act.activation(parts[n // 2 % 4][:, 1, (n % 2) * HALF:(n % 2 + 1) * HALF],
                                   rest[n % 4][:], ACT.Copy).then_inc(mid, 1)

                for u in range(4):
                    xt_copy(0, 0, u, 0)
                act.dma_start(xs[0][:], X[:, 2 * TB:3 * TB, :]).then_inc(xs_in[0], 16)
                with act.Fori(0, B // 2) as i:
                    for n in range(N + 2):
                        if n < N:
                            k, j = n // PERB, n % PERB // 2
                            if n % 2 == 0:
                                xt_copy(i, 1 - k, j, 4 + 4 * k)
                                if n == 6:
                                    act.dma_start(xs[1][:], X[:, 3 * TB:4 * TB, :]).then_inc(xs_in[1], 16)
                            else:
                                act.wait_ge(v_done, i * 8 + 4 * k + j + 1)
                                src = psV[j % 2][:].rearrange("p (t g w) -> p g t w", t=2, g=gb)
                                act.activation(VA[:, bass.ds((2 * i + k) * gb, gb), 2 * j:2 * j + 2, :], src,
                                               ACT.Copy).then_inc(v_read, 1)
                            first(i, n)
                        if n >= 2:
                            second(i, n - 2)

            @block.vector
            def _(dve):
                dve.sem_inc(qk_read, 6)
                dve.wait_ge(weights, 64)

                def rotate(i, n):
                    h = n % 2
                    dve.wait_ge(qk_done, i * N + n + 1)
                    if n >= 2:
                        dve.wait_ge(added, i * N + n - 1)
                    ps, col = psQ[n % 2], slice(h * HALF, (h + 1) * HALF)
                    dve.tensor_tensor(t1[n % 2][:], ps[:], cos[:, col], ALU.mult).then_inc(qk_read, 1)
                    for q in range(2):
                        a0, b0 = 64 * q, 64 * (1 - q)
                        dve.tensor_tensor(t2[n % 2][a0:a0 + 64, :], ps[b0:b0 + 64, :], sin[b0:b0 + 64, col],
                                          ALU.mult).then_inc(qk_read, 1)

                def subtract(i, n):
                    dve.wait_ge(hi, i * N + n + 1)
                    dve.tensor_tensor(rest[n % 4][:], rot[n % 4][:],
                                      parts[n // 2 % 4][:, 0, (n % 2) * HALF:(n % 2 + 1) * HALF],
                                      ALU.subtract).then_inc(less, 1)

                with dve.Fori(0, B // 2) as i:
                    for n in range(N + 2):
                        if n < N:
                            rotate(i, n)
                        if n >= 2:
                            subtract(i, n - 2)

            @block.tensor
            def _(pe):
                pe.wait_ge(weights, 64)

                def transposes(i, k, u, turns):
                    c, h = u // 2, u % 2
                    pe.wait_ge(xt_in, i * 8 + turns + u + 1)
                    for t in range(4):
                        last = pe.transpose(psT[u % 2][:, t * P:(t + 1) * P], xs[k][:, 4 * h + t, c * P:(c + 1) * P], ident[:])
                    last.then_inc(turned, 1)

                pe.wait_ge(xs_in[0], 16)
                for u in range(4):
                    transposes(0, 0, u, 0)
                with pe.Fori(0, B // 2) as i:
                    for n in range(N):
                        k, unit = n // PERB, n % PERB
                        g, h, j = unit // 2, unit % 2, unit // 2
                        if unit == 0:
                            pe.wait_ge(xt_in, i * 8 + 4 * k + 6)
                            if k == 0:
                                pe.wait_ge(xs_in[1], i * 16 + 16)
                            else:
                                pe.wait_ge(xs_in[0], 32)
                        pe.wait_ge(qk_read, i * (3 * N) + 3 * n + 3)
                        for c in range(DC):
                            last = pe.matmul(psQ[n % 2][:], wqk[:, c, g * P:(g + 1) * P],
                                             xt[k][:, c, h * HALF:(h + 1) * HALF], start=(c == 0), stop=(c == DC - 1))
                        last.then_inc(qk_done, 1)
                        if h == 0:
                            transposes(i, 1 - k, j, 4 + 4 * k)
                        else:
                            pe.wait_ge(v_read, i * 8 + 4 * k + j + 1)
                            for t in range(2):
                                for c in range(DC):
                                    last = pe.matmul(psV[j % 2][:, t * D:(t + 1) * D],
                                                     xt[k][:, c, (2 * j + t) * P:(2 * j + t + 1) * P], wv[:, c, :],
                                                     start=(c == 0), stop=(c == DC - 1))
                            last.then_inc(v_done, 1)
def attend(nc, a, keep, sems, tag, dh, groups, causal):
    gb = groups // B
    scale = dh ** -0.5
    shared = 4 * DV // (D // gb)
    vh = 4 // shared
    VA, AO, PT, ident, identb = keep["VA"], keep["AO"], keep["PT"], keep["ident"], keep["identb"]
    steps = [(q, t, max(0, t - 4 * q) * P if causal else 0) for q in range(2) for t in range(TB)
             if not causal or t < 4 * (q + 1)]
    ends = [max(n for n, st in enumerate(steps) if st[0] == q) for q in range(2)]
    pieces = []
    for s in range(4):
        for t in range(TB):
            keys = (t + 1) * P if causal else S
            for h in range(2):
                n = min(HALF, keys - h * HALF)
                if n > 0:
                    pieces.append((s, t, h, n, causal and h * HALF + n == keys))
    NS, NPc = len(steps), len(pieces)
    per = NPc // NS
    LATE = 3
    assert NPc == per * NS
    NL = len(SPLIT_Q) * 2
    LD = 16 * NL

    with ExitStack() as ctx:
        m = Mem(nc, ctx)
        Q = [m.sb(f"{tag}_attn_Q{k}", [P, 4, S], BF16) for k in range(3)]
        K = [m.sb(f"{tag}_attn_K{k}", [P, 4, S], BF16) for k in range(3)]
        V = [m.sb(f"{tag}_attn_V{k}", [P, TB, vh, 32]) for k in range(3)]
        E = [m.sb(f"{tag}_attn_E{k}", [P, HALF]) for k in range(8)]
        mask = m.sb(f"{tag}_attn_mask", [P, 2, P])
        maskb = m.sb(f"{tag}_attn_maskb", [P, 2, P], BF16)
        tops = m.sb(f"{tag}_attn_tops", [P, 4 * TB, 2])
        negm = [m.sb(f"{tag}_attn_negm{k}", [P, 4 * TB]) for k in range(3)]
        mrest = [m.sb(f"{tag}_attn_mrest{k}", [4 * TB, 2, P]) for k in range(3)]
        mparts = [m.sb(f"{tag}_attn_mparts{k}", [4 * TB, 3, P], BF16) for k in range(3)]
        oT = [m.sb(f"{tag}_attn_oT{k}", [P, HALF]) for k in range(2)]
        rec = [m.sb(f"{tag}_attn_rec{k}", [P, 4, 4]) for k in range(2)]
        if shared == 2:
            lam4 = m.sb(f"{tag}_attn_lam4", [P, 4, dh])
            lamp = m.sb(f"{tag}_attn_lamp", [P, 2, dh])
            lams = m.sb(f"{tag}_attn_lams", [P, 2])
            lame = m.sb(f"{tag}_attn_lame", [P, 2])
            lamd = m.sb(f"{tag}_attn_lamd", [P, 1])
            neglam = m.sb(f"{tag}_attn_neglam", [P, 1])
            o1 = [m.sb(f"{tag}_attn_o1{k}", [P, 4, 2, DV]) for k in range(2)]
            o2 = [m.sb(f"{tag}_attn_o2{k}", [P, 4, 2, DV]) for k in range(2)]
        psS = [m.ps(f"{tag}_attn_psS{k}", HALF) for k in range(3)]
        psM = [m.ps(f"{tag}_attn_psM{k}", HALF) for k in range(3)]
        psO = [m.ps(f"{tag}_attn_psO{k}", HALF) for k in range(2)]
        ones = sems.sem(f"{tag}_attn_ones")
        v_blank = sems.sem(f"{tag}_attn_v_blank")
        blank = sems.sem(f"{tag}_attn_blank")
        maskin = sems.sem(f"{tag}_attn_maskin")
        masks = sems.sem(f"{tag}_attn_masks")
        ld = [sems.sem(f"{tag}_attn_ld{k}") for k in range(3)]
        mx = [sems.sem(f"{tag}_attn_mx{k}") for k in range(3)]
        v_in = sems.sem(f"{tag}_attn_v_in")
        s_done = sems.sem(f"{tag}_attn_s_done")
        e_done = sems.sem(f"{tag}_attn_e_done")
        o_done = sems.sem(f"{tag}_attn_o_done")
        o_out = sems.sem(f"{tag}_attn_o_out")
        o_back = sems.sem(f"{tag}_attn_o_back")
        o_read = sems.sem(f"{tag}_attn_o_read")
        o_rec = sems.sem(f"{tag}_attn_o_rec")
        m_done = sems.sem(f"{tag}_attn_m_done")
        m_read = sems.sem(f"{tag}_attn_m_read")
        m_neg = sems.sem(f"{tag}_attn_m_neg")
        m_cut = sems.sem(f"{tag}_attn_m_cut")
        lam = sems.sem(f"{tag}_attn_lam")
        lamin = sems.sem(f"{tag}_attn_lamin")
        NM = NPc + 1
        NR = 1 if shared == 1 else 3

        def bank(g, uses, k):
            return (g.base * uses + k) % 3

        def run(eng, turn):
            run_turns(eng, lambda t, live: turn(t, *live), groups, 2, 3)

        def in_turn(new, last):
            return range(NS if new or last else LATE + 5)

        with nc.Block() as block:
            @block.sync
            def _(sp):
                sp.dma_start(mask[:], a["causal"]).then_inc(maskin, 16)
                if shared == 2:
                    sp.dma_start(lam4[:], a[f"{tag}_lambda"].rearrange("(o k) d -> o k d", o=1).broadcast_to([P, 4, dh])).then_inc(lamin, 16)

                def load(g):
                    if g.base >= 3 or g.n is not None:
                        sp.wait_ge(s_done, (g + -2).times(4 * NS))
                    for (buf, split, src) in ((Q, SPLIT_Q, PT[0]), (K, SPLIT_K, PT[1])):
                        for j, p in enumerate(split):
                            view = src[p].rearrange("(g s e) t -> g e s t", s=4, e=dh)
                            one = view[g.span()]
                            sp.dma_start(buf[g.slot][dh * j:dh * (j + 1), :, :],
                                         one.rearrange("o e s t -> (o e) s t")).then_inc(ld[g.slot], 16)

                def turn(t, new, last, old):
                    if new:
                        load(t)
                    if last:
                        g = t + -1
                        sp.wait_ge(m_cut, g.times(5, 5))
                        for j in range(3):
                            sp.dma_start(Q[g.slot][MAX_ROW + j:MAX_ROW + j + 1, :, :],
                                         mparts[g.slot][:, j, :]).then_inc(mx[g.slot], 16)

                sp.wait_ge(blank, 1)
                run(sp, turn)
                for k in range(3):
                    n = len(range(k, groups, 3))
                    sp.wait_ge(mx[k], 48 * n)

            @block.gpsimd
            def _(pool):
                for k in range(3):
                    pool.memset(K[k][MAX_ROW:STACK, :, :], 1.0).then_inc(ones, 1)
                    pool.wait_ge(ones, k + 1)
                pool.wait_ge(blank, 1)

                def copy(g):
                    if g.base >= 3 or g.n is not None:
                        pool.wait_ge(o_done, (g + -2).times(NS, 2))
                    src = VA[:, g.span(), :, :]
                    pool.tensor_copy(V[g.slot][:, :, :, 0:DV],
                                     src.rearrange("p o t (h d) -> p (o t) h d", d=DV)).then_inc(v_in, 1)

                def turn(t, new, last, old):
                    if new:
                        copy(t)

                run(pool, turn)

            @block.scalar
            def _(act):
                act.sem_inc(e_done, 3)
                if shared == 2:
                    act.wait_ge(lam, 2)
                    act.activation(lame[:], lams[:], ACT.Exp).then_inc(lam, 1)

                def turn(t, new, last, old):
                    if not last:
                        return
                    g = t + -1
                    for n, (q, kt, c0) in enumerate(steps):
                        act.wait_ge(o_done, g.times(NS, n + 1))
                        for s in range(4):
                            act.wait_ge(s_done, g.times(4 * NS, 4 * n + s + 1))
                            act.activation(E[(4 * n + s) % 8][:, c0:], psS[bank(g, 4 * NS, 4 * n + s)][:, c0:], ACT.Exp,
                                           scale=scale).then_inc(e_done, 1)

                run(act, turn)

            @block.vector
            def _(dve):
                dve.sem_inc(o_read, 2)
                for k in range(3):
                    dve.memset(V[k][:], 0.0).then_inc(v_blank, 1)
                dve.wait_ge(v_blank, 3)
                for k in range(3):
                    dve.memset(V[k][:, :, :, DV:DV + 1], 1.0).then_inc(v_blank, 1)
                dve.wait_ge(v_blank, 6)
                if len(SPLIT_Q) * dh < MAX_ROW:
                    for k in range(3):
                        for buf in (Q, K):
                            dve.memset(buf[k][0:MAX_ROW, :, :].bitcast(U32), 0).then_inc(v_blank, 1)
                    dve.wait_ge(v_blank, 12)
                dve.memset(tops[:], LOWEST).then_inc(m_neg, 1)
                dve.wait_ge(maskin, 16)
                dve.tensor_copy(maskb[:], mask[:]).then_inc(masks, 1)
                dve.wait_ge(masks, 1)
                dve.sem_inc(blank, 1)
                dve.wait_ge(m_neg, 1)
                if shared == 2:
                    dve.wait_ge(lamin, 16)
                    pairs = lam4[:].rearrange("p (c k) d -> p c k d", c=2)
                    dve.tensor_tensor(lamp[:], pairs[:, :, 0, :], pairs[:, :, 1, :], ALU.mult).then_inc(lam, 1)
                    dve.wait_ge(lam, 1)
                    dve.tensor_reduce(lams[:], lamp[:], AX, ALU.add).then_inc(lam, 1)
                    dve.wait_ge(lam, 3)
                    dve.tensor_tensor(lamd[:], lame[:, 1:2], lame[:, 0:1], ALU.subtract).then_inc(lam, 1)
                    dve.wait_ge(lam, 4)
                    dve.tensor_scalar(neglam[:], lamd[:], -LAMBDA_INIT, None, ALU.add).then_inc(lam, 1)
                    dve.wait_ge(lam, 5)

                def evacuate(g, q):
                    dve.wait_ge(o_done, g.times(NS, 2 + ends[q] + 1))
                    dve.tensor_copy(oT[q][:], psO[q][:]).then_inc(o_out, 1)

                def normalise(g, q):
                    dve.wait_ge(o_back, g.times(2, q + 1))
                    ps = psO[q][:].rearrange("p (t s c) -> p t s c", t=4, s=4)
                    dve.reciprocal(rec[q][:], ps[:, :, :, DV]).then_inc(o_rec, 1)
                    dve.wait_ge(o_rec, g.times(2 * NR, NR * q + 1))
                    dst = AO[:, g.span(), 4 * q:4 * q + 4, :].rearrange("p o t w -> p (o t) w")
                    if shared == 1:
                        dve.tensor_tensor(dst.rearrange("p t (s c) -> p t s c", s=4), ps[:, :, :, 0:DV],
                                          rec[q][:].unsqueeze(3).broadcast_to([P, 4, 4, DV]), ALU.mult).then_inc(o_read, 1)
                        return
                    for c, o in ((1, o2), (0, o1)):
                        src = ps.rearrange("p t (h c) d -> p t h c d", c=2)[:, :, :, c, 0:DV]
                        r = rec[q][:].rearrange("p t (h c) -> p t h c", c=2)[:, :, :, c]
                        ins = dve.tensor_tensor(o[q][:], src, r.unsqueeze(3).broadcast_to([P, 4, 2, DV]), ALU.mult)
                        ins.then_inc(o_rec if c else o_read, 1)
                    dve.wait_ge(o_rec, g.times(2 * NR, NR * q + 2))
                    dve.wait_ge(o_read, g.times(2, q + 3))
                    dve.scalar_tensor_tensor(out=dst, in0=o2[q][:].rearrange("p t h d -> p t (h d)"), scalar=neglam[:],
                                             in1=o1[q][:].rearrange("p t h d -> p t (h d)"), op0=ALU.mult,
                                             op1=ALU.add).then_inc(o_rec, 1)

                def reduce(t, p):
                    s, qt, h, n, _ = pieces[p]
                    dve.wait_ge(m_done, t.times(NM, p + 1))
                    dve.tensor_reduce(tops[:, s * TB + qt, h:h + 1], psM[bank(t, NM, p)][:, 0:n], AX, ALU.max).then_inc(m_read, 1)

                def combine(t):
                    dve.wait_ge(m_read, t.times(NM, NPc))
                    dve.tensor_reduce(negm[t.slot][:], tops[:], AX, ALU.max, negate=True).then_inc(m_neg, 1)

                def cut(t):
                    r, pt, ps = mrest[t.slot], mparts[t.slot], psM[bank(t, NM, NPc)][0:4 * TB, 0:P]
                    dve.wait_ge(mx[t.slot], t.over(48))
                    dve.wait_ge(m_done, t.times(NM, NM))
                    dve.tensor_copy(pt[:, 0, :], ps).then_inc(m_cut, 1)
                    dve.wait_ge(m_cut, t.times(5, 1))
                    dve.tensor_tensor(r[:, 0, :], ps, pt[:, 0, :], ALU.subtract).then_inc(m_read, 1)
                    dve.wait_ge(m_read, t.times(NM, NM))
                    dve.tensor_copy(pt[:, 1, :], r[:, 0, :]).then_inc(m_cut, 1)
                    dve.wait_ge(m_cut, t.times(5, 2))
                    dve.tensor_tensor(r[:, 1, :], r[:, 0, :], pt[:, 1, :], ALU.subtract).then_inc(m_cut, 1)
                    dve.wait_ge(m_cut, t.times(5, 3))
                    dve.tensor_copy(pt[:, 2, :], r[:, 1, :]).then_inc(m_cut, 2)

                def turn(t, new, last, old):
                    if last:
                        cut(t + -1)
                    for n in in_turn(new, last):
                        k = n - LATE
                        if old and k == 1:
                            evacuate(t + -2, 1)
                        if old and k == 3:
                            normalise(t + -2, 1)
                        if last and k == ends[0] + 2:
                            evacuate(t + -1, 0)
                        if last and k == ends[0] + 4:
                            normalise(t + -1, 0)
                        if new:
                            for p in range(n * per, (n + 1) * per):
                                reduce(t, p)
                    if new:
                        combine(t)

                run(dve, turn)
                dve.wait_ge(o_rec, 2 * NR * groups)

            @block.tensor
            def _(pe):
                pe.sem_inc(o_done, 2)
                pe.wait_ge(ones, 3)
                pe.wait_ge(blank, 1)
                pe.wait_ge(masks, 1)

                def scores(g, n, s):
                    q, kt, c0 = steps[n]
                    Qg, Kg, ps = Q[g.slot], K[g.slot], psS[bank(g, 4 * NS, 4 * n + s)]
                    pe.wait_ge(e_done, g.times(4 * NS, 4 * n + s + 1))
                    diagonal = causal and kt >= 4 * q
                    if diagonal:
                        pe.matmul(ps[:, c0:c0 + P], identb[:], maskb[:, 1, :], start=True, stop=False, skip_group_check=True)
                    pe.matmul(ps[:, c0:], Kg[0:STACK, s, kt * P:(kt + 1) * P], Qg[0:STACK, s, q * HALF + c0:(q + 1) * HALF],
                              start=not diagonal, stop=True, skip_group_check=True).then_inc(s_done, 1)

                def product(g, n):
                    q, kt, c0 = steps[n]
                    if n == 0 or steps[n - 1][0] != q:
                        pe.wait_ge(o_read, g.times(2, q + 1))
                    if n == 0:
                        pe.wait_ge(v_in, g.times(1, 1))
                    pe.wait_ge(e_done, g.times(4 * NS, 4 * n + 4 + 3))
                    for s in range(4):
                        last = pe.matmul(psO[q][32 * s:32 * s + 32, c0:HALF], V[g.slot][:, kt, s // shared, :],
                                         E[(4 * n + s) % 8][:, c0:], start=(kt == 0), stop=(n == ends[q]),
                                         skip_group_check=True)
                    last.then_inc(o_done, 1)

                def turn_back(g, q):
                    pe.wait_ge(o_out, g.times(2, q + 1))
                    for j in range(4):
                        last = pe.transpose(psO[q][:, j * P:(j + 1) * P], oT[q][:, j * P:(j + 1) * P], ident[:])
                    last.then_inc(o_back, 1)

                def piece(t, p):
                    s, qt, h, n, masked = pieces[p]
                    if p >= 2 or t.base >= 1 or t.n is not None:
                        pe.wait_ge(m_read, t.times(NM, p - 2))
                    Qt, Kt, ps = Q[t.slot], K[t.slot], psM[bank(t, NM, p)]
                    if masked:
                        pe.matmul(ps[:, n - P:n], identb[:], maskb[:, 0, :], start=True, stop=False,
                                  skip_group_check=True)
                    last = pe.matmul(ps[:, 0:n], Qt[0:MAX_ROW, s, qt * P:(qt + 1) * P], Kt[0:MAX_ROW, s, h * HALF:h * HALF + n],
                                     start=not masked, stop=True, skip_group_check=True)
                    last.then_inc(m_done, 1)

                def turn_maxima(t):
                    pe.wait_ge(m_neg, t.times(1, 2))
                    pe.wait_ge(m_read, t.times(NM, NPc))
                    pe.transpose(psM[bank(t, NM, NPc)][0:4 * TB, 0:P], negm[t.slot][:], ident[:]).then_inc(m_done, 1)

                def turn(t, new, last, old):
                    if new:
                        pe.wait_ge(ld[t.slot], t.over(LD, LD))
                    for n in in_turn(new, last):
                        k = n - LATE
                        g, step = (t + -1, k) if k >= 0 else (t + -2, NS + k)
                        live = last if k >= 0 else old
                        if last and k == 0:
                            pe.wait_ge(mx[g.slot], g.over(48, 48))
                        todo = list(range(n * per, (n + 1) * per)) if new else []
                        for s in range(4):
                            if live:
                                scores(g, step, s)
                            if n == 0 and s == 1 and last:
                                turn_maxima(t + -1)
                            if todo and (n > 0 or s > 1):
                                piece(t, todo.pop(0))
                        if live and step >= 1:
                            product(g, step - 1)
                        if old and k == 0:
                            product(t + -2, NS - 1)
                        for p in todo:
                            piece(t, p)
                        if old and k == 2:
                            turn_back(t + -2, 1)
                        if last and k == ends[0] + 3:
                            turn_back(t + -1, 0)

                run(pe, turn)
LAMBDA_INIT = 0.8 - 0.6 * math.exp(-0.3 * 12)
BLK = 4


def merge(nc, a, keep, sems, tag, groups, rms, bias=None):
    gb = groups // B
    dense = groups == 1
    X, ident, AO = keep["X"], keep["ident"], keep["AO"]
    NB = NT // BLK
    with ExitStack() as ctx:
        m = Mem(nc, ctx)
        sb = lambda name, shape, dt=F32: m.sb(f"{tag}_merge_{name}", shape, dt)
        two = lambda name, shape, dt=F32: [sb(f"{name}{k}", shape, dt) for k in range(2)]
        sem = lambda name: sems.sem(f"{tag}_merge_{name}")
        h = two("h", [P, DC, HALF] if dense else [P, BLK, D])
        wo = sb("wo", [P, DC, D])
        y = two("y", [P, BLK, D])
        st, eps = sb("st", [P, BLK, 6]), sb("eps", [P, 1])
        mv, sd, rs = two("mv", [P, BLK, 2]), two("sd", [P, BLK]), two("rs", [P, BLK])
        psY = [m.ps(f"{tag}_merge_psY{k}", BLK * D) for k in range(2)]
        if not dense:
            hT = two("hT", [P, BLK, DC, P])
            psT = [m.ps(f"{tag}_merge_psT{k}", BLK * DC * P) for k in range(2)]
        if bias:
            bo, ones = sb("bo", [1, D]), keep["ones1"]
        if rms:
            rw, sq, hm, hn = sb("rw", [P, DV]), sb("sq", [P, BLK, D]), sb("hm", [P, BLK, D]), two("hn", [P, BLK, D])
            ss, sr, ri = (sb(n, [P, BLK * H]) for n in ("ss", "sr", "ri"))
        loaded, const = sem("loaded"), sem("const")
        h_in = [sem(f"h_in{k}") for k in range(2)]
        hq = sem("hq")
        hr = sem("hr")
        hp = sem("hp")
        turned = sem("turned")
        hT_in = sem("hT_in")
        y_done = sem("y_done")
        stat = sem("stat")
        root = sem("root")
        passed = sem("passed")
        NSTAT, NHR = 5, 3
        HIN = 16 if dense else 16 * BLK
        again = lambda t: t.base >= 2 or t.n is not None
        with nc.Block() as block:
            @block.sync
            def _(sp):
                sp.dma_start(wo[:], a[f"{tag}_wo"]).then_inc(loaded, 16)
                if rms:
                    sp.dma_start(rw[:], a["L1_attn_rms_weight"].rearrange("(o d) -> o d", o=1).broadcast_to([P, DV])).then_inc(loaded, 16)
                if bias:
                    sp.dma_start(bo[:], a[bias].rearrange("(o d) -> o d", o=1)).then_inc(loaded, 16)

                def turn(t, live):
                    if again(t):
                        sp.wait_ge(*((hr, (t + -1).times(NHR)) if rms else (y_done if dense else turned, (t + -1).times(1))))
                    if dense:
                        sp.dma_start(h[t.slot][:], AO[:, :, t.span(HALF)]).then_inc(h_in[t.slot], 16)
                        return
                    b = bass.ds(t.over(gb), gb) if t.n is not None else slice(t.over(gb), t.over(gb) + gb)
                    for k in range(BLK):
                        sp.dma_start(h[t.slot][:, k, :].rearrange("p (g w) -> p g w", g=gb), AO[:, b, BLK * t.slot + k, :])\
                            .then_inc(h_in[t.slot], 16)

                run_turns(sp, turn, NB, 0, 2, 2)

            @block.scalar
            def _(act):
                act.wait_ge(const, 1)

                def deviation(u):
                    act.wait_ge(stat, u.times(NSTAT, 3))
                    act.activation(sd[u.slot][:], mv[u.slot][:, :, 1], ACT.Sqrt, bias=eps[:]).then_inc(root, 1)

                def turn(t, live):
                    u = t + -1
                    if live[0] and rms:
                        act.wait_ge(h_in[t.slot], t.over(HIN, HIN))
                        if t.base >= 1 or t.n is not None:
                            act.wait_ge(hr, (t + -1).times(NHR, 1))
                        act.activation(sq[:], h[t.slot][:], ACT.Square).then_inc(hq, 1)
                        act.wait_ge(hr, t.times(NHR, 1))
                        act.activation(sr[:], ss[:], ACT.Sqrt, bias=eps[:], scale=1.0 / DV).then_inc(hq, 1)
                    if rms and live[1]:
                        deviation(u)
                    if live[0] and not dense:
                        act.wait_ge(turned, t.times(1, 1))
                        if again(t):
                            act.wait_ge(y_done, (t + -1).times(1))
                        act.activation(hT[t.slot][:].rearrange("p t c n -> p (t c n)"), psT[t.slot][:], ACT.Copy).then_inc(hT_in, 1)
                    if not rms and live[1]:
                        deviation(u)

                run_turns(act, turn, NB, 1, 2)

            @block.gpsimd
            def _(pool):
                def turn(t, live):
                    pool.wait_ge(hr, t.times(NHR, 3))
                    if again(t):
                        pool.wait_ge(turned, (t + -1).times(1))
                    heads = lambda x: x[:].rearrange("p t (h d) -> p (t h) d", d=DV)
                    pool.tensor_tensor(heads(hn[t.slot]), heads(hm), rw[:].unsqueeze(1).broadcast_to([P, BLK * H, DV]),
                                       ALU.mult).then_inc(hp, 1)

                if rms:
                    pool.wait_ge(const, 2)
                    run_turns(pool, turn, NB, 0, 2, 2)

            @block.tensor
            def _(pe):
                pe.wait_ge(loaded, 32 if rms or bias else 16)
                src = hn if rms else h

                def turn(t, live):
                    u = t + -1
                    if live[1]:
                        if dense:
                            pe.wait_ge(h_in[u.slot], u.over(HIN, HIN))
                        else:
                            pe.wait_ge(hT_in, u.times(1, 1))
                        if again(u):
                            pe.wait_ge(stat, (u + -2).times(NSTAT, 1))
                        for k in range(BLK):
                            out = psY[u.slot][:, k * D:(k + 1) * D]
                            if bias:
                                pe.matmul(out, ones[:], bo[:], start=True, stop=False)
                            for c in range(DC):
                                last = pe.matmul(out, h[u.slot][:, c, k * P:(k + 1) * P] if dense else hT[u.slot][:, k, c, :],
                                                 wo[:, c, :], start=(c == 0 and not bias), stop=(c == DC - 1))
                        last.then_inc(y_done, 1)
                    if live[0] and not dense:
                        if rms:
                            pe.wait_ge(hp, t.times(1, 1))
                        else:
                            pe.wait_ge(h_in[t.slot], t.over(HIN, HIN))
                        if again(t):
                            pe.wait_ge(hT_in, (t + -1).times(1))
                        for k in range(BLK):
                            for c in range(DC):
                                last = pe.transpose(psT[t.slot][:, (k * DC + c) * P:(k * DC + c + 1) * P],
                                                    src[t.slot][:, k, c * P:(c + 1) * P], ident[:])
                        last.then_inc(turned, 1)

                run_turns(pe, turn, NB, 1, 2, 2)

            @block.vector
            def _(dve):
                dve.memset(eps[:], LN_EPS).then_inc(const, 1)
                if rms:
                    dve.wait_ge(loaded, 32)
                    dve.tensor_scalar(rw[:], rw[:], 1.0 - LAMBDA_INIT, None, ALU.mult).then_inc(const, 1)

                def root_mean_square(t):
                    s = Steps(dve, hr, t, NHR)
                    dve.wait_ge(hq, t.times(2, 1))
                    heads = lambda x: x[:].rearrange("p t (h d) -> p (t h) d", d=DV)
                    s.did(dve.tensor_reduce(ss[:], heads(sq), AX, ALU.add))
                    dve.wait_ge(hq, t.times(2, 2))
                    s.did(dve.reciprocal(ri[:], sr[:]))
                    s.wait()
                    dve.wait_ge(hp, t.times(1))
                    s.did(dve.tensor_tensor(heads(hm), heads(h[t.slot]), ri[:].unsqueeze(2).broadcast_to([P, BLK * H, DV]), ALU.mult))

                def norm(u):
                    s = Steps(dve, stat, u, NSTAT)
                    k = u.slot
                    dve.wait_ge(y_done, u.times(1, 1))
                    s.did(dve.tensor_tensor(y[k][:].rearrange("p t d -> p (t d)"), psY[k][:],
                                            X[:, u.span(BLK), :].rearrange("p t d -> p (t d)"), ALU.add))
                    s.wait()
                    for j in range(BLK):
                        last = dve.bn_stats(st[:, j, :], y[k][:, j, :])
                    s.did(last)
                    s.wait()
                    dve.sem_inc(passed, 1)
                    for j in range(BLK):
                        last = dve.bn_aggr(mv[k][:, j, :], st[:, j, :])
                    s.did(last)
                    dve.wait_ge(root, u.times(1, 1))
                    s.did(dve.reciprocal(rs[k][:], sd[k][:]))
                    s.wait()
                    for j in range(BLK):
                        at = u.times(BLK, j)
                        out = X[:, bass.ds(at, 1) if u.n is not None else slice(at, at + 1), :].rearrange("p o d -> p (o d)")
                        last = dve.tensor_scalar(out, y[k][:, j, :], mv[k][:, j, 0:1], rs[k][:, j:j + 1], ALU.subtract, ALU.mult)
                    s.did(last)

                def turn(t, live):
                    if live[0] and rms:
                        root_mean_square(t)
                    if live[1]:
                        norm(t + -1)

                run_turns(dve, turn, NB, 1, 2)


def cross_setup(nc, a, keep, sems):
    KT, VBD, OB, bq, bo, lg, lb, heads8 = (keep[k] for k in ("KT", "VBD", "OB", "bq", "bo", "lg", "lb", "heads8"))
    ident = keep["ident"]
    CK = 96
    with ExitStack() as ctx:
        m = Mem(nc, ctx)
        ctxT = m.sb("x0s_ctxT", [CK, 2, B, P])
        wkv = m.sb("x0s_wkv", [CK, 2, 2 * D])
        bkv = m.sb("x0s_bkv", [P, 2 * D])
        kp = m.sb("x0s_kp", [P, B, D])
        sq = m.sb("x0s_sq", [P, B, D])
        ss = m.sb("x0s_ss", [P, B])
        nr = m.sb("x0s_nr", [P, B])
        kn = m.sb("x0s_kn", [P, B, D])
        ps = m.ps("x0s_ps", B * 2 * D)
        psT = m.ps("x0s_psT", 2 * B * 64)
        loaded = sems.sem("x0s_loaded")
        products = sems.sem("x0s_products")
        done = sems.sem("x0s_done")
        root = sems.sem("x0s_root")
        turned = sems.sem("x0s_turned")
        with nc.Block() as block:
            @block.sync
            def _(sp):
                for dst, src in ((ctxT[:], a["ctxT2"]), (wkv[:], a["L0x_wkv"]),
                                 (bkv[:, 0:D], a["L0_xattn_bk"].rearrange("(o d) -> o d", o=1).broadcast_to([P, D])),
                                 (bkv[:, D:], a["L0_xattn_bv"].rearrange("(o d) -> o d", o=1).broadcast_to([P, D])),
                                 (bq[:], a["L0_xattn_bq"].rearrange("(o d) -> o d", o=1).broadcast_to([P, D])),
                                 (bo[:], a["L0_xattn_bo"].rearrange("(o d) -> o d", o=1).broadcast_to([P, D])),
                                 (lg[:], a["L0_xattn_ln_gamma"].rearrange("(o d) -> o d", o=1).broadcast_to([P, D])),
                                 (lb[:], a["L0_xattn_ln_beta"].rearrange("(o d) -> o d", o=1).broadcast_to([P, D])),
                                 (heads8[:], a["heads8"])):
                    sp.dma_start(dst, src).then_inc(loaded, 16)

            @block.tensor
            def _(pe):
                pe.wait_ge(loaded, 144)
                for b in range(B):
                    for c in range(2):
                        last = pe.matmul(ps[:, b * 2 * D:(b + 1) * 2 * D], ctxT[:, c, b, :], wkv[:, c, :],
                                         start=(c == 0), stop=(c == 1))
                last.then_inc(products, 1)
                pe.wait_ge(done, 8)
                for c in range(DC):
                    for b in range(B):
                        last = pe.transpose(psT[:, (c * B + b) * 64:(c * B + b + 1) * 64], kn[0:64, b, c * P:(c + 1) * P],
                                            ident[0:64, 0:64])
                last.then_inc(turned, 1)

            @block.scalar
            def _(act):
                act.wait_ge(done, 5)
                act.activation(nr[:], ss[:], ACT.Sqrt).then_inc(root, 1)

            @block.vector
            def _(dve):
                chain = Chain(dve, done)
                chain.did(dve.memset(VBD[:], 0.0))
                chain.did(dve.memset(OB[:], 0.0))
                dve.wait_ge(done, 2)
                dve.memset(OB[0:64, 0:DV], 1.0)
                chain.did(dve.memset(OB[64:P, DV:2 * DV], 1.0))
                dve.wait_ge(products, 1)
                pv = ps[:].rearrange("p (b n) -> p b n", b=B)
                for b in range(B):
                    last = dve.tensor_tensor(kp[:, b, :], pv[:, b, 0:D], bkv[:, 0:D], ALU.add)
                chain.did(last)
                dve.wait_ge(done, 4)
                dve.tensor_tensor(sq[:], kp[:], kp[:], ALU.mult).then_inc(root, 1)
                dve.wait_ge(root, 1)
                chain.did(dve.tensor_reduce(ss[:], sq[:], AX, ALU.add))
                dve.wait_ge(root, 2)
                chain.did(dve.tensor_scalar(nr[:], nr[:], 1e-12, None, ALU.max))
                dve.wait_ge(done, 6)
                chain.did(dve.reciprocal(ss[:], nr[:]))
                dve.wait_ge(done, 7)
                for b in range(B):
                    last = dve.tensor_scalar(kn[:, b, :], kp[:, b, :], ss[:, b:b + 1], None, ALU.mult)
                chain.did(last)
                for b in range(B):
                    for h in range(2):
                        r = slice(64 * h, 64 * h + 64)
                        view = lambda x: x.rearrange("p (a h d) -> p a h d", a=H // 2, h=2)[:, :, h, :]
                        last = dve.tensor_tensor(VBD[r, b, :, DV * h:DV * h + DV], view(pv[r, b, D:]),
                                                 view(bkv[r, D:]), ALU.add)
                chain.did(last)
                dve.wait_ge(turned, 1)
                chain.did(dve.tensor_copy(KT[:], psT[:].rearrange("p (c b k) -> p c b k", c=DC, b=B)))


def cross(nc, a, keep, sems):
    X, ident = keep["X"], keep["ident"]
    KT, VBD, OB, bq, bo, lg, lb, heads8 = (keep[k] for k in ("KT", "VBD", "OB", "bq", "bo", "lg", "lb", "heads8"))
    NB = NT // BLK
    HP = H // 2
    with ExitStack() as ctx:
        m = Mem(nc, ctx)
        sb = lambda name, shape, dt=F32: m.sb(f"x0_{name}", shape, dt)
        two = lambda name, shape, dt=F32: [sb(f"{name}{k}", shape, dt) for k in range(2)]
        QP = sb("QP", [P, NT, D])
        wq, wo = sb("wq", [P, DC, D]), sb("wo", [P, DC, D])
        xs = two("xs", [P, BLK, D])
        xT = sb("xT", [P, DC, HALF])
        qp, sq, qn = sb("qp", [P, BLK, D]), sb("sq", [P, BLK, D]), sb("qn", [P, BLK, D])
        ss, nr, ns, rn = (sb(n, [P, BLK]) for n in ("ss", "nr", "ns", "rn"))
        qT = two("qT", [P, DC, HALF])
        KB, VB = two("KB", [P, HP, P]), two("VB", [P, HP, 2 * DV])
        E = sb("E", [P, HP, HALF])
        rec = two("rec", [P, HALF])
        aT = two("aT", [P, DC, HALF])
        y, z, zg, zb, w = (sb(n, [P, BLK, D]) for n in ("y", "z", "zg", "zb", "w"))
        st, mv = two("st", [P, BLK, 6]), two("mv", [P, BLK, 2])
        sd, rs = two("sd", [P, BLK]), two("rs", [P, BLK])
        eps = sb("eps", [P, 1])
        psA = m.ps("x0_psA", BLK * D)
        psS = [m.ps(f"x0_psS{k}", HALF) for k in range(2)]
        psO = [m.ps(f"x0_psO{k}", HALF) for k in range(2)]
        psC = m.ps("x0_psC", BLK * D)
        sem = lambda name: sems.sem(f"x0_{name}")
        weights, const = sem("weights"), sem("const")
        xs_in = [sem(f"xs_in{k}") for k in range(2)]
        a_pe = sem("a_pe")
        a_act = sem("a_act")
        a_dve = sem("a_dve")
        kb_in = sem("kb_in")
        qp_in = sem("qp_in")
        s_done = sem("s_done")
        e_done = sem("e_done")
        o_pe = sem("o_pe")
        o_dve = sem("o_dve")
        c_pe = sem("c_pe")
        n_dve = [sem("inner_dve"), sem("outer_dve")]
        n_act = [sem("inner_act"), sem("outer_act")]
        n_pool = sem("n_pool")
        passed = sem("passed")
        held = sem("held")
        NA, NORM = 6, (5, 4)

        def one(t, n=0):
            at = t.over(1) if n is None else t.times(BLK, n)
            return bass.ds(at, 1) if t.n is not None else slice(at, at + 1)

        with nc.Block() as block:
            @block.sync
            def _(sp):
                sp.dma_start(wq[:], a["L0x_wq"]).then_inc(weights, 16)
                sp.dma_start(wo[:], a["L0x_wo"]).then_inc(weights, 16)

                def turn(t, live):
                    if t.base >= 2 or t.n is not None:
                        sp.wait_ge(a_pe, (t + -2).times(3, 1))
                    sp.dma_start(xs[t.slot][:], X[:, t.span(BLK), :]).then_inc(xs_in[t.slot], 16)

                run_turns(sp, turn, NB, 0, 2, 2)

            @block.tensor
            def _(pe):
                pe.wait_ge(weights, 32)

                def turn(t, live):
                    u, v = t + -1, t + -2
                    if live[0]:
                        pe.wait_ge(xs_in[t.slot], t.over(16, 16))
                        pe.wait_ge(a_act, t.times(3))
                        for c in range(DC):
                            for k in range(BLK):
                                last = pe.transpose(psA[:, (c * BLK + k) * P:(c * BLK + k + 1) * P],
                                                    xs[t.slot][:, k, c * P:(c + 1) * P], ident[:])
                        last.then_inc(a_pe, 1)
                        pe.wait_ge(a_act, t.times(3, 1))
                        for k in range(BLK):
                            for c in range(DC):
                                last = pe.matmul(psA[:, k * D:(k + 1) * D], xT[:, c, k * P:(k + 1) * P], wq[:, c, :],
                                                 start=(c == 0), stop=(c == DC - 1))
                        last.then_inc(a_pe, 1)
                    if live[1]:
                        pe.wait_ge(kb_in, u.times(1, 1))
                        pe.wait_ge(a_act, u.times(3, 3))
                        if u.base >= 1 or u.n is not None:
                            pe.wait_ge(o_dve, (u + -1).times(4, 2))
                        for hp in range(HP):
                            pe.wait_ge(e_done, u.times(HP, hp + 1))
                            pe.matmul(psS[hp % 2][:], KB[u.slot][:, hp, :], qT[u.slot][:, hp // 4, :], start=True,
                                      stop=True).then_inc(s_done, 1)
                    if live[2]:
                        pe.wait_ge(o_dve, v.times(4, 4))
                        if v.base >= 1 or v.n is not None:
                            pe.wait_ge(n_dve[0], (v + -1).times(NORM[0], 1))
                        for k in range(BLK):
                            for c in range(DC):
                                last = pe.matmul(psC[:, k * D:(k + 1) * D], aT[v.slot][:, c, k * P:(k + 1) * P], wo[:, c, :],
                                                 start=(c == 0), stop=(c == DC - 1))
                        last.then_inc(c_pe, 1)
                    if live[1]:
                        pe.wait_ge(e_done, u.times(HP, HP + 2))
                        pe.wait_ge(o_dve, u.times(4))
                        for c, ps in enumerate((psO, psS)):
                            for out, lhs in ((ps[0], VB[u.slot]), (ps[1], None)):
                                for j in range(4):
                                    last = pe.matmul(out[32 * j:32 * j + 32, :], OB[:] if lhs is None else lhs[:, 4 * c + j, :],
                                                     E[:, 4 * c + j, :], start=True, stop=True)
                            last.then_inc(o_pe, 1)
                    if live[0]:
                        pe.wait_ge(a_dve, t.times(NA, NA))
                        for c in range(DC):
                            for k in range(BLK):
                                last = pe.transpose(psA[:, (c * BLK + k) * P:(c * BLK + k + 1) * P],
                                                    qn[:, k, c * P:(c + 1) * P], ident[:])
                        last.then_inc(a_pe, 1)

                run_turns(pe, turn, NB, 4, 2)

            @block.scalar
            def _(act):
                act.sem_inc(e_done, 2)
                act.wait_ge(const, 1)

                def turn(t, live):
                    u = t + -1
                    if live[0]:
                        act.wait_ge(a_pe, t.times(3, 1))
                        act.activation(xT[:].rearrange("p c n -> p (c n)"), psA[:], ACT.Copy).then_inc(a_act, 1)
                    if live[1]:
                        act.wait_ge(o_pe, u.times(2))
                        for hp in range(HP):
                            act.wait_ge(s_done, u.times(HP, hp + 1))
                            act.activation(E[:, hp, :], psS[hp % 2][:], ACT.Exp, scale=0.25).then_inc(e_done, 1)
                    if live[0]:
                        act.wait_ge(a_dve, t.times(NA, 3))
                        act.activation(nr[:], ss[:], ACT.Sqrt).then_inc(a_act, 1)
                    for n in (1, 0):
                        if live[3 + n]:
                            act.wait_ge(n_dve[n], (t + (-3 - n)).times(NORM[n], 3 - n))
                            act.activation(sd[n][:], mv[n][:, :, 1], ACT.Sqrt, bias=eps[:]).then_inc(n_act[n], 1)
                    if live[0]:
                        act.wait_ge(a_pe, t.times(3, 3))
                        act.activation(qT[t.slot][:].rearrange("p c n -> p (c n)"), psA[:], ACT.Copy).then_inc(a_act, 1)

                run_turns(act, turn, NB, 4, 2)

            @block.gpsimd
            def _(pool):
                def turn(t, live):
                    if live[0]:
                        if t.base >= 2 or t.n is not None:
                            pool.wait_ge(o_pe, (t + -1).times(2))
                            pool.sem_inc(held, 1)
                        for c in range(DC):
                            pool.tensor_tensor(KB[t.slot][:, c * 4:(c + 1) * 4, :].rearrange("p a (h k) -> p (a h) k", h=2),
                                               KT[:, c, one(t, None), :].broadcast_to([P, 8, 64]),
                                               heads8[:].unsqueeze(2).broadcast_to([P, 8, 64]), ALU.mult)
                        pool.tensor_copy(VB[t.slot][:].rearrange("p a n -> p (a n)"),
                                         VBD[:, one(t, None), :, :].rearrange("p o a n -> p (o a n)")).then_inc(kb_in, 1)
                        pool.wait_ge(a_dve, t.times(NA, 1))
                        pool.sem_inc(held, 1)
                        pool.tensor_tensor(QP[:, t.span(BLK), :], qp[:], bo[:].unsqueeze(1).broadcast_to([P, BLK, D]),
                                           ALU.add).then_inc(qp_in, 1)
                    if live[3]:
                        v = t + -3
                        pool.wait_ge(n_dve[0], v.times(NORM[0], 5))
                        pool.tensor_tensor(zg[:], z[:], lg[:].unsqueeze(1).broadcast_to([P, BLK, D]), ALU.mult).then_inc(n_pool, 1)
                        pool.wait_ge(n_pool, v.times(3, 1))
                        pool.tensor_tensor(zb[:], zg[:], lb[:].unsqueeze(1).broadcast_to([P, BLK, D]), ALU.add).then_inc(n_pool, 1)
                        pool.wait_ge(n_pool, v.times(3, 2))
                        pool.wait_ge(n_dve[1], v.times(NORM[1]))
                        pool.sem_inc(held, 1)
                        pool.tensor_tensor(w[:], zb[:], X[:, v.span(BLK), :], ALU.add).then_inc(n_pool, 1)

                run_turns(pool, turn, NB, 4, 2)

            @block.vector
            def _(dve):
                dve.memset(eps[:], LN_EPS).then_inc(const, 1)

                def queries(t):
                    s = Steps(dve, a_dve, t, NA)
                    dve.wait_ge(a_pe, t.times(3, 2))
                    dve.wait_ge(qp_in, t.times(1))
                    s.did(dve.tensor_tensor(qp[:], psA[:].rearrange("p (k d) -> p k d", k=BLK),
                                            bq[:].unsqueeze(1).broadcast_to([P, BLK, D]), ALU.add))
                    s.wait()
                    s.did(dve.tensor_tensor(sq[:], qp[:], qp[:], ALU.mult))
                    s.wait()
                    s.did(dve.tensor_reduce(ss[:], sq[:], AX, ALU.add))
                    dve.wait_ge(a_act, t.times(3, 2))
                    s.did(dve.tensor_scalar(ns[:], nr[:], 1e-12, None, ALU.max))
                    s.wait()
                    s.did(dve.reciprocal(rn[:], ns[:]))
                    s.wait()
                    for k in range(BLK):
                        last = dve.tensor_scalar(qn[:, k, :], qp[:, k, :], rn[:, k:k + 1], None, ALU.mult)
                    s.did(last)

                def divide(v):
                    s = Steps(dve, o_dve, v, 4)
                    dve.wait_ge(o_pe, v.times(2, 2))
                    for c, ps in ((1, psS), (0, psO)):
                        s.did(dve.reciprocal(rec[c][:], ps[1][:]))
                        s.wait()
                        s.did(dve.tensor_tensor(aT[v.slot][:, c, :], ps[0][:], rec[c][:], ALU.mult))

                def layernorm(s, t, n, src, out):
                    for k in range(BLK):
                        last = dve.bn_stats(st[n][:, k, :], src[:, k, :])
                    s.did(last)
                    s.wait()
                    dve.sem_inc(passed, 1)
                    for k in range(BLK):
                        last = dve.bn_aggr(mv[n][:, k, :], st[n][:, k, :])
                    s.did(last)
                    dve.wait_ge(n_act[n], t.times(1, 1))
                    s.did(dve.reciprocal(rs[n][:], sd[n][:]))
                    s.wait()
                    for k in range(BLK):
                        last = dve.tensor_scalar(out(k), src[:, k, :], mv[n][:, k, 0:1], rs[n][:, k:k + 1], ALU.subtract, ALU.mult)
                    s.did(last)

                def turn(t, live):
                    if live[2]:
                        divide(t + -2)
                    if live[0]:
                        queries(t)
                    if live[4]:
                        x = t + -4
                        s = Steps(dve, n_dve[1], x, NORM[1])
                        dve.wait_ge(n_pool, x.times(3, 3))
                        layernorm(s, x, 1, w, lambda k: X[:, one(x, k), :].rearrange("p o d -> p (o d)"))
                    if live[3]:
                        v = t + -3
                        s = Steps(dve, n_dve[0], v, NORM[0])
                        dve.wait_ge(c_pe, v.times(1, 1))
                        dve.wait_ge(qp_in, v.times(1, 1))
                        s.did(dve.tensor_tensor(y[:], psC[:].rearrange("p (k d) -> p k d", k=BLK), QP[:, v.span(BLK), :], ALU.add))
                        s.wait()
                        layernorm(s, v, 0, y, lambda k: z[:, k, :])

                run_turns(dve, turn, NB, 4, 2)


EX = 8
CAPACITY = int(S * 2 / EX * 1.5) + 1


def experts(nc, a, keep, sems):
    X, ident, identb = keep["X"], keep["ident"], keep["identb"]
    NB = NT // BLK
    with nc.cleanup_on_exit(), ExitStack() as ctx:
        m = Mem(nc, ctx)
        sb = lambda name, shape, dt=F32: m.sb(f"m0_{name}", shape, dt)
        two = lambda name, shape, dt=F32: [m.sb(f"m0_{name}{k}", shape, dt) for k in range(2)]
        we, wr = sb("we", [P, DC, EX * D]), sb("wr", [P, DC, EX])
        tri, trib, onesb, iota = sb("tri", [P, P]), sb("trib", [P, P], BF16), sb("onesb", [P, P], BF16), sb("iota", [P, EX])
        xs, xT = two("xs", [P, BLK, D]), two("xT", [P, DC, HALF])
        logit, top, ix = sb("logit", [P, BLK, EX]), sb("top", [P, BLK, 8]), sb("ix", [P, BLK, 8], U32)
        ixf, d, ed, den, w1, w2 = (sb(n, [P, BLK, 2] if n == "ixf" else [P, BLK]) for n in ("ixf", "d", "ed", "den", "w1", "w2"))
        oh1, oh2, g1, g2, g12 = (sb(n, [P, BLK, EX]) for n in ("oh1", "oh2", "g1", "g2", "g12"))
        chosen, before = two("chosen", [P, BLK, EX], BF16), two("before", [P, BLK, EX], BF16)
        W = two("W", [P, BLK, EX])
        z = sb("z", [P, BLK, D])
        st, mv, sd, rs, eps = sb("st", [P, BLK, 6]), sb("mv", [P, BLK, 2]), sb("sd", [P, BLK]), sb("rs", [P, BLK]), sb("eps", [P, 1])
        psA = m.ps("m0_psA", BLK * D)
        psG = m.ps("m0_psG", HALF)
        psE = [m.ps(f"m0_psE{k}", HALF) for k in range(4)]
        sem = lambda name: sems.sem(f"m0_{name}")
        weights, const = sem("weights"), sem("const")
        xs_in = [sem(f"xs_in{k}") for k in range(2)]
        g_pe = sem("g_pe")
        g_act = sem("g_act")
        g_dve = sem("g_dve")
        y_pe = sem("y_pe")
        y_dve = sem("y_dve")
        n_dve = sem("n_dve")
        n_act = sem("n_act")
        passed = sem("passed")
        NG, G_D, G_CHOSEN = 19, 4, 14
        with nc.Block() as block:
            @block.sync
            def _(sp):
                for dst, src in ((we[:], a["L0f_we"]), (wr[:], a["L0f_wr"]), (tri[:], a["tri"]),
                                 (iota[:], a["iota8"].broadcast_to([P, EX]))):
                    sp.dma_start(dst, src).then_inc(weights, 16)

                def turn(t, live):
                    if live[0]:
                        if t.base >= 2 or t.n is not None:
                            sp.wait_ge(y_dve, (t + -1).times(BLK * EX))
                        sp.dma_start(xs[t.slot][:], X[:, t.span(BLK), :]).then_inc(xs_in[t.slot], 16)

                run_turns(sp, turn, NB, 1, 2)

            @block.tensor
            def _(pe):
                pe.wait_ge(weights, 64)
                pe.wait_ge(const, 3)

                def expert_products(u, k):
                    for e in range(EX // 2):
                        n = k * (EX // 2) + e
                        if n >= 4 or u.base >= 1 or u.n is not None:
                            pe.wait_ge(y_dve, u.times(BLK * EX, 2 * (n - 3)))
                        for c in range(DC):
                            last = pe.matmul(psE[e][:], xT[u.slot][:, c, k * P:(k + 1) * P],
                                             we[:, c, e * HALF:(e + 1) * HALF], start=(c == 0), stop=(c == DC - 1))
                        last.then_inc(y_pe, 1)

                def turn(t, live):
                    u = t + -1
                    if live[0]:
                        pe.wait_ge(xs_in[t.slot], t.over(16, 16))
                        pe.wait_ge(g_act, t.times(2))
                        for c in range(DC):
                            for k in range(BLK):
                                last = pe.transpose(psA[:, (c * BLK + k) * P:(c * BLK + k + 1) * P],
                                                    xs[t.slot][:, k, c * P:(c + 1) * P], ident[:])
                        last.then_inc(g_pe, 1)
                    if live[1]:
                        expert_products(u, 0)
                    if live[0]:
                        pe.wait_ge(g_act, t.times(2, 1))
                        pe.wait_ge(g_dve, t.times(NG))
                        for k in range(BLK):
                            for c in range(DC):
                                last = pe.matmul(psG[:, k * EX:(k + 1) * EX], xT[t.slot][:, c, k * P:(k + 1) * P], wr[:, c, :],
                                                 start=(c == 0), stop=(c == DC - 1))
                        last.then_inc(g_pe, 1)
                    if live[1]:
                        expert_products(u, 1)
                        expert_products(u, 2)
                    if live[0]:
                        pe.wait_ge(g_dve, t.times(NG, G_CHOSEN + 4))
                        pe.matmul(psG[:, 0:BLK * EX], trib[:], chosen[t.slot][:].rearrange("p k e -> p (k e)"), start=True, stop=False)
                        pe.matmul(psG[:, 0:BLK * EX], onesb[:], before[t.slot][:].rearrange("p k e -> p (k e)"), start=False,
                                  stop=True).then_inc(g_pe, 1)
                    if live[1]:
                        expert_products(u, 3)

                run_turns(pe, turn, NB, 1, 2)

            @block.scalar
            def _(act):
                act.wait_ge(const, 3)

                def turn(t, live):
                    u = t + -1
                    if live[0]:
                        act.wait_ge(g_pe, t.times(3, 1))
                        if t.base >= 2 or t.n is not None:
                            act.wait_ge(y_pe, (t + -1).times(BLK * EX // 2))
                        act.activation(xT[t.slot][:].rearrange("p c n -> p (c n)"), psA[:], ACT.Copy).then_inc(g_act, 1)
                        act.wait_ge(g_dve, t.times(NG, G_D))
                        act.activation(ed[:], d[:], ACT.Exp).then_inc(g_act, 1)
                    if live[1]:
                        act.wait_ge(n_dve, u.times(4, 2))
                        act.activation(sd[:], mv[:, :, 1], ACT.Sqrt, bias=eps[:]).then_inc(n_act, 1)

                run_turns(act, turn, NB, 1, 2)

            @block.vector
            def _(dve):
                dve.memset(eps[:], LN_EPS).then_inc(const, 1)
                dve.memset(onesb[:], 1.0).then_inc(const, 1)
                dve.wait_ge(weights, 64)
                dve.tensor_copy(trib[:], tri[:]).then_inc(const, 1)

                def add_experts(u, k):
                    dve.wait_ge(g_dve, u.times(NG, NG))
                    if k == 0:
                        dve.wait_ge(n_dve, u.times(4))
                    for e in range(EX):
                        n = k * EX + e
                        dve.wait_ge(y_pe, u.times(BLK * EX // 2, k * (EX // 2) + e // 2 + 1))
                        dve.wait_ge(y_dve, u.times(BLK * EX, n))
                        dve.scalar_tensor_tensor(out=z[:, k, :], in0=psE[e // 2][:, (e % 2) * D:(e % 2 + 1) * D],
                                                 scalar=W[u.slot][:, k, e:e + 1], in1=xs[u.slot][:, k, :] if e == 0 else z[:, k, :],
                                                 op0=ALU.mult, op1=ALU.add).then_inc(y_dve, 1)

                def first(t):
                    s = Steps(dve, g_dve, t, NG)
                    ch, bf = chosen[t.slot], before[t.slot]
                    dve.wait_ge(g_pe, t.times(3, 2))
                    s.did(dve.tensor_copy(logit[:], psG[:, 0:BLK * EX].rearrange("p (k e) -> p k e", k=BLK)))
                    s.wait()
                    dve.sem_inc(passed, 1)
                    for k in range(BLK):
                        last = dve.max(top[:, k, :], logit[:, k, :])
                    s.did(last)
                    s.wait()
                    dve.sem_inc(passed, 1)
                    for k in range(BLK):
                        last = dve.max_index(ix[:, k, :], top[:, k, :], logit[:, k, :])
                    s.did(last)
                    s.did(dve.tensor_tensor(d[:], top[:, :, 1], top[:, :, 0], ALU.subtract))
                    assert s.k == G_D
                    s.wait()
                    s.did(dve.tensor_copy(ixf[:], ix[:, :, 0:2]))
                    s.wait()
                    for n, oh in ((0, oh1), (1, oh2)):
                        s.did(dve.tensor_tensor(oh[:], iota[:].unsqueeze(1).broadcast_to([P, BLK, EX]),
                                                ixf[:, :, n:n + 1].broadcast_to([P, BLK, EX]), ALU.is_equal))
                    s.wait()
                    s.did(dve.tensor_tensor(ch[:], oh1[:], oh2[:], ALU.add))
                    dve.wait_ge(g_act, t.times(2, 2))
                    s.did(dve.tensor_scalar(den[:], ed[:], 1.0, None, ALU.add))
                    s.wait()
                    s.did(dve.reciprocal(w1[:], den[:]))
                    s.wait()
                    s.did(dve.tensor_tensor(w2[:], ed[:], w1[:], ALU.mult))
                    s.wait()
                    s.did(dve.tensor_tensor(g1[:], oh1[:], w1[:].unsqueeze(2).broadcast_to([P, BLK, EX]), ALU.mult))
                    s.did(dve.tensor_tensor(g2[:], oh2[:], w2[:].unsqueeze(2).broadcast_to([P, BLK, EX]), ALU.mult))
                    s.wait()
                    s.did(dve.tensor_tensor(g12[:], g1[:], g2[:], ALU.add))
                    assert s.k == G_CHOSEN
                    if t.slot == 0:
                        s.did(dve.memset(bf[:, 0, :], 0.0))
                    else:
                        s.did(dve.tensor_tensor(bf[:, 0, :], before[0][:, BLK - 1, :], chosen[0][:, BLK - 1, :], ALU.add))
                    for k in range(1, BLK):
                        s.wait()
                        s.did(dve.tensor_tensor(bf[:, k, :], bf[:, k - 1, :], ch[:, k - 1, :], ALU.add))

                def second(t):
                    s = Steps(dve, g_dve, t, NG, G_CHOSEN + 4)
                    dve.wait_ge(g_pe, t.times(3, 3))
                    ps = psG[:, 0:BLK * EX]
                    s.did(dve.scalar_tensor_tensor(out=W[t.slot][:].rearrange("p k e -> p (k e)"), in0=ps, scalar=float(CAPACITY),
                                                   in1=g12[:].rearrange("p k e -> p (k e)"), op0=ALU.is_lt, op1=ALU.mult))

                def norm(u):
                    dve.wait_ge(y_dve, u.times(BLK * EX, BLK * EX))
                    for k in range(BLK):
                        last = dve.bn_stats(st[:, k, :], z[:, k, :])
                    last.then_inc(n_dve, 1)
                    dve.wait_ge(n_dve, u.times(4, 1))
                    dve.sem_inc(passed, 1)
                    for k in range(BLK):
                        last = dve.bn_aggr(mv[:, k, :], st[:, k, :])
                    last.then_inc(n_dve, 1)
                    dve.wait_ge(n_act, u.times(1, 1))
                    dve.reciprocal(rs[:], sd[:]).then_inc(n_dve, 1)
                    dve.wait_ge(n_dve, u.times(4, 3))
                    for k in range(BLK):
                        out = X[:, bass.ds(u.times(BLK, k), 1) if u.n is not None else slice(u.times(BLK, k), u.times(BLK, k) + 1), :]
                        last = dve.tensor_scalar(out.rearrange("p o d -> p (o d)"), z[:, k, :], mv[:, k, 0:1], rs[:, k:k + 1],
                                                 ALU.subtract, ALU.mult)
                    last.then_inc(n_dve, 1)

                def turn(t, live):
                    u = t + -1
                    if live[1]:
                        add_experts(u, 0)
                    if live[0]:
                        first(t)
                    if live[1]:
                        add_experts(u, 1)
                        add_experts(u, 2)
                    if live[0]:
                        second(t)
                    if live[1]:
                        add_experts(u, 3)
                        norm(u)

                run_turns(dve, turn, NB, 1, 2)


LH, LD = 4, 64
CK = 96
CTX = 64


def context_keys(nc, a, keep, sems):
    ident, kTc, Vc, gam, ones, maskrow = (keep[k] for k in ("ident", "kTc", "Vc", "gam", "ones1", "maskrow"))
    KD = 192
    with ExitStack() as ctx:
        m = Mem(nc, ctx)
        sb = lambda name, shape, dt=F32: m.sb(f"x1s_{name}", shape, dt)
        cx, xc, xn = sb("cx", [CTX, B, KD]), sb("xc", [CTX, B, KD]), sb("xn", [CTX, B, KD])
        lg, lb = sb("lg", [CTX, KD]), sb("lb", [CTX, KD])
        xT = sb("xT", [CK, 2, B, CTX])
        wkv = sb("wkv", [CK, 2, 2 * D])
        mask8, maskf = sb("mask8", [1, B * CTX], mybir.dt.uint8), sb("maskf", [1, B * CTX])
        st, mv, sd, rs, eps = sb("st", [CTX, B, 6]), sb("mv", [CTX, B, 2]), sb("sd", [CTX, B]), sb("rs", [CTX, B]), sb("eps", [P, 1])
        sq, kn = sb("sq", [CTX, B, D]), sb("kn", [CTX, B, D])
        ss, nr, rn = sb("ss", [CTX, B * LH]), sb("nr", [CTX, B * LH]), sb("rn", [CTX, B * LH])
        ps = m.ps("x1s_ps", B * 2 * D)
        psT = m.ps("x1s_psT", 2 * B * CTX)
        sem = lambda name: sems.sem(f"x1s_{name}")
        loaded, products, turned, done, roots = sem("loaded"), sem("products"), sem("turned"), sem("done"), sem("roots")
        kv = ps[0:CTX, :].rearrange("p (b n) -> p b n", b=B)
        row = lambda name, n: a[name].rearrange("(o d) -> o d", o=1).broadcast_to([n, a[name].shape[0]])
        with nc.Block() as block:
            @block.sync
            def _(sp):
                for dst, src in ((cx[:], a["ctx_tok"]), (wkv[:], a["L1x_wkv"]), (mask8[:], a["mask8"]),
                                 (lg[:], row("L1_xattn_ln_x_g", CTX)), (lb[:], row("L1_xattn_ln_x_b", CTX)),
                                 (gam[:, 0:LD], row("L1_xattn_qn_g", P)), (gam[:, LD:], row("L1_xattn_kn_g", P))):
                    sp.dma_start(dst, src).then_inc(loaded, 16)

            @block.tensor
            def _(pe):
                pe.wait_ge(done, 8)
                for c in range(2):
                    for b in range(B):
                        last = pe.transpose(psT[0:CK, (c * B + b) * CTX:(c * B + b + 1) * CTX], xn[:, b, c * CK:(c + 1) * CK],
                                            ident[0:CTX, 0:CTX])
                last.then_inc(turned, 1)
                pe.wait_ge(done, 9)
                for b in range(B):
                    for c in range(2):
                        last = pe.matmul(ps[0:CTX, b * 2 * D:(b + 1) * 2 * D], xT[:, c, b, :], wkv[:, c, :],
                                         start=(c == 0), stop=(c == 1))
                last.then_inc(products, 1)
                pe.wait_ge(done, 16)
                for c in range(DC):
                    for b in range(B):
                        last = pe.transpose(psT[:, (c * B + b) * CTX:(c * B + b + 1) * CTX], kn[:, b, c * P:(c + 1) * P],
                                            ident[0:CTX, 0:CTX])
                last.then_inc(turned, 1)

            @block.scalar
            def _(act):
                act.wait_ge(done, 4)
                act.activation(sd[:], mv[:, :, 1], ACT.Sqrt, bias=eps[0:CTX]).then_inc(roots, 1)
                act.wait_ge(done, 11)
                act.activation(nr[:], ss[:], ACT.Sqrt, scale=1.0 / LD).then_inc(roots, 1)

            @block.vector
            def _(dve):
                s = Chain(dve, done)
                s.did(dve.memset(eps[:], LN_EPS))
                s.did(dve.memset(ones[:], 1.0))
                dve.wait_ge(loaded, 112)
                for b in range(B):
                    last = dve.bn_stats(st[:, b, :], cx[:, b, :])
                s.did(last)
                s.wait()
                for b in range(B):
                    last = dve.bn_aggr(mv[:, b, :], st[:, b, :])
                s.did(last)
                dve.wait_ge(roots, 1)
                s.did(dve.reciprocal(rs[:], sd[:]))
                s.wait()
                for b in range(B):
                    last = dve.tensor_scalar(xc[:, b, :], cx[:, b, :], mv[:, b, 0:1], rs[:, b:b + 1], ALU.subtract, ALU.mult)
                s.did(last)
                s.wait()
                s.did(dve.tensor_tensor(xc[:], xc[:], lg[:].unsqueeze(1).broadcast_to([CTX, B, KD]), ALU.mult))
                s.wait()
                s.did(dve.tensor_tensor(xn[:], xc[:], lb[:].unsqueeze(1).broadcast_to([CTX, B, KD]), ALU.add))
                assert s.n == 8
                dve.wait_ge(turned, 1)
                s.did(dve.tensor_copy(xT[:], psT[0:CK, :].rearrange("p (c b k) -> p c b k", c=2, b=B)))
                dve.wait_ge(products, 1)
                s.did(dve.tensor_copy(kn[:], kv[:, :, 0:D]))
                s.wait()
                dve.tensor_tensor(sq[:], kn[:], kn[:], ALU.mult).then_inc(products, 1)
                dve.wait_ge(products, 2)
                s.did(dve.tensor_reduce(ss[:], sq[:].rearrange("p b (h d) -> p (b h) d", h=LH), AX, ALU.add))
                dve.wait_ge(roots, 2)
                s.did(dve.tensor_scalar(nr[:], nr[:], 1e-8, None, ALU.max))
                s.wait()
                s.did(dve.reciprocal(rn[:], nr[:]))
                s.wait()
                s.did(dve.tensor_tensor(sq[:].rearrange("p b (h d) -> p (b h) d", h=LH), kn[:].rearrange("p b (h d) -> p (b h) d", h=LH),
                                        rn[:].unsqueeze(2).broadcast_to([CTX, B * LH, LD]), ALU.mult))
                s.did(dve.tensor_scalar(gam[:, 0:LD], gam[:, 0:LD], float(LD) ** -0.5, None, ALU.mult))
                s.wait()
                s.did(dve.tensor_tensor(kn[:].rearrange("p b (h d) -> p (b h) d", h=LH), sq[:].rearrange("p b (h d) -> p (b h) d", h=LH),
                                        gam[0:CTX, LD:].unsqueeze(1).broadcast_to([CTX, B * LH, LD]), ALU.mult))
                assert s.n == 16
                for b in range(B):
                    last = dve.tensor_copy(Vc[:, b, :, :], kv[:, b, D:].rearrange("p (h d) -> p h d", h=LH))
                s.did(last)
                s.did(dve.tensor_copy(maskf[:], mask8[:]))
                s.wait()
                s.did(dve.tensor_scalar(maskrow[:], maskf[:], 1.0, -MASKED, ALU.subtract, ALU.mult))
                dve.wait_ge(turned, 2)
                s.did(dve.tensor_copy(kTc[:], psT[:].rearrange("p (c b k) -> p c b k", c=DC, b=B)))


def latent_project(nc, a, keep, sems):
    X, ident, QT, KD, VL, gam = (keep[k] for k in ("X", "ident", "QT", "KD", "VL", "gam"))
    NB = NT // BLK
    QK = 2 * D
    R = BLK * 2 * LH
    with ExitStack() as ctx:
        m = Mem(nc, ctx)
        sb = lambda name, shape, dt=F32: m.sb(f"x1p_{name}", shape, dt)
        two = lambda name, shape: [sb(f"{name}{k}", shape) for k in range(2)]
        w = sb("w", [P, DC, 3 * D])
        lg, lb = sb("lg", [P, D]), sb("lb", [P, D])
        st, mv, sd, rs, eps = sb("st", [P, BLK, 6]), sb("mv", [P, BLK, 2]), sb("sd", [P, BLK]), sb("rs", [P, BLK]), sb("eps", [P, 1])
        xc, ln = sb("xc", [P, BLK, D]), sb("ln", [P, BLK, D])
        lT, sq = sb("lT", [P, DC, HALF]), sb("sq", [P, BLK, QK])
        nrm, qo, ko = two("nrm", [P, BLK, QK]), two("qo", [P, DC, HALF]), two("ko", [P, DC, HALF])
        ss, nr, ns, rn = (sb(n, [P, R]) for n in ("ss", "nr", "ns", "rn"))
        psT, psQ, psV = m.ps("x1p_psT", BLK * D), m.ps("x1p_psQ", BLK * QK), m.ps("x1p_psV", BLK * D)
        sem = lambda name: sems.sem(f"x1p_{name}")
        loaded, const = sem("loaded"), sem("const")
        l_dve = sem("l_dve")
        l_act = sem("l_act")
        l_pool = sem("l_pool")
        l_pe = sem("l_pe")
        lt_in = sem("lt_in")
        qkv = sem("qkv")
        v_in = sem("v_in")
        sq_in = sem("sq_in")
        n_dve = sem("n_dve")
        n_act = sem("n_act")
        n_pool = sem("n_pool")
        q_pe = sem("q_pe")
        q_in = sem("q_in")
        out = [sem(f"out{k}") for k in range(2)]
        passed = sem("passed")
        row = lambda name, n: a[name].rearrange("(o d) -> o d", o=1).broadcast_to([n, a[name].shape[0]])
        with nc.Block() as block:
            @block.sync
            def _(sp):
                for dst, src in ((w[:], a["L1x_w"]), (lg[:], row("L1_xattn_ln_l_g", P)), (lb[:], row("L1_xattn_ln_l_b", P))):
                    sp.dma_start(dst, src).then_inc(loaded, 16)

                def turn(t, live):
                    for n, (dram, staged) in enumerate(((QT, qo), (KD, ko))):
                        sp.wait_ge(q_in, t.times(2, n + 1))
                        sp.dma_start(dram.rearrange("(c p) n -> p c n", p=P)[:, :, t.span(HALF)], staged[t.slot][:])\
                            .then_inc(out[t.slot], 16)

                run_turns(sp, turn, NB, 0, 2)
                for k in range(2):
                    sp.wait_ge(out[k], 32 * (NB // 2))

            @block.tensor
            def _(pe):
                pe.wait_ge(loaded, 48)

                def product(u, ps, cols):
                    width = cols.stop - cols.start
                    for k in range(BLK):
                        for c in range(DC):
                            last = pe.matmul(ps[:, k * width:(k + 1) * width], lT[:, c, k * P:(k + 1) * P], w[:, c, cols],
                                             start=(c == 0), stop=(c == DC - 1))
                    last.then_inc(qkv, 1)

                def back(v, n):
                    for c in range(DC):
                        for k in range(BLK):
                            last = pe.transpose(psT[:, (c * BLK + k) * P:(c * BLK + k + 1) * P],
                                                nrm[v.slot][:, k, n * D + c * P:n * D + (c + 1) * P], ident[:])
                    last.then_inc(q_pe, 1)

                def turn(t, live):
                    u, v = t + -1, t + -2
                    if live[1]:
                        pe.wait_ge(lt_in, u.times(1, 1))
                        pe.wait_ge(n_dve, u.times(4))
                        product(u, psQ, slice(0, QK))
                    if live[2]:
                        pe.wait_ge(n_pool, v.times(1, 1))
                        pe.wait_ge(lt_in, v.times(1, 2 if live[1] else 1))
                        pe.wait_ge(q_in, v.times(2))
                        back(v, 0)
                    if live[1]:
                        pe.wait_ge(v_in, u.times(1))
                        product(u, psV, slice(QK, 3 * D))
                    if live[2]:
                        pe.wait_ge(q_in, v.times(2, 1))
                        back(v, 1)
                    if live[0]:
                        pe.wait_ge(l_pool, t.times(2, 2))
                        if live[2]:
                            pe.wait_ge(q_in, v.times(2, 2))
                        pe.wait_ge(lt_in, t.times(1))
                        for c in range(DC):
                            for k in range(BLK):
                                last = pe.transpose(psT[:, (c * BLK + k) * P:(c * BLK + k + 1) * P], ln[:, k, c * P:(c + 1) * P], ident[:])
                        last.then_inc(l_pe, 1)

                run_turns(pe, turn, NB, 2, 2)

            @block.scalar
            def _(act):
                act.wait_ge(const, 1)

                def turn(t, live):
                    u, v = t + -1, t + -2
                    if live[0]:
                        act.wait_ge(l_dve, t.times(4, 2))
                        act.activation(sd[:], mv[:, :, 1], ACT.Sqrt, bias=eps[:]).then_inc(l_act, 1)
                    if live[1]:
                        act.wait_ge(qkv, u.times(2, 1))
                        act.wait_ge(n_dve, u.times(4))
                        act.activation(sq[:].rearrange("p k n -> p (k n)"), psQ[:], ACT.Square).then_inc(sq_in, 1)
                    if live[2]:
                        if v.base >= 2 or v.n is not None:
                            act.wait_ge(out[v.slot], v.over(32))
                        act.wait_ge(q_pe, v.times(2, 1))
                        act.activation(qo[v.slot][:].rearrange("p c n -> p (c n)"), psT[:], ACT.Copy).then_inc(q_in, 1)
                    if live[1]:
                        act.wait_ge(n_dve, u.times(4, 1))
                        act.activation(nr[:], ss[:], ACT.Sqrt, scale=1.0 / LD).then_inc(n_act, 1)
                        act.wait_ge(qkv, u.times(2, 2))
                        act.activation(VL[:, u.span(BLK), :, :], psV[:].rearrange("p (k h d) -> p k h d", k=BLK, h=LH),
                                       ACT.Copy).then_inc(v_in, 1)
                    if live[2]:
                        act.wait_ge(q_pe, v.times(2, 2))
                        act.activation(ko[v.slot][:].rearrange("p c n -> p (c n)"), psT[:], ACT.Copy).then_inc(q_in, 1)
                    if live[0]:
                        act.wait_ge(l_pe, t.times(1, 1))
                        act.activation(lT[:].rearrange("p c n -> p (c n)"), psT[:], ACT.Copy).then_inc(lt_in, 1)

                run_turns(act, turn, NB, 2, 2)

            @block.gpsimd
            def _(pool):
                pool.wait_ge(loaded, 48)

                def turn(t, live):
                    u = t + -1
                    if live[0]:
                        pool.wait_ge(l_dve, t.times(4, 4))
                        pool.wait_ge(l_pe, t.times(1))
                        pool.tensor_tensor(ln[:], xc[:], lg[:].unsqueeze(1).broadcast_to([P, BLK, D]), ALU.mult).then_inc(l_pool, 1)
                        pool.wait_ge(l_pool, t.times(2, 1))
                        pool.tensor_tensor(ln[:], ln[:], lb[:].unsqueeze(1).broadcast_to([P, BLK, D]), ALU.add).then_inc(l_pool, 1)
                    if live[1]:
                        pool.wait_ge(n_dve, u.times(4, 4))
                        for q in range(2):
                            for k in range(BLK):
                                x = nrm[u.slot][:, k, q * D:(q + 1) * D].rearrange("p (h d) -> p h d", h=LH)
                                last = pool.tensor_tensor(x, x, gam[:, q * LD:(q + 1) * LD].unsqueeze(1).broadcast_to([P, LH, LD]), ALU.mult)
                        last.then_inc(n_pool, 1)

                run_turns(pool, turn, NB, 1, 2)

            @block.vector
            def _(dve):
                dve.memset(eps[:], LN_EPS).then_inc(const, 1)

                def turn(t, live):
                    u = t + -1
                    if live[0]:
                        s = Steps(dve, l_dve, t, 4)
                        xk = lambda k: X[:, bass.ds(t.times(BLK, k), 1) if t.n is not None else slice(t.times(BLK, k), t.times(BLK, k) + 1), :]\
                            .rearrange("p o d -> p (o d)")
                        for k in range(BLK):
                            last = dve.bn_stats(st[:, k, :], xk(k))
                        s.did(last)
                        s.wait()
                        dve.sem_inc(passed, 1)
                        for k in range(BLK):
                            last = dve.bn_aggr(mv[:, k, :], st[:, k, :])
                        s.did(last)
                        dve.wait_ge(l_act, t.times(1, 1))
                        s.did(dve.reciprocal(rs[:], sd[:]))
                        s.wait()
                        dve.wait_ge(l_pool, t.times(2))
                        for k in range(BLK):
                            last = dve.tensor_scalar(xc[:, k, :], xk(k), mv[:, k, 0:1], rs[:, k:k + 1], ALU.subtract, ALU.mult)
                        s.did(last)
                    if live[1]:
                        s = Steps(dve, n_dve, u, 4)
                        dve.wait_ge(sq_in, u.times(1, 1))
                        s.did(dve.tensor_reduce(ss[:], sq[:].rearrange("p k (h d) -> p (k h) d", h=2 * LH), AX, ALU.add))
                        dve.wait_ge(n_act, u.times(1, 1))
                        s.did(dve.tensor_scalar(ns[:], nr[:], 1e-8, None, ALU.max))
                        s.wait()
                        s.did(dve.reciprocal(rn[:], ns[:]))
                        s.wait()
                        if u.base >= 2 or u.n is not None:
                            dve.wait_ge(q_pe, (u + -1).times(2))
                        s.did(dve.tensor_tensor(nrm[u.slot][:].rearrange("p k (h d) -> p (k h) d", h=2 * LH),
                                                psQ[:].rearrange("p (k h d) -> p (k h) d", k=BLK, h=2 * LH),
                                                rn[:].unsqueeze(2).broadcast_to([P, R, LD]), ALU.mult))

                run_turns(dve, turn, NB, 1, 2)


def latent_attend(nc, a, keep, sems):
    ident, QT, KD, VL, kTc, Vc, ones, maskrow, AO = (keep[k] for k in ("ident", "QT", "KD", "VL", "kTc", "Vc", "ones1", "maskrow", "AO"))
    UNITS = TB * LH
    STEP = 2 * LH
    NP = TB + 1
    with ExitStack() as ctx:
        m = Mem(nc, ctx)
        two = lambda name, shape, dt=F32: [m.sb(f"x1_{name}{k}", shape, dt) for k in range(2)]
        qs = two("qs", [P, DC, P])
        Kb, Vb, mb = two("Kb", [P, DC, S + CTX]), two("Vb", [P, NP, LH, P]), two("mb", [1, CTX])
        E, Ec = two("E", [P, S]), two("Ec", [P, CTX])
        ET = two("ET", [P, NP, P])
        mx = two("mx", [P, 2])
        nm = two("nm", [P, 1])
        rc = two("rc", [P, P])
        psS = [m.ps(f"x1_psS{k}", S) for k in range(2)]
        psC = m.ps("x1_psC", HALF)
        psE = m.ps("x1_psE", S)
        psO = m.ps("x1_psO", HALF)
        sem = lambda name: sems.sem(f"x1_{name}")
        qs_in = [sem(f"qs_in{k}") for k in range(2)]
        kv_in = [sem(f"kv_in{k}") for k in range(2)]
        s_pe = sem("s_pe")
        m_dve = sem("m_dve")
        e_act = sem("e_act")
        t_pe = sem("t_pe")
        t_dve = sem("t_dve")
        t_act = sem("t_act")
        c_pe = sem("c_pe")
        c_act = sem("c_act")
        o_pe = sem("o_pe")
        o_dve = sem("o_dve")
        blank = sem("blank")
        passed = sem("passed")

        def batches(eng, body):
            with eng.Fori(0, B // 2) as o:
                for k in range(2):
                    def units(turn, count, lag, step, first=0):
                        run_turns(eng, lambda t, live: turn(In(t, o, k, count), live), count, lag, step, first)
                    body(units, k, o)

        class In(At):

            def __init__(self, t, o, k, count):
                super().__init__(t.base, t.n, t.step)
                self.o, self.k, self.count = o, k, count

            def __add__(self, d):
                return In(At(self.base + d, self.n, self.step), self.o, self.k, self.count)

            def times(self, a, b=0):
                return self.o * (2 * self.count * a) + (self.k * self.count * a + b) + At.times(self, a)

        with nc.Block() as block:
            @block.gpsimd
            def _(pool):
                for k in range(2):
                    pool.memset(Vb[k][:], 1.0).then_inc(blank, 1)
                    pool.wait_ge(blank, k + 1)
                for b in range(B):
                    k = b % 2
                    if b >= 2:
                        pool.wait_ge(o_pe, (b - 1) * UNITS + 1)
                    pairs = lambda x: x.rearrange("p t (c h) d -> p t c h d", h=2)
                    values = [(pairs(Vb[k][:, 0:TB])[:, :, :, h, LD * h:LD * h + LD], pairs(VL[:, b * TB:(b + 1) * TB])[:, :, :, h, :])
                              for h in range(2)]
                    values += [(pairs(Vb[k][0:CTX, TB:NP])[:, 0, :, h, LD * h:LD * h + LD], pairs(Vc[:, b:b + 1])[:, 0, :, h, :])
                               for h in range(2)]
                    for dst, src in (*values, (Kb[k][:, :, 0:S], KD.rearrange("(c p) n -> p c n", p=P)[:, :, b * S:(b + 1) * S]),
                                     (Kb[k][:, :, S:], kTc[:, :, b, :]), (mb[k][:], maskrow[:, b * CTX:(b + 1) * CTX])):
                        pool.dma_start(dst, src).then_inc(kv_in[k], 16)

            @block.sync
            def _(sp):
                def body(units, k, o):
                    def turn(t, live):
                        sp.wait_ge(s_pe, t.times(LH))
                        n = bass.ds(t.times(P), P)
                        sp.dma_start(qs[t.slot][:], QT.rearrange("(c p) n -> p c n", p=P)[:, :, n]).then_inc(qs_in[t.slot], 16)

                    units(turn, TB, 0, 2)

                batches(sp, body)

            @block.tensor
            def _(pe):
                pe.sem_inc(s_pe, LH)
                pe.sem_inc(t_pe, 2)
                pe.sem_inc(c_pe, 1)
                pe.sem_inc(o_pe, 1)

                def body(units, j, o):
                    def scores(u):
                        h, k = u.slot % LH, u.slot % 2
                        if h == 0:
                            tiles = u.o * TB + (j * TB // 2 + 1) + (u.base // STEP if u.n is None else u.n + u.base // STEP)
                            pe.wait_ge(qs_in[u.slot // LH], tiles * 16)
                        pe.wait_ge(e_act, u.times(2))
                        pe.sem_inc(passed, 1)
                        rows = slice(LD * (h % 2), LD * (h % 2) + LD)
                        q, key = qs[u.slot // LH][rows, h // 2, :], Kb[j][rows, h // 2, :]
                        for i in range(2):
                            pe.matmul(psS[k][:, i * HALF:(i + 1) * HALF], q, key[:, i * HALF:(i + 1) * HALF], start=True, stop=True)
                        pe.wait_ge(e_act, u.times(2, 1))
                        pe.wait_ge(c_act, u.times(1))
                        pe.sem_inc(passed, 1)
                        out = psC[:, k * CTX:(k + 1) * CTX]
                        pe.matmul(out, ones[:], mb[j][:], start=True, stop=False)
                        pe.matmul(out, q, key[:, S:], start=False, stop=True).then_inc(s_pe, 1)

                    def transposes(u):
                        k = u.slot % 2
                        pe.wait_ge(e_act, u.times(2, 4))
                        pe.wait_ge(t_dve, u.times(1))
                        for i in range(4):
                            last = pe.transpose(psE[:, i * P:(i + 1) * P], E[k][:, i * P:(i + 1) * P], ident[:])
                        last.then_inc(t_pe, 1)
                        pe.wait_ge(t_act, u.times(1))
                        for i in range(4, 8):
                            last = pe.transpose(psE[:, i * P:(i + 1) * P], E[k][:, i * P:(i + 1) * P], ident[:])
                        last.then_inc(t_pe, 1)

                    def context_transposes(u, after):
                        pe.wait_ge(e_act, (u + after).times(2, 3 if after else 4))
                        pe.sem_inc(passed, 1)
                        pe.transpose(psC[0:CTX, P:2 * P], Ec[u.slot % 2][:], ident[:]).then_inc(c_pe, 1)

                    def outputs(u):
                        k, h = u.slot % 2, u.slot % LH
                        pe.wait_ge(t_dve, u.times(1, 1))
                        pe.wait_ge(t_act, u.times(1, 1))
                        pe.wait_ge(c_act, u.times(1, 2))
                        pe.wait_ge(o_dve, u.times(2))
                        out = psO[:, h * P:(h + 1) * P]
                        for i in range(TB):
                            pe.matmul(out, Vb[j][:, i, h, :], ET[k][:, i, :], start=(i == 0), stop=False)
                        pe.matmul(out, Vb[j][0:CTX, TB, h, :], ET[k][0:CTX, TB, :], start=False, stop=True).then_inc(o_pe, 1)

                    def turn(t, live):
                        if live[0]:
                            scores(t)
                        if live[1]:
                            transposes(t + -1)
                        if live[2]:
                            outputs(t + -2)
                        if live[1]:
                            context_transposes(t + -1, 1 if live[0] else 0)

                    pe.wait_ge(kv_in[j], o * 112 + 112)
                    units(turn, UNITS, 2, STEP)

                batches(pe, body)

            @block.scalar
            def _(act):
                act.sem_inc(e_act, 2)
                act.sem_inc(c_act, 1)

                def turn(t, live):
                    if live[1]:
                        u = t + -1
                        k = u.slot % 2
                        act.wait_ge(t_pe, u.times(2, 4))
                        act.wait_ge(o_pe, u.times(1))
                        act.activation(ET[k][:, 4:8, :].rearrange("p j n -> p (j n)"), psE[:, HALF:], ACT.Copy).then_inc(t_act, 1)
                    if live[0]:
                        act.wait_ge(t_pe, t.times(2))
                        act.wait_ge(c_pe, t.times(1))
                        k = t.slot % 2
                        act.wait_ge(m_dve, t.times(2, 2))
                        act.activation(Ec[k][:], psC[:, k * CTX:(k + 1) * CTX], ACT.Exp, bias=nm[k][:]).then_inc(e_act, 1)
                        act.activation(E[k][:], psS[k][:], ACT.Exp, bias=nm[k][:]).then_inc(e_act, 1)
                    if live[1]:
                        u = t + -1
                        act.wait_ge(c_pe, u.times(1, 2))
                        act.activation(ET[u.slot % 2][0:CTX, TB, :], psC[0:CTX, P:2 * P], ACT.Copy).then_inc(c_act, 1)

                batches(act, lambda units, k, o: units(turn, UNITS, 1, STEP))

            @block.vector
            def _(dve):
                def turn(t, live):
                    if live[0]:
                        k = t.slot % 2
                        dve.wait_ge(s_pe, t.times(1, 1 + LH))
                        dve.tensor_reduce(mx[k][:, 0:1], psS[k][:], AX, ALU.max)
                        dve.tensor_reduce(mx[k][:, 1:2], psC[:, k * CTX:(k + 1) * CTX], AX, ALU.max).then_inc(m_dve, 1)
                        dve.wait_ge(m_dve, t.times(2, 1))
                        dve.wait_ge(e_act, t.times(2))
                        dve.tensor_scalar(nm[k][:], mx[k][:, 0:1], mx[k][:, 1:2], -1.0, ALU.max, ALU.mult).then_inc(m_dve, 1)
                    if live[1]:
                        u = t + -1
                        dve.wait_ge(t_pe, u.times(2, 3))
                        dve.wait_ge(o_pe, u.times(1))
                        dve.tensor_copy(ET[u.slot % 2][:, 0:4, :].rearrange("p j n -> p (j n)"), psE[:, 0:HALF]).then_inc(t_dve, 1)
                    if live[2]:
                        u = t + -2
                        h, k = u.slot % LH, u.slot % 2
                        dve.wait_ge(o_pe, u.times(1, 2))
                        mine, other = (slice(LD * r, LD * r + LD) for r in (h % 2, 1 - h % 2))
                        out = psO[:, h * P:(h + 1) * P]
                        dve.reciprocal(rc[k][mine, :], out[other, :]).then_inc(o_dve, 1)
                        dve.wait_ge(o_dve, u.times(2, 1))
                        tile = In(At(u.base // LH, u.n, STEP // LH), u.o, u.k, TB).times(P)
                        dve.tensor_tensor(AO[mine, h // 2, bass.ds(tile, P)], out[mine, :], rc[k][mine, :], ALU.mult).then_inc(o_dve, 1)

                batches(dve, lambda units, k, o: units(turn, UNITS, 2, STEP))


HC = 4
TAKEN = S // 2


def choose(nc, a, keep, sems):
    X, ident, HT, SEL, SELB = (keep[k] for k in ("X", "ident", "HT", "SEL", "SELB"))
    NB = NT // BLK
    RE = B * EX
    BITS = 31
    with ExitStack() as ctx:
        m = Mem(nc, ctx)
        sb = lambda name, shape, dt=F32: m.sb(f"f1_{name}", shape, dt)
        xs = [sb(f"xs{k}", [P, BLK, D]) for k in range(2)]
        xt = [sb(f"xt{k}", [P, DC, HALF]) for k in range(2)]
        XT = sb("XT", [P, DC, B * S])
        w1, b1, wg, bg = sb("w1", [P, DC, HC * P]), sb("b1", [P, HC]), sb("wg", [P, DC, EX]), sb("bg", [P, EX])
        iota = sb("iota", [P, EX])
        G = [P, NT, EX]
        logit, less, ex, gate, hot1, hot2, hot, masked = (sb(n, G) for n in ("logit", "less", "ex", "gate", "hot1", "hot2", "hot", "masked"))
        top, ix = sb("top", [P, NT, 8]), sb("ix", [P, NT, 8], U32)
        ixf, mx, sm, rc = sb("ixf", [P, NT, 2]), sb("mx", [P, NT]), sb("sm", [P, NT]), sb("rc", [P, NT])
        den = [sb(f"den{k}", [P, TB, EX]) for k in range(4)]
        rden = sb("rden", [P, TB, EX])
        route, routes = sb("route", [P, TB, B, EX]), sb("routes", [P, TB, B, EX])
        v, gt, eq, rank, tie = (sb(n, [RE, S]) for n in ("v", "gt", "eq", "rank", "tie"))
        sel, selb = sb("sel", [RE, S]), sb("selb", [RE, S], BF16)
        bits_i, bits_f = sb("bits_i", [RE, BITS], I32), sb("bits_f", [RE, BITS])
        T, cand, gain = sb("T", [RE, 1], I32), sb("cand", [RE, 1], I32), sb("gain", [RE, 1], I32)
        cnt, above, room = sb("cnt", [RE, 1]), sb("above", [RE, 1]), sb("room", [RE, 1])
        psT = m.ps("f1_psT", BLK * D)
        psG = m.ps("f1_psG", HALF)
        psR = m.ps("f1_psR", S)
        psH = [m.ps(f"f1_psH{k}", HALF) for k in range(3)]
        sem = lambda name: sems.sem(f"f1_{name}")
        loaded = sem("loaded")
        xs_in = [sem(f"xs_in{k}") for k in range(2)]
        x_pe = sem("x_pe")
        x_act = sem("x_act")
        kept = [sem(f"kept{k}") for k in range(2)]
        g_pe = sem("g_pe")
        done = sem("done")
        exps = sem("exps")
        r_pe = sem("r_pe")
        h_pe = sem("h_pe")
        h_act = sem("h_act")
        found = sem("found")
        stored = sem("chosen")
        passed = sem("passed")
        NLESS, NROUTE = 3, 21
        with nc.Block() as block:
            @block.sync
            def _(sp):
                for dst, src in ((w1[:], a["L1f_w1"]), (b1[:], a["L1f_b1"]), (wg[:], a["L1f_wg"]),
                                 (bg[:], a["L1_ffn_w_gate_b"].rearrange("(o d) -> o d", o=1).broadcast_to([P, EX])),
                                 (iota[:], a["iota8"].broadcast_to([P, EX])),
                                 (bits_i[:], a["bits_i"].broadcast_to([RE, BITS])), (bits_f[:], a["bits_f"].broadcast_to([RE, BITS]))):
                    sp.dma_start(dst, src).then_inc(loaded, 16)

                def turn(t, live):
                    u = t + -1
                    if live[0]:
                        if t.base >= 2 or t.n is not None:
                            sp.wait_ge(x_pe, (t + -1).times(1))
                        sp.dma_start(xs[t.slot][:], X[:, t.span(BLK), :]).then_inc(xs_in[t.slot], 16)
                    if live[1]:
                        sp.wait_ge(x_act, u.times(1, 1))
                        sp.dma_start(XT[:, :, u.span(HALF)], xt[u.slot][:]).then_inc(kept[u.slot], 16)

                run_turns(sp, turn, NB, 1, 2)
                sp.wait_ge(done, NROUTE + 7)
                sp.dma_start(SEL, sel[:]).then_inc(stored, 16)
                sp.dma_start(SELB, selb[:]).then_inc(stored, 16)
                sp.wait_ge(stored, 32)

            @block.tensor
            def _(pe):
                pe.wait_ge(loaded, 112)

                def turn(t, live):
                    u = t + -1
                    if live[0]:
                        pe.wait_ge(xs_in[t.slot], t.over(16, 16))
                        pe.wait_ge(x_act, t.times(1))
                        for c in range(DC):
                            for k in range(BLK):
                                last = pe.transpose(psT[:, (c * BLK + k) * P:(c * BLK + k + 1) * P], xs[t.slot][:, k, c * P:(c + 1) * P], ident[:])
                        last.then_inc(x_pe, 1)
                    if live[1]:
                        pe.wait_ge(x_act, u.times(1, 1))
                        for k in range(BLK):
                            for c in range(DC):
                                col = slice((u.base * BLK + k) * EX, (u.base * BLK + k + 1) * EX) if u.n is None \
                                    else bass.ds(u.times(BLK * EX, k * EX), EX)
                                last = pe.matmul(psG[:, col], xt[u.slot][:, c, k * P:(k + 1) * P], wg[:, c, :],
                                                 start=(c == 0), stop=(c == DC - 1))
                        last.then_inc(g_pe, 1)

                run_turns(pe, turn, NB, 1, 2)
                for k in range(2):
                    pe.wait_ge(kept[k], 16 * (NB // 2))

                def hidden_block(i):
                    for h in range(HC):
                        n = i * HC + h
                        pe.wait_ge(h_act, n + 1)
                        for c in range(DC):
                            last = pe.matmul(psH[n % 3][:], w1[:, c, h * P:(h + 1) * P], XT[:, c, i * HALF:(i + 1) * HALF],
                                             start=(c == 0), stop=(c == DC - 1))
                        last.then_inc(h_pe, 1)

                hidden_block(0)
                hidden_block(1)
                pe.wait_ge(done, NROUTE)
                for t in range(TB):
                    last = pe.transpose(psR[0:RE, t * P:(t + 1) * P], routes[:, t, :, :].rearrange("p b e -> p (b e)"), ident[:])
                last.then_inc(r_pe, 1)
                for i in range(2, NB):
                    hidden_block(i)

            @block.scalar
            def _(act):
                act.sem_inc(h_act, 3)
                act.wait_ge(loaded, 112)

                def turn(t, live):
                    act.wait_ge(x_pe, t.times(1, 1))
                    if t.base >= 2 or t.n is not None:
                        act.wait_ge(kept[t.slot], t.over(16))
                        act.wait_ge(g_pe, (t + -1).times(1))
                    act.activation(xt[t.slot][:].rearrange("p c n -> p (c n)"), psT[:], ACT.Copy).then_inc(x_act, 1)

                run_turns(act, turn, NB, 0, 2, 2)
                act.wait_ge(done, NLESS)
                act.activation(ex[:], less[:], ACT.Exp).then_inc(exps, 1)
                for n in range(NB * HC):
                    act.wait_ge(h_pe, n + 1)
                    act.activation(HT[:, n % HC, n // HC * HALF:(n // HC + 1) * HALF], psH[n % 3][:], ACT.Gelu,
                                   bias=b1[:, n % HC:n % HC + 1]).then_inc(h_act, 1)

            @block.vector
            def _(dve):
                s = Chain(dve, done)
                dve.wait_ge(loaded, 112)
                dve.wait_ge(g_pe, NB)
                s.did(dve.tensor_tensor(logit[:], psG[:, 0:NT * EX].rearrange("p (t e) -> p t e", e=EX),
                                        bg[:].unsqueeze(1).broadcast_to(G), ALU.add))
                s.wait()
                s.did(dve.tensor_reduce(mx[:], logit[:], AX, ALU.max))
                s.wait()
                s.did(dve.tensor_tensor(less[:], logit[:], mx[:].unsqueeze(2).broadcast_to(G), ALU.subtract))
                assert s.n == NLESS
                dve.wait_ge(exps, 1)
                s.did(dve.tensor_reduce(sm[:], ex[:], AX, ALU.add))
                s.wait()
                s.did(dve.reciprocal(rc[:], sm[:]))
                s.wait()
                s.did(dve.tensor_tensor(gate[:], ex[:], rc[:].unsqueeze(2).broadcast_to(G), ALU.mult))
                s.wait()
                for t in range(NT):
                    last = dve.max(top[:, t, :], gate[:, t, :])
                s.did(last)
                s.wait()
                for t in range(NT):
                    last = dve.max_index(ix[:, t, :], top[:, t, :], gate[:, t, :])
                s.did(last)
                s.wait()
                s.did(dve.tensor_copy(ixf[:], ix[:, :, 0:2]))
                s.wait()
                for n, hot_n in ((0, hot1), (1, hot2)):
                    s.did(dve.tensor_tensor(hot_n[:], iota[:].unsqueeze(1).broadcast_to(G), ixf[:, :, n:n + 1].broadcast_to(G), ALU.is_equal))
                s.wait()
                s.did(dve.tensor_tensor(hot[:], hot1[:], hot2[:], ALU.add))
                s.wait()
                s.did(dve.tensor_tensor(masked[:], gate[:], hot[:], ALU.mult))
                s.wait()
                mb = masked[:].rearrange("p (b t) e -> p b t e", b=B)
                s.did(dve.tensor_tensor(den[0][:], mb[:, 0], mb[:, 1], ALU.add))
                for n in (2, 3):
                    s.wait()
                    s.did(dve.tensor_tensor(den[n - 1][:], den[n - 2][:], mb[:, n], ALU.add))
                s.wait()
                s.did(dve.tensor_scalar(den[3][:], den[2][:], 1e-6, None, ALU.add))
                s.wait()
                s.did(dve.reciprocal(rden[:], den[3][:]))
                s.wait()
                for b in range(B):
                    last = dve.tensor_tensor(route[:, :, b, :], mb[:, b], rden[:], ALU.mult)
                s.did(last)
                s.wait()
                s.did(dve.tensor_scalar(routes[:], route[:], float(B), None, ALU.mult))
                s.did(dve.memset(T[:], 0))
                assert s.n == NROUTE, s.n
                dve.wait_ge(r_pe, 1)
                s.did(dve.tensor_copy(v[:], psR[0:RE, :]))
                s.wait()
                with dve.Fori(0, BITS) as i:
                    dve.wait_ge(found, i * 4)
                    dve.tensor_tensor(cand[:], T[:], bits_i[:, bass.ds(i, 1)], ALU.bitwise_or).then_inc(found, 1)
                    dve.wait_ge(found, i * 4 + 1)
                    dve.tensor_scalar(gt[:], v[:], cand[:].bitcast(F32), None, ALU.is_ge, ALU.add, accum_out=cnt[:]).then_inc(found, 1)
                    dve.wait_ge(found, i * 4 + 2)
                    dve.scalar_tensor_tensor(out=gain[:], in0=cnt[:], scalar=float(TAKEN), in1=bits_f[:, bass.ds(i, 1)],
                                             op0=ALU.is_ge, op1=ALU.mult).then_inc(found, 1)
                    dve.wait_ge(found, i * 4 + 3)
                    dve.tensor_tensor(T[:], T[:], gain[:], ALU.bitwise_or).then_inc(found, 1)
                dve.wait_ge(found, BITS * 4)
                T_f = T[:].bitcast(F32)
                s.did(dve.tensor_scalar(gt[:], v[:], T_f, None, ALU.is_gt, ALU.add, accum_out=above[:]))
                s.did(dve.tensor_scalar(eq[:], v[:], T_f, None, ALU.is_equal))
                s.wait()
                s.did(dve.tensor_scalar(room[:], above[:], -1.0, float(TAKEN), ALU.mult, ALU.add))
                s.did(dve.tensor_tensor_scan(rank[:], eq[:], eq[:], 0.0, ALU.add, ALU.bypass))
                s.wait()
                s.did(dve.scalar_tensor_tensor(out=tie[:], in0=rank[:], scalar=room[:], in1=eq[:], op0=ALU.is_le, op1=ALU.mult))
                s.wait()
                dve.tensor_tensor(selb[:], tie[:], gt[:], ALU.add)
                s.did(dve.tensor_tensor(sel[:], tie[:], gt[:], ALU.add))
                assert s.n == NROUTE + 7, s.n


def take(nc, a, keep, sems):
    X, HT, SEL, SELB = (keep[k] for k in ("X", "HT", "SEL", "SELB"))
    NB = NT // BLK
    with ExitStack() as ctx:
        m = Mem(nc, ctx)
        sb = lambda name, shape, dt=F32: m.sb(f"f1t_{name}", shape, dt)
        w2, b2 = sb("w2", [P, HC, D]), sb("b2", [EX, D])
        sw = [sb(f"sw{k}", [P, HC, HALF], BF16) for k in range(2)]
        sk = [sb(f"sk{k}", [EX, HALF]) for k in range(2)]
        hm = [sb(f"hm{k}", [P, HC, HALF]) for k in range(2)]
        y = sb("y", [P, BLK, D])
        st, mv, sd, rs, eps = sb("st", [P, BLK, 6]), sb("mv", [P, BLK, 2]), sb("sd", [P, BLK]), sb("rs", [P, BLK]), sb("eps", [P, 1])
        psY = [m.ps(f"f1t_psY{k}", BLK * D) for k in range(2)]
        sem = lambda name: sems.sem(f"f1t_{name}")
        loaded, const = sem("loaded"), sem("const")
        s_in = [sem(f"s_in{k}") for k in range(2)]
        h_dve = sem("h_dve")
        y_pe = sem("y_pe")
        n_dve = sem("n_dve")
        n_act = sem("n_act")
        passed = sem("passed")
        with nc.Block() as block:
            @block.sync
            def _(sp):
                for dst, src in ((w2[:], a["L1f_w2"]), (b2[:], a["L1_ffn_b2"])):
                    sp.dma_start(dst, src).then_inc(loaded, 16)

                def turn(t, live):
                    if t.base >= 2 or t.n is not None:
                        sp.wait_ge(h_dve, (t + -1).times(1))
                        sp.wait_ge(y_pe, (t + -1).times(1))
                    n = slice(t.slot * HALF, (t.slot + 1) * HALF)
                    b = t.over(1) if t.n is None else bass.ds(t.over(1), 1)
                    b = slice(b, b + 1) if t.n is None else b
                    for e in range(2):
                        src = SELB.rearrange("(b c e) n -> e b c n", b=B, e=2)[e][b, :, n]
                        sp.dma_start(sw[t.slot][64 * e:64 * e + 64, :, :], src.broadcast_to([64, HC, HALF])).then_inc(s_in[t.slot], 16)
                    sp.dma_start(sk[t.slot][:], SEL.rearrange("(b e) n -> b e n", b=B)[b, :, n].rearrange("o e n -> (o e) n"))\
                        .then_inc(s_in[t.slot], 16)

                run_turns(sp, turn, NB, 0, 2, 2)

            @block.tensor
            def _(pe):
                pe.wait_ge(loaded, 32)

                def turn(t, live):
                    pe.wait_ge(h_dve, t.times(1, 1))
                    pe.wait_ge(s_in[t.slot], t.over(48, 48))
                    if t.base >= 2 or t.n is not None:
                        pe.wait_ge(n_dve, (t + -2).times(5, 1))
                    for k in range(BLK):
                        out = psY[t.slot][:, k * D:(k + 1) * D]
                        pe.matmul(out, sk[t.slot][:, k * P:(k + 1) * P], b2[:], start=True, stop=False)
                        for c in range(HC):
                            last = pe.matmul(out, hm[t.slot][:, c, k * P:(k + 1) * P], w2[:, c, :], start=False, stop=(c == HC - 1))
                    last.then_inc(y_pe, 1)

                run_turns(pe, turn, NB, 0, 2, 2)

            @block.scalar
            def _(act):
                act.wait_ge(const, 1)
                with act.Fori(0, NB) as i:
                    act.wait_ge(n_dve, i * 5 + 3)
                    act.activation(sd[:], mv[:, :, 1], ACT.Sqrt, bias=eps[:]).then_inc(n_act, 1)

            @block.vector
            def _(dve):
                dve.memset(eps[:], LN_EPS).then_inc(const, 1)

                def turn(t, live):
                    u = t + -1
                    if live[0]:
                        dve.wait_ge(s_in[t.slot], t.over(48, 48))
                        if t.base >= 2 or t.n is not None:
                            dve.wait_ge(y_pe, (t + -1).times(1))
                        dve.tensor_tensor(hm[t.slot][:], HT[:, :, t.span(HALF)], sw[t.slot][:], ALU.mult).then_inc(h_dve, 1)
                    if live[1]:
                        dve.wait_ge(y_pe, u.times(1, 1))
                        dve.wait_ge(n_dve, u.times(5))
                        dve.tensor_tensor(y[:], psY[u.slot][:].rearrange("p (k d) -> p k d", k=BLK), X[:, u.span(BLK), :],
                                          ALU.add).then_inc(n_dve, 1)
                        dve.wait_ge(n_dve, u.times(5, 1))
                        for k in range(BLK):
                            last = dve.bn_stats(st[:, k, :], y[:, k, :])
                        last.then_inc(n_dve, 1)
                        dve.wait_ge(n_dve, u.times(5, 2))
                        dve.sem_inc(passed, 1)
                        for k in range(BLK):
                            last = dve.bn_aggr(mv[:, k, :], st[:, k, :])
                        last.then_inc(n_dve, 1)
                        dve.wait_ge(n_act, u.times(1, 1))
                        dve.reciprocal(rs[:], sd[:]).then_inc(n_dve, 1)
                        dve.wait_ge(n_dve, u.times(5, 4))
                        for k in range(BLK):
                            out = X[:, bass.ds(u.times(BLK, k), 1) if u.n is not None else slice(u.times(BLK, k), u.times(BLK, k) + 1), :]
                            last = dve.tensor_scalar(out.rearrange("p o d -> p (o d)"), y[:, k, :], mv[:, k, 0:1], rs[:, k:k + 1],
                                                     ALU.subtract, ALU.mult)
                        last.then_inc(n_dve, 1)

                run_turns(dve, turn, NB, 1, 2, 2)


def store(nc, a, keep, sems):
    out = sems.sem("stored")
    with nc.Block() as block:
        @block.sync
        def _(sp):
            sp.dma_start(a["y"].rearrange("(t p) d -> p t d", p=P), keep["X"][:]).then_inc(out, 16)
            sp.wait_ge(out, 16)


def attention(nc, a, keep, sems, layer, dh, groups):
    with nc.cleanup_on_exit(), ExitStack() as own:
        w = 4 * DV * 16 // groups
        mem = Mem(nc, own)
        keep["VA"] = mem.sb(f"L{layer}_VA", [P, groups, TB, w])
        project(nc, a, keep, sems, f"L{layer}", dh // 2, groups)
        keep["AO"] = mem.sb(f"L{layer}_AO", [P, groups, TB, w])
        attend(nc, a, keep, sems, f"L{layer}", dh, groups, layer == 0)
        merge(nc, a, keep, sems, f"L{layer}", groups, layer == 1)


def cross_attention(nc, a, keep, sems):
    with nc.cleanup_on_exit(), ExitStack() as own:
        mem = Mem(nc, own)
        keep["KT"] = mem.sb("L0x_KT", [P, DC, B, 64])
        keep["VBD"], keep["OB"] = mem.sb("L0x_VBD", [P, B, H // 2, 2 * DV]), mem.sb("L0x_OB", [P, 2 * DV])
        for name in ("bq", "bo", "lg", "lb"):
            keep[name] = mem.sb(f"L0x_{name}", [P, D])
        keep["heads8"] = mem.sb("L0x_heads8", [P, 8])
        cross_setup(nc, a, keep, sems)
        cross(nc, a, keep, sems)


def latent_attention(nc, a, keep, sems):
    with nc.cleanup_on_exit(), ExitStack() as own:
        mem = Mem(nc, own)
        keep["QT"], keep["KD"] = (nc.dram_tensor(n, (D, B * S), F32).ap() for n in ("queries", "keys"))
        keep["ones1"], keep["maskrow"] = mem.sb("L1x_ones", [1, P]), mem.sb("L1x_maskrow", [1, B * CTX])
        keep["kTc"], keep["Vc"] = mem.sb("L1x_kTc", [P, DC, B, CTX]), mem.sb("L1x_Vc", [CTX, B, LH, LD])
        keep["gam"] = mem.sb("L1x_gam", [P, 2 * LD])
        keep["VL"] = mem.sb("L1x_VL", [P, NT, LH, LD])
        context_keys(nc, a, keep, sems)
        latent_project(nc, a, keep, sems)
        keep["AO"] = mem.sb("L1x_AO", [P, DC, B * S])
        latent_attend(nc, a, keep, sems)
        merge(nc, a, keep, sems, "L1x", 1, False, bias="L1_xattn_bo")


def expert_choice(nc, a, keep, sems):
    with nc.cleanup_on_exit(), ExitStack() as own:
        keep["SEL"] = nc.dram_tensor("choice", (B * EX, S), F32).ap()
        keep["SELB"] = nc.dram_tensor("choice_bf16", (B * EX, S), BF16).ap()
        keep["HT"] = Mem(nc, own).sb("L1f_HT", [P, HC, B * S])
        choose(nc, a, keep, sems)
        take(nc, a, keep, sems)


def decoder(nc, a, stages=None):
    with ExitStack() as ctx:
        sems = Mem(nc, ctx)
        keep = {"X": sems.sb("X", [P, NT, D]), "ident": sems.sb("ident", [P, P]), "identb": sems.sb("identb", [P, P], BF16)}
        keep["PT"] = [nc.dram_tensor(f"parts_{n}", (3, B * D, S), BF16).ap() for n in "qk"]
        load_start(nc, a, keep, sems)
        for name, sublayer, args in (("A0", attention, (0, 16, 16)), ("X0", cross_attention, ()), ("M0", experts, ()),
                                     ("A1", attention, (1, 8, 32)), ("X1", latent_attention, ()), ("F1", expert_choice, ())):
            if stages is None or name in stages:
                sublayer(nc, a, keep, sems, *args)
        store(nc, a, keep, sems)


def layouts(x):
    o = {k: np.ascontiguousarray(v) for k, v in x.items()}
    f = {}

    def chunked(wt):
        return np.ascontiguousarray(wt.reshape(-1, P, wt.shape[1]).transpose(1, 0, 2))

    f["x"] = o["x"].reshape(B * S, D)
    f["ident"] = np.eye(P, dtype=np.float32)
    q, k = np.arange(P)[:, None], np.arange(P)[None, :]
    upper = np.where(k > q, np.float32(MASKED), np.float32(0))
    f["causal"] = np.ascontiguousarray(np.stack([upper, upper.T], 1)).astype(np.float32)
    t = np.arange(S, dtype=np.float32)
    for layer, ne in ((0, 8), (1, 4)):
        ns = 64 // ne
        c, h, s, e = np.meshgrid(np.arange(DC), np.arange(2), np.arange(ns), np.arange(ne), indexing="ij")
        inner = h * ne + e if layer == 0 else 2 * e + h
        order = ((c * ns + s) * 2 * ne + inner).reshape(-1)
        wq, wk = (o[f"L{layer}_attn_W{n}"][order] for n in "qk")
        f[f"L{layer}_wqk"] = chunked(np.concatenate([wq, wk], 0).T)
        f[f"L{layer}_wv"] = chunked(o[f"L{layer}_attn_Wv"].T)
        f[f"L{layer}_wo"] = chunked(o[f"L{layer}_attn_Wo"].T)
        if layer == 0:
            speed = np.float32(1) / np.power(np.float32(10000), np.arange(0, 16, 2, dtype=np.float32) / np.float32(16))
        else:
            speed = np.float32(1) / np.power(np.float32(10000), np.linspace(0, 1, 4, dtype=np.float32))
        angle = (speed.astype(np.float32)[:, None] * t[None, :]).astype(np.float32)
        f[f"L{layer}_cos"] = np.ascontiguousarray(np.tile(np.cos(angle), (P // ne, 1))).astype(np.float32)
        sin = np.tile(np.sin(angle), (64 // ne, 1)).astype(np.float32)
        f[f"L{layer}_sin"] = np.ascontiguousarray(np.concatenate([sin, -sin], 0))
    cT = o["ctx_768"].transpose(2, 0, 1).reshape(2, 96, B, 64)
    f["ctxT2"] = np.ascontiguousarray(np.concatenate([cT, cT], 3).transpose(1, 0, 2, 3))
    wkv = np.concatenate([o["L0_xattn_Wk"], o["L0_xattn_Wv"]], 1)
    f["L0x_wkv"] = np.ascontiguousarray(wkv.reshape(2, 96, 2 * D).transpose(1, 0, 2))
    f["L0x_wq"], f["L0x_wo"] = chunked(o["L0_xattn_Wq"]), chunked(o["L0_xattn_Wo"])
    for n in ("bq", "bk", "bv", "bo", "ln_gamma", "ln_beta"):
        f[f"L0_xattn_{n}"] = o[f"L0_xattn_{n}"]
    f["heads8"] = (np.arange(P)[:, None] // DV == np.arange(8)[None, :]).astype(np.float32)
    f["ctx_tok"] = np.ascontiguousarray(o["ctx_768"].transpose(1, 0, 2))
    f["mask8"] = o["mask_BxS2_bk0"].reshape(1, B * CTX)
    f["L1x_wkv"] = np.ascontiguousarray(o["L1_xattn_Wkv"].T.reshape(2, CK, 2 * D).transpose(1, 0, 2))
    f["L1x_w"] = chunked(np.concatenate([o["L1_xattn_Wq"], o["L1_xattn_Wlkv"]], 0).T)
    f["L1x_wo"] = chunked(o["L1_xattn_Wo"].T)
    for n in ("ln_x_g", "ln_x_b", "ln_l_g", "ln_l_b", "qn_g", "kn_g", "bo"):
        f[f"L1_xattn_{n}"] = o[f"L1_xattn_{n}"]
    f["L1f_w1"] = chunked(o["L1_ffn_W1"].transpose(1, 0, 2).reshape(D, HC * P))
    f["L1f_b1"] = np.ascontiguousarray(o["L1_ffn_b1"].reshape(HC, P).T)
    f["L1f_w2"] = chunked(o["L1_ffn_W2"].reshape(HC * P, D))
    f["L1f_wg"] = chunked(o["L1_ffn_w_gate_w"])
    f["bits_i"] = (1 << np.arange(30, -1, -1)).astype(np.int32)[None, :]
    f["bits_f"] = f["bits_i"].astype(np.float32)
    for n in ("w_gate_b", "b2"):
        f[f"L1_ffn_{n}"] = o[f"L1_ffn_{n}"]
    f["L0f_we"] = chunked(o["L0_ffn_We"].transpose(1, 0, 2).reshape(D, EX * D))
    f["L0f_wr"] = chunked(o["L0_ffn_Wr"].T)
    f["tri"] = np.triu(np.ones((P, P), np.float32), 1)
    f["iota8"] = np.arange(EX, dtype=np.float32)[None, :]
    f["L1_lambda"] = np.stack([o[f"L1_attn_lambda_{n}"] for n in ("q1", "k1", "q2", "k2")])
    f["L1_attn_rms_weight"] = o["L1_attn_rms_weight"]
    return f


def kernel(**inputs):
    import concourse.bacc as bacc
    from concourse.bass_utils import run_bass_kernel_spmd

    nc = bacc.Bacc("TRN2", target_bir_lowering=False, num_devices=1)
    arrays, a = {}, {}
    for name, value in layouts({k: np.asarray(v) for k, v in inputs.items()}).items():
        arrays[f"in_{name}"] = value
        a[name] = nc.dram_tensor(f"in_{name}", value.shape, mybir.dt.from_np(value.dtype), kind="ExternalInput").ap()
    a["y"] = nc.dram_tensor("out_y", (B * S, D), F32, kind="ExternalOutput").ap()
    decoder(nc, a)
    result = run_bass_kernel_spmd(nc, [arrays], core_ids=[0])
    return result.results[0]["out_y"].reshape(B, S, D)
```
